# Optimizing a Trainium2 kernel written in Bass

```python
import numpy as np
import jax
import jax.numpy as jnp

def _softmax(x, axis=-1):
    return jax.nn.softmax(x, axis=axis)

def _gelu(x):
    return jax.nn.gelu(x, approximate=True)

def _silu(x):
    return jax.nn.silu(x)

def _sigmoid(x):
    return jax.nn.sigmoid(x)

def _layernorm(x, axis=-1, eps=1e-05):
    m = jnp.mean(x, axis=axis, keepdims=True)
    v = jnp.var(x, axis=axis, keepdims=True)
    return (x - m) / jnp.sqrt(v + eps)

def _scatter_add(tgt, idx, src, axis=0):
    return tgt.at[idx].add(src)

def _segment_sum(src, seg, n):
    return jax.ops.segment_sum(src, seg, n)
kernel_name = 'mk_flamingo_gated_d4_seqx_r8_8def96'

def setup_inputs(seed: int=0):
    np.random.seed(seed)
    _w = jnp.asarray

    def _rec_inputs():
        import jax
        import jax.numpy as jnp
        _rk = jax.random.key(seed)
        x = -0.0003929 + 0.9999 * jax.random.normal(jax.random.fold_in(_rk, 1), (64, 64, 128), jnp.float32)
        _lenS = 64 - jax.random.randint(jax.random.fold_in(_rk, 7), (64,), 0, max(1, 64 // 4) + 1, jnp.int32)
        _lenS2 = 64 - jax.random.randint(jax.random.fold_in(_rk, 8), (64,), 0, max(1, 64 // 4) + 1, jnp.int32)
        _ctx_768P = jax.random.normal(jax.random.fold_in(_rk, 11), (64, 16, 96), jnp.float32)
        _ctx_768c = jax.random.dirichlet(jax.random.fold_in(_rk, 511), 0.3 * jnp.ones((16,), jnp.float32), (64, 64))
        _ctx_768t = jnp.einsum('bsk,bkd->bsd', _ctx_768c, _ctx_768P)
        _ctx_768t = _ctx_768t * jax.lax.rsqrt(jnp.mean(jnp.square(_ctx_768t)) + 1e-12) * 0.953939
        ctx_768 = -0.000630117 + 0.999904 * (_ctx_768t + 0.3 * jax.random.normal(jax.random.fold_in(_rk, 611), (64, 64, 96), jnp.float32))
        _validS = jnp.arange(64)[None, :] < _lenS[:, None]
        _validS2 = jnp.arange(64)[None, :] < _lenS2[:, None]
        _causal = jnp.tril(jnp.ones((64, 64), dtype=bool))
        mask_BxS2_bk0 = jnp.logical_not(jnp.broadcast_to(_validS2[:, :], (64, 64)))
        _g = jax.random.normal(jax.random.fold_in(_rk, 9001), (2, 4), jnp.float32)
        _g = jnp.sign(_g) * jnp.maximum(jnp.abs(_g), 1.0) + (_g == 0) * 1.0
        g_xattn = _g[0]
        g_ffn = _g[1]
        return (x, ctx_768, mask_BxS2_bk0, g_xattn, g_ffn)
    x, ctx_768, mask_BxS2_bk0, g_xattn, g_ffn = _rec_inputs()

    def _L0_xattn_setup():
        import jax, jax.numpy as jnp
        import numpy as np
        NUM_HEAD = 16
        LN_EPS = 1e-05

        def _layernorm(x, g, b):
            m = jnp.mean(x, axis=-1, keepdims=True)
            v = jnp.var(x, axis=-1, keepdims=True)
            return (x - m) * jax.lax.rsqrt(v + LN_EPS) * g + b
        B, T, N, D, L = (32, 64, 77, 128, 96)
        ks = jax.random.split(jax.random.key(seed), 6)
        s = 0.02
        return {'x': jax.random.normal(ks[0], (B, T, D), jnp.float32), 'xf': jax.random.normal(ks[1], (B, N, L), jnp.float32), 'q_w': jax.random.normal(ks[2], (D, D), jnp.float32) * s, 'q_b': jnp.zeros((D,), jnp.float32), 'k_w': jax.random.normal(ks[3], (L, D), jnp.float32) * s, 'k_b': jnp.zeros((D,), jnp.float32), 'v_w': jax.random.normal(ks[4], (L, D), jnp.float32) * s, 'v_b': jnp.zeros((D,), jnp.float32), 'ln_g': jnp.ones((D,), jnp.float32), 'ln_b': jnp.zeros((D,), jnp.float32), 'tln_g': jnp.ones((L,), jnp.float32), 'tln_b': jnp.zeros((L,), jnp.float32)}
    _L0_xattn_all = _L0_xattn_setup()
    _L0_xattn_in = {k: v for k, v in _L0_xattn_all.items() if k in ('q_w', 'q_b', 'k_w', 'k_b', 'v_w', 'v_b', 'ln_g', 'ln_b', 'tln_g', 'tln_b')}
    del _L0_xattn_all

    def _L0_ffn_setup():
        import jax, jax.numpy as jnp
        import numpy as np
        H = 128
        I = 64
        E = 32
        TOP_K = 6
        N_GROUP = 8
        TOPK_GROUP = 4
        SCALE = 2.5
        N_SHARED = 2
        SI = I * N_SHARED
        B, S = (2, 128)
        key = jax.random.key(seed)
        ks = jax.random.split(key, 8)
        x = jax.random.normal(ks[0], (B, S, H), jnp.float32)
        gate_weight = jax.random.normal(ks[1], (E, H), jnp.float32) * 0.02
        e_score_correction_bias = jax.random.normal(ks[2], (E,), jnp.float32) * 0.01
        experts_gate_up = jax.random.normal(ks[3], (E, 2 * I, H), jnp.float32) * 0.02
        experts_down = jax.random.normal(ks[4], (E, H, I), jnp.float32) * 0.02
        shared_gate_w = jax.random.normal(ks[5], (SI, H), jnp.float32) * 0.02
        shared_up_w = jax.random.normal(ks[6], (SI, H), jnp.float32) * 0.02
        shared_down_w = jax.random.normal(ks[7], (H, SI), jnp.float32) * 0.02
        return {'x': x, 'gate_weight': gate_weight, 'e_score_correction_bias': e_score_correction_bias, 'experts_gate_up': experts_gate_up, 'experts_down': experts_down, 'shared_gate_w': shared_gate_w, 'shared_up_w': shared_up_w, 'shared_down_w': shared_down_w}
    _L0_ffn_all = _L0_ffn_setup()
    _L0_ffn_in = {k: v for k, v in _L0_ffn_all.items() if k in ('gate_weight', 'e_score_correction_bias', 'experts_gate_up', 'experts_down', 'shared_gate_w', 'shared_up_w', 'shared_down_w')}
    del _L0_ffn_all

    def _L1_xattn_setup():
        import jax, jax.numpy as jnp
        import numpy as np
        NUM_HEADS = 16
        CLAMP = 10000.0
        key = jax.random.key(seed)
        ks = jax.random.split(key, 8)
        B, Nq, Nkv, Cq, Ckv = (4, 256, 256, 128, 96)
        s_q = 1.0 / np.sqrt(Cq)
        s_kv = 1.0 / np.sqrt(Ckv)
        return {'query': jax.random.normal(ks[0], (B, Nq, Cq), jnp.float32), 'key_value': jax.random.normal(ks[1], (B, Nkv, Ckv), jnp.float32), 'Wq': jax.random.normal(ks[2], (Cq, Cq), jnp.float32) * s_q, 'bq': jnp.zeros((Cq,), jnp.float32), 'Wk': jax.random.normal(ks[3], (Ckv, Cq), jnp.float32) * s_kv, 'bk': jnp.zeros((Cq,), jnp.float32), 'Wv': jax.random.normal(ks[4], (Ckv, Cq), jnp.float32) * s_kv, 'bv': jnp.zeros((Cq,), jnp.float32), 'Wo': jax.random.normal(ks[5], (Cq, Cq), jnp.float32) * s_q, 'bo': jnp.zeros((Cq,), jnp.float32)}
    _L1_xattn_all = _L1_xattn_setup()
    _L1_xattn_in = {k: v for k, v in _L1_xattn_all.items() if k in ('Wq', 'bq', 'Wk', 'bk', 'Wv', 'bv', 'Wo', 'bo')}
    del _L1_xattn_all

    def _L1_ffn_setup():
        import jax, jax.numpy as jnp
        import numpy as np
        D, H, E, K, S = (128, 256, 8, 2, 1)
        B, L = (4, 256)
        key = jax.random.key(seed)
        ks = jax.random.split(key, 9)
        std = 0.02
        return {'x': jax.random.normal(ks[0], (B, L, D), dtype=jnp.float32), 'router_w': jax.random.normal(ks[1], (E, D), dtype=jnp.float32) * std, 'experts_bias': jnp.zeros((E,), dtype=jnp.float32), 'w1': jax.random.normal(ks[2], (E, D, H), dtype=jnp.float32) * std, 'w3': jax.random.normal(ks[3], (E, D, H), dtype=jnp.float32) * std, 'w2': jax.random.normal(ks[4], (E, H, D), dtype=jnp.float32) * std, 'sw1': jax.random.normal(ks[5], (S, D, H), dtype=jnp.float32) * std, 'sw3': jax.random.normal(ks[6], (S, D, H), dtype=jnp.float32) * std, 'sw2': jax.random.normal(ks[7], (S, H, D), dtype=jnp.float32) * std}
    _L1_ffn_all = _L1_ffn_setup()
    _L1_ffn_in = {k: v for k, v in _L1_ffn_all.items() if k in ('router_w', 'experts_bias', 'w1', 'w3', 'w2', 'sw1', 'sw3', 'sw2')}
    del _L1_ffn_all

    def _L2_xattn_setup():
        import jax, jax.numpy as jnp
        import numpy as np
        H = 8
        D = 64
        SCALE = D ** (-0.5)
        key = jax.random.key(seed)
        ks = jax.random.split(key, 7)
        B, Nq, Nkv = (2, 256, 256)
        Cq, Ck, I = (128, 96, H * D)
        return {'x': jax.random.normal(ks[0], (B, Nq, Cq), jnp.float32), 'context': jax.random.normal(ks[1], (B, Nkv, Ck), jnp.float32), 'Wq': jax.random.normal(ks[2], (Cq, I), jnp.float32) * Cq ** (-0.5), 'Wk': jax.random.normal(ks[3], (Ck, I), jnp.float32) * Ck ** (-0.5), 'Wv': jax.random.normal(ks[4], (Ck, I), jnp.float32) * Ck ** (-0.5), 'Wo': jax.random.normal(ks[5], (I, Cq), jnp.float32) * I ** (-0.5), 'bo': jnp.zeros((Cq,), jnp.float32)}
    _L2_xattn_all = _L2_xattn_setup()
    _L2_xattn_in = {k: v for k, v in _L2_xattn_all.items() if k in ('Wq', 'Wk', 'Wv', 'Wo', 'bo')}
    del _L2_xattn_all

    def _L2_ffn_setup():
        import jax, jax.numpy as jnp
        import numpy as np
        DIM = 128
        HIDDEN = 128
        NUM_EXPERTS = 8
        TOP_K = 2
        key = jax.random.key(seed)
        ks = jax.random.split(key, 8)
        std = 0.02
        x = jax.random.normal(ks[0], (2, 128, DIM), dtype=jnp.float32)
        gate_w = jax.random.normal(ks[1], (NUM_EXPERTS, DIM), dtype=jnp.float32) * std
        w1 = jax.random.normal(ks[2], (NUM_EXPERTS, DIM, HIDDEN), dtype=jnp.float32) * std
        w2 = jax.random.normal(ks[3], (NUM_EXPERTS, HIDDEN, DIM), dtype=jnp.float32) * std
        w3 = jax.random.normal(ks[4], (NUM_EXPERTS, DIM, HIDDEN), dtype=jnp.float32) * std
        w1s = jax.random.normal(ks[5], (1, DIM, HIDDEN), dtype=jnp.float32) * std
        w2s = jax.random.normal(ks[6], (1, HIDDEN, DIM), dtype=jnp.float32) * std
        w3s = jax.random.normal(ks[7], (1, DIM, HIDDEN), dtype=jnp.float32) * std
        return {'x': x, 'gate_w': gate_w, 'w1': w1, 'w2': w2, 'w3': w3, 'w1s': w1s, 'w2s': w2s, 'w3s': w3s}
    _L2_ffn_all = _L2_ffn_setup()
    _L2_ffn_in = {k: v for k, v in _L2_ffn_all.items() if k in ('gate_w', 'w1', 'w2', 'w3', 'w1s', 'w2s', 'w3s')}
    del _L2_ffn_all

    def _L3_xattn_setup():
        import jax, jax.numpy as jnp
        import numpy as np
        DIM_IN, DIM_LAT, DIM_HEAD = (96, 128, 64)
        INNER = max(DIM_LAT, DIM_IN)
        HEADS = INNER // DIM_HEAD
        SCALE = DIM_HEAD ** (-0.5)
        RMS_EPS = 1e-08
        LN_EPS = 1e-05

        def layernorm(x, g, b):
            mu = jnp.mean(x, axis=-1, keepdims=True)
            var = jnp.mean((x - mu) ** 2, axis=-1, keepdims=True)
            return (x - mu) * jax.lax.rsqrt(var + LN_EPS) * g + b

        def rmsnorm(x, gamma):
            norm = jnp.sqrt(jnp.sum(x * x, axis=-1, keepdims=True)) * x.shape[-1] ** (-0.5)
            return x / jnp.maximum(norm, RMS_EPS) * gamma
        key = jax.random.key(seed)
        ks = jax.random.split(key, 12)
        b, n, m = (4, 512, 64)
        x = jax.random.normal(ks[0], (b, n, DIM_IN), jnp.float32)
        latents = jax.random.normal(ks[1], (b, m, DIM_LAT), jnp.float32)
        mask = jax.random.randint(ks[2], (b, n), 0, 2).astype(bool)
        s = lambda k, sh, fan: jax.random.normal(k, sh, jnp.float32) * fan ** (-0.5)
        return {'x': x, 'latents': latents, 'mask': mask, 'ln_x_g': jnp.ones((DIM_IN,), jnp.float32), 'ln_x_b': jnp.zeros((DIM_IN,), jnp.float32), 'ln_l_g': jnp.ones((DIM_LAT,), jnp.float32), 'ln_l_b': jnp.zeros((DIM_LAT,), jnp.float32), 'qn_g': jnp.ones((DIM_HEAD,), jnp.float32), 'kn_g': jnp.ones((DIM_HEAD,), jnp.float32), 'Wq': s(ks[3], (INNER, DIM_LAT), DIM_LAT), 'Wkv': s(ks[4], (2 * INNER, DIM_IN), DIM_IN), 'Wlkv': s(ks[5], (2 * INNER, DIM_LAT), DIM_LAT), 'Wo': s(ks[6], (DIM_LAT, INNER), INNER), 'bo': jnp.zeros((DIM_LAT,), jnp.float32)}
    _L3_xattn_all = _L3_xattn_setup()
    _L3_xattn_in = {k: v for k, v in _L3_xattn_all.items() if k in ('ln_x_g', 'ln_x_b', 'ln_l_g', 'ln_l_b', 'qn_g', 'kn_g', 'Wq', 'Wkv', 'Wlkv', 'Wo', 'bo')}
    del _L3_xattn_all

    def _L3_ffn_setup():
        import jax, jax.numpy as jnp
        import numpy as np
        EPS_LN = 1e-05
        EPS_GATE = 1e-08

        def layer_norm(x, gamma, beta):
            mu = jnp.mean(x, axis=-1, keepdims=True)
            var = jnp.mean(jnp.square(x - mu), axis=-1, keepdims=True)
            return (x - mu) * jax.lax.rsqrt(var + EPS_LN) * gamma + beta
        key = jax.random.key(seed)
        ks = jax.random.split(key, 8)
        B, S, D, E, H = (4, 512, 128, 4, 256)
        s_in = 1.0 / np.sqrt(D)
        s_h = 1.0 / np.sqrt(H)
        return {'h': jax.random.normal(ks[0], (B, S, D), dtype=jnp.float32), 'router_w': jax.random.uniform(ks[1], (E, D), jnp.float32, -s_in, s_in), 'rn_g': jnp.ones((D,), jnp.float32), 'rn_b': jnp.zeros((D,), jnp.float32), 'w1': jax.random.uniform(ks[2], (E, D, H), jnp.float32, -s_in, s_in), 'ln_g': jnp.ones((E, H), jnp.float32), 'ln_b': jnp.zeros((E, H), jnp.float32), 'w2': jax.random.uniform(ks[3], (E, H, D), jnp.float32, -s_h, s_h), 'on_g': jnp.ones((D,), jnp.float32), 'on_b': jnp.zeros((D,), jnp.float32)}
    _L3_ffn_all = _L3_ffn_setup()
    _L3_ffn_in = {k: v for k, v in _L3_ffn_all.items() if k in ('router_w', 'rn_g', 'rn_b', 'w1', 'ln_g', 'ln_b', 'w2', 'on_g', 'on_b')}
    del _L3_ffn_all
    return {'x': x, 'ctx_768': ctx_768, 'mask_BxS2_bk0': mask_BxS2_bk0, 'g_xattn': g_xattn, 'g_ffn': g_ffn, 'L0_xattn_q_w': _L0_xattn_in['q_w'], 'L0_xattn_q_b': _L0_xattn_in['q_b'], 'L0_xattn_k_w': _L0_xattn_in['k_w'], 'L0_xattn_k_b': _L0_xattn_in['k_b'], 'L0_xattn_v_w': _L0_xattn_in['v_w'], 'L0_xattn_v_b': _L0_xattn_in['v_b'], 'L0_xattn_ln_g': _L0_xattn_in['ln_g'], 'L0_xattn_ln_b': _L0_xattn_in['ln_b'], 'L0_xattn_tln_g': _L0_xattn_in['tln_g'], 'L0_xattn_tln_b': _L0_xattn_in['tln_b'], 'L0_ffn_gate_weight': _L0_ffn_in['gate_weight'], 'L0_ffn_e_score_correction_bias': _L0_ffn_in['e_score_correction_bias'], 'L0_ffn_experts_gate_up': _L0_ffn_in['experts_gate_up'], 'L0_ffn_experts_down': _L0_ffn_in['experts_down'], 'L0_ffn_shared_gate_w': _L0_ffn_in['shared_gate_w'], 'L0_ffn_shared_up_w': _L0_ffn_in['shared_up_w'], 'L0_ffn_shared_down_w': _L0_ffn_in['shared_down_w'], 'L1_xattn_Wq': _L1_xattn_in['Wq'], 'L1_xattn_bq': _L1_xattn_in['bq'], 'L1_xattn_Wk': _L1_xattn_in['Wk'], 'L1_xattn_bk': _L1_xattn_in['bk'], 'L1_xattn_Wv': _L1_xattn_in['Wv'], 'L1_xattn_bv': _L1_xattn_in['bv'], 'L1_xattn_Wo': _L1_xattn_in['Wo'], 'L1_xattn_bo': _L1_xattn_in['bo'], 'L1_ffn_router_w': _L1_ffn_in['router_w'], 'L1_ffn_experts_bias': _L1_ffn_in['experts_bias'], 'L1_ffn_w1': _L1_ffn_in['w1'], 'L1_ffn_w3': _L1_ffn_in['w3'], 'L1_ffn_w2': _L1_ffn_in['w2'], 'L1_ffn_sw1': _L1_ffn_in['sw1'], 'L1_ffn_sw3': _L1_ffn_in['sw3'], 'L1_ffn_sw2': _L1_ffn_in['sw2'], 'L2_xattn_Wq': _L2_xattn_in['Wq'], 'L2_xattn_Wk': _L2_xattn_in['Wk'], 'L2_xattn_Wv': _L2_xattn_in['Wv'], 'L2_xattn_Wo': _L2_xattn_in['Wo'], 'L2_xattn_bo': _L2_xattn_in['bo'], 'L2_ffn_gate_w': _L2_ffn_in['gate_w'], 'L2_ffn_w1': _L2_ffn_in['w1'], 'L2_ffn_w2': _L2_ffn_in['w2'], 'L2_ffn_w3': _L2_ffn_in['w3'], 'L2_ffn_w1s': _L2_ffn_in['w1s'], 'L2_ffn_w2s': _L2_ffn_in['w2s'], 'L2_ffn_w3s': _L2_ffn_in['w3s'], 'L3_xattn_ln_x_g': _L3_xattn_in['ln_x_g'], 'L3_xattn_ln_x_b': _L3_xattn_in['ln_x_b'], 'L3_xattn_ln_l_g': _L3_xattn_in['ln_l_g'], 'L3_xattn_ln_l_b': _L3_xattn_in['ln_l_b'], 'L3_xattn_qn_g': _L3_xattn_in['qn_g'], 'L3_xattn_kn_g': _L3_xattn_in['kn_g'], 'L3_xattn_Wq': _L3_xattn_in['Wq'], 'L3_xattn_Wkv': _L3_xattn_in['Wkv'], 'L3_xattn_Wlkv': _L3_xattn_in['Wlkv'], 'L3_xattn_Wo': _L3_xattn_in['Wo'], 'L3_xattn_bo': _L3_xattn_in['bo'], 'L3_ffn_router_w': _L3_ffn_in['router_w'], 'L3_ffn_rn_g': _L3_ffn_in['rn_g'], 'L3_ffn_rn_b': _L3_ffn_in['rn_b'], 'L3_ffn_w1': _L3_ffn_in['w1'], 'L3_ffn_ln_g': _L3_ffn_in['ln_g'], 'L3_ffn_ln_b': _L3_ffn_in['ln_b'], 'L3_ffn_w2': _L3_ffn_in['w2'], 'L3_ffn_on_g': _L3_ffn_in['on_g'], 'L3_ffn_on_b': _L3_ffn_in['on_b']}

def reference(x, ctx_768, mask_BxS2_bk0, g_xattn, g_ffn, L0_xattn_q_w, L0_xattn_q_b, L0_xattn_k_w, L0_xattn_k_b, L0_xattn_v_w, L0_xattn_v_b, L0_xattn_ln_g, L0_xattn_ln_b, L0_xattn_tln_g, L0_xattn_tln_b, L0_ffn_gate_weight, L0_ffn_e_score_correction_bias, L0_ffn_experts_gate_up, L0_ffn_experts_down, L0_ffn_shared_gate_w, L0_ffn_shared_up_w, L0_ffn_shared_down_w, L1_xattn_Wq, L1_xattn_bq, L1_xattn_Wk, L1_xattn_bk, L1_xattn_Wv, L1_xattn_bv, L1_xattn_Wo, L1_xattn_bo, L1_ffn_router_w, L1_ffn_experts_bias, L1_ffn_w1, L1_ffn_w3, L1_ffn_w2, L1_ffn_sw1, L1_ffn_sw3, L1_ffn_sw2, L2_xattn_Wq, L2_xattn_Wk, L2_xattn_Wv, L2_xattn_Wo, L2_xattn_bo, L2_ffn_gate_w, L2_ffn_w1, L2_ffn_w2, L2_ffn_w3, L2_ffn_w1s, L2_ffn_w2s, L2_ffn_w3s, L3_xattn_ln_x_g, L3_xattn_ln_x_b, L3_xattn_ln_l_g, L3_xattn_ln_l_b, L3_xattn_qn_g, L3_xattn_kn_g, L3_xattn_Wq, L3_xattn_Wkv, L3_xattn_Wlkv, L3_xattn_Wo, L3_xattn_bo, L3_ffn_router_w, L3_ffn_rn_g, L3_ffn_rn_b, L3_ffn_w1, L3_ffn_ln_g, L3_ffn_ln_b, L3_ffn_w2, L3_ffn_on_g, L3_ffn_on_b):
    import jax
    import jax.numpy as jnp

    def _L0_xattn_ref(x, xf, q_w, q_b, k_w, k_b, v_w, v_b, ln_g, ln_b, tln_g, tln_b):
        import jax, jax.numpy as jnp
        import numpy as np
        NUM_HEAD = 16
        LN_EPS = 1e-05

        def _layernorm(x, g, b):
            m = jnp.mean(x, axis=-1, keepdims=True)
            v = jnp.var(x, axis=-1, keepdims=True)
            return (x - m) * jax.lax.rsqrt(v + LN_EPS) * g + b
        B, T, D = x.shape
        N = xf.shape[1]
        H = NUM_HEAD
        dh = D // H
        xn = _layernorm(x, ln_g, ln_b)
        xfn = _layernorm(xf, tln_g, tln_b)
        q = (xn @ q_w + q_b).reshape(B, T, H, dh)
        k = (xfn @ k_w + k_b).reshape(B, N, H, dh)
        v = (xfn @ v_w + v_b).reshape(B, N, H, dh)
        att = jnp.einsum('bthd,bnhd->btnh', q, k) / np.float32(np.sqrt(dh))
        w = jax.nn.softmax(att, axis=2)
        y = jnp.einsum('btnh,bnhd->bthd', w, v).reshape(B, T, D)
        return y

    def _L0_ffn_ref(x, gate_weight, e_score_correction_bias, experts_gate_up, experts_down, shared_gate_w, shared_up_w, shared_down_w):
        import jax, jax.numpy as jnp
        import numpy as np
        H = 128
        I = 64
        E = 32
        TOP_K = 6
        N_GROUP = 8
        TOPK_GROUP = 4
        SCALE = 2.5
        N_SHARED = 2
        SI = I * N_SHARED
        B, S = (2, 128)
        b, s, h = x.shape
        xf = x.reshape(-1, h)
        T = xf.shape[0]
        logits = xf.astype(jnp.float32) @ gate_weight.astype(jnp.float32).T
        scores = jax.nn.sigmoid(logits)
        sfc = scores + e_score_correction_bias[None, :]
        gs = E // N_GROUP
        group_scores = sfc.reshape(T, N_GROUP, gs).max(axis=-1)
        _, gidx = jax.lax.top_k(group_scores, TOPK_GROUP)
        gmask = jnp.zeros((T, N_GROUP), bool).at[jnp.arange(T)[:, None], gidx].set(True)
        smask = jnp.repeat(gmask, gs, axis=1)
        masked = jnp.where(smask, sfc, 0.0)
        _, topk_idx = jax.lax.top_k(masked, TOP_K)
        tw = jnp.take_along_axis(scores, topk_idx, axis=1)
        tw = tw / (tw.sum(-1, keepdims=True) + 1e-20)
        tw = (tw * SCALE).astype(xf.dtype)
        combine = jnp.zeros((T, E), xf.dtype).at[jnp.arange(T)[:, None], topk_idx].add(tw)

        def expert_step(acc, inp):
            gu, dn, c = inp
            g = xf @ gu[:I].T
            u = xf @ gu[I:].T
            o = jax.nn.silu(g) * u @ dn.T
            return (acc + c[:, None] * o, None)
        routed, _ = jax.lax.scan(expert_step, jnp.zeros_like(xf), (experts_gate_up, experts_down, combine.T))
        sh = jax.nn.silu(xf @ shared_gate_w.T) * (xf @ shared_up_w.T)
        shared_out = sh @ shared_down_w.T
        return (routed + shared_out).reshape(b, s, h)

    def _L1_xattn_ref(query, key_value, Wq, bq, Wk, bk, Wv, bv, Wo, bo):
        import jax, jax.numpy as jnp
        import numpy as np
        NUM_HEADS = 16
        CLAMP = 10000.0
        B, Nq, Cq = query.shape
        Nkv = key_value.shape[1]
        H = NUM_HEADS
        D = Cq // H
        scale = D ** (-0.5)
        q = (query @ Wq + bq).reshape(B, Nq, H, D).transpose(0, 2, 1, 3)
        k = (key_value @ Wk + bk).reshape(B, Nkv, H, D).transpose(0, 2, 1, 3)
        v = (key_value @ Wv + bv).reshape(B, Nkv, H, D).transpose(0, 2, 1, 3)
        attn = jnp.einsum('bhqd,bhkd->bhqk', q, k) * scale
        attn = jnp.clip(attn, -CLAMP, CLAMP)
        attn = jax.nn.softmax(attn, axis=-1)
        attn = jnp.where(jnp.any(jnp.isnan(attn)), jnp.asarray(1.0 / Nkv, attn.dtype), attn)
        x = jnp.einsum('bhqk,bhkd->bqhd', attn, v).reshape(B, Nq, Cq)
        return x @ Wo + bo

    def _L1_ffn_ref(x, router_w, experts_bias, w1, w3, w2, sw1, sw3, sw2):
        import jax, jax.numpy as jnp
        import numpy as np
        D, H, E, K, S = (128, 256, 8, 2, 1)
        B, L = (4, 256)
        b, l, d = x.shape
        xf = x.reshape(-1, d)
        sg = jnp.einsum('td,sdh->tsh', xf, sw1)
        su = jnp.einsum('td,sdh->tsh', xf, sw3)
        shared_out = jnp.einsum('tsh,shd->td', jax.nn.silu(sg) * su, sw2)
        logits = xf @ router_w.T + experts_bias
        rw, sel = jax.lax.top_k(logits, K)
        rw = jax.nn.softmax(rw.astype(jnp.float32), axis=-1).astype(x.dtype)
        cw = (jax.nn.one_hot(sel, E, dtype=x.dtype) * rw[..., None]).sum(axis=1)
        g = jnp.einsum('td,edh->teh', xf, w1)
        u = jnp.einsum('td,edh->teh', xf, w3)
        eo = jax.nn.silu(g) * u
        moe_out = jnp.einsum('te,teh,ehd->td', cw, eo, w2)
        return (moe_out + shared_out).reshape(b, l, d)

    def _L2_xattn_ref(x, context, Wq, Wk, Wv, Wo, bo):
        import jax, jax.numpy as jnp
        import numpy as np
        H = 8
        D = 64
        SCALE = D ** (-0.5)
        B, Nq, _ = x.shape
        Nkv = context.shape[1]
        q = (x @ Wq).reshape(B, Nq, H, D)
        k = (context @ Wk).reshape(B, Nkv, H, D)
        v = (context @ Wv).reshape(B, Nkv, H, D)
        sim = jnp.einsum('bihd,bjhd->bhij', q, k) * SCALE
        attn = jax.nn.softmax(sim, axis=-1)
        out = jnp.einsum('bhij,bjhd->bihd', attn, v).reshape(B, Nq, H * D)
        return out @ Wo + bo

    def _L2_ffn_ref(x, gate_w, w1, w2, w3, w1s, w2s, w3s):
        import jax, jax.numpy as jnp
        import numpy as np
        DIM = 128
        HIDDEN = 128
        NUM_EXPERTS = 8
        TOP_K = 2
        bs, slen, dim = x.shape
        xt = x.reshape(bs * slen, dim)
        logits = xt @ gate_w.T
        scores = jax.nn.softmax(logits.astype(jnp.float32), axis=1).astype(x.dtype)
        top_scores, sel = jax.lax.top_k(scores, TOP_K)
        sel_flat = sel.reshape(-1)
        order = jnp.argsort(sel_flat, stable=True)
        top_scores_sorted = top_scores.reshape(-1)[order]
        token_idx = order // TOP_K
        eid = sel_flat[order]
        routed_in = xt[token_idx] * top_scores_sorted[:, None]
        out_routed = jnp.zeros_like(routed_in)
        for e in range(NUM_EXPERTS):
            m = (eid == e)[:, None]
            xe = jnp.where(m, routed_in, 0.0)
            h = jax.nn.silu(xe @ w1[e]) * (xe @ w3[e])
            out_routed = out_routed + jnp.where(m, h @ w2[e], 0.0)
        hs = jax.nn.silu(xt @ w1s[0]) * (xt @ w3s[0])
        out = hs @ w2s[0]
        out = out.at[token_idx].add(out_routed)
        return out.reshape(bs, slen, dim)

    def _L3_xattn_ref(x, latents, mask, ln_x_g, ln_x_b, ln_l_g, ln_l_b, qn_g, kn_g, Wq, Wkv, Wlkv, Wo, bo):
        import jax, jax.numpy as jnp
        import numpy as np
        DIM_IN, DIM_LAT, DIM_HEAD = (96, 128, 64)
        INNER = max(DIM_LAT, DIM_IN)
        HEADS = INNER // DIM_HEAD
        SCALE = DIM_HEAD ** (-0.5)
        RMS_EPS = 1e-08
        LN_EPS = 1e-05

        def layernorm(x, g, b):
            mu = jnp.mean(x, axis=-1, keepdims=True)
            var = jnp.mean((x - mu) ** 2, axis=-1, keepdims=True)
            return (x - mu) * jax.lax.rsqrt(var + LN_EPS) * g + b

        def rmsnorm(x, gamma):
            norm = jnp.sqrt(jnp.sum(x * x, axis=-1, keepdims=True)) * x.shape[-1] ** (-0.5)
            return x / jnp.maximum(norm, RMS_EPS) * gamma
        b, n, _ = x.shape
        m = latents.shape[1]
        xn = layernorm(x, ln_x_g, ln_x_b)
        ln = layernorm(latents, ln_l_g, ln_l_b)
        q = ln @ Wq.T
        kv = jnp.concatenate([xn @ Wkv.T, ln @ Wlkv.T], axis=1)
        k, v = (kv[..., :INNER], kv[..., INNER:])
        split_heads = lambda t: t.reshape(t.shape[0], t.shape[1], HEADS, DIM_HEAD).transpose(0, 2, 1, 3)
        q, k, v = (split_heads(q), split_heads(k), split_heads(v))
        qn = rmsnorm(q, qn_g) * SCALE
        kn = rmsnorm(k, kn_g)
        attn = jnp.einsum('bhid,bhjd->bhij', qn, kn)
        full_mask = jnp.pad(mask, ((0, 0), (0, m)), constant_values=True)
        attn = jnp.where(full_mask[:, None, None, :], attn, -jnp.finfo(attn.dtype).max)
        attn = jax.nn.softmax(attn, axis=-1)
        out = jnp.einsum('bhij,bhjd->bhid', attn, v)
        out = out.transpose(0, 2, 1, 3).reshape(b, m, INNER)
        return out @ Wo.T + bo

    def _L3_ffn_ref(h, router_w, rn_g, rn_b, w1, ln_g, ln_b, w2, on_g, on_b):
        import jax, jax.numpy as jnp
        import numpy as np
        EPS_LN = 1e-05
        EPS_GATE = 1e-08

        def layer_norm(x, gamma, beta):
            mu = jnp.mean(x, axis=-1, keepdims=True)
            var = jnp.mean(jnp.square(x - mu), axis=-1, keepdims=True)
            return (x - mu) * jax.lax.rsqrt(var + EPS_LN) * gamma + beta
        D = h.shape[-1]
        h_norm = layer_norm(h, rn_g, rn_b)
        g = jax.nn.softmax(jnp.einsum('bsd,ed->bse', h_norm, router_w), axis=-1)
        top2_w, top2_idx = jax.lax.top_k(g, 2)
        top2_w = top2_w / (jnp.sum(top2_w, axis=-1, keepdims=True) + EPS_GATE)
        hid = jnp.einsum('bsd,edh->bseh', h, w1)
        hid = jax.nn.relu(layer_norm(hid, ln_g, ln_b))
        expert_out = jnp.einsum('bseh,ehd->bsed', hid, w2)
        idx = jnp.broadcast_to(top2_idx[..., None], top2_idx.shape + (D,))
        top2_out = jnp.take_along_axis(expert_out, idx, axis=-2)
        out = jnp.sum(top2_out * top2_w[..., None], axis=-2)
        return layer_norm(out, on_g, on_b)
    x = x + jnp.tanh(g_xattn[0]) * _L0_xattn_ref(_layernorm(x, axis=-1), ctx_768, L0_xattn_q_w, L0_xattn_q_b, L0_xattn_k_w, L0_xattn_k_b, L0_xattn_v_w, L0_xattn_v_b, L0_xattn_ln_g, L0_xattn_ln_b, L0_xattn_tln_g, L0_xattn_tln_b)
    x = x + jnp.tanh(g_ffn[0]) * _L0_ffn_ref(_layernorm(x, axis=-1), L0_ffn_gate_weight, L0_ffn_e_score_correction_bias, L0_ffn_experts_gate_up, L0_ffn_experts_down, L0_ffn_shared_gate_w, L0_ffn_shared_up_w, L0_ffn_shared_down_w)
    x = x + jnp.tanh(g_xattn[1]) * _L1_xattn_ref(_layernorm(x, axis=-1), ctx_768, L1_xattn_Wq, L1_xattn_bq, L1_xattn_Wk, L1_xattn_bk, L1_xattn_Wv, L1_xattn_bv, L1_xattn_Wo, L1_xattn_bo)
    x = x + jnp.tanh(g_ffn[1]) * _L1_ffn_ref(_layernorm(x, axis=-1), L1_ffn_router_w, L1_ffn_experts_bias, L1_ffn_w1, L1_ffn_w3, L1_ffn_w2, L1_ffn_sw1, L1_ffn_sw3, L1_ffn_sw2)
    x = x + jnp.tanh(g_xattn[2]) * _L2_xattn_ref(_layernorm(x, axis=-1), ctx_768, L2_xattn_Wq, L2_xattn_Wk, L2_xattn_Wv, L2_xattn_Wo, L2_xattn_bo)
    x = x + jnp.tanh(g_ffn[2]) * _L2_ffn_ref(_layernorm(x, axis=-1), L2_ffn_gate_w, L2_ffn_w1, L2_ffn_w2, L2_ffn_w3, L2_ffn_w1s, L2_ffn_w2s, L2_ffn_w3s)
    x = x + jnp.tanh(g_xattn[3]) * _L3_xattn_ref(ctx_768, _layernorm(x, axis=-1), mask_BxS2_bk0, L3_xattn_ln_x_g, L3_xattn_ln_x_b, L3_xattn_ln_l_g, L3_xattn_ln_l_b, L3_xattn_qn_g, L3_xattn_kn_g, L3_xattn_Wq, L3_xattn_Wkv, L3_xattn_Wlkv, L3_xattn_Wo, L3_xattn_bo)
    x = x + jnp.tanh(g_ffn[3]) * _L3_ffn_ref(_layernorm(x, axis=-1), L3_ffn_router_w, L3_ffn_rn_g, L3_ffn_rn_b, L3_ffn_w1, L3_ffn_ln_g, L3_ffn_ln_b, L3_ffn_w2, L3_ffn_on_g, L3_ffn_on_b)
    return x

_drawn_inputs = setup_inputs


def setup_inputs(seed=0):
    import zlib

    import numpy as np

    out = dict(_drawn_inputs(seed))
    spreads = {'L0_xattn_q_b': (0.0, 0.8),
     'L0_xattn_k_b': (0.0, 2.0),
     'L0_xattn_v_b': (0.0, 0.1),
     'L0_xattn_ln_g': (1.0, 0.6),
     'L0_xattn_ln_b': (0.0, 0.8),
     'L0_xattn_tln_g': (1.0, 0.2),
     'L0_xattn_tln_b': (0.0, 0.1),
     'L1_xattn_bq': (0.0, 0.1),
     'L1_xattn_bk': (0.0, 2.0),
     'L1_xattn_bv': (0.0, 0.1),
     'L1_xattn_bo': (0.0, 0.1),
     'L1_ffn_experts_bias': (0.0, 0.432),
     'L2_xattn_bo': (0.0, 0.1),
     'L3_xattn_ln_x_g': (1.0, 0.2),
     'L3_xattn_ln_x_b': (0.0, 0.275),
     'L3_xattn_ln_l_g': (1.0, 0.2),
     'L3_xattn_ln_l_b': (0.0, 0.1),
     'L3_xattn_qn_g': (1.0, 0.2),
     'L3_xattn_kn_g': (1.0, 0.2),
     'L3_xattn_bo': (0.0, 0.1),
     'L3_ffn_rn_g': (1.0, 0.2),
     'L3_ffn_rn_b': (0.0, 0.1),
     'L3_ffn_ln_g': (1.0, 0.2),
     'L3_ffn_ln_b': (0.0, 0.1),
     'L3_ffn_on_g': (1.0, 0.2),
     'L3_ffn_on_b': (0.0, 0.1)}
    factors = {'L0_xattn_q_w': 3.615,
     'L0_xattn_k_w': 3.368,
     'L0_ffn_gate_weight': 4.557,
     'L0_ffn_e_score_correction_bias': 5.401,
     'L0_ffn_experts_gate_up': 3.779,
     'L0_ffn_experts_down': 3.8,
     'L0_ffn_shared_gate_w': 3.91,
     'L0_ffn_shared_up_w': 2.717,
     'L0_ffn_shared_down_w': 2.988,
     'L1_ffn_router_w': 2.987,
     'L1_ffn_w1': 3.214,
     'L1_ffn_w2': 2.688,
     'L2_ffn_gate_w': 8.0,
     'L2_ffn_w1': 8.0,
     'L2_ffn_w2': 8.0,
     'L2_ffn_w3': 8.0,
     'L2_ffn_w1s': 3.125,
     'L2_ffn_w2s': 3.112,
     'L2_ffn_w3s': 3.185}
    for name, (base, spread) in spreads.items():
        noise = np.random.default_rng([zlib.crc32(name.encode()), seed]).standard_normal(out[name].shape)
        drawn = base * np.exp(spread * noise) if base else spread * noise
        out[name] = jnp.asarray(drawn.astype(out[name].dtype))
    for name, factor in factors.items():
        out[name] = (out[name] * factor).astype(out[name].dtype)
    return out
```

```python
import concourse.bass as bass
from concourse import mybir
from contextlib import ExitStack

F32 = mybir.dt.float32
F32R = mybir.dt.float32r
U8 = mybir.dt.uint8
I32 = mybir.dt.int32
ALU = mybir.AluOpType
ACT = mybir.ActivationFunctionType
AX = mybir.AxisListType

P = 128
SEQS, SEQ, D, DC = 64, 64, 128, 96
TILES = SEQS * SEQ // P
UNIT = 4
UNITS = TILES // UNIT
COLS = UNIT * P
EPS = 1e-5
A0, F0, A1, F1, A2, F2, A3, F3 = range(8)
ATTENTION = (A0, A1, A2, A3)
HEADS, DH = 16, 8
GROUP = HEADS // 2
CLAMP = 10000.0
HEADS2, DH2 = 8, 64
PAIRS2 = HEADS2 // 2
HEADS3 = 2
KEYS3 = 2 * SEQ
MASKED = 1e30
EXPERTS = {F0: 32, F1: 8, F2: 8, F3: 4}
TOP = {F0: 6, F1: 2, F2: 2, F3: 2}
SHARED = {F0: 1, F1: 2, F2: 1}
CHUNKS = {F0: 17, F1: 18, F2: 9}
HID3 = 256
FRONT2, FRONT3 = 14, 11
PAD = 16


class Signal:

    def __init__(self, sem, counts, phases):
        self.sem, self.counts, self.start = sem, counts, {}
        total = 0
        for p in phases:
            self.start[p] = total
            total += UNITS * counts.get(p, 0)

    def value(self, p, s, n):
        return self.start[p] + s * self.counts[p] + n

    def due(self, p, s, n):
        value = self.value(p, s, n)
        return not isinstance(value, int) or value > self.start[p]


class Steps:

    def __init__(self, signal, p, s, n=0):
        self.sem, self.counted, self.p, self.s, self.n = signal.sem, signal, p, s, n

    def one(self):
        self.n += 1
        return 1

    def value(self):
        return self.counted.value(self.p, self.s, self.n)

    def ended(self):
        assert self.n == self.counted.counts[self.p], (self.p, self.n)


def over_units(eng, body):
    body(0, 0, False)
    with eng.Fori(0, (UNITS - 2) // 2) as i:
        body(i * 2 + 1, 1, False)
        body(i * 2 + 2, 0, False)
    body(UNITS - 1, 1, True)


def build(nc, A, out, phases=tuple(range(8))):
    ctx = ExitStack()
    with ctx:
        K = allocate(nc, ctx, A, out, phases)
        block = ctx.enter_context(nc.Block())

        @block.sync
        def _(sp):
            sync_program(nc, sp, K)

        @block.gpsimd
        def _(pool):
            pool_program(nc, pool, K)

        @block.scalar
        def _(act):
            scalar_program(nc, act, K)

        @block.vector
        def _(dve):
            vector_program(nc, dve, K)

        @block.tensor
        def _(pe):
            tensor_program(nc, pe, K)


class Kernel:
    pass


def allocate(nc, ctx, A, out, phases):
    K = Kernel()
    K.A, K.out, K.phases = A, out, phases

    def sb(name, shape, dt=F32):
        return ctx.enter_context(nc.sbuf_tensor(name, shape, dt))

    def signal(name, counts):
        return Signal(ctx.enter_context(nc.semaphore(name)), counts, phases)

    def once(name):
        return ctx.enter_context(nc.semaphore(name))

    every = {p: 1 for p in range(8)}
    attn = {p: 1 for p in ATTENTION}
    four = {p: UNIT for p in ATTENTION}
    K.ln_steps = signal("ln_steps", {p: 11 for p in range(8)})
    K.rstd_ready = signal("rstd_ready", every)
    K.y_ready = signal("y_ready", every)
    own = {p: 1 for p in range(8) if p not in (A2, A3)}
    K.yT_psum = signal("yT_psum", own)
    K.yT_ready = signal("yT_ready", own)
    K.ctx_loaded = signal("ctx_loaded", {p: 16 for p in ATTENTION})
    K.cln_steps = signal("cln_steps", {A0: 11, A3: 11})
    K.crstd_ready = signal("crstd_ready", {A0: 1, A3: 1})
    K.c_ready = signal("c_ready", {A0: 1, A3: 1})
    K.cT_psum = signal("cT_psum", {A0: 1, A1: 1})
    K.cT_ready = signal("cT_ready", {A0: 1, A1: 1})
    K.q_psum = signal("q_psum", {A0: 1, A1: 1})
    K.q_ready = signal("q_ready", {A0: 1, A1: 1})
    K.k_psum = signal("k_psum", {A0: 1, A1: 1})
    K.k_ready = signal("k_ready", {A0: 1, A1: 1})
    K.v_psum = signal("v_psum", {A0: 1, A1: 1})
    K.v_ready = signal("v_ready", {A0: 1, A1: 1, A3: 1})
    K.front_psum = signal("front_psum", {A2: FRONT2, A3: FRONT3})
    K.front_read = signal("front_read", {A2: FRONT2, A3: FRONT3})
    K.kbd_ready = signal("kbd_ready", {A0: UNIT, A1: UNIT})
    K.s_psum = signal("s_psum", four)
    K.max_steps = signal("max_steps", {A0: UNIT, A1: 2 * UNIT, A2: UNIT, A3: 2 * UNIT})
    K.shift_ready = signal("shift_ready", four)
    K.probs_ready = signal("probs_ready", four)
    K.pT_psum = signal("pT_psum", four)
    K.pT_ready = signal("pT_ready", four)
    K.av_psum = signal("av_psum", four)
    K.sum_steps = signal("sum_steps", four)
    K.out_ready = signal("out_ready", four)
    K.oT_psum = signal("oT_psum", {A1: 1, A2: PAIRS2, A3: 1})
    K.oT_ready = signal("oT_ready", {A1: 1, A2: PAIRS2, A3: 1})
    K.proj_psum = signal("proj_psum", {A1: 1, A2: 1, A3: 1})
    K.res_steps = signal("res_steps", {A0: 1, A1: 1, A2: 1, A3: 1, F3: 11})
    K.x_done = signal("x_done", every)
    K.squares = signal("squares", {A3: 1})
    K.rms_steps = signal("rms_steps", {A3: 2})
    K.rms_ready = signal("rms_ready", {A3: 1})
    K.qk_normed = signal("qk_normed", {A3: 1})
    K.maskbias = signal("maskbias", {A3: 1})
    ch = dict(CHUNKS)
    routed = {p: CHUNKS[p] - SHARED[p] for p in CHUNKS}
    K.g_psum = signal("g_psum", ch | {F3: 8})
    K.u_psum = signal("u_psum", ch)
    K.c_psum = signal("c_psum", routed | {F3: 4})
    K.scaled_ready = signal("scaled_ready", {F2: 8})
    K.silu_ready = signal("silu_ready", ch)
    K.prod_steps = signal("prod_steps", {F0: routed[F0], F1: routed[F1]})
    K.hid_ready = signal("hid_ready", ch | {F3: 8})
    K.down_done = signal("down_done", ch | {F3: 8})
    K.dt_ready = signal("dt_ready", {p: 1 for p in EXPERTS})
    K.outT_psum = signal("outT_psum", {p: 1 for p in EXPERTS})
    K.logits_psum = signal("logits_psum", {p: 1 for p in EXPERTS})
    K.logits_ready = signal("logits_ready", {F0: 1})
    K.exp_ready = signal("exp_ready", {F1: 1, F2: 1, F3: 1})
    K.route_steps = signal("route_steps", {F0: 39, F1: 21, F2: 22, F3: 27})
    K.cw_psum = signal("cw_psum", {p: 1 for p in EXPERTS})
    K.cw_steps = signal("cw_steps", {p: 1 for p in EXPERTS})
    K.cwT_ready = signal("cwT_ready", {p: 1 for p in EXPERTS})
    K.sq_ready = signal("sq_ready", {F3: 8})
    K.ss_psum = signal("ss_psum", {F3: 4})
    K.sd_ready = signal("sd_ready", {F3: 4})
    K.rinv_ready = signal("rinv_ready", {F3: 4})
    K.z_ready = signal("z_ready", {F3: 8})
    K.relu_ready = signal("relu_ready", {F3: 8})
    K.ostat_ready = signal("ostat_ready", {F3: 1})
    K.onorm_ready = signal("onorm_ready", {F3: 1})
    K.r2_steps = signal("r2_steps", {F3: 3})
    K.r2_ready = signal("r2_ready", {F3: 1})
    K.scale_steps = signal("scale_steps", {F3: 2})
    K.x_loaded = once("x_loaded")
    K.par_loaded = once("par_loaded")
    K.loaded = {p: once(f"weights_{p}") for p in range(8)}
    K.stored = once("stored")
    K.prep = once("prep")
    K.ident_ready = once("ident_ready")
    K.const_steps = once("const_steps")
    K.gates_ready = once("gates_ready")
    K.par_steps = once("par_steps")
    K.prep_psum = once("prep_psum")
    K.prep_ready = once("prep_ready")
    K.fill = once("fill")
    K.sel_ready = once("sel_ready")
    K.l3w_psum = once("l3w_psum")
    K.l3w_ready = once("l3w_ready")
    K.w3_steps = once("w3_steps")
    K.bias3_psum = once("bias3_psum")
    K.router_psum = once("router_psum")
    K.router_ready = once("router_ready")

    K.X = sb("X", [P, TILES, D])
    K.mask_words = sb("mask_words", [P, TILES, SEQ // 4], I32)
    K.mask = K.mask_words[:, :, :].bitcast(U8)
    K.ident = sb("ident", [P, P])
    K.ones = sb("ones", [P, P])
    K.gates = sb("gates", [P, 8])
    K.cols = sb("cols", [P, 48])
    K.rows = sb("rows", [P, 7 * D + 40])
    K.wp = {
        A0: {n: sb(f"L0_{n}", [r, D]) for n, r in (("q", D), ("k", DC), ("v", DC))},
        A1: {n: sb(f"L1_{n}", [r, D]) for n, r in (("q", D), ("k", DC), ("v", DC), ("o", D))},
        A2: {"q": sb("L2_q", [D, 4 * D]), "k": sb("L2_k", [DC, 4 * D]), "v": sb("L2_v", [DC, 4 * D]),
             "o": sb("L2_o", [D, 4, D])},
        A3: {"raw": sb("L3_raw", [P, 6, D]), "qkv": sb("L3_qkv", [D, 3 * D]), "kv": sb("L3_kv", [DC, 2 * D]),
             "o": sb("L3_o", [D, D])},
    }
    K.wf = {p: sb(f"L{p // 2}_experts", [P, 3, CHUNKS[p], P])[:, :, :, :] for p in (F0, F1)}
    late = K.wf[F0].rearrange("p w j n -> p (w j n)")
    n2 = 3 * CHUNKS[F2] * P
    K.wf[F2] = late[:, 0:n2].rearrange("p (w j n) -> p w j n", w=3, j=CHUNKS[F2])
    K.w1 = late[:, n2:n2 + 4 * HID3].rearrange("p (e h) -> p e h", e=4)
    K.w2 = late[:, n2 + 4 * HID3:n2 + 8 * HID3].rearrange("p (c d) -> p c d", c=8)
    K.router_raw = sb("router_raw", [52, D])
    K.router = sb("router", [P, 52])
    K.sel = sb("sel", [64, 16, P], F32R)
    K.cwT = sb("cwT", [64, 2, COLS], F32R)
    K.yT = [sb(f"yT{b}", [P, COLS]) for b in range(2)]
    K.yt = sb("yt", [P, UNIT, D])
    K.stats = sb("stats", [P, UNIT, 6])
    K.lnw = sb("lnw", [P, 6, UNIT])
    K.cstats = sb("cstats", [P, UNIT, 6])
    K.clnw = sb("clnw", [P, 6, UNIT])
    K.minus_half = sb("minus_half", [P, 32])
    K.route = sb("route", [P, 2048])
    K.touch = sb("touch", [P, 1])
    K.arena_cols = 20224
    K.arena = sb("arena", [P, K.arena_cols])
    K.ps = ctx.enter_context(nc.psum_tensor("ps", [P, 8, 512], F32))
    K.bank = [K.ps[:, i, :] for i in range(8)]

    K.col = {n: K.cols[:, i:i + 1] for i, n in enumerate(
        ["q_b", "k_b", "ln_g", "ln_b", "tln_g", "tln_b", "bq", "bk", "bv",
         "ln_l_g", "ln_l_b", "ln_x_g", "ln_x_b", "rn_g", "rn_b", "qn_g", "kn_g"])}
    K.ln3_g = K.cols[:, 20:28]
    K.ln3_b = K.cols[:, 28:36]
    K.logit_bias3 = K.cols[:, 36:40]
    K.row = {n: K.rows[:, i * D:(i + 1) * D] for i, n in enumerate(["v_b", "bo1", "bo2", "bo3", "on_g", "on_b"])}
    K.ebias0 = K.rows[:, 6 * D:6 * D + 32]
    K.ebias1 = K.rows[:, 6 * D + 32:6 * D + 40]
    K.eps_col = K.cols[:, 40:41]
    K.rcol = {F0: K.router[:, 0:32], F1: K.router[:, 32:40], F2: K.router[:, 40:48], F3: K.router[:, 48:52]}
    K.v = {p: carve(K, p) for p in range(8)}
    return K


class Views:

    def __init__(self, K):
        self.K, self.at = K, 0

    def take(self, *shape, rows=P):
        n = 1
        for x in shape:
            n *= x
        v = self.K.arena[0:rows, self.at:self.at + n]
        self.at += n
        assert self.at <= self.K.arena_cols, self.at
        names = " ".join("abcde"[:len(shape)])
        if len(shape) > 1:
            v = v.rearrange(f"p ({names}) -> p {names}", **{n: x for n, x in zip("abcde", shape)})
        return v


def carve(K, p):
    V = Views(K)
    if p in ATTENTION:
        V.ctx = [V.take(UNIT, DC) for _ in range(2)]
        V.ctxn = V.take(UNIT, DC)
        V.cT = [V.take(COLS, rows=DC) for _ in range(2)]
    if p in (A0, A1):
        zeroed = V.at
        V.qz = [V.take(2, UNIT, P) for _ in range(2)]
        V.vd = [V.take(UNIT, GROUP, 2, 2, DH + 1) for _ in range(2)]
        V.zeroed = (zeroed, V.at)
        V.ksel = [V.take(2, UNIT, SEQ) for _ in range(2)]
        V.kbd = [V.take(2, GROUP, SEQ) for _ in range(2)]
        V.probs = [V.take(HEADS, SEQ) for _ in range(2)]
        V.pT = [V.take(GROUP, P) for _ in range(2)]
        V.out = V.take(UNIT, D)
        V.outT = V.take(COLS)
        V.res = V.take(UNIT, D)
        V.max = V.take(2, HEADS)
        V.rsum = V.take(HEADS)
        V.diag = V.take(GROUP)
    if p == A2:
        V.q = [V.take(PAIRS2, COLS) for _ in range(2)]
        V.k = [V.take(PAIRS2, COLS) for _ in range(2)]
        V.vd = V.take(UNIT, 2, PAIRS2, DH2 + 1)
        V.probs = [V.take(PAIRS2, 2, SEQ) for _ in range(2)]
        V.pT = [V.take(PAIRS2, P) for _ in range(2)]
        V.out = V.take(UNIT, PAIRS2, 2, DH2)
        V.outT = V.take(PAIRS2, COLS)
        V.res = V.take(UNIT, D)
        V.max = V.take(2, 2, PAIRS2)
        V.rsum = V.take(2, PAIRS2)
    if p == A3:
        V.raw = V.take(UNIT, 5, D)
        V.sq = V.take(UNIT, 3, D)
        V.ss = V.take(UNIT, 3, 2)
        V.rms = V.take(UNIT, 3, 2)
        V.normed = V.take(3, UNIT, D)
        V.q = [V.take(COLS) for _ in range(2)]
        V.k = [V.take(UNIT, 2, 2, SEQ) for _ in range(2)]
        V.vd = [V.take(UNIT, 2, 2, DH2 + 1) for _ in range(2)]
        V.mb = [V.take(UNIT, KEYS3) for _ in range(2)]
        V.probs = [V.take(2, KEYS3) for _ in range(2)]
        V.pT = [V.take(2, P) for _ in range(2)]
        V.out = V.take(UNIT, 2, DH2)
        V.outT = V.take(COLS)
        V.res = V.take(UNIT, D)
        V.max = V.take(2, 2)
        V.rsum = V.take(2)
    if p in CHUNKS:
        V.silu = [V.take(COLS) for _ in range(2)]
        V.prod = [V.take(COLS) for _ in range(2)]
        V.hid = [V.take(COLS) for _ in range(2)]
        V.scaled = [V.take(COLS) for _ in range(2)]
    if p == F3:
        V.sq = [V.take(COLS) for _ in range(4)]
        V.sd = [V.take(COLS) for _ in range(2)]
        V.rinv = [V.take(COLS) for _ in range(2)]
        V.z = [V.take(COLS) for _ in range(4)]
        V.relu = [V.take(COLS) for _ in range(4)]
        V.hid = [V.take(COLS) for _ in range(4)]
        V.onorm = V.take(UNIT, D)
        V.gated = V.take(UNIT, D)
        V.selraw_b = V.take(P)
        V.wmean = V.take(4)
    if p in EXPERTS:
        V.dt = V.take(COLS)
        V.selraw = V.take(16, P, rows=64)
    return V


def xs(K, s, t):
    return K.X[:, bass.ds(s * UNIT + t, 1), :].rearrange("p a d -> p (a d)")


def xu(K, s):
    return K.X[:, bass.ds(s * UNIT, UNIT), :]


def half(x):
    return slice(SEQ * x, SEQ * (x + 1))


def sync_program(nc, sp, K):
    A = K.A
    x_v = A["x"].rearrange("(t b) s d -> (b s) t d", b=2)
    c_v = A["ctx_768"].rearrange("(t b) s d -> (b s) t d", b=2)

    def load_ctx(p, s, b):
        if p in (A0, A3):
            if K.c_ready.due(p, s, 0):
                sp.wait_ge(K.c_ready.sem, K.c_ready.value(p, s, 0))
        elif p == A1:
            if K.cT_psum.due(p, s, 0):
                sp.wait_ge(K.cT_psum.sem, K.cT_psum.value(p, s, 0))
        else:
            if K.front_psum.due(p, s, 1 - FRONT2):
                sp.wait_ge(K.front_psum.sem, K.front_psum.value(p, s, 1 - FRONT2))
        sp.dma_start(K.v[p].ctx[b], c_v[:, bass.ds(s * UNIT, UNIT), :]).then_inc(K.ctx_loaded.sem, 16)

    def column(name, vec, rows=slice(0, P)):
        n = rows.stop - rows.start
        sp.dma_start(K.col[name][rows], vec.rearrange("(p o) -> p o", p=n)).then_inc(K.par_loaded, 16)

    def row(dst, vec):
        n = vec.shape[0]
        sp.dma_start(dst, vec.rearrange("(o n) -> o n", o=1).to_broadcast([P, n])).then_inc(K.par_loaded, 16)

    K.par_n = 0
    for s in range(UNITS):
        sp.dma_start(K.X[:, s * UNIT:(s + 1) * UNIT, :], x_v[:, s * UNIT:(s + 1) * UNIT, :]).then_inc(K.x_loaded, 16)
    row(K.gates[:, 0:4], A["g_xattn"])
    row(K.gates[:, 4:8], A["g_ffn"])
    for n in ("q_b", "k_b", "ln_g", "ln_b"):
        column(n, A[f"L0_xattn_{n}"])
    for n in ("tln_g", "tln_b"):
        column(n, A[f"L0_xattn_{n}"], slice(0, DC))
    for n in ("bq", "bk", "bv"):
        column(n, A[f"L1_xattn_{n}"])
    for n in ("ln_l_g", "ln_l_b"):
        column(n, A[f"L3_xattn_{n}"])
    for n in ("ln_x_g", "ln_x_b"):
        column(n, A[f"L3_xattn_{n}"], slice(0, DC))
    for n in ("rn_g", "rn_b"):
        column(n, A[f"L3_ffn_{n}"])
    for n in ("qn_g", "kn_g"):
        for h in range(2):
            column(n, A[f"L3_xattn_{n}"], half(h))
    with nc.allow_non_contiguous_dma("sixteen short vectors"):
        for dst, n in ((K.ln3_g, "ln_g"), (K.ln3_b, "ln_b")):
            sp.dma_start(dst, A[f"L3_ffn_{n}"].rearrange("e (c p) -> p (e c)", p=P)).then_inc(K.par_loaded, 16)
    row(K.row["v_b"], A["L0_xattn_v_b"])
    row(K.row["bo1"], A["L1_xattn_bo"])
    row(K.row["bo2"], A["L2_xattn_bo"])
    row(K.row["bo3"], A["L3_xattn_bo"])
    row(K.row["on_g"], A["L3_ffn_on_g"])
    row(K.row["on_b"], A["L3_ffn_on_b"])
    row(K.ebias0, A["L0_ffn_e_score_correction_bias"])
    row(K.ebias1, A["L1_ffn_experts_bias"])

    def load(p, dst, src):
        sp.dma_start(dst, src).then_inc(K.loaded[p], 16)

    for n in ("q", "k", "v"):
        load(A0, K.wp[A0][n][:, :], A[f"L0_xattn_{n}_w"])
    if K.phases[0] == A0:
        load_ctx(A0, 0, 0)
    for at, name in ((0, "L0_ffn_gate_weight"), (32, "L1_ffn_router_w"), (40, "L2_ffn_gate_w"), (48, "L3_ffn_router_w")):
        n = A[name].shape[0]
        sp.dma_start(K.router_raw[at:at + n, :], A[name]).then_inc(K.par_loaded, 16)
    if F0 in K.phases:
        raw = K.wf[F1]
        load(F0, raw[:, 0, 0, :], A["L0_ffn_shared_gate_w"])
        load(F0, raw[:, 1, 0, :], A["L0_ffn_shared_up_w"])
        load(F0, raw[:, 2, 0, :], A["L0_ffn_shared_down_w"])
        gu = A["L0_ffn_experts_gate_up"].rearrange("(j m) r h -> m r j h", m=2)
        for m in range(2):
            for which in range(2):
                load(F0, raw[half(m), which, 1:17, :], gu[m, half(which), :, :])
        dn = A["L0_ffn_experts_down"].rearrange("(j m) h i -> m h j i", m=2)
        for m in range(2):
            load(F0, raw[:, 2, 1:17, half(m)], dn[m])
    for n in ("q", "k", "v", "o"):
        load(A1, K.wp[A1][n][:, :], A[f"L1_xattn_W{n}"])
    for n in ("q", "k", "v"):
        load(A2, K.wp[A2][n][:, :], A[f"L2_xattn_W{n}"])
    load(A2, K.wp[A2]["o"][:, :, :], A["L2_xattn_Wo"].rearrange("(c p) n -> p c n", p=P))
    L3 = K.wp[A3]["raw"]
    load(A3, L3[:, 0, :], A["L3_xattn_Wq"])
    load(A3, L3[:, 1:3, :], A["L3_xattn_Wlkv"].rearrange("(c p) n -> p c n", p=P))
    load(A3, L3[:, 3, :], A["L3_xattn_Wo"])
    load(A3, L3[:, 4:6, 0:DC], A["L3_xattn_Wkv"].rearrange("(c p) n -> p c n", p=P))
    mask = A["mask"].rearrange("(t b) k -> b t k", b=2)
    for x in range(2):
        load(A3, K.mask_words[half(x), :, :], mask[x:x + 1].to_broadcast([SEQ, TILES, SEQ // 4]))

    def load_late():
        for which, n in ((0, "w1"), (1, "w3"), (2, "w2")):
            load(F2, K.wf[F2][:, which, 0, :], A[f"L2_ffn_{n}s"][0])
            load(F2, K.wf[F2][:, which, 1:9, :], A[f"L2_ffn_{n}"].rearrange("e d h -> d e h"))
        load(F3, K.w1, A["L3_ffn_w1"].rearrange("e d h -> d e h"))
        load(F3, K.w2, A["L3_ffn_w2"].rearrange("e (c p) d -> p (e c) d", p=P))

    def load_f1():
        for which, n in ((0, "w1"), (1, "w3")):
            for at, src in ((0, A[f"L1_ffn_s{n}"]), (2, A[f"L1_ffn_{n}"])):
                e = src.shape[0]
                load(F1, K.wf[F1][:, which, at:at + 2 * e, :].rearrange("p (e c) h -> p e (c h)", e=e),
                     src.rearrange("e d h -> d e h"))
        for at, src in ((0, A["L1_ffn_sw2"]), (2, A["L1_ffn_w2"])):
            e = src.shape[0]
            load(F1, K.wf[F1][:, 2, at:at + 2 * e, :], src.rearrange("e (c p) d -> p (e c) d", p=P))

    if F0 not in K.phases:
        load_f1()
        load_late()
    for p in K.phases:
        if p in ATTENTION:
            if p != K.phases[0]:
                sp.wait_ge(K.x_done.sem, K.x_done.start[p])
            if not (p == A0 and K.phases[0] == A0):
                load_ctx(p, 0, 0)
            if p == A1 and F0 in K.phases:
                load_f1()
                load_late()

            def body(s, b, last):
                if not last:
                    load_ctx(p, s + 1, 1 - b)
            over_units(sp, body)
    for p in range(8):
        if p != F0 or F0 in K.phases:
            sp.wait_ge(K.loaded[p], 16 * LOADS[p])
    last = K.phases[-1]
    out_v = K.out.rearrange("(t b) s d -> (b s) t d", b=2)
    for s in range(UNITS):
        sp.wait_ge(K.x_done.sem, K.x_done.value(last, s, 1))
        sp.dma_start(out_v[:, s * UNIT:(s + 1) * UNIT, :], K.X[:, s * UNIT:(s + 1) * UNIT, :]).then_inc(K.stored, 16)
    sp.wait_ge(K.stored, 16 * UNITS)


PAR = 16 * (2 + 4 + 2 + 3 + 2 + 2 + 2 + 4 + 2 + 8 + 4)
YT_PIECE = {A2: 5, A3: 1}
LOADS = {A0: 3, F0: 3 + 4 + 2, A1: 4, F1: 6, A2: 4, F2: 6, A3: 6, F3: 2}
PREP_GROUPS = [(i, min(4, 51 - i)) for i in range(0, 51, 4)]
PREP_F0 = len(PREP_GROUPS)


def whole_first(first, y, t):
    if first:
        return slice(0, P), slice(t * P, (t + 1) * P)
    return half(y), slice(t * P + y * SEQ, t * P + (y + 1) * SEQ)


def ln_statistics(nc, dve, K, p, s, steps, stats, w, source, n, twice):
    for t in range(UNIT):
        dve.bn_stats(stats[:, t, :], source(t)).then_inc(steps.sem, steps.one())
    mean2, dif, m2, sq, mean, var = (w[:, i, :] for i in range(6))
    dve.wait_ge(steps.sem, steps.value())
    dve.tensor_tensor(mean2, stats[:, :, 1], stats[:, :, 4], ALU.add).then_inc(steps.sem, steps.one())
    dve.tensor_tensor(dif, stats[:, :, 1], stats[:, :, 4], ALU.subtract).then_inc(steps.sem, steps.one())
    dve.tensor_tensor(m2, stats[:, :, 2], stats[:, :, 5], ALU.add).then_inc(steps.sem, steps.one())
    dve.wait_ge(steps.sem, steps.value())
    dve.tensor_scalar(mean, mean2, 0.5, None, ALU.mult).then_inc(steps.sem, steps.one())
    dve.scalar_tensor_tensor(out=sq, in0=dif, scalar=0.25, in1=dif, op0=ALU.mult, op1=ALU.mult).then_inc(steps.sem, steps.one())
    dve.wait_ge(steps.sem, steps.value())
    dve.scalar_tensor_tensor(out=var, in0=m2, scalar=1.0 / n, in1=sq, op0=ALU.mult, op1=ALU.add).then_inc(steps.sem, steps.one())
    dve.wait_ge(steps.sem, steps.value())
    a, b = (1.0 + EPS, EPS * EPS) if twice else (1.0, EPS)
    dve.tensor_scalar(dif, var, a, b, ALU.mult, ALU.add).then_inc(steps.sem, steps.one())


def ln_apply(nc, dve, out, source, w, ready):
    for t in range(UNIT):
        last = dve.tensor_scalar(out[:, t, :], source(t), w[:, 4, t:t + 1], w[:, 0, t:t + 1],
                                 ALU.subtract, ALU.mult)
    last.then_inc(ready.sem, 1)


def x_statistics(nc, dve, K, p, s):
    steps = Steps(K.ln_steps, p, s)
    ln_statistics(nc, dve, K, p, s, steps, K.stats, K.lnw, lambda t: xs(K, s, t), D, p in (A0, A3))
    steps.ended()


def x_normed(nc, dve, K, p, s):
    dve.wait_ge(K.rstd_ready.sem, K.rstd_ready.value(p, s, 1))
    if p in (A2, A3):
        if K.front_psum.due(p, s, YT_PIECE[p] + 1 - K.front_psum.counts[p]):
            dve.wait_ge(K.front_psum.sem, K.front_psum.value(p, s, YT_PIECE[p] + 1 - K.front_psum.counts[p]))
    else:
        if K.yT_psum.due(p, s, 0):
            dve.wait_ge(K.yT_psum.sem, K.yT_psum.value(p, s, 0))
    ln_apply(nc, dve, K.yt, lambda t: xs(K, s, t), K.lnw, K.y_ready)


def ctx_statistics(nc, dve, K, p, s, b):
    dve.wait_ge(K.ctx_loaded.sem, K.ctx_loaded.value(p, s, 16))
    steps = Steps(K.cln_steps, p, s)
    ln_statistics(nc, dve, K, p, s, steps, K.cstats, K.clnw, lambda t: K.v[p].ctx[b][:, t, :], DC, False)
    steps.ended()


def ctx_normed(nc, dve, K, p, s, b):
    dve.wait_ge(K.crstd_ready.sem, K.crstd_ready.value(p, s, 1))
    if p == A3:
        if K.front_psum.due(p, s, 1 - FRONT3):
            dve.wait_ge(K.front_psum.sem, K.front_psum.value(p, s, 1 - FRONT3))
    else:
        if K.cT_psum.due(p, s, 0):
            dve.wait_ge(K.cT_psum.sem, K.cT_psum.value(p, s, 0))
    ln_apply(nc, dve, K.v[p].ctxn, lambda t: K.v[p].ctx[b][:, t, :], K.clnw, K.c_ready)


def rstd_pool(nc, pool, K, p, s, ctx):
    steps, ready, w = (K.cln_steps, K.crstd_ready, K.clnw) if ctx else (K.ln_steps, K.rstd_ready, K.lnw)
    pool.wait_ge(steps.sem, steps.value(p, s, steps.counts[p]))
    pool.tensor_tensor(w[:, 0, :], w[:, 1, :], K.minus_half[:, 0:UNIT], ALU.pow).then_inc(ready.sem, 1)


def transpose4(nc, K, bank, source, rows, cols=P):
    for t in range(UNIT):
        last = nc.tensor.transpose(bank[0:rows, t * P:(t + 1) * P], source(t), K.ident[:, :])
    return last


def yT_evacuate(nc, act, K, p, s, b, bank):
    ready = K.front_read if p in (A2, A3) else K.yT_ready
    if p not in (A2, A3):
        act.wait_ge(K.yT_psum.sem, K.yT_psum.value(p, s, 1))
    g, o = {A0: ("ln_g", "ln_b"), A3: ("ln_l_g", "ln_l_b")}.get(p, (None, None))
    if g:
        act.activation(K.yT[b][:, :], bank, ACT.Identity, scale=K.col[g], bias=K.col[o]).then_inc(ready.sem, 1)
    else:
        act.activation(K.yT[b][:, :], bank, ACT.Copy).then_inc(ready.sem, 1)


def cT_evacuate(nc, act, K, p, s, b, bank):
    ready = K.front_read if p in (A2, A3) else K.cT_ready
    if p not in (A2, A3):
        act.wait_ge(K.cT_psum.sem, K.cT_psum.value(p, s, 1))
    g, o = {A0: ("tln_g", "tln_b"), A3: ("ln_x_g", "ln_x_b")}.get(p, (None, None))
    dst = K.v[p].cT[b]
    if g:
        act.activation(dst, bank[0:DC, :], ACT.Identity, scale=K.col[g][0:DC], bias=K.col[o][0:DC]).then_inc(ready.sem, 1)
    else:
        act.activation(dst, bank[0:DC, :], ACT.Copy).then_inc(ready.sem, 1)


S_BANKS = ((0, 1), (2, 3))
PT_BANKS = (4, 5)
O_BANK, X_BANK = 6, 7


def small_tensor(nc, pe, K, p):
    V, W = K.v[p], K.wp[p]
    bank, mm = K.bank, nc.tensor.matmul

    def context(s, b):
        if p == A0:
            pe.wait_ge(K.c_ready.sem, K.c_ready.value(p, s, 1))
        else:
            pe.wait_ge(K.ctx_loaded.sem, K.ctx_loaded.value(p, s, 16))
        if K.v_ready.due(p, s, 0):
            pe.wait_ge(K.v_ready.sem, K.v_ready.value(p, s, 0))
        tail_free(s)
        src = V.ctxn if p == A0 else V.ctx[b]
        transpose4(nc, K, bank[X_BANK], lambda t: src[:, t, :], DC).then_inc(K.cT_psum.sem, 1)

    def tail_free(s):
        if p == A1:
            if K.x_done.due(p, s, -1):
                pe.wait_ge(K.x_done.sem, K.x_done.value(p, s, -1))

    def stream(s):
        pe.wait_ge(K.y_ready.sem, K.y_ready.value(p, s, 1))
        pe.wait_ge(K.cT_ready.sem, K.cT_ready.value(p, s, 1))
        transpose4(nc, K, bank[X_BANK], lambda t: K.yt[:, t, :], P).then_inc(K.yT_psum.sem, 1)

    def queries(s, b):
        pe.wait_ge(K.yT_ready.sem, K.yT_ready.value(p, s, 1))
        mm(bank[X_BANK], W["q"][:, :], K.yT[b][:, :], start=True, stop=True).then_inc(K.q_psum.sem, 1)

    def keys(s, b):
        pe.wait_ge(K.q_ready.sem, K.q_ready.value(p, s, 1))
        mm(bank[X_BANK], W["k"][:, :], V.cT[b], start=True, stop=True).then_inc(K.k_psum.sem, 1)

    def values(s, b):
        pe.wait_ge(K.k_ready.sem, K.k_ready.value(p, s, 1))
        for t in range(UNIT):
            last = mm(bank[X_BANK][:, t * P:(t + 1) * P], V.cT[b][:, t * P:(t + 1) * P], W["v"][:, :],
                      start=True, stop=True)
        last.then_inc(K.v_psum.sem, 1)

    def scores(s, b, t):
        pe.wait_ge(K.kbd_ready.sem, K.kbd_ready.value(p, s, t + 1))
        if K.shift_ready.due(p, s, t - 1):
            pe.wait_ge(K.shift_ready.sem, K.shift_ready.value(p, s, t - 1))
        if t == 0:
            pe.wait_ge(K.q_ready.sem, K.q_ready.value(p, s, 1))
        for g in range(2):
            last = mm(bank[S_BANKS[t % 2][g]], V.qz[b][:, g, t, :], V.kbd[t % 2][:, g, :, :].rearrange("p h k -> p (h k)"),
                      start=True, stop=True)
        last.then_inc(K.s_psum.sem, 1)

    def turned(s, t):
        pe.wait_ge(K.probs_ready.sem, K.probs_ready.value(p, s, t + 1))
        if K.pT_ready.due(p, s, t):
            pe.wait_ge(K.pT_ready.sem, K.pT_ready.value(p, s, t))
        pr = V.probs[t % 2].rearrange("p h k -> p (h k)")
        for j in range(GROUP):
            last = nc.tensor.transpose(bank[PT_BANKS[j // 4]][:, (j % 4) * P:(j % 4 + 1) * P],
                                       pr[:, j * P:(j + 1) * P], K.ident[:, :])
        last.then_inc(K.pT_psum.sem, 1)

    def weighted(s, b, t):
        pe.wait_ge(K.pT_ready.sem, K.pT_ready.value(p, s, t + 1))
        if K.out_ready.due(p, s, t):
            pe.wait_ge(K.out_ready.sem, K.out_ready.value(p, s, t))
        if t == 0:
            pe.wait_ge(K.v_ready.sem, K.v_ready.value(p, s, 1))
        n = 2 * 2 * (DH + 1)
        for j in range(GROUP):
            last = mm(bank[O_BANK][:, j * n:(j + 1) * n], V.pT[t % 2][:, j, :],
                      V.vd[b][:, t, j, :, :, :].rearrange("p x h d -> p (x h d)"), start=True, stop=True)
        last.then_inc(K.av_psum.sem, 1)

    def project(s, nxt):
        pe.wait_ge(K.out_ready.sem, K.out_ready.value(p, s, UNIT))
        if nxt is not None:
            pe.wait_ge(K.v_ready.sem, K.v_ready.value(p, nxt, 1))
        transpose4(nc, K, bank[X_BANK], lambda t: V.out[:, t, :], P).then_inc(K.oT_psum.sem, 1)
        pe.wait_ge(K.oT_ready.sem, K.oT_ready.value(p, s, 1))
        for t in range(UNIT):
            last = mm(bank[X_BANK][:, t * P:(t + 1) * P], V.outT[:, t * P:(t + 1) * P], W["o"][:, :],
                      start=True, stop=True)
        last.then_inc(K.proj_psum.sem, 1)

    pe.wait_ge(K.loaded[p], 16 * LOADS[p])
    context(0, 0)
    stream(0)
    queries(0, 0)
    keys(0, 0)
    values(0, 0)

    def body(s, b, last):
        scores(s, b, 0)
        scores(s, b, 1)
        turned(s, 0)
        scores(s, b, 2)
        weighted(s, b, 0)
        if not last:
            context(s + 1, 1 - b)
        turned(s, 1)
        scores(s, b, 3)
        weighted(s, b, 1)
        if not last:
            stream(s + 1)
        turned(s, 2)
        weighted(s, b, 2)
        if not last:
            queries(s + 1, 1 - b)
        turned(s, 3)
        if not last:
            keys(s + 1, 1 - b)
        weighted(s, b, 3)
        if not last:
            values(s + 1, 1 - b)
        if p == A1:
            project(s, None if last else s + 1)
    over_units(pe, body)


def small_scalar(nc, act, K, p):
    V = K.v[p]
    bank = K.bank
    x = bank[X_BANK]

    def queries(s, b):
        act.wait_ge(K.q_psum.sem, K.q_psum.value(p, s, 1))
        name = "q_b" if p == A0 else "bq"
        xv = x.rearrange("p (t y q) -> p t y q", t=UNIT, y=2)
        for g in range(2):
            for y in range(2):
                last = act.activation(V.qz[b][half(y), g, :, half(y)], xv[half(g), :, y, :], ACT.Identity,
                                      bias=K.col[name][half(g)])
        last.then_inc(K.q_ready.sem, 1)

    def values(s, b):
        act.wait_ge(K.v_psum.sem, K.v_psum.value(p, s, 1))
        xv = x.rearrange("p (t j h d) -> p t j h d", t=UNIT, j=GROUP, h=2)
        for y in range(2):
            for hh in range(2):
                last = act.activation(V.vd[b][half(hh), :, :, y, hh, 0:DH], xv[half(y), :, :, hh, :], ACT.Copy)
        last.then_inc(K.v_ready.sem, 1)

    def probs(s, t):
        act.wait_ge(K.shift_ready.sem, K.shift_ready.value(p, s, t + 1))
        pr = V.probs[t % 2]
        act.activation(pr, pr, ACT.Exp, scale=DH ** -0.5).then_inc(K.probs_ready.sem, 1)

    def turned(s, t):
        if p == A0:
            act.wait_ge(K.pT_psum.sem, K.pT_psum.value(p, s, t + 1))
            if K.av_psum.due(p, s, t - 1):
                act.wait_ge(K.av_psum.sem, K.av_psum.value(p, s, t - 1))
            act.activation(V.pT[t % 2], K.ps[:, PT_BANKS[0]:PT_BANKS[1] + 1, :].rearrange("p b (j q) -> p (b j) q", q=P),
                           ACT.Copy).then_inc(K.pT_ready.sem, 1)

    cT_evacuate(nc, act, K, p, 0, 0, x)
    yT_evacuate(nc, act, K, p, 0, 0, x)
    queries(0, 0)
    values(0, 0)

    def body(s, b, last):
        probs(s, 0)
        probs(s, 1)
        turned(s, 0)
        probs(s, 2)
        if not last:
            cT_evacuate(nc, act, K, p, s + 1, 1 - b, x)
        turned(s, 1)
        probs(s, 3)
        if not last:
            yT_evacuate(nc, act, K, p, s + 1, 1 - b, x)
        turned(s, 2)
        if not last:
            queries(s + 1, 1 - b)
        turned(s, 3)
        if not last:
            values(s + 1, 1 - b)
        if p == A1:
            act.wait_ge(K.oT_psum.sem, K.oT_psum.value(p, s, 1))
            if K.proj_psum.due(p, s, 0):
                act.wait_ge(K.proj_psum.sem, K.proj_psum.value(p, s, 0))
            act.activation(V.outT, x, ACT.Identity, bias=K.col["bv"]).then_inc(K.oT_ready.sem, 1)
    over_units(act, body)


def small_vector(nc, dve, K, p):
    V = K.v[p]
    x = K.bank[X_BANK]

    def keys(s, b):
        dve.wait_ge(K.k_psum.sem, K.k_psum.value(p, s, 1))
        if K.kbd_ready.due(p, s, -UNIT):
            dve.wait_ge(K.kbd_ready.sem, K.kbd_ready.value(p, s, -UNIT))
        name = "k_b" if p == A0 else "bk"
        xv = x.rearrange("p (t y k) -> p t y k", t=UNIT, y=2)
        for g in range(2):
            for y in range(2):
                last = dve.tensor_scalar(V.ksel[b][half(y), g, :, :], xv[half(g), :, y, :], K.col[name][half(g)], None,
                                         ALU.add)
        last.then_inc(K.k_ready.sem, 1)

    def shift(s, t):
        steps = Steps(K.max_steps, p, s, t * (K.max_steps.counts[p] // UNIT))
        dve.wait_ge(K.s_psum.sem, K.s_psum.value(p, s, t + 1))
        lo, hi = S_BANKS[t % 2]
        sc = K.ps[:, lo:hi + 1, :].rearrange("p b (h k) -> p (b h) k", k=SEQ)
        mx = V.max[:, t % 2, :]
        dve.tensor_reduce(mx, sc, axis=AX.X, op=ALU.max).then_inc(steps.sem, steps.one())
        c = CLAMP * DH ** 0.5
        if p == A1:
            dve.wait_ge(steps.sem, steps.value())
            dve.tensor_scalar(mx, mx, c, -c, ALU.min, ALU.max).then_inc(steps.sem, steps.one())
        dve.wait_ge(steps.sem, steps.value())
        if K.pT_psum.due(p, s, t - 1):
            dve.wait_ge(K.pT_psum.sem, K.pT_psum.value(p, s, t - 1))
        mxb = mx.unsqueeze(2).to_broadcast([P, HEADS, SEQ])
        if p == A1:
            dve.scalar_tensor_tensor(out=V.probs[t % 2], in0=sc, scalar=-c, in1=mxb, op0=ALU.max,
                                     op1=ALU.subtract).then_inc(K.shift_ready.sem, 1)
        else:
            dve.tensor_tensor(V.probs[t % 2], sc, mxb, ALU.subtract).then_inc(K.shift_ready.sem, 1)

    def turned(s, t):
        if p == A1:
            dve.wait_ge(K.pT_psum.sem, K.pT_psum.value(p, s, t + 1))
            if K.av_psum.due(p, s, t - 1):
                dve.wait_ge(K.av_psum.sem, K.av_psum.value(p, s, t - 1))
            dve.tensor_scalar(V.pT[t % 2], K.ps[:, PT_BANKS[0]:PT_BANKS[1] + 1, :].rearrange("p b (j q) -> p (b j) q", q=P),
                              1.0, None, ALU.min).then_inc(K.pT_ready.sem, 1)

    def outputs(s, t):
        dve.wait_ge(K.av_psum.sem, K.av_psum.value(p, s, t + 1))
        if t == 0 and p == A1:
            if K.oT_psum.due(p, s, 0):
                dve.wait_ge(K.oT_psum.sem, K.oT_psum.value(p, s, 0))
        steps = Steps(K.sum_steps, p, s, t)
        o = K.bank[O_BANK][:, 0:GROUP * 4 * (DH + 1)].rearrange("p (j y h d) -> p j y h d", j=GROUP, y=2, h=2)
        rs = V.rsum.rearrange("p (j h) -> p j h", h=2)
        for y in range(2):
            last = dve.reciprocal(rs[half(y)], o[half(y), :, y, :, DH])
        last.then_inc(steps.sem, steps.one())
        dve.wait_ge(steps.sem, steps.value())
        for y in range(2):
            last = dve.tensor_tensor(V.out[half(y), t, :].rearrange("p (j h d) -> p j h d", j=GROUP, h=2),
                                     o[half(y), :, y, :, 0:DH],
                                     rs[half(y)].unsqueeze(3).to_broadcast([SEQ, GROUP, 2, DH]), ALU.mult)
        last.then_inc(K.out_ready.sem, 1)

    def residual(s):
        if p == A0:
            dve.wait_ge(K.out_ready.sem, K.out_ready.value(p, s, UNIT))
            src, add = V.out, K.row["v_b"]
        else:
            dve.wait_ge(K.proj_psum.sem, K.proj_psum.value(p, s, 1))
            src, add = x.rearrange("p (t d) -> p t d", t=UNIT), K.row["bo1"]
        add_residual(nc, dve, K, p, s, V.res, src, add)

    x_statistics(nc, dve, K, p, 0)
    if p == A0:
        ctx_statistics(nc, dve, K, p, 0, 0)
    x_normed(nc, dve, K, p, 0)
    if p == A0:
        ctx_normed(nc, dve, K, p, 0, 0)
    keys(0, 0)

    def body(s, b, last):
        shift(s, 0)
        if not last:
            x_statistics(nc, dve, K, p, s + 1)
            if p == A0:
                ctx_statistics(nc, dve, K, p, s + 1, 1 - b)
        shift(s, 1)
        turned(s, 0)
        if not last:
            if p == A0:
                ctx_normed(nc, dve, K, p, s + 1, 1 - b)
            x_normed(nc, dve, K, p, s + 1)
        shift(s, 2)
        outputs(s, 0)
        turned(s, 1)
        shift(s, 3)
        outputs(s, 1)
        turned(s, 2)
        outputs(s, 2)
        if not last:
            keys(s + 1, 1 - b)
        turned(s, 3)
        outputs(s, 3)
        residual(s)
    over_units(dve, body)


def add_residual(nc, dve, K, p, s, tmp, src, add):
    gate = K.gates[:, p // 2:p // 2 + 1]
    if K.x_done.due(p, s, 0):
        dve.wait_ge(K.x_done.sem, K.x_done.value(p, s, 0))
    dve.tensor_tensor(tmp, src, add.unsqueeze(1).to_broadcast([P, UNIT, D]), ALU.add).then_inc(K.res_steps.sem, 1)
    dve.wait_ge(K.res_steps.sem, K.res_steps.value(p, s, 1))
    dve.scalar_tensor_tensor(out=xu(K, s), in0=tmp, scalar=gate, in1=xu(K, s), op0=ALU.mult,
                             op1=ALU.add).then_inc(K.x_done.sem, 1)


def small_pool(nc, pool, K, p):
    V = K.v[p]

    def spread(s, b, t):
        if t == 0:
            pool.wait_ge(K.k_ready.sem, K.k_ready.value(p, s, 1))
        if K.s_psum.due(p, s, t - 1):
            pool.wait_ge(K.s_psum.sem, K.s_psum.value(p, s, t - 1))
        for g in range(2):
            last = pool.tensor_tensor(V.kbd[t % 2][:, g, :, :],
                                      V.ksel[b][:, g, t, :].unsqueeze(1).to_broadcast([P, GROUP, SEQ]),
                                      V.diag.unsqueeze(2).to_broadcast([P, GROUP, SEQ]), ALU.mult)
        last.then_inc(K.kbd_ready.sem, 1)

    rstd_pool(nc, pool, K, p, 0, False)
    if p == A0:
        rstd_pool(nc, pool, K, p, 0, True)

    def body(s, b, last):
        spread(s, b, 0)
        spread(s, b, 1)
        if not last:
            rstd_pool(nc, pool, K, p, s + 1, False)
            if p == A0:
                rstd_pool(nc, pool, K, p, s + 1, True)
        spread(s, b, 2)
        spread(s, b, 3)
    over_units(pool, body)


def small_fill(nc, pool, K, p, count):
    V = K.v[p]
    lo, hi = V.zeroed
    pool.memset(K.arena[:, lo:hi], 0.0).then_inc(K.fill, 1)
    pool.memset(V.diag, 1.0).then_inc(K.fill, 1)
    pool.wait_ge(K.fill, count + 2)
    for b in range(2):
        for hh in range(2):
            pool.memset(V.vd[b][half(hh), :, :, :, hh, DH].rearrange("p t j y -> p (t j) y"), 1.0)
    for y in range(2):
        dg = V.diag[half(y)]
        pool.affine_select(out=dg, in_=dg, compare_op=ALU.is_ge, fill=0.0, base=0,
                           pattern=[[-DH, GROUP]], channel_multiplier=1).then_inc(K.fill, 1)
    pool.wait_ge(K.fill, count + 4)
    for y in range(2):
        dg = V.diag[half(y)]
        pool.affine_select(out=dg, in_=dg, compare_op=ALU.is_ge, fill=0.0, base=DH - 1,
                           pattern=[[DH, GROUP]], channel_multiplier=-1).then_inc(K.fill, 1)
    pool.wait_ge(K.fill, count + 6)
    return count + 6


PT2_BANK = 2
O2_BANKS = (3, 4)


def piece_bank(K, i):
    return K.bank[5 + i % 3]


def l2_tensor(nc, pe, K):
    p = A2
    V, W = K.v[p], K.wp[p]
    mm = nc.tensor.matmul

    def piece(s, b, i):
        if K.front_read.due(p, s, max(0, i - 2)):
            pe.wait_ge(K.front_read.sem, K.front_read.value(p, s, max(0, i - 2)))
        if i == 0:
            pe.wait_ge(K.ctx_loaded.sem, K.ctx_loaded.value(p, s, 16))
            if K.x_done.due(p, s, -1):
                pe.wait_ge(K.x_done.sem, K.x_done.value(p, s, -1))
        bank = piece_bank(K, i)
        if i == 0:
            last = transpose4(nc, K, bank, lambda t: V.ctx[b][:, t, :], DC)
        elif i < 5:
            pe.wait_ge(K.front_read.sem, K.front_read.value(p, s, 1))
            last = mm(bank, W["k"][:, (i - 1) * P:i * P], V.cT[b], start=True, stop=True)
        elif i == 5:
            pe.wait_ge(K.y_ready.sem, K.y_ready.value(p, s, 1))
            last = transpose4(nc, K, bank, lambda t: K.yt[:, t, :], P)
        elif i < 10:
            pe.wait_ge(K.front_read.sem, K.front_read.value(p, s, 6))
            last = mm(bank, W["q"][:, (i - 6) * P:(i - 5) * P], K.yT[b][:, :], start=True, stop=True)
        else:
            t = i - 10
            last = mm(bank, V.cT[b][:, t * P:(t + 1) * P], W["v"][:, :], start=True, stop=True)
        last.then_inc(K.front_psum.sem, 1)

    def scores(s, b, t):
        if K.shift_ready.due(p, s, t):
            pe.wait_ge(K.shift_ready.sem, K.shift_ready.value(p, s, t))
        pe.wait_ge(K.front_read.sem, K.front_read.value(p, s, 10))
        for j in range(PAIRS2):
            for h in range(2):
                for y in range(2):
                    tok = slice(t * P + y * SEQ, t * P + (y + 1) * SEQ)
                    rows, qs = whole_first(j + h + y == 0, y, t)
                    last = mm(K.bank[h][rows, j * SEQ:(j + 1) * SEQ], V.q[b][half(h), j, qs],
                              V.k[b][half(h), j, tok], start=True, stop=True)
        last.then_inc(K.s_psum.sem, 1)

    def turned(s, t):
        pe.wait_ge(K.probs_ready.sem, K.probs_ready.value(p, s, t + 1))
        if K.pT_ready.due(p, s, t):
            pe.wait_ge(K.pT_ready.sem, K.pT_ready.value(p, s, t))
        for j in range(PAIRS2):
            last = nc.tensor.transpose(K.bank[PT2_BANK][:, j * P:(j + 1) * P],
                                       V.probs[t % 2][:, j, :, :].rearrange("p h k -> p (h k)"), K.ident[:, :])
        last.then_inc(K.pT_psum.sem, 1)

    def weighted(s, t):
        pe.wait_ge(K.pT_ready.sem, K.pT_ready.value(p, s, t + 1))
        if K.out_ready.due(p, s, t):
            pe.wait_ge(K.out_ready.sem, K.out_ready.value(p, s, t))
        if t == 0:
            pe.wait_ge(K.front_read.sem, K.front_read.value(p, s, FRONT2))
        n = DH2 + 1
        for j in range(PAIRS2):
            for h in range(2):
                for y in range(2):
                    rows, qs = whole_first(j + h + y == 0, y, 0)
                    last = mm(K.bank[O2_BANKS[h]][rows, j * n:(j + 1) * n], V.pT[t % 2][half(h), j, qs],
                              V.vd[half(h), t, y, j, :], start=True, stop=True)
        last.then_inc(K.av_psum.sem, 1)

    def project(s, nxt):
        pe.wait_ge(K.out_ready.sem, K.out_ready.value(p, s, UNIT))
        if nxt is not None:
            pe.wait_ge(K.front_read.sem, K.front_read.value(p, nxt, FRONT2))
        for j in range(PAIRS2):
            if K.oT_ready.due(p, s, j - 2):
                pe.wait_ge(K.oT_ready.sem, K.oT_ready.value(p, s, j - 2))
            transpose4(nc, K, piece_bank(K, FRONT2 + j),
                       lambda t: V.out[:, t, j, :, :].rearrange("p h d -> p (h d)"), P).then_inc(K.oT_psum.sem, 1)
        pe.wait_ge(K.oT_ready.sem, K.oT_ready.value(p, s, PAIRS2))
        bank = piece_bank(K, FRONT2 + PAIRS2)
        for t in range(UNIT):
            for j in range(PAIRS2):
                last = mm(bank[:, t * P:(t + 1) * P], V.outT[:, j, t * P:(t + 1) * P], W["o"][:, j, :],
                          start=j == 0, stop=j == PAIRS2 - 1)
        last.then_inc(K.proj_psum.sem, 1)

    pe.wait_ge(K.loaded[p], 16 * LOADS[p])
    for i in range(FRONT2):
        piece(0, 0, i)

    def body(s, b, last):
        def pieces(lo, hi):
            if not last:
                for i in range(lo, hi):
                    piece(s + 1, 1 - b, i)
        scores(s, b, 0)
        pieces(0, 2)
        turned(s, 0)
        scores(s, b, 1)
        weighted(s, 0)
        pieces(2, 5)
        turned(s, 1)
        scores(s, b, 2)
        weighted(s, 1)
        pieces(5, 8)
        turned(s, 2)
        scores(s, b, 3)
        weighted(s, 2)
        pieces(8, 10)
        turned(s, 3)
        weighted(s, 3)
        pieces(10, 14)
        project(s, None if last else s + 1)
    over_units(pe, body)


def l2_scalar(nc, act, K):
    p = A2
    V = K.v[p]

    def piece(s, b, i):
        act.wait_ge(K.front_psum.sem, K.front_psum.value(p, s, i + 1))
        bank = piece_bank(K, i)
        if i == 0:
            cT_evacuate(nc, act, K, p, s, b, bank)
        elif i < 5:
            act.activation(V.k[b][:, i - 1, :], bank, ACT.Copy).then_inc(K.front_read.sem, 1)
        elif i == 5:
            yT_evacuate(nc, act, K, p, s, b, bank)
        elif i < 10:
            act.activation(V.q[b][:, i - 6, :], bank, ACT.Copy).then_inc(K.front_read.sem, 1)
        else:
            t = i - 10
            if K.av_psum.due(p, s, 0):
                act.wait_ge(K.av_psum.sem, K.av_psum.value(p, s, 0))
            v = bank.rearrange("p (j h d) -> p j h d", j=PAIRS2, h=2)
            for y in range(2):
                for h in range(2):
                    last = act.activation(V.vd[half(h), t, y, :, 0:DH2], v[half(y), :, h, :], ACT.Copy)
            last.then_inc(K.front_read.sem, 1)

    def probs(s, t):
        act.wait_ge(K.shift_ready.sem, K.shift_ready.value(p, s, t + 1))
        pr = V.probs[t % 2]
        act.activation(pr, pr, ACT.Exp, scale=DH2 ** -0.5).then_inc(K.probs_ready.sem, 1)

    def turned(s, t):
        act.wait_ge(K.pT_psum.sem, K.pT_psum.value(p, s, t + 1))
        if K.av_psum.due(p, s, t - 1):
            act.wait_ge(K.av_psum.sem, K.av_psum.value(p, s, t - 1))
        act.activation(V.pT[t % 2], K.bank[PT2_BANK].rearrange("p (j q) -> p j q", q=P),
                       ACT.Copy).then_inc(K.pT_ready.sem, 1)

    for i in range(FRONT2):
        piece(0, 0, i)

    def body(s, b, last):
        def pieces(lo, hi):
            if not last:
                for i in range(lo, hi):
                    piece(s + 1, 1 - b, i)
        pieces(0, 1)
        probs(s, 0)
        pieces(1, 2)
        turned(s, 0)
        probs(s, 1)
        pieces(2, 5)
        turned(s, 1)
        probs(s, 2)
        pieces(5, 8)
        turned(s, 2)
        probs(s, 3)
        pieces(8, 10)
        turned(s, 3)
        pieces(10, 14)
        for j in range(PAIRS2):
            act.wait_ge(K.oT_psum.sem, K.oT_psum.value(p, s, j + 1))
            if K.proj_psum.due(p, s, 0):
                act.wait_ge(K.proj_psum.sem, K.proj_psum.value(p, s, 0))
            act.activation(V.outT[:, j, :], piece_bank(K, FRONT2 + j), ACT.Copy).then_inc(K.oT_ready.sem, 1)
    over_units(act, body)


def l2_vector(nc, dve, K):
    p = A2
    V = K.v[p]

    def shift(s, t):
        steps = Steps(K.max_steps, p, s, t)
        dve.wait_ge(K.s_psum.sem, K.s_psum.value(p, s, t + 1))
        sc = K.ps[:, 0:2, 0:PAIRS2 * SEQ].rearrange("p h (j k) -> p h j k", k=SEQ)
        mx = V.max[:, t % 2, :, :]
        dve.tensor_reduce(mx, sc, axis=AX.X, op=ALU.max).then_inc(steps.sem, steps.one())
        dve.wait_ge(steps.sem, steps.value())
        if K.pT_psum.due(p, s, t - 1):
            dve.wait_ge(K.pT_psum.sem, K.pT_psum.value(p, s, t - 1))
        dve.tensor_tensor(V.probs[t % 2].rearrange("p j h k -> p h j k"), sc,
                          mx.unsqueeze(3).to_broadcast([P, 2, PAIRS2, SEQ]), ALU.subtract).then_inc(K.shift_ready.sem, 1)

    def outputs(s, t):
        dve.wait_ge(K.av_psum.sem, K.av_psum.value(p, s, t + 1))
        if t == 0:
            if K.oT_psum.due(p, s, 0):
                dve.wait_ge(K.oT_psum.sem, K.oT_psum.value(p, s, 0))
        steps = Steps(K.sum_steps, p, s, t)
        o = K.ps[:, O2_BANKS[0]:O2_BANKS[1] + 1, 0:PAIRS2 * (DH2 + 1)].rearrange("p h (j d) -> p h j d", j=PAIRS2)
        dve.reciprocal(V.rsum, o[:, :, :, DH2]).then_inc(steps.sem, steps.one())
        dve.wait_ge(steps.sem, steps.value())
        dve.tensor_tensor(V.out[:, t].rearrange("p j h d -> p h j d"), o[:, :, :, 0:DH2],
                          V.rsum.unsqueeze(3).to_broadcast([P, 2, PAIRS2, DH2]), ALU.mult).then_inc(K.out_ready.sem, 1)

    x_statistics(nc, dve, K, p, 0)
    x_normed(nc, dve, K, p, 0)

    def body(s, b, last):
        shift(s, 0)
        if not last:
            x_statistics(nc, dve, K, p, s + 1)
        shift(s, 1)
        outputs(s, 0)
        if not last:
            x_normed(nc, dve, K, p, s + 1)
        shift(s, 2)
        outputs(s, 1)
        shift(s, 3)
        outputs(s, 2)
        outputs(s, 3)
        dve.wait_ge(K.proj_psum.sem, K.proj_psum.value(p, s, 1))
        add_residual(nc, dve, K, p, s, V.res,
                     piece_bank(K, FRONT2 + PAIRS2).rearrange("p (t d) -> p t d", t=UNIT), K.row["bo2"])
    over_units(dve, body)


def norm_pool(nc, pool, K, p):
    rstd_pool(nc, pool, K, p, 0, False)

    def body(s, b, last):
        if not last:
            rstd_pool(nc, pool, K, p, s + 1, False)
    over_units(pool, body)


S3_BANKS = ((0, 1), (2, 3))
PT3_BANK, O3_BANK = 4, 5
PIECE3 = (6, 7, 6, 7, 6, 7, 6, 7, 6, 7, 6)
OT3_BANK, Y3_BANK = 6, 7


def l3_tensor(nc, pe, K):
    p = A3
    V, W = K.v[p], K.wp[p]
    mm = nc.tensor.matmul

    def piece(s, b, i):
        bank = K.bank[PIECE3[i]]
        if i == 0:
            pe.wait_ge(K.c_ready.sem, K.c_ready.value(p, s, 1))
            if K.front_read.due(p, s, 0):
                pe.wait_ge(K.front_read.sem, K.front_read.value(p, s, 0))
            last = transpose4(nc, K, bank, lambda t: V.ctxn[:, t, :], DC)
        elif i == 1:
            pe.wait_ge(K.y_ready.sem, K.y_ready.value(p, s, 1))
            last = transpose4(nc, K, bank, lambda t: K.yt[:, t, :], P)
        elif i < 4:
            pe.wait_ge(K.front_read.sem, K.front_read.value(p, s, i - 1))
            for t in range(2):
                tt = 2 * (i - 2) + t
                last = mm(bank[:, t * 2 * D:(t + 1) * 2 * D], V.cT[b][:, tt * P:(tt + 1) * P], W["kv"][:, :],
                          start=True, stop=True)
        elif i < 8:
            t = i - 4
            pe.wait_ge(K.front_read.sem, K.front_read.value(p, s, i - 1))
            last = mm(bank[:, 0:3 * D], K.yT[b][:, t * P:(t + 1) * P], W["qkv"][:, :], start=True, stop=True)
        else:
            if i == 8:
                pe.wait_ge(K.qk_normed.sem, K.qk_normed.value(p, s, 1))
                pe.wait_ge(K.front_read.sem, K.front_read.value(p, s, 8))
            elif i == 9:
                if K.x_done.due(p, s, 0):
                    pe.wait_ge(K.x_done.sem, K.x_done.value(p, s, 0))
            else:
                pe.wait_ge(K.front_read.sem, K.front_read.value(p, s, 9))
            last = transpose4(nc, K, bank, lambda t: V.normed[:, i - 8, t, :], P)
        last.then_inc(K.front_psum.sem, 1)

    def scores(s, b, t):
        if t == 0:
            pe.wait_ge(K.front_read.sem, K.front_read.value(p, s, FRONT3))
        if K.shift_ready.due(p, s, t - 1):
            pe.wait_ge(K.shift_ready.sem, K.shift_ready.value(p, s, t - 1))
        for h in range(2):
            for y in range(2):
                rows, qs = whole_first(h + y == 0, y, t)
                last = mm(K.bank[S3_BANKS[t % 2][h]][rows, 0:KEYS3], V.q[b][half(h), qs],
                          V.k[b][half(h), t, y, :, :].rearrange("p c k -> p (c k)"), start=True, stop=True)
        last.then_inc(K.s_psum.sem, 1)

    def turned(s, t):
        pe.wait_ge(K.probs_ready.sem, K.probs_ready.value(p, s, t + 1))
        if K.pT_ready.due(p, s, t):
            pe.wait_ge(K.pT_ready.sem, K.pT_ready.value(p, s, t))
        for h in range(2):
            last = nc.tensor.transpose(K.bank[PT3_BANK][:, h * P:(h + 1) * P], V.probs[t % 2][:, h, :], K.ident[:, :])
        last.then_inc(K.pT_psum.sem, 1)

    def weighted(s, b, t):
        pe.wait_ge(K.pT_ready.sem, K.pT_ready.value(p, s, t + 1))
        if K.out_ready.due(p, s, t):
            pe.wait_ge(K.out_ready.sem, K.out_ready.value(p, s, t))
        if t == 0:
            pe.wait_ge(K.v_ready.sem, K.v_ready.value(p, s, 1))
        n = DH2 + 1
        for h in range(2):
            for y in range(2):
                last = mm(K.bank[O3_BANK][half(y), h * n:(h + 1) * n], V.pT[t % 2][:, h, half(y)],
                          V.vd[b][:, t, y, h, :], start=True, stop=True)
        last.then_inc(K.av_psum.sem, 1)

    def project(s, nxt):
        pe.wait_ge(K.out_ready.sem, K.out_ready.value(p, s, UNIT))
        if nxt is not None:
            pe.wait_ge(K.front_read.sem, K.front_read.value(p, nxt, 8))
        transpose4(nc, K, K.bank[OT3_BANK], lambda t: V.out[:, t].rearrange("p h d -> p (h d)"), P).then_inc(K.oT_psum.sem, 1)
        pe.wait_ge(K.oT_ready.sem, K.oT_ready.value(p, s, 1))
        for t in range(UNIT):
            last = mm(K.bank[Y3_BANK][:, t * P:(t + 1) * P], V.outT[:, t * P:(t + 1) * P], W["o"][:, :],
                      start=True, stop=True)
        last.then_inc(K.proj_psum.sem, 1)

    def pieces(s, b, lo, hi):
        for i in range(lo, hi):
            piece(s, b, i)

    pe.wait_ge(K.loaded[p], 16 * LOADS[p])
    raw = W["raw"]
    for n, i in enumerate((0, 1, 2, 3)):
        nc.tensor.transpose(K.bank[0][:, n * P:(n + 1) * P], raw[:, i, :], K.ident[:, :])
    for c in range(2):
        last = nc.tensor.transpose(K.bank[1][0:DC, c * P:(c + 1) * P], raw[:, 4 + c, 0:DC], K.ident[:, :])
    last.then_inc(K.l3w_psum, 1)
    pe.wait_ge(K.l3w_ready, 3)
    pieces(0, 0, 0, FRONT3)

    def body(s, b, last):
        scores(s, b, 0)
        scores(s, b, 1)
        turned(s, 0)
        scores(s, b, 2)
        weighted(s, b, 0)
        if not last:
            pieces(s + 1, 1 - b, 0, 2)
        turned(s, 1)
        scores(s, b, 3)
        weighted(s, b, 1)
        if not last:
            pieces(s + 1, 1 - b, 2, 8)
        turned(s, 2)
        weighted(s, b, 2)
        turned(s, 3)
        weighted(s, b, 3)
        project(s, None if last else s + 1)
        if not last:
            pieces(s + 1, 1 - b, 8, 11)
    over_units(pe, body)


def l3_scalar(nc, act, K):
    p = A3
    V, W = K.v[p], K.wp[p]

    def piece(s, b, i):
        act.wait_ge(K.front_psum.sem, K.front_psum.value(p, s, i + 1))
        bank = K.bank[PIECE3[i]]
        if i == 0:
            cT_evacuate(nc, act, K, p, s, b, bank)
            return
        if i == 1:
            yT_evacuate(nc, act, K, p, s, b, bank)
            return
        if i < 8:
            if K.squares.due(p, s, 0):
                act.wait_ge(K.squares.sem, K.squares.value(p, s, 0))
            if K.qk_normed.due(p, s, 0):
                act.wait_ge(K.qk_normed.sem, K.qk_normed.value(p, s, 0))
            if K.v_ready.due(p, s, 0):
                act.wait_ge(K.v_ready.sem, K.v_ready.value(p, s, 0))
        if i < 4:
            last = act.activation(V.raw[:, 2 * (i - 2):2 * (i - 1), 3:5, :].rearrange("p t c d -> p t (c d)"),
                                  bank.rearrange("p (t n) -> p t n", t=2), ACT.Copy)
        elif i < 8:
            last = act.activation(V.raw[:, i - 4, 0:3, :].rearrange("p c d -> p (c d)"), bank[:, 0:3 * D], ACT.Copy)
        elif i == 8:
            last = act.activation(V.q[b], bank, ACT.Copy, scale=K.col["qn_g"])
        else:
            last = act.activation(V.k[b][:, :, :, 10 - i, :] if i == 10 else V.k[b][:, :, :, 1, :],
                                  bank.rearrange("p (t y k) -> p t y k", t=UNIT, y=2), ACT.Copy, scale=K.col["kn_g"])
        last.then_inc(K.front_read.sem, 1)

    def probs(s, t):
        act.wait_ge(K.shift_ready.sem, K.shift_ready.value(p, s, t + 1))
        pr = V.probs[t % 2]
        act.activation(pr, pr, ACT.Exp, scale=DH2 ** -0.5).then_inc(K.probs_ready.sem, 1)

    def turned(s, t):
        act.wait_ge(K.pT_psum.sem, K.pT_psum.value(p, s, t + 1))
        if K.av_psum.due(p, s, t - 1):
            act.wait_ge(K.av_psum.sem, K.av_psum.value(p, s, t - 1))
        act.activation(V.pT[t % 2], K.bank[PT3_BANK][:, 0:2 * P].rearrange("p (h q) -> p h q", q=P),
                       ACT.Copy).then_inc(K.pT_ready.sem, 1)

    act.wait_ge(K.l3w_psum, 1)
    act.activation(W["qkv"][:, :], K.bank[0][:, 0:3 * P], ACT.Copy).then_inc(K.l3w_ready, 1)
    act.activation(W["o"][:, :], K.bank[0][:, 3 * P:4 * P], ACT.Copy).then_inc(K.l3w_ready, 1)
    act.activation(W["kv"][:, :], K.bank[1][0:DC, 0:2 * P], ACT.Copy).then_inc(K.l3w_ready, 1)
    for i in range(FRONT3):
        piece(0, 0, i)

    def body(s, b, last):
        def pieces(lo, hi):
            if not last:
                for i in range(lo, hi):
                    piece(s + 1, 1 - b, i)
        probs(s, 0)
        probs(s, 1)
        turned(s, 0)
        probs(s, 2)
        pieces(0, 2)
        turned(s, 1)
        probs(s, 3)
        pieces(2, 8)
        turned(s, 2)
        turned(s, 3)
        act.wait_ge(K.oT_psum.sem, K.oT_psum.value(p, s, 1))
        if K.proj_psum.due(p, s, 0):
            act.wait_ge(K.proj_psum.sem, K.proj_psum.value(p, s, 0))
        act.activation(V.outT, K.bank[OT3_BANK], ACT.Copy).then_inc(K.oT_ready.sem, 1)
        pieces(8, 11)
    over_units(act, body)


def l3_vector(nc, dve, K):
    p = A3
    V = K.v[p]

    def shift(s, b, t):
        steps = Steps(K.max_steps, p, s, 2 * t)
        dve.wait_ge(K.s_psum.sem, K.s_psum.value(p, s, t + 1))
        if K.pT_psum.due(p, s, t - 1):
            dve.wait_ge(K.pT_psum.sem, K.pT_psum.value(p, s, t - 1))
        if t == 0:
            dve.wait_ge(K.maskbias.sem, K.maskbias.value(p, s, 1))
        lo, hi = S3_BANKS[t % 2]
        pr, mx = V.probs[t % 2], V.max[:, t % 2, :]
        dve.tensor_tensor(pr, K.ps[:, lo:hi + 1, 0:KEYS3],
                          V.mb[b][:, t, :].unsqueeze(1).to_broadcast([P, 2, KEYS3]), ALU.add).then_inc(steps.sem, steps.one())
        dve.wait_ge(steps.sem, steps.value())
        dve.tensor_reduce(mx, pr, axis=AX.X, op=ALU.max).then_inc(steps.sem, steps.one())
        dve.wait_ge(steps.sem, steps.value())
        dve.tensor_tensor(pr, pr, mx.unsqueeze(2).to_broadcast([P, 2, KEYS3]), ALU.subtract).then_inc(K.shift_ready.sem, 1)

    def outputs(s, t):
        dve.wait_ge(K.av_psum.sem, K.av_psum.value(p, s, t + 1))
        if t == 0:
            if K.oT_psum.due(p, s, 0):
                dve.wait_ge(K.oT_psum.sem, K.oT_psum.value(p, s, 0))
        steps = Steps(K.sum_steps, p, s, t)
        o = K.bank[O3_BANK][:, 0:2 * (DH2 + 1)].rearrange("p (h d) -> p h d", h=2)
        dve.reciprocal(V.rsum, o[:, :, DH2]).then_inc(steps.sem, steps.one())
        dve.wait_ge(steps.sem, steps.value())
        dve.tensor_tensor(V.out[:, t], o[:, :, 0:DH2], V.rsum.unsqueeze(2).to_broadcast([P, 2, DH2]),
                          ALU.mult).then_inc(K.out_ready.sem, 1)

    def mask_bias(s, b):
        if K.shift_ready.due(p, s, -UNIT):
            dve.wait_ge(K.shift_ready.sem, K.shift_ready.value(p, s, -UNIT))
        dve.tensor_scalar(V.mb[b][:, :, 0:SEQ], K.mask[:, bass.ds(s * UNIT, UNIT), :], 1.0, MASKED,
                          ALU.subtract, ALU.mult).then_inc(K.maskbias.sem, 1)

    def square_sums(s, b):
        dve.wait_ge(K.squares.sem, K.squares.value(p, s, 1))
        dve.wait_ge(K.front_read.sem, K.front_read.value(p, s, 8))
        for src, slot in ((0, 4), (1, 2)):
            for y in range(2):
                last = dve.tensor_copy(V.vd[b][half(src), :, y, :, 0:DH2],
                                       V.raw[half(y), :, slot, :].rearrange("p t (h d) -> p t h d", h=2))
        last.then_inc(K.v_ready.sem, 1)
        steps = Steps(K.rms_steps, p, s)
        dve.tensor_reduce(V.ss, V.sq.rearrange("p t c (h d) -> p t c h d", h=2), axis=AX.X, op=ALU.add).then_inc(steps.sem, steps.one())
        dve.wait_ge(steps.sem, steps.value())
        dve.tensor_scalar(V.ss, V.ss, 1.0 / DH2, 1e-16, ALU.mult, ALU.max).then_inc(steps.sem, steps.one())
        steps.ended()

    def rms_normed(s):
        dve.wait_ge(K.rms_ready.sem, K.rms_ready.value(p, s, 1))
        if K.front_psum.due(p, s, 0):
            dve.wait_ge(K.front_psum.sem, K.front_psum.value(p, s, 0))
        for c, slot in enumerate((0, 1, 3)):
            last = dve.tensor_tensor(V.normed[:, c, :, :].rearrange("p t (h d) -> p t h d", h=2),
                                     V.raw[:, :, slot, :].rearrange("p t (h d) -> p t h d", h=2),
                                     V.rms[:, :, c, :].unsqueeze(3).to_broadcast([P, UNIT, 2, DH2]), ALU.mult)
        last.then_inc(K.qk_normed.sem, 1)

    x_statistics(nc, dve, K, p, 0)
    ctx_statistics(nc, dve, K, p, 0, 0)
    ctx_normed(nc, dve, K, p, 0, 0)
    x_normed(nc, dve, K, p, 0)
    mask_bias(0, 0)
    square_sums(0, 0)
    rms_normed(0)

    def body(s, b, last):
        shift(s, b, 0)
        if not last:
            ctx_statistics(nc, dve, K, p, s + 1, 1 - b)
            x_statistics(nc, dve, K, p, s + 1)
        shift(s, b, 1)
        if not last:
            ctx_normed(nc, dve, K, p, s + 1, 1 - b)
            x_normed(nc, dve, K, p, s + 1)
        shift(s, b, 2)
        outputs(s, 0)
        shift(s, b, 3)
        if not last:
            mask_bias(s + 1, 1 - b)
        outputs(s, 1)
        outputs(s, 2)
        outputs(s, 3)
        if not last:
            square_sums(s + 1, 1 - b)
        dve.wait_ge(K.proj_psum.sem, K.proj_psum.value(p, s, 1))
        add_residual(nc, dve, K, p, s, V.res, K.bank[Y3_BANK].rearrange("p (t d) -> p t d", t=UNIT), K.row["bo3"])
        if not last:
            rms_normed(s + 1)
    over_units(dve, body)


def l3_pool(nc, pool, K):
    p = A3
    V = K.v[p]

    def front(s):
        rstd_pool(nc, pool, K, p, s, True)
        rstd_pool(nc, pool, K, p, s, False)

    def squares(s):
        pool.wait_ge(K.front_read.sem, K.front_read.value(p, s, 8))
        if K.rms_steps.due(p, s, 0):
            pool.wait_ge(K.rms_steps.sem, K.rms_steps.value(p, s, 0))
        pool.tensor_tensor(V.sq[:, :, 0:2, :], V.raw[:, :, 0:2, :], V.raw[:, :, 0:2, :], ALU.mult)
        pool.tensor_tensor(V.sq[:, :, 2, :], V.raw[:, :, 3, :], V.raw[:, :, 3, :], ALU.mult).then_inc(K.squares.sem, 1)
        pool.wait_ge(K.rms_steps.sem, K.rms_steps.value(p, s, 2))
        pool.tensor_tensor(V.rms.rearrange("p t c h -> p (t c h)"), V.ss.rearrange("p t c h -> p (t c h)"),
                           K.minus_half[:, 0:UNIT * 6], ALU.pow).then_inc(K.rms_ready.sem, 1)

    front(0)
    squares(0)

    def body(s, b, last):
        if not last:
            front(s + 1)
            squares(s + 1)
    over_units(pool, body)


G_BANKS, U_BANKS, C_BANKS, D_BANK, R_BANK = (0, 1), (2, 3), (4, 7), 5, 6
AT = {F0: (3, 5, 9), F1: (3, 5, 9), F2: (2, 4, 6)}


def expert_of(p, r):
    return r // 2 if p == F1 else r


def front_tensor(nc, pe, K, p, s, b, part, bank):
    if part == 0:
        pe.wait_ge(K.y_ready.sem, K.y_ready.value(p, s, 1))
        if K.x_done.due(p, s, -1):
            pe.wait_ge(K.x_done.sem, K.x_done.value(p, s, -1))
        transpose4(nc, K, bank, lambda t: K.yt[:, t, :], P).then_inc(K.yT_psum.sem, 1)
    elif part == 1:
        pe.wait_ge(K.yT_ready.sem, K.yT_ready.value(p, s, 1))
        E = EXPERTS[p]
        for t in range(UNIT):
            last = nc.tensor.matmul(bank[:, t * E:(t + 1) * E], K.yT[b][:, t * P:(t + 1) * P], K.rcol[p], start=True, stop=True)
        last.then_inc(K.logits_psum.sem, 1)
    else:
        E = 32 if p == F0 else 8
        pe.wait_ge(K.route_steps.sem, K.route_steps.value(p, s, K.route_steps.counts[p]))
        cw = route_views(K, p).cw
        transpose4(nc, K, bank, lambda t: cw[:, t, :], E).then_inc(K.cw_psum.sem, 1)


def back_tensor(nc, pe, K, p, s, nxt, bank):
    pe.wait_ge(K.dt_ready.sem, K.dt_ready.value(p, s, 1))
    if nxt is not None:
        pe.wait_ge(K.cwT_ready.sem, K.cwT_ready.value(p, nxt, 1))
    transpose4(nc, K, bank, lambda t: K.v[p].dt[:, t * P:(t + 1) * P], P).then_inc(K.outT_psum.sem, 1)


def experts_tensor(nc, pe, K, p):
    V, W = K.v[p], K.wf[p]
    J, SH = CHUNKS[p], SHARED[p]
    mm, bank = nc.tensor.matmul, K.bank

    def combine(s, b, r):
        if r == 0:
            pe.wait_ge(K.cwT_ready.sem, K.cwT_ready.value(p, s, 1))
        if p == F2:
            if K.scaled_ready.due(p, s, r - 1):
                pe.wait_ge(K.scaled_ready.sem, K.scaled_ready.value(p, s, r - 1))
        else:
            if K.hid_ready.due(p, s, r + SH - 1):
                pe.wait_ge(K.hid_ready.sem, K.hid_ready.value(p, s, r + SH - 1))
        mm(bank[C_BANKS[r % 2]], K.sel[:, expert_of(p, r), :], K.cwT[:, b, :], start=True, stop=True).then_inc(K.c_psum.sem, 1)

    def body(s, b, last):
        pe.wait_ge(K.yT_ready.sem, K.yT_ready.value(p, s, 1))
        for j in range(J + 1):
            if j < J:
                if p == F2 and j + 1 - SH >= 0 and j + 1 < J:
                    combine(s, b, j + 1 - SH)
                rhs = K.yT[b][:, :]
                if p == F2 and j >= SH:
                    pe.wait_ge(K.scaled_ready.sem, K.scaled_ready.value(p, s, j - SH + 1))
                    rhs = V.scaled[(j - SH) % 2]
                if K.silu_ready.due(p, s, j - 1):
                    pe.wait_ge(K.silu_ready.sem, K.silu_ready.value(p, s, j - 1))
                mm(bank[G_BANKS[j % 2]], W[:, 0, j, :], rhs, start=True, stop=True).then_inc(K.g_psum.sem, 1)
                if K.hid_ready.due(p, s, j - 1):
                    pe.wait_ge(K.hid_ready.sem, K.hid_ready.value(p, s, j - 1))
                mm(bank[U_BANKS[j % 2]], W[:, 1, j, :], rhs, start=True, stop=True).then_inc(K.u_psum.sem, 1)
                if p != F2 and j >= SH:
                    combine(s, b, j - SH)
            if j >= 1:
                if j == 1:
                    if K.dt_ready.due(p, s, 0):
                        pe.wait_ge(K.dt_ready.sem, K.dt_ready.value(p, s, 0))
                pe.wait_ge(K.hid_ready.sem, K.hid_ready.value(p, s, j))
                mm(bank[D_BANK], W[:, 2, j - 1, :], V.hid[(j - 1) % 2], start=j == 1, stop=j == J).then_inc(K.down_done.sem, 1)
            if not last and j in AT[p]:
                front_tensor(nc, pe, K, p, s + 1, 1 - b, AT[p].index(j), bank[R_BANK])
        back_tensor(nc, pe, K, p, s, None if last else s + 1, bank[R_BANK])

    pe.wait_ge(K.loaded[p], 16 * LOADS[p])
    if p == F0:
        raw = K.wf[F1]
        for n, (i0, m) in enumerate(PREP_GROUPS):
            if n >= 2:
                pe.wait_ge(K.prep_ready, n - 1)
            for i in range(m):
                last = nc.tensor.transpose(bank[n % 2][:, i * P:(i + 1) * P], raw[:, (i0 + i) // 17, (i0 + i) % 17, :],
                                           K.ident[:, :])
            last.then_inc(K.prep_psum, 1)
        pe.wait_ge(K.prep_ready, PREP_F0)
    for part in range(3):
        front_tensor(nc, pe, K, p, 0, 0, part, bank[R_BANK])
    over_units(pe, body)


def experts_scalar(nc, act, K, p):
    V = K.v[p]
    J = CHUNKS[p]

    def body(s, b, last):
        for j in range(J):
            act.wait_ge(K.g_psum.sem, K.g_psum.value(p, s, j + 1))
            if K.hid_ready.due(p, s, j - 1):
                act.wait_ge(K.hid_ready.sem, K.hid_ready.value(p, s, j - 1))
            act.activation(V.silu[j % 2], K.bank[G_BANKS[j % 2]], ACT.Silu).then_inc(K.silu_ready.sem, 1)
            if not last and j in AT[p]:
                front_scalar(nc, act, K, p, s + 1, 1 - b, AT[p].index(j), K.bank[R_BANK])
        scale_outputs(nc, act, K, p, s, K.bank[D_BANK])

    if p == F0:
        for n, (i0, m) in enumerate(PREP_GROUPS):
            act.wait_ge(K.prep_psum, n + 1)
            act.activation(K.wf[F0].rearrange("p w j n -> p (w j) n")[:, i0:i0 + m, :],
                           K.bank[n % 2][:, 0:m * P].rearrange("p (w n) -> p w n", n=P), ACT.Copy).then_inc(K.prep_ready, 1)
    for part in range(3):
        front_scalar(nc, act, K, p, 0, 0, part, K.bank[R_BANK])
    over_units(act, body)


def scale_outputs(nc, act, K, p, s, bank):
    act.wait_ge(K.down_done.sem, K.down_done.value(p, s, K.down_done.counts[p]))
    if K.outT_psum.due(p, s, 0):
        act.wait_ge(K.outT_psum.sem, K.outT_psum.value(p, s, 0))
    scale = 1.0 if p == F3 else K.gates[:, 4 + p // 2:5 + p // 2]
    act.activation(K.v[p].dt, bank, ACT.Copy, scale=scale).then_inc(K.dt_ready.sem, 1)


def front_scalar(nc, act, K, p, s, b, part, bank):
    R = route_views(K, p)
    if part == 0:
        yT_evacuate(nc, act, K, p, s, b, bank)
    elif part == 1 and p == F0:
        act.wait_ge(K.logits_psum.sem, K.logits_psum.value(p, s, 1))
        if K.route_steps.due(p, s, 0):
            act.wait_ge(K.route_steps.sem, K.route_steps.value(p, s, 0))
        act.activation(R.score, bank[:, 0:UNIT * 32].rearrange("p (t e) -> p t e", t=UNIT), ACT.Tanh,
                       scale=0.5).then_inc(K.logits_ready.sem, 1)
    elif part == 1:
        act.wait_ge(K.route_steps.sem, K.route_steps.value(p, s, R1_STEPS[p]))
        act.activation(R.e, R.d, ACT.Exp).then_inc(K.exp_ready.sem, 1)


R1_STEPS = {F1: 7, F2: 3, F3: 4}


def route_views(K, p):
    R = Kernel()
    E = 32 if p == F0 else 8
    R.E, at = E, 0
    tile = K.route

    def take(*shape):
        nonlocal at
        n = 1
        for x in shape:
            n *= x
        v = tile[:, at:at + n]
        at += n
        assert at <= 2048
        if len(shape) > 1:
            v = v.rearrange("p (a b) -> p a b", a=shape[0])
        return v

    R.count = [take(UNIT, PAD + 32) for _ in range(3)]
    R.score, R.biased, R.masked = take(UNIT, E), take(UNIT, E), take(UNIT, E)
    R.best, R.tmp, R.d, R.e, R.sel, R.cw = (take(UNIT, n) for n in (8, E, E, E, E, E))
    R.group, R.gsel = take(UNIT, 8), take(UNIT, 8)
    R.n, R.sum, R.inv = take(UNIT, 1), take(UNIT, 1), take(UNIT, 1)
    R.touch = take(UNIT, 1)
    return R


def select_top(nc, dve, R, steps, out, values, threshold, E, k):
    eq = R.count[0]
    thr = threshold.to_broadcast([P, UNIT, E])
    tmp = R.tmp[:, :, 0:E]
    dve.tensor_tensor(out, values, thr, ALU.is_gt).then_inc(steps.sem, steps.one())
    dve.tensor_tensor(eq[:, :, PAD:PAD + E], values, thr, ALU.is_equal).then_inc(steps.sem, steps.one())
    dve.wait_ge(steps.sem, steps.value())
    dve.tensor_reduce(R.n, out, axis=AX.X, op=ALU.add).then_inc(steps.sem, steps.one())
    src, at, sh = eq, 1, 1
    while sh < E:
        dst = R.count[at]
        dve.tensor_tensor(dst[:, :, PAD:PAD + E], src[:, :, PAD:PAD + E], src[:, :, PAD - sh:PAD - sh + E],
                          ALU.add).then_inc(steps.sem, steps.one())
        dve.wait_ge(steps.sem, steps.value())
        src, at, sh = dst, 3 - at, 2 * sh
    dve.tensor_tensor(tmp, src[:, :, PAD:PAD + E], R.n.to_broadcast([P, UNIT, E]), ALU.add).then_inc(steps.sem, steps.one())
    dve.wait_ge(steps.sem, steps.value())
    dve.scalar_tensor_tensor(out=tmp, in0=tmp, scalar=float(k), in1=eq[:, :, PAD:PAD + E], op0=ALU.is_le,
                             op1=ALU.mult).then_inc(steps.sem, steps.one())
    dve.wait_ge(steps.sem, steps.value())
    dve.tensor_tensor(out, out, tmp, ALU.add).then_inc(steps.sem, steps.one())
    dve.wait_ge(steps.sem, steps.value())


def best8(nc, dve, R, steps, values):
    dve.wait_ge(steps.sem, steps.value())
    dve.tensor_copy(R.touch, values[:, :, 0:1]).then_inc(steps.sem, steps.one())
    for t in range(UNIT):
        dve.max(R.best[:, t, :], values[:, t, :]).then_inc(steps.sem, steps.one())
    dve.wait_ge(steps.sem, steps.value())


def route_first(nc, dve, K, p, s, bank):
    R = route_views(K, p)
    steps = Steps(K.route_steps, p, s)
    if p == F0:
        return steps
    dve.wait_ge(K.logits_psum.sem, K.logits_psum.value(p, s, 1))
    n = EXPERTS[p]
    lg = bank[:, 0:UNIT * n].rearrange("p (t e) -> p t e", t=UNIT)
    if p == F1:
        dve.tensor_tensor(R.score, lg, K.ebias1.unsqueeze(1).to_broadcast([P, UNIT, 8]), ALU.add).then_inc(steps.sem, steps.one())
        best8(nc, dve, R, steps, R.score)
        dve.tensor_tensor(R.d, R.score, R.best[:, :, 0:1].to_broadcast([P, UNIT, 8]), ALU.subtract).then_inc(steps.sem, steps.one())
    elif p == F2:
        dve.tensor_copy(R.score, lg).then_inc(steps.sem, steps.one())
        dve.wait_ge(steps.sem, steps.value())
        dve.tensor_reduce(R.sum, R.score, axis=AX.X, op=ALU.max).then_inc(steps.sem, steps.one())
        dve.wait_ge(steps.sem, steps.value())
        dve.tensor_tensor(R.d, R.score, R.sum.to_broadcast([P, UNIT, 8]), ALU.subtract).then_inc(steps.sem, steps.one())
    else:
        dve.wait_ge(K.r2_ready.sem, K.r2_ready.value(p, s, 1))
        r2 = K.lnw[:, 2, :].unsqueeze(2)
        dve.tensor_tensor(R.tmp[:, :, 0:4], lg, r2.to_broadcast([P, UNIT, 4]), ALU.mult).then_inc(steps.sem, steps.one())
        dve.wait_ge(steps.sem, steps.value())
        dve.tensor_tensor(R.score[:, :, 0:4], R.tmp[:, :, 0:4], K.logit_bias3.unsqueeze(1).to_broadcast([P, UNIT, 4]),
                          ALU.add).then_inc(steps.sem, steps.one())
        dve.wait_ge(steps.sem, steps.value())
        dve.tensor_reduce(R.sum, R.score, axis=AX.X, op=ALU.max).then_inc(steps.sem, steps.one())
        dve.wait_ge(steps.sem, steps.value())
        dve.tensor_tensor(R.d, R.score, R.sum.to_broadcast([P, UNIT, 8]), ALU.subtract).then_inc(steps.sem, steps.one())
    assert steps.n == R1_STEPS[p]
    return steps


def route_second(nc, dve, K, p, s, steps):
    R = route_views(K, p)
    E, k = R.E, TOP[p]

    def over_sum(out, values, extra, scale):
        dve.tensor_reduce(R.sum, values, axis=AX.X, op=ALU.add).then_inc(steps.sem, steps.one())
        dve.wait_ge(steps.sem, steps.value())
        dve.tensor_scalar(R.sum, R.sum, extra, None, ALU.add).then_inc(steps.sem, steps.one())
        dve.wait_ge(steps.sem, steps.value())
        dve.reciprocal(R.inv, R.sum).then_inc(steps.sem, steps.one())
        dve.wait_ge(steps.sem, steps.value())
        dve.scalar_tensor_tensor(out=out, in0=values, scalar=scale, in1=R.inv.to_broadcast([P, UNIT, E]),
                                 op0=ALU.mult, op1=ALU.mult).then_inc(steps.sem, steps.one())

    if p == F0:
        dve.wait_ge(K.logits_ready.sem, K.logits_ready.value(p, s, 1))
        dve.tensor_scalar(R.score, R.score, 0.5, 0.5, ALU.mult, ALU.add).then_inc(steps.sem, steps.one())
        dve.wait_ge(steps.sem, steps.value())
        dve.tensor_tensor(R.biased, R.score, K.ebias0.unsqueeze(1).to_broadcast([P, UNIT, 32]), ALU.add).then_inc(steps.sem, steps.one())
        dve.wait_ge(steps.sem, steps.value())
        grouped = R.biased.rearrange("p t (g e) -> p (t g) e", e=4)
        dve.tensor_reduce(R.group.rearrange("p t g -> p (t g)"), grouped, axis=AX.X, op=ALU.max).then_inc(steps.sem, steps.one())
        best8(nc, dve, R, steps, R.group)
        select_top(nc, dve, R, steps, R.gsel, R.group, R.best[:, :, 3:4], 8, 4)
        dve.tensor_tensor(R.masked.rearrange("p t (g e) -> p (t g) e", e=4), grouped,
                          R.gsel.rearrange("p t g -> p (t g)").unsqueeze(2).to_broadcast([P, UNIT * 8, 4]),
                          ALU.mult).then_inc(steps.sem, steps.one())
        best8(nc, dve, R, steps, R.masked)
        select_top(nc, dve, R, steps, R.sel, R.masked, R.best[:, :, k - 1:k], 32, k)
        dve.tensor_tensor(R.d, R.score, R.sel, ALU.mult).then_inc(steps.sem, steps.one())
        dve.wait_ge(steps.sem, steps.value())
        if K.cw_psum.due(p, s, 0):
            dve.wait_ge(K.cw_psum.sem, K.cw_psum.value(p, s, 0))
        over_sum(R.cw, R.d, 1e-20, 2.5)
    elif p == F1:
        select_top(nc, dve, R, steps, R.sel, R.score, R.best[:, :, k - 1:k], 8, k)
        dve.wait_ge(K.exp_ready.sem, K.exp_ready.value(p, s, 1))
        dve.tensor_tensor(R.tmp, R.e, R.sel, ALU.mult).then_inc(steps.sem, steps.one())
        dve.wait_ge(steps.sem, steps.value())
        if K.cw_psum.due(p, s, 0):
            dve.wait_ge(K.cw_psum.sem, K.cw_psum.value(p, s, 0))
        over_sum(R.cw, R.tmp, 0.0, 1.0)
    else:
        dve.wait_ge(K.exp_ready.sem, K.exp_ready.value(p, s, 1))
        over_sum(R.masked, R.e, 0.0, 1.0)
        best8(nc, dve, R, steps, R.masked)
        select_top(nc, dve, R, steps, R.sel, R.masked, R.best[:, :, k - 1:k], 8, k)
        if K.cw_psum.due(p, s, 0):
            dve.wait_ge(K.cw_psum.sem, K.cw_psum.value(p, s, 0))
        if p == F2:
            dve.tensor_tensor(R.cw, R.masked, R.sel, ALU.mult).then_inc(steps.sem, steps.one())
        else:
            dve.tensor_tensor(R.biased, R.masked, R.sel, ALU.mult).then_inc(steps.sem, steps.one())
            dve.wait_ge(steps.sem, steps.value())
            over_sum(R.cw, R.biased, 1e-8, 1.0)
    steps.ended()


def split_combine(nc, dve, K, p, s, b, bank):
    E = 32 if p == F0 else 8
    dve.wait_ge(K.cw_psum.sem, K.cw_psum.value(p, s, 1))
    if K.c_psum.due(p, s, -K.c_psum.counts[p]):
        dve.wait_ge(K.c_psum.sem, K.c_psum.value(p, s, -K.c_psum.counts[p]))
    dve.tensor_copy(K.cwT[0:E, b, :], bank[0:E, :]).then_inc(K.cw_steps.sem, 1)
    dve.wait_ge(K.cw_steps.sem, K.cw_steps.value(p, s, 1))
    dve.tensor_tensor(K.cwT[32:32 + E, b, :], bank[0:E, :], K.cwT[0:E, b, :].bitcast(F32),
                      ALU.subtract).then_inc(K.cwT_ready.sem, 1)


def experts_vector(nc, dve, K, p):
    V = K.v[p]
    J, SH = CHUNKS[p], SHARED[p]
    r_bank = K.bank[R_BANK]

    def scaled(s, b, r):
        dve.wait_ge(K.c_psum.sem, K.c_psum.value(p, s, r + 1))
        if r == 0:
            dve.wait_ge(K.yT_ready.sem, K.yT_ready.value(p, s, 1))
        if K.u_psum.due(p, s, r + SH - 1):
            dve.wait_ge(K.u_psum.sem, K.u_psum.value(p, s, r + SH - 1))
        dve.tensor_tensor(V.scaled[r % 2], K.yT[b][:, :], K.bank[C_BANKS[r % 2]], ALU.mult).then_inc(K.scaled_ready.sem, 1)

    def body(s, b, last):
        for j in range(J):
            if p == F2 and j + 1 < J:
                scaled(s, b, j + 1 - SH)
            dve.wait_ge(K.silu_ready.sem, K.silu_ready.value(p, s, j + 1))
            dve.wait_ge(K.u_psum.sem, K.u_psum.value(p, s, j + 1))
            if K.down_done.due(p, s, j - 1):
                dve.wait_ge(K.down_done.sem, K.down_done.value(p, s, j - 1))
            u = K.bank[U_BANKS[j % 2]]
            if p == F2 or j < SH:
                dve.tensor_tensor(V.hid[j % 2], V.silu[j % 2], u, ALU.mult).then_inc(K.hid_ready.sem, 1)
            else:
                r = j - SH
                dve.tensor_tensor(V.prod[j % 2], V.silu[j % 2], u, ALU.mult).then_inc(K.prod_steps.sem, 1)
                dve.wait_ge(K.c_psum.sem, K.c_psum.value(p, s, r + 1))
                dve.wait_ge(K.prod_steps.sem, K.prod_steps.value(p, s, r + 1))
                dve.tensor_tensor(V.hid[j % 2], V.prod[j % 2], K.bank[C_BANKS[r % 2]], ALU.mult).then_inc(K.hid_ready.sem, 1)
            if last:
                continue
            if j == 0:
                x_statistics(nc, dve, K, p, s + 1)
            if j == 1:
                x_normed(nc, dve, K, p, s + 1)
            if j == AT[p][1]:
                steps = route_first(nc, dve, K, p, s + 1, r_bank)
            if j == AT[p][1] + 1:
                route_second(nc, dve, K, p, s + 1, steps)
            if j == AT[p][2]:
                split_combine(nc, dve, K, p, s + 1, 1 - b, r_bank)
        dve.wait_ge(K.outT_psum.sem, K.outT_psum.value(p, s, 1))
        dve.tensor_tensor(xu(K, s), r_bank.rearrange("p (t d) -> p t d", t=UNIT), xu(K, s), ALU.add).then_inc(K.x_done.sem, 1)

    x_statistics(nc, dve, K, p, 0)
    x_normed(nc, dve, K, p, 0)
    steps = route_first(nc, dve, K, p, 0, r_bank)
    route_second(nc, dve, K, p, 0, steps)
    split_combine(nc, dve, K, p, 0, 0, r_bank)
    over_units(dve, body)


H3_BANKS, SS_BANK, C3_BANK, D3_BANK, R3_BANK = (0, 1, 2, 3), 4, 5, 6, 7
E3 = EXPERTS[F3]


def l3_experts_tensor(nc, pe, K):
    p = F3
    V = K.v[p]
    mm, bank = nc.tensor.matmul, K.bank

    def body(s, b, last):
        pe.wait_ge(K.yT_ready.sem, K.yT_ready.value(p, s, 1))
        for i in range(E3 + 2):
            if i < E3:
                for c in range(2):
                    q = 2 * i + c
                    if K.z_ready.due(p, s, q - 3):
                        pe.wait_ge(K.z_ready.sem, K.z_ready.value(p, s, q - 3))
                    mm(bank[H3_BANKS[q % 4]], K.w1[:, i, c * P:(c + 1) * P], K.yT[b][:, :],
                       start=True, stop=True).then_inc(K.g_psum.sem, 1)
            if not last and i in (0, 2, 3):
                front_tensor(nc, pe, K, p, s + 1, 1 - b, (0, 2, 3).index(i), bank[R3_BANK])
            if 1 <= i <= E3:
                e = i - 1
                pe.wait_ge(K.sq_ready.sem, K.sq_ready.value(p, s, 2 * e + 2))
                if K.sd_ready.due(p, s, e):
                    pe.wait_ge(K.sd_ready.sem, K.sd_ready.value(p, s, e))
                for c in range(2):
                    ss = mm(bank[SS_BANK], K.ones[:, :], V.sq[(2 * e + c) % 4], start=c == 0, stop=c == 1)
                ss.then_inc(K.ss_psum.sem, 1)
                if e == 0:
                    pe.wait_ge(K.cwT_ready.sem, K.cwT_ready.value(p, s, 1))
                if K.hid_ready.due(p, s, 2 * e):
                    pe.wait_ge(K.hid_ready.sem, K.hid_ready.value(p, s, 2 * e))
                mm(bank[C3_BANK], K.sel[:, e, :], K.cwT[:, b, :], start=True, stop=True).then_inc(K.c_psum.sem, 1)
            if i >= 2:
                e = i - 2
                if e == 0:
                    if K.dt_ready.due(p, s, 0):
                        pe.wait_ge(K.dt_ready.sem, K.dt_ready.value(p, s, 0))
                for c in range(2):
                    q = 2 * e + c
                    pe.wait_ge(K.hid_ready.sem, K.hid_ready.value(p, s, q + 1))
                    mm(bank[D3_BANK], K.w2[:, q, :], V.hid[q % 4], start=q == 0, stop=q == 7).then_inc(K.down_done.sem, 1)
        back_tensor(nc, pe, K, p, s, None if last else s + 1, bank[R3_BANK])

    pe.wait_ge(K.w3_steps, 4 + 1)
    mm(bank[R3_BANK][:, 0:4], V.selraw_b, K.rcol[F3], start=True, stop=True).then_inc(K.bias3_psum, 1)
    pe.wait_ge(K.w3_steps, 4 + 1 + 2)
    for part in range(3):
        front_tensor(nc, pe, K, p, 0, 0, part, bank[R3_BANK])
    over_units(pe, body)


def l3_experts_scalar(nc, act, K):
    p = F3
    V = K.v[p]
    r_bank = K.bank[R3_BANK]

    def body(s, b, last):
        for i in range(E3 + 2):
            if i < E3:
                for c in range(2):
                    q = 2 * i + c
                    act.wait_ge(K.g_psum.sem, K.g_psum.value(p, s, q + 1))
                    if K.ss_psum.due(p, s, i - 1):
                        act.wait_ge(K.ss_psum.sem, K.ss_psum.value(p, s, i - 1))
                    act.activation(V.sq[q % 4], K.bank[H3_BANKS[q % 4]], ACT.Square).then_inc(K.sq_ready.sem, 1)
            if not last and i in (0, 2):
                front_scalar(nc, act, K, p, s + 1, 1 - b, (0, 2).index(i), r_bank)
            if 1 <= i <= E3:
                e = i - 1
                act.wait_ge(K.ss_psum.sem, K.ss_psum.value(p, s, e + 1))
                if K.rinv_ready.due(p, s, e - 1):
                    act.wait_ge(K.rinv_ready.sem, K.rinv_ready.value(p, s, e - 1))
                act.activation(V.sd[e % 2], K.bank[SS_BANK], ACT.Sqrt, scale=1.0 / HID3, bias=K.eps_col).then_inc(K.sd_ready.sem, 1)
            if i >= 2:
                for c in range(2):
                    q = 2 * (i - 2) + c
                    act.wait_ge(K.z_ready.sem, K.z_ready.value(p, s, q + 1))
                    if K.hid_ready.due(p, s, q - 3):
                        act.wait_ge(K.hid_ready.sem, K.hid_ready.value(p, s, q - 3))
                    act.activation(V.relu[q % 4], V.z[q % 4], ACT.Relu, scale=K.ln3_g[:, q:q + 1],
                                   bias=K.ln3_b[:, q:q + 1]).then_inc(K.relu_ready.sem, 1)
        scale_outputs(nc, act, K, p, s, K.bank[D3_BANK])

    for part in range(3):
        front_scalar(nc, act, K, p, 0, 0, part, r_bank)
    over_units(act, body)


def l3_experts_vector(nc, dve, K):
    p = F3
    V = K.v[p]
    r_bank = K.bank[R3_BANK]

    def second_norm(s):
        w = K.lnw
        steps = Steps(K.r2_steps, p, s)
        dve.wait_ge(K.rstd_ready.sem, K.rstd_ready.value(p, s, 1))
        dve.tensor_tensor(w[:, 3, :], w[:, 0, :], w[:, 0, :], ALU.mult).then_inc(steps.sem, steps.one())
        dve.wait_ge(steps.sem, steps.value())
        dve.tensor_tensor(w[:, 3, :], w[:, 3, :], w[:, 5, :], ALU.mult).then_inc(steps.sem, steps.one())
        dve.wait_ge(steps.sem, steps.value())
        dve.tensor_scalar(w[:, 3, :], w[:, 3, :], EPS, None, ALU.add).then_inc(steps.sem, steps.one())

    def normed(s):
        second_norm(s)
        x_normed(nc, dve, K, p, s)

    def back(s):
        steps = Steps(K.res_steps, p, s)
        dve.wait_ge(K.outT_psum.sem, K.outT_psum.value(p, s, 1))
        out = r_bank.rearrange("p (t d) -> p t d", t=UNIT)
        ln_statistics(nc, dve, K, p, s, steps, K.cstats, K.clnw, lambda t: out[:, t, :], D, False)
        steps.ended()
        dve.wait_ge(K.ostat_ready.sem, K.ostat_ready.value(p, s, 1))
        if K.scale_steps.due(p, s, 0):
            dve.wait_ge(K.scale_steps.sem, K.scale_steps.value(p, s, 0))
        ln_apply(nc, dve, V.onorm, lambda t: out[:, t, :], K.clnw, K.onorm_ready)
        dve.wait_ge(K.scale_steps.sem, K.scale_steps.value(p, s, 2))
        dve.tensor_tensor(xu(K, s), V.gated, xu(K, s), ALU.add).then_inc(K.x_done.sem, 1)

    def body(s, b, last):
        for i in range(E3 + 1):
            if i < E3:
                dve.wait_ge(K.sd_ready.sem, K.sd_ready.value(p, s, i + 1))
                if K.z_ready.due(p, s, 2 * (i - 1)):
                    dve.wait_ge(K.z_ready.sem, K.z_ready.value(p, s, 2 * (i - 1)))
                dve.reciprocal(V.rinv[i % 2], V.sd[i % 2]).then_inc(K.rinv_ready.sem, 1)
                dve.wait_ge(K.rinv_ready.sem, K.rinv_ready.value(p, s, i + 1))
                for c in range(2):
                    q = 2 * i + c
                    if K.relu_ready.due(p, s, q - 3):
                        dve.wait_ge(K.relu_ready.sem, K.relu_ready.value(p, s, q - 3))
                    dve.tensor_tensor(V.z[q % 4], K.bank[H3_BANKS[q % 4]], V.rinv[i % 2], ALU.mult).then_inc(K.z_ready.sem, 1)
            if i >= 1:
                for c in range(2):
                    q = 2 * (i - 1) + c
                    dve.wait_ge(K.relu_ready.sem, K.relu_ready.value(p, s, q + 1))
                    dve.wait_ge(K.c_psum.sem, K.c_psum.value(p, s, i))
                    if K.down_done.due(p, s, q - 3):
                        dve.wait_ge(K.down_done.sem, K.down_done.value(p, s, q - 3))
                    dve.tensor_tensor(V.hid[q % 4], V.relu[q % 4], K.bank[C3_BANK], ALU.mult).then_inc(K.hid_ready.sem, 1)
            if last:
                continue
            if i == 0:
                steps = route_first(nc, dve, K, p, s + 1, r_bank)
            if i == 1:
                route_second(nc, dve, K, p, s + 1, steps)
            if i == 2:
                split_combine(nc, dve, K, p, s + 1, 1 - b, r_bank)
        back(s)

    dve.wait_ge(K.loaded[p], 16 * LOADS[p])
    w1 = K.w1
    dve.tensor_reduce(V.wmean, w1, axis=AX.X, op=ALU.add).then_inc(K.w3_steps, 1)
    dve.wait_ge(K.w3_steps, 1)
    dve.tensor_scalar(V.wmean, V.wmean, 1.0 / HID3, None, ALU.mult).then_inc(K.w3_steps, 1)
    dve.wait_ge(K.w3_steps, 2)
    dve.tensor_tensor(w1, w1, V.wmean.unsqueeze(2).to_broadcast([P, E3, HID3]), ALU.subtract).then_inc(K.w3_steps, 1)
    dve.tensor_copy(V.selraw_b, K.col["rn_b"].to_broadcast([P, P])).then_inc(K.w3_steps, 1)
    dve.tensor_scalar(K.rows[:, 4 * D:6 * D], K.rows[:, 4 * D:6 * D], K.gates[:, 7:8], None, ALU.mult).then_inc(K.w3_steps, 1)
    dve.wait_ge(K.bias3_psum, 1)
    dve.tensor_copy(K.logit_bias3, r_bank[:, 0:4]).then_inc(K.w3_steps, 1)
    dve.tensor_scalar(K.rcol[F3], K.rcol[F3], K.col["rn_g"], None, ALU.mult).then_inc(K.w3_steps, 1)
    dve.wait_ge(K.w3_steps, 7)
    x_statistics(nc, dve, K, p, 0)
    normed(0)
    steps = route_first(nc, dve, K, p, 0, r_bank)
    route_second(nc, dve, K, p, 0, steps)
    split_combine(nc, dve, K, p, 0, 0, r_bank)

    def with_front(s, b, last):
        if not last:
            x_statistics(nc, dve, K, p, s + 1)
            normed(s + 1)
        body(s, b, last)
    over_units(dve, with_front)


def l3_experts_pool(nc, pool, K):
    p = F3
    V = K.v[p]

    def front(s):
        rstd_pool(nc, pool, K, p, s, False)
        pool.wait_ge(K.r2_steps.sem, K.r2_steps.value(p, s, 3))
        pool.tensor_tensor(K.lnw[:, 2, :], K.lnw[:, 3, :], K.minus_half[:, 0:UNIT], ALU.pow).then_inc(K.r2_ready.sem, 1)

    def back(s):
        pool.wait_ge(K.res_steps.sem, K.res_steps.value(p, s, K.res_steps.counts[p]))
        pool.tensor_tensor(K.clnw[:, 0, :], K.clnw[:, 1, :], K.minus_half[:, 0:UNIT], ALU.pow).then_inc(K.ostat_ready.sem, 1)
        pool.wait_ge(K.onorm_ready.sem, K.onorm_ready.value(p, s, 1))
        if K.x_done.due(p, s, 0):
            pool.wait_ge(K.x_done.sem, K.x_done.value(p, s, 0))
        pool.tensor_tensor(V.gated, V.onorm, K.row["on_g"].unsqueeze(1).to_broadcast([P, UNIT, D]), ALU.mult)\
            .then_inc(K.scale_steps.sem, 1)
        pool.wait_ge(K.scale_steps.sem, K.scale_steps.value(p, s, 1))
        pool.tensor_tensor(V.gated, V.gated, K.row["on_b"].unsqueeze(1).to_broadcast([P, UNIT, D]), ALU.add)\
            .then_inc(K.scale_steps.sem, 1)

    front(0)

    def body(s, b, last):
        if not last:
            front(s + 1)
        back(s)
    over_units(pool, body)


def fill_values(nc, pool, K, p):
    V = K.v[p]
    if p == A2:
        pool.memset(V.vd[:, :, :, :, DH2].rearrange("p t y j -> p (t y) j"), 1.0)
    if p == A3:
        for b in range(2):
            pool.memset(V.vd[b][:, :, :, :, DH2].rearrange("p t y h -> p (t y) h"), 1.0)
            pool.memset(V.mb[b][:, :, SEQ:KEYS3], 0.0)
    pool.memset(K.touch[:, :], 0.0).then_inc(K.fill, 1)


def fill_selectors(nc, pool, K, p, count):
    V = K.v[p]
    pool.memset(V.selraw, 0.0)
    pool.memset(K.cwT[:, :, :].bitcast(F32), 0.0)
    R = route_views(K, p)
    for c in R.count:
        pool.memset(c[:, :, 0:PAD], 0.0)
    pool.memset(R.score, -MASKED)
    pool.memset(K.touch[:, :], 0.0).then_inc(K.fill, 1)
    pool.wait_ge(K.fill, count + 1)
    for lo in (0, 32):
        v = V.selraw[lo:lo + 32]
        if p == F0:
            v = v.rearrange("p a (m i) -> p a m i", m=2)
            pattern = [[-2, 16], [-1, 2], [0, SEQ]]
        else:
            pattern = [[-1, 16], [0, P]]
        pool.affine_select(out=v, in_=v, compare_op=ALU.not_equal, fill=1.0, base=0, pattern=pattern,
                           channel_multiplier=1).then_inc(K.fill, 1)


FILLS = {A0: 6, A1: 6, A2: 1, A3: 1, F0: 3, F1: 3, F2: 3, F3: 3}


def fills(K, p):
    return sum(FILLS[q] for q in K.phases[:K.phases.index(p) + 1])


def pool_program(nc, pool, K):
    pool.memset(K.ident[:, :], 0.0).then_inc(K.const_steps, 1)
    pool.memset(K.ones[:, :], 1.0).then_inc(K.const_steps, 1)
    pool.memset(K.minus_half[:, :], -0.5).then_inc(K.const_steps, 1)
    pool.memset(K.eps_col, EPS).then_inc(K.const_steps, 1)
    pool.wait_ge(K.const_steps, 4)
    pool.affine_select(out=K.ident[:, :], in_=K.ident[:, :], compare_op=ALU.not_equal, fill=1.0, base=0,
                       pattern=[[-1, P]], channel_multiplier=1).then_inc(K.const_steps, 1)
    count = 0
    for p in K.phases:
        if p != K.phases[0]:
            pool.wait_ge(K.x_done.sem, K.x_done.start[p])
        if p in (A0, A1):
            assert small_fill(nc, pool, K, p, count) == count + FILLS[p]
            small_pool(nc, pool, K, p)
        elif p in ATTENTION:
            fill_values(nc, pool, K, p)
            (norm_pool(nc, pool, K, p) if p == A2 else l3_pool(nc, pool, K))
        else:
            fill_selectors(nc, pool, K, p, count)
            (l3_experts_pool(nc, pool, K) if p == F3 else norm_pool(nc, pool, K, p))
        count += FILLS[p]


def started(eng, K):
    eng.wait_ge(K.const_steps, 5)
    eng.wait_ge(K.par_loaded, PAR)
    eng.wait_ge(K.x_loaded, 16 * UNITS)


def scalar_program(nc, act, K):
    started(act, K)
    act.activation(K.gates[:, :], K.gates[:, :], ACT.Tanh).then_inc(K.gates_ready, 1)
    for p in K.phases:
        if p != K.phases[0]:
            act.wait_ge(K.x_done.sem, K.x_done.start[p])
        act.wait_ge(K.fill, fills(K, p))
        if p in (A0, A1):
            small_scalar(nc, act, K, p)
        elif p == A2:
            l2_scalar(nc, act, K)
        elif p == A3:
            l3_scalar(nc, act, K)
        elif p == F3:
            l3_experts_scalar(nc, act, K)
        else:
            experts_scalar(nc, act, K, p)


def vector_program(nc, dve, K):
    started(dve, K)
    dve.wait_ge(K.gates_ready, 1)
    dve.wait_ge(K.router_psum, 1)
    dve.tensor_copy(K.router[:, :], K.bank[7][:, 0:52]).then_inc(K.router_ready, 1)
    dve.wait_ge(K.router_ready, 1)
    for p in K.phases:
        if p != K.phases[0]:
            dve.wait_ge(K.x_done.sem, K.x_done.start[p])
        dve.wait_ge(K.fill, fills(K, p))
        if p in (A0, A1):
            small_vector(nc, dve, K, p)
        elif p == A2:
            l2_vector(nc, dve, K)
        elif p == A3:
            l3_vector(nc, dve, K)
        else:
            dve.tensor_copy(K.sel[:, :, :], K.v[p].selraw).then_inc(K.sel_ready, 1)
            (l3_experts_vector(nc, dve, K) if p == F3 else experts_vector(nc, dve, K, p))


def tensor_program(nc, pe, K):
    started(pe, K)
    nc.tensor.transpose(K.bank[7][:, 0:52], K.router_raw[:, :], K.ident[0:52, 0:52]).then_inc(K.router_psum, 1)
    pe.wait_ge(K.router_ready, 1)
    sels = 0
    for p in K.phases:
        if p != K.phases[0]:
            pe.wait_ge(K.x_done.sem, K.x_done.start[p])
        pe.wait_ge(K.fill, fills(K, p))
        if p in EXPERTS:
            sels += 1
            pe.wait_ge(K.sel_ready, sels)
        if p in (A0, A1):
            small_tensor(nc, pe, K, p)
        elif p == A2:
            l2_tensor(nc, pe, K)
        elif p == A3:
            l3_tensor(nc, pe, K)
        elif p == F3:
            l3_experts_tensor(nc, pe, K)
        else:
            experts_tensor(nc, pe, K, p)


def kernel(**inputs):
    import numpy as np
    import concourse.bacc as bacc
    from concourse.bass_utils import run_bass_kernel_spmd

    nc = bacc.Bacc("TRN2", target_bir_lowering=False, num_devices=1)
    arrays, args = {}, {}
    for name, value in inputs.items():
        a = np.ascontiguousarray(value)
        key = name
        if a.dtype == np.bool_:
            a, key = a.view(np.int32), "mask"
        arrays[f"in_{name}"] = a
        args[key] = nc.dram_tensor(f"in_{name}", a.shape, mybir.dt.from_np(a.dtype), kind="ExternalInput").ap()
    out = nc.dram_tensor("out", (SEQS, SEQ, D), F32, kind="ExternalOutput").ap()
    build(nc, args, out)
    r = run_bass_kernel_spmd(nc, [arrays], core_ids=[0])
    return r.results[0]["out"]
```

```python
import concourse.bass as bass
from concourse import mybir
from contextlib import ExitStack

F32 = mybir.dt.float32
F32R = mybir.dt.float32r
U8 = mybir.dt.uint8
I32 = mybir.dt.int32
ALU = mybir.AluOpType
ACT = mybir.ActivationFunctionType
AX = mybir.AxisListType

P = 128
SEQS, SEQ, D, DC = 64, 64, 128, 96
TILES = SEQS * SEQ // P
UNIT = 4
UNITS = TILES // UNIT
COLS = UNIT * P
EPS = 1e-5
A0, F0, A1, F1, A2, F2, A3, F3 = range(8)
ATTENTION = (A0, A1, A2, A3)
HEADS, DH = 16, 8
GROUP = HEADS // 2
CLAMP = 10000.0
HEADS2, DH2 = 8, 64
PAIRS2 = HEADS2 // 2
HEADS3 = 2
KEYS3 = 2 * SEQ
MASKED = 1e30
EXPERTS = {F0: 32, F1: 8, F2: 8, F3: 4}
TOP = {F0: 6, F1: 2, F2: 2, F3: 2}
SHARED = {F0: 1, F1: 2, F2: 1}
CHUNKS = {F0: 17, F1: 18, F2: 9}
HID3 = 256
FRONT2, FRONT3 = 14, 11
PAD = 16


class Signal:

    def __init__(self, sem, counts, phases):
        self.sem, self.counts, self.start = sem, counts, {}
        total = 0
        for p in phases:
            self.start[p] = total
            total += UNITS * counts.get(p, 0)

    def value(self, p, s, n):
        return self.start[p] + s * self.counts[p] + n

    def due(self, p, s, n):
        value = self.value(p, s, n)
        return not isinstance(value, int) or value > self.start[p]


class Steps:

    def __init__(self, signal, p, s, n=0):
        self.sem, self.counted, self.p, self.s, self.n = signal.sem, signal, p, s, n

    def one(self):
        self.n += 1
        return 1

    def value(self):
        return self.counted.value(self.p, self.s, self.n)

    def ended(self):
        assert self.n == self.counted.counts[self.p], (self.p, self.n)


def over_units(eng, body):
    body(0, 0, False)
    with eng.Fori(0, (UNITS - 2) // 2) as i:
        body(i * 2 + 1, 1, False)
        body(i * 2 + 2, 0, False)
    body(UNITS - 1, 1, True)


def over_units_ahead(eng, body):
    body(0, 0, 2)
    with eng.Fori(0, (UNITS - 4) // 2) as i:
        body(i * 2 + 1, 1, 2)
        body(i * 2 + 2, 0, 2)
    for s in range(UNITS - 3, UNITS):
        body(s, s % 2, min(2, UNITS - 1 - s))


def build(nc, A, out, phases=tuple(range(8))):
    ctx = ExitStack()
    with ctx:
        K = allocate(nc, ctx, A, out, phases)
        block = ctx.enter_context(nc.Block())

        @block.sync
        def _(sp):
            sync_program(nc, sp, K)

        @block.gpsimd
        def _(pool):
            pool_program(nc, pool, K)

        @block.scalar
        def _(act):
            scalar_program(nc, act, K)

        @block.vector
        def _(dve):
            vector_program(nc, dve, K)

        @block.tensor
        def _(pe):
            tensor_program(nc, pe, K)


class Kernel:
    pass


def allocate(nc, ctx, A, out, phases):
    K = Kernel()
    K.A, K.out, K.phases = A, out, phases

    def sb(name, shape, dt=F32):
        return ctx.enter_context(nc.sbuf_tensor(name, shape, dt))

    def signal(name, counts):
        return Signal(ctx.enter_context(nc.semaphore(name)), counts, phases)

    def once(name):
        return ctx.enter_context(nc.semaphore(name))

    every = {p: 1 for p in range(8)}
    attn = {p: 1 for p in ATTENTION}
    four = {p: UNIT for p in ATTENTION}
    K.ln_steps = signal("ln_steps", {p: 11 for p in range(8)})
    K.rstd_ready = signal("rstd_ready", every)
    K.y_ready = signal("y_ready", every)
    own = {p: 1 for p in range(8) if p not in (A2, A3)}
    K.yT_psum = signal("yT_psum", own)
    K.yT_ready = signal("yT_ready", own)
    K.ctx_loaded = signal("ctx_loaded", {p: 16 for p in ATTENTION})
    K.cln_steps = signal("cln_steps", {A0: 11, A3: 11})
    K.crstd_ready = signal("crstd_ready", {A0: 1, A3: 1})
    K.c_ready = signal("c_ready", {A0: 1, A3: 1})
    K.cT_psum = signal("cT_psum", {A0: 1, A1: 1})
    K.cT_ready = signal("cT_ready", {A0: 1, A1: 1})
    K.q_psum = signal("q_psum", {A0: 1, A1: 1})
    K.q_ready = signal("q_ready", {A0: 1, A1: 1})
    K.k_psum = signal("k_psum", {A0: 1, A1: 1})
    K.k_ready = signal("k_ready", {A0: 1, A1: 1})
    K.v_psum = signal("v_psum", {A0: 1, A1: 1})
    K.v_ready = signal("v_ready", {A0: 1, A1: 1, A3: 1})
    K.front_psum = signal("front_psum", {A2: FRONT2, A3: FRONT3})
    K.front_read = signal("front_read", {A2: FRONT2, A3: FRONT3})
    K.kbd_ready = signal("kbd_ready", {A0: UNIT, A1: UNIT})
    K.s_psum = signal("s_psum", four)
    K.max_steps = signal("max_steps", {A0: UNIT, A1: 2 * UNIT, A2: UNIT, A3: 2 * UNIT})
    K.shift_ready = signal("shift_ready", four)
    K.probs_ready = signal("probs_ready", four)
    K.pT_psum = signal("pT_psum", four)
    K.pT_ready = signal("pT_ready", four)
    K.av_psum = signal("av_psum", four)
    K.sum_steps = signal("sum_steps", four)
    K.out_ready = signal("out_ready", four)
    K.oT_psum = signal("oT_psum", {A1: 1, A2: PAIRS2, A3: 1})
    K.oT_ready = signal("oT_ready", {A1: 1, A2: PAIRS2, A3: 1})
    K.proj_psum = signal("proj_psum", {A1: 1, A2: 1, A3: 1})
    K.res_steps = signal("res_steps", {A0: 1, A1: 1, A2: 1, A3: 1, F3: 11})
    K.x_done = signal("x_done", every)
    K.squares = signal("squares", {A3: 1})
    K.rms_steps = signal("rms_steps", {A3: 2})
    K.rms_ready = signal("rms_ready", {A3: 1})
    K.qk_normed = signal("qk_normed", {A3: 1})
    K.maskbias = signal("maskbias", {A3: 1})
    ch = dict(CHUNKS)
    routed = {p: CHUNKS[p] - SHARED[p] for p in CHUNKS}
    K.g_psum = signal("g_psum", ch | {F3: H3})
    K.u_psum = signal("u_psum", ch)
    K.c_psum = signal("c_psum", routed)
    K.scaled_ready = signal("scaled_ready", {F2: 8})
    K.silu_ready = signal("silu_ready", ch)
    K.prod_steps = signal("prod_steps", {F0: routed[F0], F1: routed[F1]})
    K.hid_ready = signal("hid_ready", ch | {F3: Q3})
    K.down_done = signal("down_done", ch | {F3: E3})
    K.dt_ready = signal("dt_ready", {p: 1 for p in CHUNKS})
    K.outT_psum = signal("outT_psum", {p: 1 for p in CHUNKS})
    K.logits_psum = signal("logits_psum", {p: 1 for p in EXPERTS})
    K.logits_ready = signal("logits_ready", {F0: 1})
    K.exp_ready = signal("exp_ready", {F1: 1, F2: 1, F3: 1})
    K.route_steps = signal("route_steps", {F0: 39, F1: 21, F2: 22, F3: 27})
    K.cw_psum = signal("cw_psum", {p: 1 for p in CHUNKS})
    K.cw_steps = signal("cw_steps", {p: 1 for p in CHUNKS})
    K.cwT_ready = signal("cwT_ready", {p: 1 for p in CHUNKS})
    K.sq_ready = signal("sq_ready", {F3: UNIT})
    K.var_steps = signal("var_steps", {F3: UNIT})
    K.rinv_ready = signal("rinv_ready", {F3: UNIT})
    K.z_ready = signal("z_ready", {F3: UNIT})
    K.zT_psum = signal("zT_psum", {F3: Q3})
    K.mix_steps = signal("mix_steps", {F3: E3})
    K.ostat_ready = signal("ostat_ready", {F3: 1})
    K.onorm_ready = signal("onorm_ready", {F3: 1})
    K.r2_steps = signal("r2_steps", {F3: 3})
    K.r2_ready = signal("r2_ready", {F3: 1})
    K.scale_steps = signal("scale_steps", {F3: 2})
    K.x_loaded = once("x_loaded")
    K.par_loaded = once("par_loaded")
    K.loaded = {p: once(f"weights_{p}") for p in range(8)}
    K.stored = once("stored")
    K.prep = once("prep")
    K.ident_ready = once("ident_ready")
    K.const_steps = once("const_steps")
    K.gates_ready = once("gates_ready")
    K.par_steps = once("par_steps")
    K.prep_psum = once("prep_psum")
    K.prep_ready = once("prep_ready")
    K.fill = once("fill")
    K.sel_ready = once("sel_ready")
    K.l3w_psum = once("l3w_psum")
    K.l3w_ready = once("l3w_ready")
    K.w3_steps = once("w3_steps")
    K.bias3_psum = once("bias3_psum")
    K.router_psum = once("router_psum")
    K.router_ready = once("router_ready")

    K.X = sb("X", [P, TILES, D])
    K.mask_words = sb("mask_words", [P, TILES, SEQ // 4], I32)
    K.mask = K.mask_words[:, :, :].bitcast(U8)
    K.ident = sb("ident", [P, P])
    K.ones = sb("ones", [P, P])
    K.gates = sb("gates", [P, 8])
    K.cols = sb("cols", [P, 48])
    K.rows = sb("rows", [P, 7 * D + 40])
    K.wp = {
        A0: {n: sb(f"L0_{n}", [r, D]) for n, r in (("q", D), ("k", DC), ("v", DC))},
        A1: {n: sb(f"L1_{n}", [r, D]) for n, r in (("q", D), ("k", DC), ("v", DC), ("o", D))},
        A2: {"q": sb("L2_q", [D, 4 * D]), "k": sb("L2_k", [DC, 4 * D]), "v": sb("L2_v", [DC, 4 * D]),
             "o": sb("L2_o", [D, 4, D])},
        A3: {"raw": sb("L3_raw", [P, 6, D]), "qkv": sb("L3_qkv", [D, 3 * D]), "kv": sb("L3_kv", [DC, 2 * D]),
             "o": sb("L3_o", [D, D])},
    }
    K.wf = {p: sb(f"L{p // 2}_experts", [P, 3, CHUNKS[p], P])[:, :, :, :] for p in (F0, F1)}
    late = K.wf[F0].rearrange("p w j n -> p (w j n)")
    n2 = 3 * CHUNKS[F2] * P
    K.wf[F2] = late[:, 0:n2].rearrange("p (w j n) -> p w j n", w=3, j=CHUNKS[F2])
    K.w1 = late[:, n2:n2 + 4 * HID3].rearrange("p (e h) -> p e h", e=4)
    K.w2 = late[:, n2 + 4 * HID3:n2 + 8 * HID3].rearrange("p (c d) -> p c d", c=8)
    K.router_raw = sb("router_raw", [52, D])
    K.router = sb("router", [P, 52])
    K.sel = sb("sel", [64, 16, P], F32R)
    K.cwT = sb("cwT", [64, 2, COLS], F32R)
    K.yT = [sb(f"yT{b}", [P, COLS]) for b in range(2)]
    K.yt = sb("yt", [P, UNIT, D])
    K.stats = sb("stats", [P, UNIT, 6])
    K.lnw = sb("lnw", [P, 6, UNIT])
    K.cstats = sb("cstats", [P, UNIT, 6])
    K.clnw = sb("clnw", [P, 6, UNIT])
    K.minus_half = sb("minus_half", [P, 32])
    K.route = sb("route", [P, 2048])
    K.touch = sb("touch", [P, 1])
    K.arena_cols = 20224
    K.arena = sb("arena", [P, K.arena_cols])
    K.ps = ctx.enter_context(nc.psum_tensor("ps", [P, 8, 512], F32))
    K.bank = [K.ps[:, i, :] for i in range(8)]

    K.col = {n: K.cols[:, i:i + 1] for i, n in enumerate(
        ["q_b", "k_b", "ln_g", "ln_b", "tln_g", "tln_b", "bq", "bk", "bv",
         "ln_l_g", "ln_l_b", "ln_x_g", "ln_x_b", "rn_g", "rn_b", "qn_g", "kn_g"])}
    K.ln3_g = K.cols[:, 20:28]
    K.ln3_b = K.cols[:, 28:36]
    K.logit_bias3 = K.cols[:, 36:40]
    K.row = {n: K.rows[:, i * D:(i + 1) * D] for i, n in enumerate(["v_b", "bo1", "bo2", "bo3", "on_g", "on_b"])}
    K.ebias0 = K.rows[:, 6 * D:6 * D + 32]
    K.ebias1 = K.rows[:, 6 * D + 32:6 * D + 40]
    K.eps_col = K.cols[:, 40:41]
    K.rcol = {F0: K.router[:, 0:32], F1: K.router[:, 32:40], F2: K.router[:, 40:48], F3: K.router[:, 48:52]}
    K.v = {p: carve(K, p) for p in range(8)}
    return K


class Views:

    def __init__(self, K):
        self.K, self.at = K, 0

    def take(self, *shape, rows=P):
        n = 1
        for x in shape:
            n *= x
        v = self.K.arena[0:rows, self.at:self.at + n]
        self.at += n
        assert self.at <= self.K.arena_cols, self.at
        names = " ".join("abcde"[:len(shape)])
        if len(shape) > 1:
            v = v.rearrange(f"p ({names}) -> p {names}", **{n: x for n, x in zip("abcde", shape)})
        return v


def carve(K, p):
    V = Views(K)
    if p in ATTENTION:
        V.ctx = [V.take(UNIT, DC) for _ in range(2)]
        V.ctxn = V.take(UNIT, DC)
        V.cT = [V.take(COLS, rows=DC) for _ in range(2)]
    if p in (A0, A1):
        zeroed = V.at
        V.qz = [V.take(2, UNIT, P) for _ in range(2)]
        V.vd = [V.take(UNIT, GROUP, 2, 2, DH + 1) for _ in range(2)]
        V.zeroed = (zeroed, V.at)
        V.ksel = [V.take(2, UNIT, SEQ) for _ in range(2)]
        V.kbd = [V.take(2, GROUP, SEQ) for _ in range(2)]
        V.probs = [V.take(HEADS, SEQ) for _ in range(2)]
        V.pT = [V.take(GROUP, P) for _ in range(2)]
        V.out = [V.take(UNIT, D) for _ in range(2)]
        V.outT = V.take(COLS)
        V.res = V.take(UNIT, D)
        V.max = V.take(2, HEADS)
        V.rsum = V.take(HEADS)
        V.diag = V.take(GROUP)
    if p == A2:
        V.q = [V.take(PAIRS2, COLS) for _ in range(2)]
        V.k = [V.take(PAIRS2, COLS) for _ in range(2)]
        V.vd = V.take(UNIT, 2, PAIRS2, DH2 + 1)
        V.probs = [V.take(PAIRS2, 2, SEQ) for _ in range(2)]
        V.pT = [V.take(PAIRS2, P) for _ in range(2)]
        V.out = V.take(UNIT, PAIRS2, 2, DH2)
        V.outT = V.take(PAIRS2, COLS)
        V.res = V.take(UNIT, D)
        V.max = V.take(2, 2, PAIRS2)
        V.rsum = V.take(2, PAIRS2)
    if p == A3:
        V.raw = V.take(UNIT, 5, D)
        V.sq = V.take(UNIT, 3, D)
        V.ss = V.take(UNIT, 3, 2)
        V.rms = V.take(UNIT, 3, 2)
        V.normed = V.take(3, UNIT, D)
        V.q = [V.take(COLS) for _ in range(2)]
        V.k = [V.take(UNIT, 2, 2, SEQ) for _ in range(2)]
        V.vd = [V.take(UNIT, 2, 2, DH2 + 1) for _ in range(2)]
        V.mb = [V.take(UNIT, KEYS3) for _ in range(2)]
        V.probs = [V.take(2, KEYS3) for _ in range(2)]
        V.pT = [V.take(2, P) for _ in range(2)]
        V.out = V.take(UNIT, 2, DH2)
        V.outT = V.take(COLS)
        V.res = V.take(UNIT, D)
        V.max = V.take(2, 2)
        V.rsum = V.take(2)
    if p in CHUNKS:
        V.silu = [V.take(COLS) for _ in range(2)]
        V.prod = [V.take(COLS) for _ in range(2)]
        V.hid = [V.take(COLS) for _ in range(2)]
        V.scaled = [V.take(COLS) for _ in range(2)]
    if p == F3:
        V.z = [V.take(UNIT, E3 * HID3) for _ in range(2)]
        V.hid = [V.take(COLS) for _ in range(4)]
        V.sq = V.take(2 * E3, HID3)
        V.ss, V.var, V.rinv = V.take(2, E3), V.take(2, E3), V.take(2, E3)
        V.cw = [V.take(UNIT, 8) for _ in range(2)]
        V.mixed = V.take(UNIT, D)
        V.onorm = V.take(UNIT, D)
        V.gated = V.take(UNIT, D)
        V.rn_b = V.take(P)
        V.wmean = V.take(E3)
    if p in CHUNKS:
        V.dt = V.take(COLS)
        V.selraw = V.take(16, P, rows=64)
    return V


def xs(K, s, t):
    return K.X[:, bass.ds(s * UNIT + t, 1), :].rearrange("p a d -> p (a d)")


def xu(K, s):
    return K.X[:, bass.ds(s * UNIT, UNIT), :]


def half(x):
    return slice(SEQ * x, SEQ * (x + 1))


def sync_program(nc, sp, K):
    A = K.A
    x_v = A["x"].rearrange("(t b) s d -> (b s) t d", b=2)
    c_v = A["ctx_768"].rearrange("(t b) s d -> (b s) t d", b=2)

    def load_ctx(p, s, b):
        if p in (A0, A3):
            if K.c_ready.due(p, s, 0):
                sp.wait_ge(K.c_ready.sem, K.c_ready.value(p, s, 0))
        elif p == A1:
            if K.cT_psum.due(p, s, 0):
                sp.wait_ge(K.cT_psum.sem, K.cT_psum.value(p, s, 0))
        else:
            if K.front_psum.due(p, s, 1 - FRONT2):
                sp.wait_ge(K.front_psum.sem, K.front_psum.value(p, s, 1 - FRONT2))
        sp.dma_start(K.v[p].ctx[b], c_v[:, bass.ds(s * UNIT, UNIT), :]).then_inc(K.ctx_loaded.sem, 16)

    def column(name, vec, rows=slice(0, P)):
        n = rows.stop - rows.start
        sp.dma_start(K.col[name][rows], vec.rearrange("(p o) -> p o", p=n)).then_inc(K.par_loaded, 16)

    def row(dst, vec):
        n = vec.shape[0]
        sp.dma_start(dst, vec.rearrange("(o n) -> o n", o=1).to_broadcast([P, n])).then_inc(K.par_loaded, 16)

    K.par_n = 0
    for s in range(UNITS):
        sp.dma_start(K.X[:, s * UNIT:(s + 1) * UNIT, :], x_v[:, s * UNIT:(s + 1) * UNIT, :]).then_inc(K.x_loaded, 16)
    row(K.gates[:, 0:4], A["g_xattn"])
    row(K.gates[:, 4:8], A["g_ffn"])
    for n in ("q_b", "k_b", "ln_g", "ln_b"):
        column(n, A[f"L0_xattn_{n}"])
    for n in ("tln_g", "tln_b"):
        column(n, A[f"L0_xattn_{n}"], slice(0, DC))
    for n in ("bq", "bk", "bv"):
        column(n, A[f"L1_xattn_{n}"])
    for n in ("ln_l_g", "ln_l_b"):
        column(n, A[f"L3_xattn_{n}"])
    for n in ("ln_x_g", "ln_x_b"):
        column(n, A[f"L3_xattn_{n}"], slice(0, DC))
    for n in ("rn_g", "rn_b"):
        column(n, A[f"L3_ffn_{n}"])
    for n in ("qn_g", "kn_g"):
        for h in range(2):
            column(n, A[f"L3_xattn_{n}"], half(h))
    with nc.allow_non_contiguous_dma("sixteen short vectors"):
        for dst, n in ((K.ln3_g, "ln_g"), (K.ln3_b, "ln_b")):
            sp.dma_start(dst, A[f"L3_ffn_{n}"].rearrange("e (c p) -> p (e c)", p=P)).then_inc(K.par_loaded, 16)
    row(K.row["v_b"], A["L0_xattn_v_b"])
    row(K.row["bo1"], A["L1_xattn_bo"])
    row(K.row["bo2"], A["L2_xattn_bo"])
    row(K.row["bo3"], A["L3_xattn_bo"])
    row(K.row["on_g"], A["L3_ffn_on_g"])
    row(K.row["on_b"], A["L3_ffn_on_b"])
    row(K.ebias0, A["L0_ffn_e_score_correction_bias"])
    row(K.ebias1, A["L1_ffn_experts_bias"])

    def load(p, dst, src):
        sp.dma_start(dst, src).then_inc(K.loaded[p], 16)

    for n in ("q", "k", "v"):
        load(A0, K.wp[A0][n][:, :], A[f"L0_xattn_{n}_w"])
    if K.phases[0] == A0:
        load_ctx(A0, 0, 0)
    for at, name in ((0, "L0_ffn_gate_weight"), (32, "L1_ffn_router_w"), (40, "L2_ffn_gate_w"), (48, "L3_ffn_router_w")):
        n = A[name].shape[0]
        sp.dma_start(K.router_raw[at:at + n, :], A[name]).then_inc(K.par_loaded, 16)
    if F0 in K.phases:
        raw = K.wf[F1]
        load(F0, raw[:, 0, 0, :], A["L0_ffn_shared_gate_w"])
        load(F0, raw[:, 1, 0, :], A["L0_ffn_shared_up_w"])
        load(F0, raw[:, 2, 0, :], A["L0_ffn_shared_down_w"])
        gu = A["L0_ffn_experts_gate_up"].rearrange("(j m) r h -> m r j h", m=2)
        for m in range(2):
            for which in range(2):
                load(F0, raw[half(m), which, 1:17, :], gu[m, half(which), :, :])
        dn = A["L0_ffn_experts_down"].rearrange("(j m) h i -> m h j i", m=2)
        for m in range(2):
            load(F0, raw[:, 2, 1:17, half(m)], dn[m])
    for n in ("q", "k", "v", "o"):
        load(A1, K.wp[A1][n][:, :], A[f"L1_xattn_W{n}"])
    for n in ("q", "k", "v"):
        load(A2, K.wp[A2][n][:, :], A[f"L2_xattn_W{n}"])
    load(A2, K.wp[A2]["o"][:, :, :], A["L2_xattn_Wo"].rearrange("(c p) n -> p c n", p=P))
    L3 = K.wp[A3]["raw"]
    load(A3, L3[:, 0, :], A["L3_xattn_Wq"])
    load(A3, L3[:, 1:3, :], A["L3_xattn_Wlkv"].rearrange("(c p) n -> p c n", p=P))
    load(A3, L3[:, 3, :], A["L3_xattn_Wo"])
    load(A3, L3[:, 4:6, 0:DC], A["L3_xattn_Wkv"].rearrange("(c p) n -> p c n", p=P))
    mask = A["mask"].rearrange("(t b) k -> b t k", b=2)
    for x in range(2):
        load(A3, K.mask_words[half(x), :, :], mask[x:x + 1].to_broadcast([SEQ, TILES, SEQ // 4]))

    def load_late():
        for which, n in ((0, "w1"), (1, "w3"), (2, "w2")):
            load(F2, K.wf[F2][:, which, 0, :], A[f"L2_ffn_{n}s"][0])
            load(F2, K.wf[F2][:, which, 1:9, :], A[f"L2_ffn_{n}"].rearrange("e d h -> d e h"))
        load(F3, K.w1, A["L3_ffn_w1"].rearrange("e d h -> d e h"))
        load(F3, K.w2, A["L3_ffn_w2"].rearrange("e (c p) d -> p (e c) d", p=P))

    def load_f1():
        for which, n in ((0, "w1"), (1, "w3")):
            for at, src in ((0, A[f"L1_ffn_s{n}"]), (2, A[f"L1_ffn_{n}"])):
                e = src.shape[0]
                load(F1, K.wf[F1][:, which, at:at + 2 * e, :].rearrange("p (e c) h -> p e (c h)", e=e),
                     src.rearrange("e d h -> d e h"))
        for at, src in ((0, A["L1_ffn_sw2"]), (2, A["L1_ffn_w2"])):
            e = src.shape[0]
            load(F1, K.wf[F1][:, 2, at:at + 2 * e, :], src.rearrange("e (c p) d -> p (e c) d", p=P))

    if F0 not in K.phases:
        load_f1()
        load_late()
    for p in K.phases:
        if p in ATTENTION:
            if p != K.phases[0]:
                sp.wait_ge(K.x_done.sem, K.x_done.start[p])
            if not (p == A0 and K.phases[0] == A0):
                load_ctx(p, 0, 0)
            if p == A1 and F0 in K.phases:
                load_f1()
                load_late()

            def body(s, b, last):
                if not last:
                    load_ctx(p, s + 1, 1 - b)
            over_units(sp, body)
    for p in range(8):
        if p != F0 or F0 in K.phases:
            sp.wait_ge(K.loaded[p], 16 * LOADS[p])
    last = K.phases[-1]
    out_v = K.out.rearrange("(t b) s d -> (b s) t d", b=2)
    for s in range(UNITS):
        sp.wait_ge(K.x_done.sem, K.x_done.value(last, s, 1))
        sp.dma_start(out_v[:, s * UNIT:(s + 1) * UNIT, :], K.X[:, s * UNIT:(s + 1) * UNIT, :]).then_inc(K.stored, 16)
    sp.wait_ge(K.stored, 16 * UNITS)


PAR = 16 * (2 + 4 + 2 + 3 + 2 + 2 + 2 + 4 + 2 + 8 + 4)
YT_PIECE = {A2: 5, A3: 1}
LOADS = {A0: 3, F0: 3 + 4 + 2, A1: 4, F1: 6, A2: 4, F2: 6, A3: 6, F3: 2}
PREP_GROUPS = [(i, min(4, 51 - i)) for i in range(0, 51, 4)]
PREP_F0 = len(PREP_GROUPS)


def whole_first(first, y, t):
    if first:
        return slice(0, P), slice(t * P, (t + 1) * P)
    return half(y), slice(t * P + y * SEQ, t * P + (y + 1) * SEQ)


def ln_statistics(nc, dve, K, p, s, steps, stats, w, source, n, twice):
    for t in range(UNIT):
        dve.bn_stats(stats[:, t, :], source(t)).then_inc(steps.sem, steps.one())
    mean2, dif, m2, sq, mean, var = (w[:, i, :] for i in range(6))
    dve.wait_ge(steps.sem, steps.value())
    dve.tensor_tensor(mean2, stats[:, :, 1], stats[:, :, 4], ALU.add).then_inc(steps.sem, steps.one())
    dve.tensor_tensor(dif, stats[:, :, 1], stats[:, :, 4], ALU.subtract).then_inc(steps.sem, steps.one())
    dve.tensor_tensor(m2, stats[:, :, 2], stats[:, :, 5], ALU.add).then_inc(steps.sem, steps.one())
    dve.wait_ge(steps.sem, steps.value())
    dve.tensor_scalar(mean, mean2, 0.5, None, ALU.mult).then_inc(steps.sem, steps.one())
    dve.scalar_tensor_tensor(out=sq, in0=dif, scalar=0.25, in1=dif, op0=ALU.mult, op1=ALU.mult).then_inc(steps.sem, steps.one())
    dve.wait_ge(steps.sem, steps.value())
    dve.scalar_tensor_tensor(out=var, in0=m2, scalar=1.0 / n, in1=sq, op0=ALU.mult, op1=ALU.add).then_inc(steps.sem, steps.one())
    dve.wait_ge(steps.sem, steps.value())
    a, b = (1.0 + EPS, EPS * EPS) if twice else (1.0, EPS)
    dve.tensor_scalar(dif, var, a, b, ALU.mult, ALU.add).then_inc(steps.sem, steps.one())


def ln_apply(nc, dve, out, source, w, ready):
    for t in range(UNIT):
        last = dve.tensor_scalar(out[:, t, :], source(t), w[:, 4, t:t + 1], w[:, 0, t:t + 1],
                                 ALU.subtract, ALU.mult)
    last.then_inc(ready.sem, 1)


def x_statistics(nc, dve, K, p, s):
    steps = Steps(K.ln_steps, p, s)
    ln_statistics(nc, dve, K, p, s, steps, K.stats, K.lnw, lambda t: xs(K, s, t), D, p in (A0, A3))
    steps.ended()


def x_normed(nc, dve, K, p, s):
    dve.wait_ge(K.rstd_ready.sem, K.rstd_ready.value(p, s, 1))
    if p in (A2, A3):
        if K.front_psum.due(p, s, YT_PIECE[p] + 1 - K.front_psum.counts[p]):
            dve.wait_ge(K.front_psum.sem, K.front_psum.value(p, s, YT_PIECE[p] + 1 - K.front_psum.counts[p]))
    else:
        if K.yT_psum.due(p, s, 0):
            dve.wait_ge(K.yT_psum.sem, K.yT_psum.value(p, s, 0))
    ln_apply(nc, dve, K.yt, lambda t: xs(K, s, t), K.lnw, K.y_ready)


def ctx_statistics(nc, dve, K, p, s, b):
    dve.wait_ge(K.ctx_loaded.sem, K.ctx_loaded.value(p, s, 16))
    steps = Steps(K.cln_steps, p, s)
    ln_statistics(nc, dve, K, p, s, steps, K.cstats, K.clnw, lambda t: K.v[p].ctx[b][:, t, :], DC, False)
    steps.ended()


def ctx_normed(nc, dve, K, p, s, b):
    dve.wait_ge(K.crstd_ready.sem, K.crstd_ready.value(p, s, 1))
    if p == A3:
        if K.front_psum.due(p, s, 1 - FRONT3):
            dve.wait_ge(K.front_psum.sem, K.front_psum.value(p, s, 1 - FRONT3))
    else:
        if K.cT_psum.due(p, s, 0):
            dve.wait_ge(K.cT_psum.sem, K.cT_psum.value(p, s, 0))
    ln_apply(nc, dve, K.v[p].ctxn, lambda t: K.v[p].ctx[b][:, t, :], K.clnw, K.c_ready)


def rstd_pool(nc, pool, K, p, s, ctx):
    steps, ready, w = (K.cln_steps, K.crstd_ready, K.clnw) if ctx else (K.ln_steps, K.rstd_ready, K.lnw)
    pool.wait_ge(steps.sem, steps.value(p, s, steps.counts[p]))
    pool.tensor_tensor(w[:, 0, :], w[:, 1, :], K.minus_half[:, 0:UNIT], ALU.pow).then_inc(ready.sem, 1)


def transpose4(nc, K, bank, source, rows, cols=P):
    for t in range(UNIT):
        last = nc.tensor.transpose(bank[0:rows, t * P:(t + 1) * P], source(t), K.ident[:, :])
    return last


def yT_evacuate(nc, act, K, p, s, b, bank):
    ready = K.front_read if p in (A2, A3) else K.yT_ready
    if p not in (A2, A3):
        act.wait_ge(K.yT_psum.sem, K.yT_psum.value(p, s, 1))
    g, o = {A0: ("ln_g", "ln_b"), A3: ("ln_l_g", "ln_l_b")}.get(p, (None, None))
    if g:
        act.activation(K.yT[b][:, :], bank, ACT.Identity, scale=K.col[g], bias=K.col[o]).then_inc(ready.sem, 1)
    else:
        act.activation(K.yT[b][:, :], bank, ACT.Copy).then_inc(ready.sem, 1)


def cT_evacuate(nc, act, K, p, s, b, bank):
    ready = K.front_read if p in (A2, A3) else K.cT_ready
    if p not in (A2, A3):
        act.wait_ge(K.cT_psum.sem, K.cT_psum.value(p, s, 1))
    g, o = {A0: ("tln_g", "tln_b"), A3: ("ln_x_g", "ln_x_b")}.get(p, (None, None))
    dst = K.v[p].cT[b]
    if g:
        act.activation(dst, bank[0:DC, :], ACT.Identity, scale=K.col[g][0:DC], bias=K.col[o][0:DC]).then_inc(ready.sem, 1)
    else:
        act.activation(dst, bank[0:DC, :], ACT.Copy).then_inc(ready.sem, 1)


S_BANKS = ((0, 1), (2, 3))
PT_BANKS = (4, 5)
O_BANK, X_BANK = 6, 7


def small_tensor(nc, pe, K, p):
    V, W = K.v[p], K.wp[p]
    bank, mm = K.bank, nc.tensor.matmul

    def context(s, b):
        if p == A0:
            pe.wait_ge(K.c_ready.sem, K.c_ready.value(p, s, 1))
        else:
            pe.wait_ge(K.ctx_loaded.sem, K.ctx_loaded.value(p, s, 16))
        if K.v_ready.due(p, s, 0):
            pe.wait_ge(K.v_ready.sem, K.v_ready.value(p, s, 0))
        src = V.ctxn if p == A0 else V.ctx[b]
        transpose4(nc, K, bank[X_BANK], lambda t: src[:, t, :], DC).then_inc(K.cT_psum.sem, 1)

    def keys(s, b):
        pe.wait_ge(K.cT_ready.sem, K.cT_ready.value(p, s, 1))
        mm(bank[X_BANK], W["k"][:, :], V.cT[b], start=True, stop=True).then_inc(K.k_psum.sem, 1)

    def stream(s):
        pe.wait_ge(K.y_ready.sem, K.y_ready.value(p, s, 1))
        pe.wait_ge(K.k_ready.sem, K.k_ready.value(p, s, 1))
        transpose4(nc, K, bank[X_BANK], lambda t: K.yt[:, t, :], P).then_inc(K.yT_psum.sem, 1)

    def queries(s, b):
        pe.wait_ge(K.yT_ready.sem, K.yT_ready.value(p, s, 1))
        mm(bank[X_BANK], W["q"][:, :], K.yT[b][:, :], start=True, stop=True).then_inc(K.q_psum.sem, 1)

    def values(s, b):
        pe.wait_ge(K.q_ready.sem, K.q_ready.value(p, s, 1))
        if p == A1 and K.x_done.due(p, s, -1):
            pe.wait_ge(K.x_done.sem, K.x_done.value(p, s, -1))
        for t in range(UNIT):
            last = mm(bank[X_BANK][:, t * P:(t + 1) * P], V.cT[b][:, t * P:(t + 1) * P], W["v"][:, :],
                      start=True, stop=True)
        last.then_inc(K.v_psum.sem, 1)

    def scores(s, b, t):
        pe.wait_ge(K.kbd_ready.sem, K.kbd_ready.value(p, s, t + 1))
        if K.shift_ready.due(p, s, t - 1):
            pe.wait_ge(K.shift_ready.sem, K.shift_ready.value(p, s, t - 1))
        if t == 0:
            pe.wait_ge(K.q_ready.sem, K.q_ready.value(p, s, 1))
        for g in range(2):
            last = mm(bank[S_BANKS[t % 2][g]], V.qz[b][:, g, t, :], V.kbd[t % 2][:, g, :, :].rearrange("p h k -> p (h k)"),
                      start=True, stop=True)
        last.then_inc(K.s_psum.sem, 1)

    def turned(s, t):
        pe.wait_ge(K.probs_ready.sem, K.probs_ready.value(p, s, t + 1))
        if K.pT_ready.due(p, s, t):
            pe.wait_ge(K.pT_ready.sem, K.pT_ready.value(p, s, t))
        pr = V.probs[t % 2].rearrange("p h k -> p (h k)")
        for j in range(GROUP):
            last = nc.tensor.transpose(bank[PT_BANKS[j // 4]][:, (j % 4) * P:(j % 4 + 1) * P],
                                       pr[:, j * P:(j + 1) * P], K.ident[:, :])
        last.then_inc(K.pT_psum.sem, 1)

    def weighted(s, b, t):
        pe.wait_ge(K.pT_ready.sem, K.pT_ready.value(p, s, t + 1))
        if K.out_ready.due(p, s, t):
            pe.wait_ge(K.out_ready.sem, K.out_ready.value(p, s, t))
        if t == 0:
            pe.wait_ge(K.v_ready.sem, K.v_ready.value(p, s, 1))
        n = 2 * 2 * (DH + 1)
        for j in range(GROUP):
            last = mm(bank[O_BANK][:, j * n:(j + 1) * n], V.pT[t % 2][:, j, :],
                      V.vd[b][:, t, j, :, :, :].rearrange("p x h d -> p (x h d)"), start=True, stop=True)
        last.then_inc(K.av_psum.sem, 1)

    def outputs_turned(s, b, following):
        pe.wait_ge(K.out_ready.sem, K.out_ready.value(p, s, UNIT))
        if following is not None:
            pe.wait_ge(K.q_ready.sem, K.q_ready.value(p, following, 1))
        elif K.x_done.due(p, s, 0):
            pe.wait_ge(K.x_done.sem, K.x_done.value(p, s, 0))
        transpose4(nc, K, bank[X_BANK], lambda t: V.out[b][:, t, :], P).then_inc(K.oT_psum.sem, 1)

    def project(s):
        pe.wait_ge(K.oT_ready.sem, K.oT_ready.value(p, s, 1))
        for t in range(UNIT):
            last = mm(bank[X_BANK][:, t * P:(t + 1) * P], V.outT[:, t * P:(t + 1) * P], W["o"][:, :],
                      start=True, stop=True)
        last.then_inc(K.proj_psum.sem, 1)

    pe.wait_ge(K.loaded[p], 16 * LOADS[p])
    context(0, 0)
    keys(0, 0)
    stream(0)
    queries(0, 0)
    values(0, 0)
    scores(0, 0, 0)
    scores(0, 0, 1)

    def body(s, b, later):
        n, nb = s + 1, 1 - b
        back = p == A1 and not (isinstance(s, int) and s == 0)
        turned(s, 0)
        if later:
            context(n, nb)
        scores(s, b, 2)
        if later:
            keys(n, nb)
        weighted(s, b, 0)
        if later:
            stream(n)
        turned(s, 1)
        if later:
            queries(n, nb)
        scores(s, b, 3)
        if back:
            outputs_turned(s - 1, nb, n if later else None)
        weighted(s, b, 1)
        if back:
            project(s - 1)
        turned(s, 2)
        if later:
            scores(n, nb, 0)
            values(n, nb)
        weighted(s, b, 2)
        turned(s, 3)
        if later:
            scores(n, nb, 1)
        weighted(s, b, 3)
    over_units_ahead(pe, body)
    if p == A1:
        outputs_turned(UNITS - 1, 1, None)
        project(UNITS - 1)


def small_scalar(nc, act, K, p):
    V = K.v[p]
    bank = K.bank
    x = bank[X_BANK]

    def queries(s, b):
        act.wait_ge(K.q_psum.sem, K.q_psum.value(p, s, 1))
        name = "q_b" if p == A0 else "bq"
        xv = x.rearrange("p (t y q) -> p t y q", t=UNIT, y=2)
        for g in range(2):
            for y in range(2):
                last = act.activation(V.qz[b][half(y), g, :, half(y)], xv[half(g), :, y, :], ACT.Identity,
                                      bias=K.col[name][half(g)])
        last.then_inc(K.q_ready.sem, 1)

    def values(s, b):
        act.wait_ge(K.v_psum.sem, K.v_psum.value(p, s, 1))
        xv = x.rearrange("p (t j h d) -> p t j h d", t=UNIT, j=GROUP, h=2)
        for y in range(2):
            for hh in range(2):
                last = act.activation(V.vd[b][half(hh), :, :, y, hh, 0:DH], xv[half(y), :, :, hh, :], ACT.Copy)
        last.then_inc(K.v_ready.sem, 1)

    def probs(s, t):
        act.wait_ge(K.shift_ready.sem, K.shift_ready.value(p, s, t + 1))
        pr = V.probs[t % 2]
        act.activation(pr, pr, ACT.Exp, scale=DH ** -0.5).then_inc(K.probs_ready.sem, 1)

    def turned(s, t):
        if p == A0:
            act.wait_ge(K.pT_psum.sem, K.pT_psum.value(p, s, t + 1))
            if K.av_psum.due(p, s, t - 1):
                act.wait_ge(K.av_psum.sem, K.av_psum.value(p, s, t - 1))
            act.activation(V.pT[t % 2], K.ps[:, PT_BANKS[0]:PT_BANKS[1] + 1, :].rearrange("p b (j q) -> p (b j) q", q=P),
                           ACT.Copy).then_inc(K.pT_ready.sem, 1)

    def outputs_turned(s):
        act.wait_ge(K.oT_psum.sem, K.oT_psum.value(p, s, 1))
        if K.proj_psum.due(p, s, 0):
            act.wait_ge(K.proj_psum.sem, K.proj_psum.value(p, s, 0))
        act.activation(V.outT, x, ACT.Identity, bias=K.col["bv"]).then_inc(K.oT_ready.sem, 1)

    cT_evacuate(nc, act, K, p, 0, 0, x)
    yT_evacuate(nc, act, K, p, 0, 0, x)
    queries(0, 0)
    values(0, 0)
    probs(0, 0)
    probs(0, 1)

    def body(s, b, later):
        n, nb = s + 1, 1 - b
        turned(s, 0)
        if later:
            cT_evacuate(nc, act, K, p, n, nb, x)
        probs(s, 2)
        if later:
            yT_evacuate(nc, act, K, p, n, nb, x)
        turned(s, 1)
        if later:
            queries(n, nb)
        probs(s, 3)
        if p == A1 and not (isinstance(s, int) and s == 0):
            outputs_turned(s - 1)
        turned(s, 2)
        if later:
            values(n, nb)
            probs(n, 0)
        turned(s, 3)
        if later:
            probs(n, 1)
    over_units_ahead(act, body)
    if p == A1:
        outputs_turned(UNITS - 1)


def small_vector(nc, dve, K, p):
    V = K.v[p]
    x = K.bank[X_BANK]

    def keys(s, b):
        dve.wait_ge(K.k_psum.sem, K.k_psum.value(p, s, 1))
        if K.kbd_ready.due(p, s, -UNIT):
            dve.wait_ge(K.kbd_ready.sem, K.kbd_ready.value(p, s, -UNIT))
        name = "k_b" if p == A0 else "bk"
        xv = x.rearrange("p (t y k) -> p t y k", t=UNIT, y=2)
        for g in range(2):
            for y in range(2):
                last = dve.tensor_scalar(V.ksel[b][half(y), g, :, :], xv[half(g), :, y, :], K.col[name][half(g)], None,
                                         ALU.add)
        last.then_inc(K.k_ready.sem, 1)

    def shift(s, t):
        steps = Steps(K.max_steps, p, s, t * (K.max_steps.counts[p] // UNIT))
        dve.wait_ge(K.s_psum.sem, K.s_psum.value(p, s, t + 1))
        lo, hi = S_BANKS[t % 2]
        sc = K.ps[:, lo:hi + 1, :].rearrange("p b (h k) -> p (b h) k", k=SEQ)
        mx = V.max[:, t % 2, :]
        dve.tensor_reduce(mx, sc, axis=AX.X, op=ALU.max).then_inc(steps.sem, steps.one())
        c = CLAMP * DH ** 0.5
        if p == A1:
            dve.wait_ge(steps.sem, steps.value())
            dve.tensor_scalar(mx, mx, c, -c, ALU.min, ALU.max).then_inc(steps.sem, steps.one())
        dve.wait_ge(steps.sem, steps.value())
        if K.pT_psum.due(p, s, t - 1):
            dve.wait_ge(K.pT_psum.sem, K.pT_psum.value(p, s, t - 1))
        mxb = mx.unsqueeze(2).to_broadcast([P, HEADS, SEQ])
        if p == A1:
            dve.scalar_tensor_tensor(out=V.probs[t % 2], in0=sc, scalar=-c, in1=mxb, op0=ALU.max,
                                     op1=ALU.subtract).then_inc(K.shift_ready.sem, 1)
        else:
            dve.tensor_tensor(V.probs[t % 2], sc, mxb, ALU.subtract).then_inc(K.shift_ready.sem, 1)

    def turned(s, t):
        if p == A1:
            dve.wait_ge(K.pT_psum.sem, K.pT_psum.value(p, s, t + 1))
            if K.av_psum.due(p, s, t - 1):
                dve.wait_ge(K.av_psum.sem, K.av_psum.value(p, s, t - 1))
            dve.tensor_scalar(V.pT[t % 2], K.ps[:, PT_BANKS[0]:PT_BANKS[1] + 1, :].rearrange("p b (j q) -> p (b j) q", q=P),
                              1.0, None, ALU.min).then_inc(K.pT_ready.sem, 1)

    def outputs(s, b, t):
        dve.wait_ge(K.av_psum.sem, K.av_psum.value(p, s, t + 1))
        if t == 0 and p == A1:
            if K.oT_psum.due(p, s, -1):
                dve.wait_ge(K.oT_psum.sem, K.oT_psum.value(p, s, -1))
        steps = Steps(K.sum_steps, p, s, t)
        o = K.bank[O_BANK][:, 0:GROUP * 4 * (DH + 1)].rearrange("p (j y h d) -> p j y h d", j=GROUP, y=2, h=2)
        rs = V.rsum.rearrange("p (j h) -> p j h", h=2)
        for y in range(2):
            last = dve.reciprocal(rs[half(y)], o[half(y), :, y, :, DH])
        last.then_inc(steps.sem, steps.one())
        dve.wait_ge(steps.sem, steps.value())
        for y in range(2):
            last = dve.tensor_tensor(V.out[b][half(y), t, :].rearrange("p (j h d) -> p j h d", j=GROUP, h=2),
                                     o[half(y), :, y, :, 0:DH],
                                     rs[half(y)].unsqueeze(3).to_broadcast([SEQ, GROUP, 2, DH]), ALU.mult)
        last.then_inc(K.out_ready.sem, 1)

    def residual(s, b):
        if p == A0:
            dve.wait_ge(K.out_ready.sem, K.out_ready.value(p, s, UNIT))
            src, add = V.out[b], K.row["v_b"]
        else:
            dve.wait_ge(K.proj_psum.sem, K.proj_psum.value(p, s, 1))
            src, add = x.rearrange("p (t d) -> p t d", t=UNIT), K.row["bo1"]
        add_residual(nc, dve, K, p, s, V.res, src, add)

    def statistics(s, b):
        x_statistics(nc, dve, K, p, s)
        if p == A0:
            ctx_statistics(nc, dve, K, p, s, b)

    def normed(s, b):
        if p == A0:
            ctx_normed(nc, dve, K, p, s, b)
        x_normed(nc, dve, K, p, s)

    statistics(0, 0)
    normed(0, 0)
    keys(0, 0)
    statistics(1, 1)
    shift(0, 0)
    normed(1, 1)
    shift(0, 1)

    def body(s, b, later):
        n, nb = s + 1, 1 - b
        turned(s, 0)
        shift(s, 2)
        if later:
            keys(n, nb)
        outputs(s, b, 0)
        turned(s, 1)
        shift(s, 3)
        if later == 2:
            statistics(s + 2, b)
        outputs(s, b, 1)
        if not (isinstance(s, int) and s == 0):
            residual(s - 1, nb)
        turned(s, 2)
        if later == 2:
            normed(s + 2, b)
        outputs(s, b, 2)
        if later:
            shift(n, 0)
        turned(s, 3)
        outputs(s, b, 3)
        if later:
            shift(n, 1)
    over_units_ahead(dve, body)
    residual(UNITS - 1, 1)


def add_residual(nc, dve, K, p, s, tmp, src, add):
    gate = K.gates[:, p // 2:p // 2 + 1]
    if K.x_done.due(p, s, 0):
        dve.wait_ge(K.x_done.sem, K.x_done.value(p, s, 0))
    dve.tensor_tensor(tmp, src, add.unsqueeze(1).to_broadcast([P, UNIT, D]), ALU.add).then_inc(K.res_steps.sem, 1)
    dve.wait_ge(K.res_steps.sem, K.res_steps.value(p, s, 1))
    dve.scalar_tensor_tensor(out=xu(K, s), in0=tmp, scalar=gate, in1=xu(K, s), op0=ALU.mult,
                             op1=ALU.add).then_inc(K.x_done.sem, 1)


def small_pool(nc, pool, K, p):
    V = K.v[p]

    def spread(s, b, t):
        if t == 0:
            pool.wait_ge(K.k_ready.sem, K.k_ready.value(p, s, 1))
        if K.s_psum.due(p, s, t - 1):
            pool.wait_ge(K.s_psum.sem, K.s_psum.value(p, s, t - 1))
        for g in range(2):
            last = pool.tensor_tensor(V.kbd[t % 2][:, g, :, :],
                                      V.ksel[b][:, g, t, :].unsqueeze(1).to_broadcast([P, GROUP, SEQ]),
                                      V.diag.unsqueeze(2).to_broadcast([P, GROUP, SEQ]), ALU.mult)
        last.then_inc(K.kbd_ready.sem, 1)

    def factors(s):
        rstd_pool(nc, pool, K, p, s, False)
        if p == A0:
            rstd_pool(nc, pool, K, p, s, True)

    factors(0)
    spread(0, 0, 0)
    spread(0, 0, 1)
    factors(1)

    def body(s, b, later):
        n, nb = s + 1, 1 - b
        spread(s, b, 2)
        spread(s, b, 3)
        if later == 2:
            factors(s + 2)
        if later:
            spread(n, nb, 0)
            spread(n, nb, 1)
    over_units_ahead(pool, body)


def small_fill(nc, pool, K, p, count):
    V = K.v[p]
    lo, hi = V.zeroed
    pool.memset(K.arena[:, lo:hi], 0.0).then_inc(K.fill, 1)
    pool.memset(V.diag, 1.0).then_inc(K.fill, 1)
    pool.wait_ge(K.fill, count + 2)
    for b in range(2):
        for hh in range(2):
            pool.memset(V.vd[b][half(hh), :, :, :, hh, DH].rearrange("p t j y -> p (t j) y"), 1.0)
    for y in range(2):
        dg = V.diag[half(y)]
        pool.affine_select(out=dg, in_=dg, compare_op=ALU.is_ge, fill=0.0, base=0,
                           pattern=[[-DH, GROUP]], channel_multiplier=1).then_inc(K.fill, 1)
    pool.wait_ge(K.fill, count + 4)
    for y in range(2):
        dg = V.diag[half(y)]
        pool.affine_select(out=dg, in_=dg, compare_op=ALU.is_ge, fill=0.0, base=DH - 1,
                           pattern=[[DH, GROUP]], channel_multiplier=-1).then_inc(K.fill, 1)
    pool.wait_ge(K.fill, count + 6)
    return count + 6


PT2_BANK = 2
O2_BANKS = (3, 4)


def piece_bank(K, i):
    return K.bank[5 + i % 3]


def l2_tensor(nc, pe, K):
    p = A2
    V, W = K.v[p], K.wp[p]
    mm = nc.tensor.matmul

    def piece(s, b, i):
        if K.front_read.due(p, s, max(0, i - 2)):
            pe.wait_ge(K.front_read.sem, K.front_read.value(p, s, max(0, i - 2)))
        if i == 0:
            pe.wait_ge(K.ctx_loaded.sem, K.ctx_loaded.value(p, s, 16))
            if K.x_done.due(p, s, -1):
                pe.wait_ge(K.x_done.sem, K.x_done.value(p, s, -1))
        bank = piece_bank(K, i)
        if i == 0:
            last = transpose4(nc, K, bank, lambda t: V.ctx[b][:, t, :], DC)
        elif i < 5:
            pe.wait_ge(K.front_read.sem, K.front_read.value(p, s, 1))
            last = mm(bank, W["k"][:, (i - 1) * P:i * P], V.cT[b], start=True, stop=True)
        elif i == 5:
            pe.wait_ge(K.y_ready.sem, K.y_ready.value(p, s, 1))
            last = transpose4(nc, K, bank, lambda t: K.yt[:, t, :], P)
        elif i < 10:
            pe.wait_ge(K.front_read.sem, K.front_read.value(p, s, 6))
            last = mm(bank, W["q"][:, (i - 6) * P:(i - 5) * P], K.yT[b][:, :], start=True, stop=True)
        else:
            t = i - 10
            last = mm(bank, V.cT[b][:, t * P:(t + 1) * P], W["v"][:, :], start=True, stop=True)
        last.then_inc(K.front_psum.sem, 1)

    def scores(s, b, t):
        if K.shift_ready.due(p, s, t):
            pe.wait_ge(K.shift_ready.sem, K.shift_ready.value(p, s, t))
        pe.wait_ge(K.front_read.sem, K.front_read.value(p, s, 10))
        for j in range(PAIRS2):
            for h in range(2):
                for y in range(2):
                    tok = slice(t * P + y * SEQ, t * P + (y + 1) * SEQ)
                    rows, qs = whole_first(j + h + y == 0, y, t)
                    last = mm(K.bank[h][rows, j * SEQ:(j + 1) * SEQ], V.q[b][half(h), j, qs],
                              V.k[b][half(h), j, tok], start=True, stop=True)
        last.then_inc(K.s_psum.sem, 1)

    def turned(s, t):
        pe.wait_ge(K.probs_ready.sem, K.probs_ready.value(p, s, t + 1))
        if K.pT_ready.due(p, s, t):
            pe.wait_ge(K.pT_ready.sem, K.pT_ready.value(p, s, t))
        for j in range(PAIRS2):
            last = nc.tensor.transpose(K.bank[PT2_BANK][:, j * P:(j + 1) * P],
                                       V.probs[t % 2][:, j, :, :].rearrange("p h k -> p (h k)"), K.ident[:, :])
        last.then_inc(K.pT_psum.sem, 1)

    def weighted(s, t):
        pe.wait_ge(K.pT_ready.sem, K.pT_ready.value(p, s, t + 1))
        if K.out_ready.due(p, s, t):
            pe.wait_ge(K.out_ready.sem, K.out_ready.value(p, s, t))
        if t == 0:
            pe.wait_ge(K.front_read.sem, K.front_read.value(p, s, FRONT2))
        n = DH2 + 1
        for j in range(PAIRS2):
            for h in range(2):
                for y in range(2):
                    rows, qs = whole_first(j + h + y == 0, y, 0)
                    last = mm(K.bank[O2_BANKS[h]][rows, j * n:(j + 1) * n], V.pT[t % 2][half(h), j, qs],
                              V.vd[half(h), t, y, j, :], start=True, stop=True)
        last.then_inc(K.av_psum.sem, 1)

    def project(s, nxt):
        pe.wait_ge(K.out_ready.sem, K.out_ready.value(p, s, UNIT))
        if nxt is not None:
            pe.wait_ge(K.front_read.sem, K.front_read.value(p, nxt, FRONT2))
        for j in range(PAIRS2):
            if K.oT_ready.due(p, s, j - 2):
                pe.wait_ge(K.oT_ready.sem, K.oT_ready.value(p, s, j - 2))
            transpose4(nc, K, piece_bank(K, FRONT2 + j),
                       lambda t: V.out[:, t, j, :, :].rearrange("p h d -> p (h d)"), P).then_inc(K.oT_psum.sem, 1)
        pe.wait_ge(K.oT_ready.sem, K.oT_ready.value(p, s, PAIRS2))
        bank = piece_bank(K, FRONT2 + PAIRS2)
        for t in range(UNIT):
            for j in range(PAIRS2):
                last = mm(bank[:, t * P:(t + 1) * P], V.outT[:, j, t * P:(t + 1) * P], W["o"][:, j, :],
                          start=j == 0, stop=j == PAIRS2 - 1)
        last.then_inc(K.proj_psum.sem, 1)

    pe.wait_ge(K.loaded[p], 16 * LOADS[p])
    for i in range(FRONT2):
        piece(0, 0, i)

    def body(s, b, last):
        def pieces(lo, hi):
            if not last:
                for i in range(lo, hi):
                    piece(s + 1, 1 - b, i)
        scores(s, b, 0)
        pieces(0, 2)
        turned(s, 0)
        scores(s, b, 1)
        weighted(s, 0)
        pieces(2, 5)
        turned(s, 1)
        scores(s, b, 2)
        weighted(s, 1)
        pieces(5, 8)
        turned(s, 2)
        scores(s, b, 3)
        weighted(s, 2)
        pieces(8, 10)
        turned(s, 3)
        weighted(s, 3)
        pieces(10, 14)
        project(s, None if last else s + 1)
    over_units(pe, body)


def l2_scalar(nc, act, K):
    p = A2
    V = K.v[p]

    def piece(s, b, i):
        act.wait_ge(K.front_psum.sem, K.front_psum.value(p, s, i + 1))
        bank = piece_bank(K, i)
        if i == 0:
            cT_evacuate(nc, act, K, p, s, b, bank)
        elif i < 5:
            act.activation(V.k[b][:, i - 1, :], bank, ACT.Copy).then_inc(K.front_read.sem, 1)
        elif i == 5:
            yT_evacuate(nc, act, K, p, s, b, bank)
        elif i < 10:
            act.activation(V.q[b][:, i - 6, :], bank, ACT.Copy).then_inc(K.front_read.sem, 1)
        else:
            t = i - 10
            if K.av_psum.due(p, s, 0):
                act.wait_ge(K.av_psum.sem, K.av_psum.value(p, s, 0))
            v = bank.rearrange("p (j h d) -> p j h d", j=PAIRS2, h=2)
            for y in range(2):
                for h in range(2):
                    last = act.activation(V.vd[half(h), t, y, :, 0:DH2], v[half(y), :, h, :], ACT.Copy)
            last.then_inc(K.front_read.sem, 1)

    def probs(s, t):
        act.wait_ge(K.shift_ready.sem, K.shift_ready.value(p, s, t + 1))
        pr = V.probs[t % 2]
        act.activation(pr, pr, ACT.Exp, scale=DH2 ** -0.5).then_inc(K.probs_ready.sem, 1)

    def turned(s, t):
        act.wait_ge(K.pT_psum.sem, K.pT_psum.value(p, s, t + 1))
        if K.av_psum.due(p, s, t - 1):
            act.wait_ge(K.av_psum.sem, K.av_psum.value(p, s, t - 1))
        act.activation(V.pT[t % 2], K.bank[PT2_BANK].rearrange("p (j q) -> p j q", q=P),
                       ACT.Copy).then_inc(K.pT_ready.sem, 1)

    for i in range(FRONT2):
        piece(0, 0, i)

    def body(s, b, last):
        def pieces(lo, hi):
            if not last:
                for i in range(lo, hi):
                    piece(s + 1, 1 - b, i)
        pieces(0, 1)
        probs(s, 0)
        pieces(1, 2)
        turned(s, 0)
        probs(s, 1)
        pieces(2, 5)
        turned(s, 1)
        probs(s, 2)
        pieces(5, 8)
        turned(s, 2)
        probs(s, 3)
        pieces(8, 10)
        turned(s, 3)
        pieces(10, 14)
        for j in range(PAIRS2):
            act.wait_ge(K.oT_psum.sem, K.oT_psum.value(p, s, j + 1))
            if K.proj_psum.due(p, s, 0):
                act.wait_ge(K.proj_psum.sem, K.proj_psum.value(p, s, 0))
            act.activation(V.outT[:, j, :], piece_bank(K, FRONT2 + j), ACT.Copy).then_inc(K.oT_ready.sem, 1)
    over_units(act, body)


def l2_vector(nc, dve, K):
    p = A2
    V = K.v[p]

    def shift(s, t):
        steps = Steps(K.max_steps, p, s, t)
        dve.wait_ge(K.s_psum.sem, K.s_psum.value(p, s, t + 1))
        sc = K.ps[:, 0:2, 0:PAIRS2 * SEQ].rearrange("p h (j k) -> p h j k", k=SEQ)
        mx = V.max[:, t % 2, :, :]
        dve.tensor_reduce(mx, sc, axis=AX.X, op=ALU.max).then_inc(steps.sem, steps.one())
        dve.wait_ge(steps.sem, steps.value())
        if K.pT_psum.due(p, s, t - 1):
            dve.wait_ge(K.pT_psum.sem, K.pT_psum.value(p, s, t - 1))
        dve.tensor_tensor(V.probs[t % 2].rearrange("p j h k -> p h j k"), sc,
                          mx.unsqueeze(3).to_broadcast([P, 2, PAIRS2, SEQ]), ALU.subtract).then_inc(K.shift_ready.sem, 1)

    def outputs(s, t):
        dve.wait_ge(K.av_psum.sem, K.av_psum.value(p, s, t + 1))
        if t == 0:
            if K.oT_psum.due(p, s, 0):
                dve.wait_ge(K.oT_psum.sem, K.oT_psum.value(p, s, 0))
        steps = Steps(K.sum_steps, p, s, t)
        o = K.ps[:, O2_BANKS[0]:O2_BANKS[1] + 1, 0:PAIRS2 * (DH2 + 1)].rearrange("p h (j d) -> p h j d", j=PAIRS2)
        dve.reciprocal(V.rsum, o[:, :, :, DH2]).then_inc(steps.sem, steps.one())
        dve.wait_ge(steps.sem, steps.value())
        dve.tensor_tensor(V.out[:, t].rearrange("p j h d -> p h j d"), o[:, :, :, 0:DH2],
                          V.rsum.unsqueeze(3).to_broadcast([P, 2, PAIRS2, DH2]), ALU.mult).then_inc(K.out_ready.sem, 1)

    x_statistics(nc, dve, K, p, 0)
    x_normed(nc, dve, K, p, 0)

    def body(s, b, last):
        shift(s, 0)
        if not last:
            x_statistics(nc, dve, K, p, s + 1)
        shift(s, 1)
        outputs(s, 0)
        if not last:
            x_normed(nc, dve, K, p, s + 1)
        shift(s, 2)
        outputs(s, 1)
        shift(s, 3)
        outputs(s, 2)
        outputs(s, 3)
        dve.wait_ge(K.proj_psum.sem, K.proj_psum.value(p, s, 1))
        add_residual(nc, dve, K, p, s, V.res,
                     piece_bank(K, FRONT2 + PAIRS2).rearrange("p (t d) -> p t d", t=UNIT), K.row["bo2"])
    over_units(dve, body)


def norm_pool(nc, pool, K, p):
    rstd_pool(nc, pool, K, p, 0, False)

    def body(s, b, last):
        if not last:
            rstd_pool(nc, pool, K, p, s + 1, False)
    over_units(pool, body)


S3_BANKS = ((0, 1), (2, 3))
PT3_BANK, O3_BANK = 4, 5
PIECE3 = (6, 7, 6, 7, 6, 7, 6, 7, 6, 7, 6)
OT3_BANK, Y3_BANK = 6, 7


def l3_tensor(nc, pe, K):
    p = A3
    V, W = K.v[p], K.wp[p]
    mm = nc.tensor.matmul

    def piece(s, b, i):
        bank = K.bank[PIECE3[i]]
        if i == 0:
            pe.wait_ge(K.c_ready.sem, K.c_ready.value(p, s, 1))
            if K.front_read.due(p, s, 0):
                pe.wait_ge(K.front_read.sem, K.front_read.value(p, s, 0))
            last = transpose4(nc, K, bank, lambda t: V.ctxn[:, t, :], DC)
        elif i == 1:
            pe.wait_ge(K.y_ready.sem, K.y_ready.value(p, s, 1))
            last = transpose4(nc, K, bank, lambda t: K.yt[:, t, :], P)
        elif i < 4:
            pe.wait_ge(K.front_read.sem, K.front_read.value(p, s, i - 1))
            for t in range(2):
                tt = 2 * (i - 2) + t
                last = mm(bank[:, t * 2 * D:(t + 1) * 2 * D], V.cT[b][:, tt * P:(tt + 1) * P], W["kv"][:, :],
                          start=True, stop=True)
        elif i < 8:
            t = i - 4
            pe.wait_ge(K.front_read.sem, K.front_read.value(p, s, i - 1))
            last = mm(bank[:, 0:3 * D], K.yT[b][:, t * P:(t + 1) * P], W["qkv"][:, :], start=True, stop=True)
        else:
            if i == 8:
                pe.wait_ge(K.qk_normed.sem, K.qk_normed.value(p, s, 1))
                pe.wait_ge(K.front_read.sem, K.front_read.value(p, s, 8))
            elif i == 9:
                if K.x_done.due(p, s, 0):
                    pe.wait_ge(K.x_done.sem, K.x_done.value(p, s, 0))
            else:
                pe.wait_ge(K.front_read.sem, K.front_read.value(p, s, 9))
            last = transpose4(nc, K, bank, lambda t: V.normed[:, i - 8, t, :], P)
        last.then_inc(K.front_psum.sem, 1)

    def scores(s, b, t):
        if t == 0:
            pe.wait_ge(K.front_read.sem, K.front_read.value(p, s, FRONT3))
        if K.shift_ready.due(p, s, t - 1):
            pe.wait_ge(K.shift_ready.sem, K.shift_ready.value(p, s, t - 1))
        for h in range(2):
            for y in range(2):
                rows, qs = whole_first(h + y == 0, y, t)
                last = mm(K.bank[S3_BANKS[t % 2][h]][rows, 0:KEYS3], V.q[b][half(h), qs],
                          V.k[b][half(h), t, y, :, :].rearrange("p c k -> p (c k)"), start=True, stop=True)
        last.then_inc(K.s_psum.sem, 1)

    def turned(s, t):
        pe.wait_ge(K.probs_ready.sem, K.probs_ready.value(p, s, t + 1))
        if K.pT_ready.due(p, s, t):
            pe.wait_ge(K.pT_ready.sem, K.pT_ready.value(p, s, t))
        for h in range(2):
            last = nc.tensor.transpose(K.bank[PT3_BANK][:, h * P:(h + 1) * P], V.probs[t % 2][:, h, :], K.ident[:, :])
        last.then_inc(K.pT_psum.sem, 1)

    def weighted(s, b, t):
        pe.wait_ge(K.pT_ready.sem, K.pT_ready.value(p, s, t + 1))
        if K.out_ready.due(p, s, t):
            pe.wait_ge(K.out_ready.sem, K.out_ready.value(p, s, t))
        if t == 0:
            pe.wait_ge(K.v_ready.sem, K.v_ready.value(p, s, 1))
        n = DH2 + 1
        for h in range(2):
            for y in range(2):
                last = mm(K.bank[O3_BANK][half(y), h * n:(h + 1) * n], V.pT[t % 2][:, h, half(y)],
                          V.vd[b][:, t, y, h, :], start=True, stop=True)
        last.then_inc(K.av_psum.sem, 1)

    def project(s, nxt):
        pe.wait_ge(K.out_ready.sem, K.out_ready.value(p, s, UNIT))
        if nxt is not None:
            pe.wait_ge(K.front_read.sem, K.front_read.value(p, nxt, 8))
        transpose4(nc, K, K.bank[OT3_BANK], lambda t: V.out[:, t].rearrange("p h d -> p (h d)"), P).then_inc(K.oT_psum.sem, 1)
        pe.wait_ge(K.oT_ready.sem, K.oT_ready.value(p, s, 1))
        for t in range(UNIT):
            last = mm(K.bank[Y3_BANK][:, t * P:(t + 1) * P], V.outT[:, t * P:(t + 1) * P], W["o"][:, :],
                      start=True, stop=True)
        last.then_inc(K.proj_psum.sem, 1)

    def pieces(s, b, lo, hi):
        for i in range(lo, hi):
            piece(s, b, i)

    pe.wait_ge(K.loaded[p], 16 * LOADS[p])
    raw = W["raw"]
    for n, i in enumerate((0, 1, 2, 3)):
        nc.tensor.transpose(K.bank[0][:, n * P:(n + 1) * P], raw[:, i, :], K.ident[:, :])
    for c in range(2):
        last = nc.tensor.transpose(K.bank[1][0:DC, c * P:(c + 1) * P], raw[:, 4 + c, 0:DC], K.ident[:, :])
    last.then_inc(K.l3w_psum, 1)
    pe.wait_ge(K.l3w_ready, 3)
    pieces(0, 0, 0, FRONT3)

    def body(s, b, last):
        scores(s, b, 0)
        scores(s, b, 1)
        turned(s, 0)
        scores(s, b, 2)
        weighted(s, b, 0)
        if not last:
            pieces(s + 1, 1 - b, 0, 2)
        turned(s, 1)
        scores(s, b, 3)
        weighted(s, b, 1)
        if not last:
            pieces(s + 1, 1 - b, 2, 8)
        turned(s, 2)
        weighted(s, b, 2)
        turned(s, 3)
        weighted(s, b, 3)
        project(s, None if last else s + 1)
        if not last:
            pieces(s + 1, 1 - b, 8, 11)
    over_units(pe, body)


def l3_scalar(nc, act, K):
    p = A3
    V, W = K.v[p], K.wp[p]

    def piece(s, b, i):
        act.wait_ge(K.front_psum.sem, K.front_psum.value(p, s, i + 1))
        bank = K.bank[PIECE3[i]]
        if i == 0:
            cT_evacuate(nc, act, K, p, s, b, bank)
            return
        if i == 1:
            yT_evacuate(nc, act, K, p, s, b, bank)
            return
        if i < 8:
            if K.squares.due(p, s, 0):
                act.wait_ge(K.squares.sem, K.squares.value(p, s, 0))
            if K.qk_normed.due(p, s, 0):
                act.wait_ge(K.qk_normed.sem, K.qk_normed.value(p, s, 0))
            if K.v_ready.due(p, s, 0):
                act.wait_ge(K.v_ready.sem, K.v_ready.value(p, s, 0))
        if i < 4:
            last = act.activation(V.raw[:, 2 * (i - 2):2 * (i - 1), 3:5, :].rearrange("p t c d -> p t (c d)"),
                                  bank.rearrange("p (t n) -> p t n", t=2), ACT.Copy)
        elif i < 8:
            last = act.activation(V.raw[:, i - 4, 0:3, :].rearrange("p c d -> p (c d)"), bank[:, 0:3 * D], ACT.Copy)
        elif i == 8:
            last = act.activation(V.q[b], bank, ACT.Copy, scale=K.col["qn_g"])
        else:
            last = act.activation(V.k[b][:, :, :, 10 - i, :] if i == 10 else V.k[b][:, :, :, 1, :],
                                  bank.rearrange("p (t y k) -> p t y k", t=UNIT, y=2), ACT.Copy, scale=K.col["kn_g"])
        last.then_inc(K.front_read.sem, 1)

    def probs(s, t):
        act.wait_ge(K.shift_ready.sem, K.shift_ready.value(p, s, t + 1))
        pr = V.probs[t % 2]
        act.activation(pr, pr, ACT.Exp, scale=DH2 ** -0.5).then_inc(K.probs_ready.sem, 1)

    def turned(s, t):
        act.wait_ge(K.pT_psum.sem, K.pT_psum.value(p, s, t + 1))
        if K.av_psum.due(p, s, t - 1):
            act.wait_ge(K.av_psum.sem, K.av_psum.value(p, s, t - 1))
        act.activation(V.pT[t % 2], K.bank[PT3_BANK][:, 0:2 * P].rearrange("p (h q) -> p h q", q=P),
                       ACT.Copy).then_inc(K.pT_ready.sem, 1)

    act.wait_ge(K.l3w_psum, 1)
    act.activation(W["qkv"][:, :], K.bank[0][:, 0:3 * P], ACT.Copy).then_inc(K.l3w_ready, 1)
    act.activation(W["o"][:, :], K.bank[0][:, 3 * P:4 * P], ACT.Copy).then_inc(K.l3w_ready, 1)
    act.activation(W["kv"][:, :], K.bank[1][0:DC, 0:2 * P], ACT.Copy).then_inc(K.l3w_ready, 1)
    for i in range(FRONT3):
        piece(0, 0, i)

    def body(s, b, last):
        def pieces(lo, hi):
            if not last:
                for i in range(lo, hi):
                    piece(s + 1, 1 - b, i)
        probs(s, 0)
        probs(s, 1)
        turned(s, 0)
        probs(s, 2)
        pieces(0, 2)
        turned(s, 1)
        probs(s, 3)
        pieces(2, 8)
        turned(s, 2)
        turned(s, 3)
        act.wait_ge(K.oT_psum.sem, K.oT_psum.value(p, s, 1))
        if K.proj_psum.due(p, s, 0):
            act.wait_ge(K.proj_psum.sem, K.proj_psum.value(p, s, 0))
        act.activation(V.outT, K.bank[OT3_BANK], ACT.Copy).then_inc(K.oT_ready.sem, 1)
        pieces(8, 11)
    over_units(act, body)


def l3_vector(nc, dve, K):
    p = A3
    V = K.v[p]

    def shift(s, b, t):
        steps = Steps(K.max_steps, p, s, 2 * t)
        dve.wait_ge(K.s_psum.sem, K.s_psum.value(p, s, t + 1))
        if K.pT_psum.due(p, s, t - 1):
            dve.wait_ge(K.pT_psum.sem, K.pT_psum.value(p, s, t - 1))
        if t == 0:
            dve.wait_ge(K.maskbias.sem, K.maskbias.value(p, s, 1))
        lo, hi = S3_BANKS[t % 2]
        pr, mx = V.probs[t % 2], V.max[:, t % 2, :]
        dve.tensor_tensor(pr, K.ps[:, lo:hi + 1, 0:KEYS3],
                          V.mb[b][:, t, :].unsqueeze(1).to_broadcast([P, 2, KEYS3]), ALU.add).then_inc(steps.sem, steps.one())
        dve.wait_ge(steps.sem, steps.value())
        dve.tensor_reduce(mx, pr, axis=AX.X, op=ALU.max).then_inc(steps.sem, steps.one())
        dve.wait_ge(steps.sem, steps.value())
        dve.tensor_tensor(pr, pr, mx.unsqueeze(2).to_broadcast([P, 2, KEYS3]), ALU.subtract).then_inc(K.shift_ready.sem, 1)

    def outputs(s, t):
        dve.wait_ge(K.av_psum.sem, K.av_psum.value(p, s, t + 1))
        if t == 0:
            if K.oT_psum.due(p, s, 0):
                dve.wait_ge(K.oT_psum.sem, K.oT_psum.value(p, s, 0))
        steps = Steps(K.sum_steps, p, s, t)
        o = K.bank[O3_BANK][:, 0:2 * (DH2 + 1)].rearrange("p (h d) -> p h d", h=2)
        dve.reciprocal(V.rsum, o[:, :, DH2]).then_inc(steps.sem, steps.one())
        dve.wait_ge(steps.sem, steps.value())
        dve.tensor_tensor(V.out[:, t], o[:, :, 0:DH2], V.rsum.unsqueeze(2).to_broadcast([P, 2, DH2]),
                          ALU.mult).then_inc(K.out_ready.sem, 1)

    def mask_bias(s, b):
        if K.shift_ready.due(p, s, -UNIT):
            dve.wait_ge(K.shift_ready.sem, K.shift_ready.value(p, s, -UNIT))
        dve.tensor_scalar(V.mb[b][:, :, 0:SEQ], K.mask[:, bass.ds(s * UNIT, UNIT), :], 1.0, MASKED,
                          ALU.subtract, ALU.mult).then_inc(K.maskbias.sem, 1)

    def square_sums(s, b):
        dve.wait_ge(K.squares.sem, K.squares.value(p, s, 1))
        dve.wait_ge(K.front_read.sem, K.front_read.value(p, s, 8))
        for src, slot in ((0, 4), (1, 2)):
            for y in range(2):
                last = dve.tensor_copy(V.vd[b][half(src), :, y, :, 0:DH2],
                                       V.raw[half(y), :, slot, :].rearrange("p t (h d) -> p t h d", h=2))
        last.then_inc(K.v_ready.sem, 1)
        steps = Steps(K.rms_steps, p, s)
        dve.tensor_reduce(V.ss, V.sq.rearrange("p t c (h d) -> p t c h d", h=2), axis=AX.X, op=ALU.add).then_inc(steps.sem, steps.one())
        dve.wait_ge(steps.sem, steps.value())
        dve.tensor_scalar(V.ss, V.ss, 1.0 / DH2, 1e-16, ALU.mult, ALU.max).then_inc(steps.sem, steps.one())
        steps.ended()

    def rms_normed(s):
        dve.wait_ge(K.rms_ready.sem, K.rms_ready.value(p, s, 1))
        if K.front_psum.due(p, s, 0):
            dve.wait_ge(K.front_psum.sem, K.front_psum.value(p, s, 0))
        for c, slot in enumerate((0, 1, 3)):
            last = dve.tensor_tensor(V.normed[:, c, :, :].rearrange("p t (h d) -> p t h d", h=2),
                                     V.raw[:, :, slot, :].rearrange("p t (h d) -> p t h d", h=2),
                                     V.rms[:, :, c, :].unsqueeze(3).to_broadcast([P, UNIT, 2, DH2]), ALU.mult)
        last.then_inc(K.qk_normed.sem, 1)

    x_statistics(nc, dve, K, p, 0)
    ctx_statistics(nc, dve, K, p, 0, 0)
    ctx_normed(nc, dve, K, p, 0, 0)
    x_normed(nc, dve, K, p, 0)
    mask_bias(0, 0)
    square_sums(0, 0)
    rms_normed(0)

    def body(s, b, last):
        shift(s, b, 0)
        if not last:
            ctx_statistics(nc, dve, K, p, s + 1, 1 - b)
            x_statistics(nc, dve, K, p, s + 1)
        shift(s, b, 1)
        if not last:
            ctx_normed(nc, dve, K, p, s + 1, 1 - b)
            x_normed(nc, dve, K, p, s + 1)
        shift(s, b, 2)
        outputs(s, 0)
        shift(s, b, 3)
        if not last:
            mask_bias(s + 1, 1 - b)
        outputs(s, 1)
        outputs(s, 2)
        outputs(s, 3)
        if not last:
            square_sums(s + 1, 1 - b)
        dve.wait_ge(K.proj_psum.sem, K.proj_psum.value(p, s, 1))
        add_residual(nc, dve, K, p, s, V.res, K.bank[Y3_BANK].rearrange("p (t d) -> p t d", t=UNIT), K.row["bo3"])
        if not last:
            rms_normed(s + 1)
    over_units(dve, body)


def l3_pool(nc, pool, K):
    p = A3
    V = K.v[p]

    def front(s):
        rstd_pool(nc, pool, K, p, s, True)
        rstd_pool(nc, pool, K, p, s, False)

    def squares(s):
        pool.wait_ge(K.front_read.sem, K.front_read.value(p, s, 8))
        if K.rms_steps.due(p, s, 0):
            pool.wait_ge(K.rms_steps.sem, K.rms_steps.value(p, s, 0))
        pool.tensor_tensor(V.sq[:, :, 0:2, :], V.raw[:, :, 0:2, :], V.raw[:, :, 0:2, :], ALU.mult)
        pool.tensor_tensor(V.sq[:, :, 2, :], V.raw[:, :, 3, :], V.raw[:, :, 3, :], ALU.mult).then_inc(K.squares.sem, 1)
        pool.wait_ge(K.rms_steps.sem, K.rms_steps.value(p, s, 2))
        pool.tensor_tensor(V.rms.rearrange("p t c h -> p (t c h)"), V.ss.rearrange("p t c h -> p (t c h)"),
                           K.minus_half[:, 0:UNIT * 6], ALU.pow).then_inc(K.rms_ready.sem, 1)

    front(0)
    squares(0)

    def body(s, b, last):
        if not last:
            front(s + 1)
            squares(s + 1)
    over_units(pool, body)


G_BANKS, U_BANKS, C_BANKS, D_BANK, R_BANK = (0, 1), (2, 3), (4, 7), 5, 6
AT = {F0: (3, 5, 9), F1: (3, 5, 9), F2: (2, 4, 6)}


def expert_of(p, r):
    return r // 2 if p == F1 else r


def front_tensor(nc, pe, K, p, s, b, part, bank):
    if part == 0:
        pe.wait_ge(K.y_ready.sem, K.y_ready.value(p, s, 1))
        if K.x_done.due(p, s, -1):
            pe.wait_ge(K.x_done.sem, K.x_done.value(p, s, -1))
        transpose4(nc, K, bank, lambda t: K.yt[:, t, :], P).then_inc(K.yT_psum.sem, 1)
    elif part == 1:
        pe.wait_ge(K.yT_ready.sem, K.yT_ready.value(p, s, 1))
        E = EXPERTS[p]
        for t in range(UNIT):
            last = nc.tensor.matmul(bank[:, t * E:(t + 1) * E], K.yT[b][:, t * P:(t + 1) * P], K.rcol[p], start=True, stop=True)
        last.then_inc(K.logits_psum.sem, 1)
    else:
        E = 32 if p == F0 else 8
        pe.wait_ge(K.route_steps.sem, K.route_steps.value(p, s, K.route_steps.counts[p]))
        cw = route_views(K, p).cw
        transpose4(nc, K, bank, lambda t: cw[:, t, :], E).then_inc(K.cw_psum.sem, 1)


def back_tensor(nc, pe, K, p, s, nxt, bank):
    pe.wait_ge(K.dt_ready.sem, K.dt_ready.value(p, s, 1))
    if nxt is not None:
        pe.wait_ge(K.cwT_ready.sem, K.cwT_ready.value(p, nxt, 1))
    transpose4(nc, K, bank, lambda t: K.v[p].dt[:, t * P:(t + 1) * P], P).then_inc(K.outT_psum.sem, 1)


def experts_tensor(nc, pe, K, p):
    V, W = K.v[p], K.wf[p]
    J, SH = CHUNKS[p], SHARED[p]
    mm, bank = nc.tensor.matmul, K.bank

    def combine(s, b, r):
        if r == 0:
            pe.wait_ge(K.cwT_ready.sem, K.cwT_ready.value(p, s, 1))
        if p == F2:
            if K.scaled_ready.due(p, s, r - 1):
                pe.wait_ge(K.scaled_ready.sem, K.scaled_ready.value(p, s, r - 1))
        else:
            if K.hid_ready.due(p, s, r + SH - 1):
                pe.wait_ge(K.hid_ready.sem, K.hid_ready.value(p, s, r + SH - 1))
        mm(bank[C_BANKS[r % 2]], K.sel[:, expert_of(p, r), :], K.cwT[:, b, :], start=True, stop=True).then_inc(K.c_psum.sem, 1)

    def body(s, b, last):
        pe.wait_ge(K.yT_ready.sem, K.yT_ready.value(p, s, 1))
        for j in range(J + 1):
            if j < J:
                if p == F2 and j + 1 - SH >= 0 and j + 1 < J:
                    combine(s, b, j + 1 - SH)
                rhs = K.yT[b][:, :]
                if p == F2 and j >= SH:
                    pe.wait_ge(K.scaled_ready.sem, K.scaled_ready.value(p, s, j - SH + 1))
                    rhs = V.scaled[(j - SH) % 2]
                if K.silu_ready.due(p, s, j - 1):
                    pe.wait_ge(K.silu_ready.sem, K.silu_ready.value(p, s, j - 1))
                mm(bank[G_BANKS[j % 2]], W[:, 0, j, :], rhs, start=True, stop=True).then_inc(K.g_psum.sem, 1)
                if K.hid_ready.due(p, s, j - 1):
                    pe.wait_ge(K.hid_ready.sem, K.hid_ready.value(p, s, j - 1))
                mm(bank[U_BANKS[j % 2]], W[:, 1, j, :], rhs, start=True, stop=True).then_inc(K.u_psum.sem, 1)
                if p != F2 and j >= SH:
                    combine(s, b, j - SH)
            if j >= 1:
                if j == 1:
                    if K.dt_ready.due(p, s, 0):
                        pe.wait_ge(K.dt_ready.sem, K.dt_ready.value(p, s, 0))
                pe.wait_ge(K.hid_ready.sem, K.hid_ready.value(p, s, j))
                mm(bank[D_BANK], W[:, 2, j - 1, :], V.hid[(j - 1) % 2], start=j == 1, stop=j == J).then_inc(K.down_done.sem, 1)
            if not last and j in AT[p]:
                front_tensor(nc, pe, K, p, s + 1, 1 - b, AT[p].index(j), bank[R_BANK])
        back_tensor(nc, pe, K, p, s, None if last else s + 1, bank[R_BANK])

    pe.wait_ge(K.loaded[p], 16 * LOADS[p])
    if p == F0:
        raw = K.wf[F1]
        for n, (i0, m) in enumerate(PREP_GROUPS):
            if n >= 2:
                pe.wait_ge(K.prep_ready, n - 1)
            for i in range(m):
                last = nc.tensor.transpose(bank[n % 2][:, i * P:(i + 1) * P], raw[:, (i0 + i) // 17, (i0 + i) % 17, :],
                                           K.ident[:, :])
            last.then_inc(K.prep_psum, 1)
        pe.wait_ge(K.prep_ready, PREP_F0)
    for part in range(3):
        front_tensor(nc, pe, K, p, 0, 0, part, bank[R_BANK])
    over_units(pe, body)


def experts_scalar(nc, act, K, p):
    V = K.v[p]
    J = CHUNKS[p]

    def body(s, b, last):
        for j in range(J):
            act.wait_ge(K.g_psum.sem, K.g_psum.value(p, s, j + 1))
            if K.hid_ready.due(p, s, j - 1):
                act.wait_ge(K.hid_ready.sem, K.hid_ready.value(p, s, j - 1))
            act.activation(V.silu[j % 2], K.bank[G_BANKS[j % 2]], ACT.Silu).then_inc(K.silu_ready.sem, 1)
            if not last and j in AT[p]:
                front_scalar(nc, act, K, p, s + 1, 1 - b, AT[p].index(j), K.bank[R_BANK])
        scale_outputs(nc, act, K, p, s, K.bank[D_BANK])

    if p == F0:
        for n, (i0, m) in enumerate(PREP_GROUPS):
            act.wait_ge(K.prep_psum, n + 1)
            act.activation(K.wf[F0].rearrange("p w j n -> p (w j) n")[:, i0:i0 + m, :],
                           K.bank[n % 2][:, 0:m * P].rearrange("p (w n) -> p w n", n=P), ACT.Copy).then_inc(K.prep_ready, 1)
    for part in range(3):
        front_scalar(nc, act, K, p, 0, 0, part, K.bank[R_BANK])
    over_units(act, body)


def scale_outputs(nc, act, K, p, s, bank):
    act.wait_ge(K.down_done.sem, K.down_done.value(p, s, K.down_done.counts[p]))
    if K.outT_psum.due(p, s, 0):
        act.wait_ge(K.outT_psum.sem, K.outT_psum.value(p, s, 0))
    scale = K.gates[:, 4 + p // 2:5 + p // 2]
    act.activation(K.v[p].dt, bank, ACT.Copy, scale=scale).then_inc(K.dt_ready.sem, 1)


def front_scalar(nc, act, K, p, s, b, part, bank):
    R = route_views(K, p)
    if part == 0:
        yT_evacuate(nc, act, K, p, s, b, bank)
    elif part == 1 and p == F0:
        act.wait_ge(K.logits_psum.sem, K.logits_psum.value(p, s, 1))
        if K.route_steps.due(p, s, 0):
            act.wait_ge(K.route_steps.sem, K.route_steps.value(p, s, 0))
        act.activation(R.score, bank[:, 0:UNIT * 32].rearrange("p (t e) -> p t e", t=UNIT), ACT.Tanh,
                       scale=0.5).then_inc(K.logits_ready.sem, 1)
    elif part == 1:
        act.wait_ge(K.route_steps.sem, K.route_steps.value(p, s, R1_STEPS[p]))
        act.activation(R.e, R.d, ACT.Exp).then_inc(K.exp_ready.sem, 1)


R1_STEPS = {F1: 7, F2: 3, F3: 4}


def route_views(K, p):
    R = Kernel()
    E = 32 if p == F0 else 8
    R.E, at = E, 0
    tile = K.route

    def take(*shape):
        nonlocal at
        n = 1
        for x in shape:
            n *= x
        v = tile[:, at:at + n]
        at += n
        assert at <= 2048
        if len(shape) > 1:
            v = v.rearrange("p (a b) -> p a b", a=shape[0])
        return v

    R.count = [take(UNIT, PAD + 32) for _ in range(3)]
    R.score, R.biased, R.masked = take(UNIT, E), take(UNIT, E), take(UNIT, E)
    R.best, R.tmp, R.d, R.e, R.sel, R.cw = (take(UNIT, n) for n in (8, E, E, E, E, E))
    R.group, R.gsel = take(UNIT, 8), take(UNIT, 8)
    R.n, R.sum, R.inv = take(UNIT, 1), take(UNIT, 1), take(UNIT, 1)
    R.touch = take(UNIT, 1)
    return R


def select_top(nc, dve, R, steps, out, values, threshold, E, k):
    eq = R.count[0]
    thr = threshold.to_broadcast([P, UNIT, E])
    tmp = R.tmp[:, :, 0:E]
    dve.tensor_tensor(out, values, thr, ALU.is_gt).then_inc(steps.sem, steps.one())
    dve.tensor_tensor(eq[:, :, PAD:PAD + E], values, thr, ALU.is_equal).then_inc(steps.sem, steps.one())
    dve.wait_ge(steps.sem, steps.value())
    dve.tensor_reduce(R.n, out, axis=AX.X, op=ALU.add).then_inc(steps.sem, steps.one())
    src, at, sh = eq, 1, 1
    while sh < E:
        dst = R.count[at]
        dve.tensor_tensor(dst[:, :, PAD:PAD + E], src[:, :, PAD:PAD + E], src[:, :, PAD - sh:PAD - sh + E],
                          ALU.add).then_inc(steps.sem, steps.one())
        dve.wait_ge(steps.sem, steps.value())
        src, at, sh = dst, 3 - at, 2 * sh
    dve.tensor_tensor(tmp, src[:, :, PAD:PAD + E], R.n.to_broadcast([P, UNIT, E]), ALU.add).then_inc(steps.sem, steps.one())
    dve.wait_ge(steps.sem, steps.value())
    dve.scalar_tensor_tensor(out=tmp, in0=tmp, scalar=float(k), in1=eq[:, :, PAD:PAD + E], op0=ALU.is_le,
                             op1=ALU.mult).then_inc(steps.sem, steps.one())
    dve.wait_ge(steps.sem, steps.value())
    dve.tensor_tensor(out, out, tmp, ALU.add).then_inc(steps.sem, steps.one())
    dve.wait_ge(steps.sem, steps.value())


def best8(nc, dve, R, steps, values):
    dve.wait_ge(steps.sem, steps.value())
    dve.tensor_copy(R.touch, values[:, :, 0:1]).then_inc(steps.sem, steps.one())
    for t in range(UNIT):
        dve.max(R.best[:, t, :], values[:, t, :]).then_inc(steps.sem, steps.one())
    dve.wait_ge(steps.sem, steps.value())


def route_first(nc, dve, K, p, s, bank):
    R = route_views(K, p)
    steps = Steps(K.route_steps, p, s)
    if p == F0:
        return steps
    dve.wait_ge(K.logits_psum.sem, K.logits_psum.value(p, s, 1))
    n = EXPERTS[p]
    lg = bank[:, 0:UNIT * n].rearrange("p (t e) -> p t e", t=UNIT)
    if p == F1:
        dve.tensor_tensor(R.score, lg, K.ebias1.unsqueeze(1).to_broadcast([P, UNIT, 8]), ALU.add).then_inc(steps.sem, steps.one())
        best8(nc, dve, R, steps, R.score)
        dve.tensor_tensor(R.d, R.score, R.best[:, :, 0:1].to_broadcast([P, UNIT, 8]), ALU.subtract).then_inc(steps.sem, steps.one())
    elif p == F2:
        dve.tensor_copy(R.score, lg).then_inc(steps.sem, steps.one())
        dve.wait_ge(steps.sem, steps.value())
        dve.tensor_reduce(R.sum, R.score, axis=AX.X, op=ALU.max).then_inc(steps.sem, steps.one())
        dve.wait_ge(steps.sem, steps.value())
        dve.tensor_tensor(R.d, R.score, R.sum.to_broadcast([P, UNIT, 8]), ALU.subtract).then_inc(steps.sem, steps.one())
    else:
        dve.wait_ge(K.r2_ready.sem, K.r2_ready.value(p, s, 1))
        r2 = K.lnw[:, 2, :].unsqueeze(2)
        dve.tensor_tensor(R.tmp[:, :, 0:4], lg, r2.to_broadcast([P, UNIT, 4]), ALU.mult).then_inc(steps.sem, steps.one())
        dve.wait_ge(steps.sem, steps.value())
        dve.tensor_tensor(R.score[:, :, 0:4], R.tmp[:, :, 0:4], K.logit_bias3.unsqueeze(1).to_broadcast([P, UNIT, 4]),
                          ALU.add).then_inc(steps.sem, steps.one())
        dve.wait_ge(steps.sem, steps.value())
        dve.tensor_reduce(R.sum, R.score, axis=AX.X, op=ALU.max).then_inc(steps.sem, steps.one())
        dve.wait_ge(steps.sem, steps.value())
        dve.tensor_tensor(R.d, R.score, R.sum.to_broadcast([P, UNIT, 8]), ALU.subtract).then_inc(steps.sem, steps.one())
    assert steps.n == R1_STEPS[p]
    return steps


def route_second(nc, dve, K, p, s, steps, b=0):
    R = route_views(K, p)
    E, k = R.E, TOP[p]

    def over_sum(out, values, extra, scale):
        dve.tensor_reduce(R.sum, values, axis=AX.X, op=ALU.add).then_inc(steps.sem, steps.one())
        dve.wait_ge(steps.sem, steps.value())
        dve.tensor_scalar(R.sum, R.sum, extra, None, ALU.add).then_inc(steps.sem, steps.one())
        dve.wait_ge(steps.sem, steps.value())
        dve.reciprocal(R.inv, R.sum).then_inc(steps.sem, steps.one())
        dve.wait_ge(steps.sem, steps.value())
        dve.scalar_tensor_tensor(out=out, in0=values, scalar=scale, in1=R.inv.to_broadcast([P, UNIT, E]),
                                 op0=ALU.mult, op1=ALU.mult).then_inc(steps.sem, steps.one())

    if p == F0:
        dve.wait_ge(K.logits_ready.sem, K.logits_ready.value(p, s, 1))
        dve.tensor_scalar(R.score, R.score, 0.5, 0.5, ALU.mult, ALU.add).then_inc(steps.sem, steps.one())
        dve.wait_ge(steps.sem, steps.value())
        dve.tensor_tensor(R.biased, R.score, K.ebias0.unsqueeze(1).to_broadcast([P, UNIT, 32]), ALU.add).then_inc(steps.sem, steps.one())
        dve.wait_ge(steps.sem, steps.value())
        grouped = R.biased.rearrange("p t (g e) -> p (t g) e", e=4)
        dve.tensor_reduce(R.group.rearrange("p t g -> p (t g)"), grouped, axis=AX.X, op=ALU.max).then_inc(steps.sem, steps.one())
        best8(nc, dve, R, steps, R.group)
        select_top(nc, dve, R, steps, R.gsel, R.group, R.best[:, :, 3:4], 8, 4)
        dve.tensor_tensor(R.masked.rearrange("p t (g e) -> p (t g) e", e=4), grouped,
                          R.gsel.rearrange("p t g -> p (t g)").unsqueeze(2).to_broadcast([P, UNIT * 8, 4]),
                          ALU.mult).then_inc(steps.sem, steps.one())
        best8(nc, dve, R, steps, R.masked)
        select_top(nc, dve, R, steps, R.sel, R.masked, R.best[:, :, k - 1:k], 32, k)
        dve.tensor_tensor(R.d, R.score, R.sel, ALU.mult).then_inc(steps.sem, steps.one())
        dve.wait_ge(steps.sem, steps.value())
        if K.cw_psum.due(p, s, 0):
            dve.wait_ge(K.cw_psum.sem, K.cw_psum.value(p, s, 0))
        over_sum(R.cw, R.d, 1e-20, 2.5)
    elif p == F1:
        select_top(nc, dve, R, steps, R.sel, R.score, R.best[:, :, k - 1:k], 8, k)
        dve.wait_ge(K.exp_ready.sem, K.exp_ready.value(p, s, 1))
        dve.tensor_tensor(R.tmp, R.e, R.sel, ALU.mult).then_inc(steps.sem, steps.one())
        dve.wait_ge(steps.sem, steps.value())
        if K.cw_psum.due(p, s, 0):
            dve.wait_ge(K.cw_psum.sem, K.cw_psum.value(p, s, 0))
        over_sum(R.cw, R.tmp, 0.0, 1.0)
    else:
        dve.wait_ge(K.exp_ready.sem, K.exp_ready.value(p, s, 1))
        over_sum(R.masked, R.e, 0.0, 1.0)
        best8(nc, dve, R, steps, R.masked)
        select_top(nc, dve, R, steps, R.sel, R.masked, R.best[:, :, k - 1:k], 8, k)
        if p == F2:
            if K.cw_psum.due(p, s, 0):
                dve.wait_ge(K.cw_psum.sem, K.cw_psum.value(p, s, 0))
            dve.tensor_tensor(R.cw, R.masked, R.sel, ALU.mult).then_inc(steps.sem, steps.one())
        else:
            dve.tensor_tensor(R.biased, R.masked, R.sel, ALU.mult).then_inc(steps.sem, steps.one())
            dve.wait_ge(steps.sem, steps.value())
            if K.mix_steps.due(p, s, -E3):
                dve.wait_ge(K.mix_steps.sem, K.mix_steps.value(p, s, -E3))
            over_sum(K.v[p].cw[b], R.biased, 1e-8, 1.0)
    steps.ended()


def split_combine(nc, dve, K, p, s, b, bank):
    E = 32 if p == F0 else 8
    dve.wait_ge(K.cw_psum.sem, K.cw_psum.value(p, s, 1))
    if K.c_psum.due(p, s, -K.c_psum.counts[p]):
        dve.wait_ge(K.c_psum.sem, K.c_psum.value(p, s, -K.c_psum.counts[p]))
    dve.tensor_copy(K.cwT[0:E, b, :], bank[0:E, :]).then_inc(K.cw_steps.sem, 1)
    dve.wait_ge(K.cw_steps.sem, K.cw_steps.value(p, s, 1))
    dve.tensor_tensor(K.cwT[32:32 + E, b, :], bank[0:E, :], K.cwT[0:E, b, :].bitcast(F32),
                      ALU.subtract).then_inc(K.cwT_ready.sem, 1)


def experts_vector(nc, dve, K, p):
    V = K.v[p]
    J, SH = CHUNKS[p], SHARED[p]
    r_bank = K.bank[R_BANK]

    def scaled(s, b, r):
        dve.wait_ge(K.c_psum.sem, K.c_psum.value(p, s, r + 1))
        if r == 0:
            dve.wait_ge(K.yT_ready.sem, K.yT_ready.value(p, s, 1))
        if K.u_psum.due(p, s, r + SH - 1):
            dve.wait_ge(K.u_psum.sem, K.u_psum.value(p, s, r + SH - 1))
        dve.tensor_tensor(V.scaled[r % 2], K.yT[b][:, :], K.bank[C_BANKS[r % 2]], ALU.mult).then_inc(K.scaled_ready.sem, 1)

    def body(s, b, last):
        for j in range(J):
            if p == F2 and j + 1 < J:
                scaled(s, b, j + 1 - SH)
            dve.wait_ge(K.silu_ready.sem, K.silu_ready.value(p, s, j + 1))
            dve.wait_ge(K.u_psum.sem, K.u_psum.value(p, s, j + 1))
            if K.down_done.due(p, s, j - 1):
                dve.wait_ge(K.down_done.sem, K.down_done.value(p, s, j - 1))
            u = K.bank[U_BANKS[j % 2]]
            if p == F2 or j < SH:
                dve.tensor_tensor(V.hid[j % 2], V.silu[j % 2], u, ALU.mult).then_inc(K.hid_ready.sem, 1)
            else:
                r = j - SH
                dve.tensor_tensor(V.prod[j % 2], V.silu[j % 2], u, ALU.mult).then_inc(K.prod_steps.sem, 1)
                dve.wait_ge(K.c_psum.sem, K.c_psum.value(p, s, r + 1))
                dve.wait_ge(K.prod_steps.sem, K.prod_steps.value(p, s, r + 1))
                dve.tensor_tensor(V.hid[j % 2], V.prod[j % 2], K.bank[C_BANKS[r % 2]], ALU.mult).then_inc(K.hid_ready.sem, 1)
            if last:
                continue
            if j == 0:
                x_statistics(nc, dve, K, p, s + 1)
            if j == 1:
                x_normed(nc, dve, K, p, s + 1)
            if j == AT[p][1]:
                steps = route_first(nc, dve, K, p, s + 1, r_bank)
            if j == AT[p][1] + 1:
                route_second(nc, dve, K, p, s + 1, steps)
            if j == AT[p][2]:
                split_combine(nc, dve, K, p, s + 1, 1 - b, r_bank)
        dve.wait_ge(K.outT_psum.sem, K.outT_psum.value(p, s, 1))
        dve.tensor_tensor(xu(K, s), r_bank.rearrange("p (t d) -> p t d", t=UNIT), xu(K, s), ALU.add).then_inc(K.x_done.sem, 1)

    x_statistics(nc, dve, K, p, 0)
    x_normed(nc, dve, K, p, 0)
    steps = route_first(nc, dve, K, p, 0, r_bank)
    route_second(nc, dve, K, p, 0, steps)
    split_combine(nc, dve, K, p, 0, 0, r_bank)
    over_units(dve, body)


H3_BANKS, T3_BANKS, D3_BANK, R3_BANK = (0, 1, 2, 3), (4, 5), 6, 7
E3 = EXPERTS[F3]
Q3 = E3 * HID3 // P
H3 = 2 * UNIT


def l3_experts_tensor(nc, pe, K):
    p = F3
    V = K.v[p]
    mm, bank = nc.tensor.matmul, K.bank

    def rows(s):
        pe.wait_ge(K.y_ready.sem, K.y_ready.value(p, s, 1))
        n = R1_STEPS[p] - K.route_steps.counts[p]
        if K.route_steps.due(p, s, n):
            pe.wait_ge(K.route_steps.sem, K.route_steps.value(p, s, n))
        transpose4(nc, K, bank[R3_BANK], lambda t: K.yt[:, t, :], P).then_inc(K.yT_psum.sem, 1)

    def logits(s, b):
        pe.wait_ge(K.yT_ready.sem, K.yT_ready.value(p, s, 1))
        for t in range(UNIT):
            last = mm(bank[R3_BANK][:, t * E3:(t + 1) * E3], K.yT[b][:, t * P:(t + 1) * P], K.rcol[p],
                      start=True, stop=True)
        last.then_inc(K.logits_psum.sem, 1)

    def hidden(s, b, i):
        t, g = i // 2, i % 2
        if i == 0:
            pe.wait_ge(K.yT_ready.sem, K.yT_ready.value(p, s, 1))
        if K.z_ready.due(p, s, t - 1):
            pe.wait_ge(K.z_ready.sem, K.z_ready.value(p, s, t - 1))
        mm(bank[H3_BANKS[i % 4]], K.yT[b][:, t * P:(t + 1) * P],
           K.w1[:, 2 * g:2 * g + 2, :].rearrange("p e h -> p (e h)"), start=True, stop=True).then_inc(K.g_psum.sem, 1)

    def turned(s, b, q):
        if q == 0:
            pe.wait_ge(K.z_ready.sem, K.z_ready.value(p, s, UNIT))
        if K.hid_ready.due(p, s, q - 1):
            pe.wait_ge(K.hid_ready.sem, K.hid_ready.value(p, s, q - 1))
        transpose4(nc, K, bank[T3_BANKS[q % 2]], lambda t: V.z[b][:, t, q * P:(q + 1) * P], P).then_inc(K.zT_psum.sem, 1)

    def down(s, e):
        pe.wait_ge(K.hid_ready.sem, K.hid_ready.value(p, s, 2 * e + 2))
        if K.mix_steps.due(p, s, e):
            pe.wait_ge(K.mix_steps.sem, K.mix_steps.value(p, s, e))
        for t in range(UNIT):
            for c in range(2):
                last = mm(bank[D3_BANK][:, t * D:(t + 1) * D], V.hid[(2 * e + c) % 4][:, t * P:(t + 1) * P],
                          K.w2[:, 2 * e + c, :], start=c == 0, stop=c == 1)
        last.then_inc(K.down_done.sem, 1)

    def body(s, b, later):
        n, nb = s + 1, 1 - b

        def first_stage(*products):
            if later:
                for i in products:
                    hidden(n, nb, i)
        turned(s, b, 0)
        first_stage(0, 1)
        turned(s, b, 1)
        turned(s, b, 2)
        first_stage(2, 3)
        turned(s, b, 3)
        down(s, 0)
        if later:
            logits(n, nb)
        turned(s, b, 4)
        first_stage(4)
        turned(s, b, 5)
        down(s, 1)
        first_stage(5)
        turned(s, b, 6)
        first_stage(6)
        turned(s, b, 7)
        down(s, 2)
        first_stage(7)
        if later == 2:
            rows(s + 2)
        down(s, 3)

    pe.wait_ge(K.w3_steps, 4 + 1)
    mm(bank[R3_BANK][:, 0:E3], V.rn_b, K.rcol[F3], start=True, stop=True).then_inc(K.bias3_psum, 1)
    pe.wait_ge(K.w3_steps, 4 + 1 + 2)
    rows(0)
    logits(0, 0)
    for i in range(H3):
        hidden(0, 0, i)
    rows(1)
    over_units_ahead(pe, body)


def l3_experts_scalar(nc, act, K):
    p = F3
    V = K.v[p]

    def squares(s, t):
        act.wait_ge(K.g_psum.sem, K.g_psum.value(p, s, 2 * t + 2))
        if K.var_steps.due(p, s, t - 1):
            act.wait_ge(K.var_steps.sem, K.var_steps.value(p, s, t - 1))
        for e in range(E3):
            last = act.activation(V.sq[:, (t % 2) * E3 + e, :], K.bank[H3_BANKS[(2 * t + e // 2) % 4]][:, (e % 2) * HID3:(e % 2 + 1) * HID3],
                                  ACT.Square, accum_out=V.ss[:, t % 2, e:e + 1])
        last.then_inc(K.sq_ready.sem, 1)

    def relu(s, q):
        act.wait_ge(K.zT_psum.sem, K.zT_psum.value(p, s, q + 1))
        if K.down_done.due(p, s, (q - 4) // 2 + 1):
            act.wait_ge(K.down_done.sem, K.down_done.value(p, s, (q - 4) // 2 + 1))
        act.activation(V.hid[q % 4], K.bank[T3_BANKS[q % 2]], ACT.Relu, scale=K.ln3_g[:, q:q + 1],
                       bias=K.ln3_b[:, q:q + 1]).then_inc(K.hid_ready.sem, 1)

    def exponentials(s):
        R = route_views(K, p)
        act.wait_ge(K.route_steps.sem, K.route_steps.value(p, s, R1_STEPS[p]))
        act.activation(R.e, R.d, ACT.Exp).then_inc(K.exp_ready.sem, 1)

    def body(s, b, later):
        n = s + 1
        relu(s, 0)
        if later:
            squares(n, 0)
        relu(s, 1)
        relu(s, 2)
        if later:
            squares(n, 1)
        relu(s, 3)
        relu(s, 4)
        relu(s, 5)
        if later:
            exponentials(n)
            squares(n, 2)
        relu(s, 6)
        relu(s, 7)
        if later:
            squares(n, 3)
        if later == 2:
            yT_evacuate(nc, act, K, p, s + 2, b, K.bank[R3_BANK])

    yT_evacuate(nc, act, K, p, 0, 0, K.bank[R3_BANK])
    exponentials(0)
    for t in range(UNIT):
        squares(0, t)
    yT_evacuate(nc, act, K, p, 1, 1, K.bank[R3_BANK])
    over_units_ahead(act, body)


def l3_experts_vector(nc, dve, K):
    p = F3
    V = K.v[p]
    r_bank = K.bank[R3_BANK]

    def second_norm(s):
        w = K.lnw
        steps = Steps(K.r2_steps, p, s)
        dve.wait_ge(K.rstd_ready.sem, K.rstd_ready.value(p, s, 1))
        dve.tensor_tensor(w[:, 3, :], w[:, 0, :], w[:, 0, :], ALU.mult).then_inc(steps.sem, steps.one())
        dve.wait_ge(steps.sem, steps.value())
        dve.tensor_tensor(w[:, 3, :], w[:, 3, :], w[:, 5, :], ALU.mult).then_inc(steps.sem, steps.one())
        dve.wait_ge(steps.sem, steps.value())
        dve.tensor_scalar(w[:, 3, :], w[:, 3, :], EPS, None, ALU.add).then_inc(steps.sem, steps.one())

    def variance(s, t):
        dve.wait_ge(K.sq_ready.sem, K.sq_ready.value(p, s, t + 1))
        if K.rinv_ready.due(p, s, t - 1):
            dve.wait_ge(K.rinv_ready.sem, K.rinv_ready.value(p, s, t - 1))
        dve.tensor_scalar(V.var[:, t % 2, :], V.ss[:, t % 2, :], 1.0 / HID3, EPS, ALU.mult,
                          ALU.add).then_inc(K.var_steps.sem, 1)

    def normed(s, b, t):
        dve.wait_ge(K.rinv_ready.sem, K.rinv_ready.value(p, s, t + 1))
        if t == 0 and K.zT_psum.due(p, s, -Q3):
            dve.wait_ge(K.zT_psum.sem, K.zT_psum.value(p, s, -Q3))
        for e in range(E3):
            last = dve.tensor_scalar(V.z[b][:, t, e * HID3:(e + 1) * HID3],
                                     K.bank[H3_BANKS[(2 * t + e // 2) % 4]][:, (e % 2) * HID3:(e % 2 + 1) * HID3],
                                     V.rinv[:, t % 2, e:e + 1], None, ALU.mult)
        last.then_inc(K.z_ready.sem, 1)

    def mix(s, b, e):
        dve.wait_ge(K.down_done.sem, K.down_done.value(p, s, e + 1))
        if e == 0:
            if K.onorm_ready.due(p, s, 0):
                dve.wait_ge(K.onorm_ready.sem, K.onorm_ready.value(p, s, 0))
        else:
            dve.wait_ge(K.mix_steps.sem, K.mix_steps.value(p, s, e))
        for t in range(UNIT):
            out, c = K.bank[D3_BANK][:, t * D:(t + 1) * D], V.cw[b][:, t, e:e + 1]
            if e == 0:
                last = dve.tensor_scalar(V.mixed[:, t, :], out, c, None, ALU.mult)
            else:
                last = dve.scalar_tensor_tensor(out=V.mixed[:, t, :], in0=out, scalar=c, in1=V.mixed[:, t, :],
                                                op0=ALU.mult, op1=ALU.add)
        last.then_inc(K.mix_steps.sem, 1)

    def back_statistics(s):
        dve.wait_ge(K.mix_steps.sem, K.mix_steps.value(p, s, E3))
        steps = Steps(K.res_steps, p, s)
        ln_statistics(nc, dve, K, p, s, steps, K.cstats, K.clnw, lambda t: V.mixed[:, t, :], D, False)
        steps.ended()

    def back_normed(s):
        dve.wait_ge(K.ostat_ready.sem, K.ostat_ready.value(p, s, 1))
        if K.scale_steps.due(p, s, 0):
            dve.wait_ge(K.scale_steps.sem, K.scale_steps.value(p, s, 0))
        ln_apply(nc, dve, V.onorm, lambda t: V.mixed[:, t, :], K.clnw, K.onorm_ready)

    def added(s):
        dve.wait_ge(K.scale_steps.sem, K.scale_steps.value(p, s, 2))
        dve.tensor_tensor(xu(K, s), V.gated, xu(K, s), ALU.add).then_inc(K.x_done.sem, 1)

    def body(s, b, later):
        n, nb = s + 1, 1 - b
        first = isinstance(s, int) and s == 0
        if later:
            variance(n, 0)
        if not first:
            back_normed(s - 1)
        if later:
            normed(n, nb, 0)
            variance(n, 1)
        mix(s, b, 0)
        if later:
            normed(n, nb, 1)
        if not first:
            added(s - 1)
        if later:
            steps = route_first(nc, dve, K, p, n, r_bank)
        mix(s, b, 1)
        if later:
            variance(n, 2)
        if later == 2:
            x_statistics(nc, dve, K, p, s + 2)
        if later:
            normed(n, nb, 2)
        if later == 2:
            second_norm(s + 2)
        mix(s, b, 2)
        if later:
            variance(n, 3)
        if later == 2:
            x_normed(nc, dve, K, p, s + 2)
        if later:
            normed(n, nb, 3)
            route_second(nc, dve, K, p, n, steps, nb)
        mix(s, b, 3)
        back_statistics(s)

    dve.wait_ge(K.loaded[p], 16 * LOADS[p])
    w1 = K.w1
    dve.tensor_reduce(V.wmean, w1, axis=AX.X, op=ALU.add).then_inc(K.w3_steps, 1)
    dve.wait_ge(K.w3_steps, 1)
    dve.tensor_scalar(V.wmean, V.wmean, 1.0 / HID3, None, ALU.mult).then_inc(K.w3_steps, 1)
    dve.wait_ge(K.w3_steps, 2)
    dve.tensor_tensor(w1, w1, V.wmean.unsqueeze(2).to_broadcast([P, E3, HID3]), ALU.subtract).then_inc(K.w3_steps, 1)
    dve.tensor_copy(V.rn_b, K.col["rn_b"].to_broadcast([P, P])).then_inc(K.w3_steps, 1)
    dve.tensor_scalar(K.rows[:, 4 * D:6 * D], K.rows[:, 4 * D:6 * D], K.gates[:, 7:8], None, ALU.mult).then_inc(K.w3_steps, 1)
    dve.wait_ge(K.bias3_psum, 1)
    dve.tensor_copy(K.logit_bias3, r_bank[:, 0:4]).then_inc(K.w3_steps, 1)
    dve.tensor_scalar(K.rcol[F3], K.rcol[F3], K.col["rn_g"], None, ALU.mult).then_inc(K.w3_steps, 1)
    dve.wait_ge(K.w3_steps, 7)
    x_statistics(nc, dve, K, p, 0)
    second_norm(0)
    x_normed(nc, dve, K, p, 0)
    steps = route_first(nc, dve, K, p, 0, r_bank)
    route_second(nc, dve, K, p, 0, steps, 0)
    x_statistics(nc, dve, K, p, 1)
    for t in range(UNIT):
        variance(0, t)
        normed(0, 0, t)
    second_norm(1)
    x_normed(nc, dve, K, p, 1)
    over_units_ahead(dve, body)
    back_normed(UNITS - 1)
    added(UNITS - 1)


def l3_experts_pool(nc, pool, K):
    p = F3
    V = K.v[p]

    def front(s):
        rstd_pool(nc, pool, K, p, s, False)
        pool.wait_ge(K.r2_steps.sem, K.r2_steps.value(p, s, 3))
        pool.tensor_tensor(K.lnw[:, 2, :], K.lnw[:, 3, :], K.minus_half[:, 0:UNIT], ALU.pow).then_inc(K.r2_ready.sem, 1)

    def factors(s, t):
        pool.wait_ge(K.var_steps.sem, K.var_steps.value(p, s, t + 1))
        if K.z_ready.due(p, s, t - 1):
            pool.wait_ge(K.z_ready.sem, K.z_ready.value(p, s, t - 1))
        pool.tensor_tensor(V.rinv[:, t % 2, :], V.var[:, t % 2, :], K.minus_half[:, 0:E3],
                           ALU.pow).then_inc(K.rinv_ready.sem, 1)

    def back_factor(s):
        pool.wait_ge(K.res_steps.sem, K.res_steps.value(p, s, K.res_steps.counts[p]))
        pool.tensor_tensor(K.clnw[:, 0, :], K.clnw[:, 1, :], K.minus_half[:, 0:UNIT], ALU.pow).then_inc(K.ostat_ready.sem, 1)

    def back_gated(s):
        pool.wait_ge(K.onorm_ready.sem, K.onorm_ready.value(p, s, 1))
        if K.x_done.due(p, s, 0):
            pool.wait_ge(K.x_done.sem, K.x_done.value(p, s, 0))
        pool.tensor_tensor(V.gated, V.onorm, K.row["on_g"].unsqueeze(1).to_broadcast([P, UNIT, D]), ALU.mult)\
            .then_inc(K.scale_steps.sem, 1)
        pool.wait_ge(K.scale_steps.sem, K.scale_steps.value(p, s, 1))
        pool.tensor_tensor(V.gated, V.gated, K.row["on_b"].unsqueeze(1).to_broadcast([P, UNIT, D]), ALU.add)\
            .then_inc(K.scale_steps.sem, 1)

    front(0)
    for t in range(UNIT):
        factors(0, t)
    front(1)

    def body(s, b, later):
        n = s + 1
        first = isinstance(s, int) and s == 0
        if later:
            factors(n, 0)
            factors(n, 1)
        if not first:
            back_gated(s - 1)
        if later:
            factors(n, 2)
        if later == 2:
            front(s + 2)
        if later:
            factors(n, 3)
        back_factor(s)
    over_units_ahead(pool, body)
    back_gated(UNITS - 1)


def fill_values(nc, pool, K, p):
    V = K.v[p]
    if p == A2:
        pool.memset(V.vd[:, :, :, :, DH2].rearrange("p t y j -> p (t y) j"), 1.0)
    if p == A3:
        for b in range(2):
            pool.memset(V.vd[b][:, :, :, :, DH2].rearrange("p t y h -> p (t y) h"), 1.0)
            pool.memset(V.mb[b][:, :, SEQ:KEYS3], 0.0)
    pool.memset(K.touch[:, :], 0.0).then_inc(K.fill, 1)


def fill_selectors(nc, pool, K, p, count):
    V = K.v[p]
    if p != F3:
        pool.memset(V.selraw, 0.0)
        pool.memset(K.cwT[:, :, :].bitcast(F32), 0.0)
    R = route_views(K, p)
    for c in R.count:
        pool.memset(c[:, :, 0:PAD], 0.0)
    pool.memset(R.score, -MASKED)
    pool.memset(K.touch[:, :], 0.0).then_inc(K.fill, 1)
    if p == F3:
        return
    pool.wait_ge(K.fill, count + 1)
    for lo in (0, 32):
        v = V.selraw[lo:lo + 32]
        if p == F0:
            v = v.rearrange("p a (m i) -> p a m i", m=2)
            pattern = [[-2, 16], [-1, 2], [0, SEQ]]
        else:
            pattern = [[-1, 16], [0, P]]
        pool.affine_select(out=v, in_=v, compare_op=ALU.not_equal, fill=1.0, base=0, pattern=pattern,
                           channel_multiplier=1).then_inc(K.fill, 1)


FILLS = {A0: 6, A1: 6, A2: 1, A3: 1, F0: 3, F1: 3, F2: 3, F3: 1}


def fills(K, p):
    return sum(FILLS[q] for q in K.phases[:K.phases.index(p) + 1])


def pool_program(nc, pool, K):
    pool.memset(K.ident[:, :], 0.0).then_inc(K.const_steps, 1)
    pool.memset(K.ones[:, :], 1.0).then_inc(K.const_steps, 1)
    pool.memset(K.minus_half[:, :], -0.5).then_inc(K.const_steps, 1)
    pool.memset(K.eps_col, EPS).then_inc(K.const_steps, 1)
    pool.wait_ge(K.const_steps, 4)
    pool.affine_select(out=K.ident[:, :], in_=K.ident[:, :], compare_op=ALU.not_equal, fill=1.0, base=0,
                       pattern=[[-1, P]], channel_multiplier=1).then_inc(K.const_steps, 1)
    count = 0
    for p in K.phases:
        if p != K.phases[0]:
            pool.wait_ge(K.x_done.sem, K.x_done.start[p])
        if p in (A0, A1):
            assert small_fill(nc, pool, K, p, count) == count + FILLS[p]
            small_pool(nc, pool, K, p)
        elif p in ATTENTION:
            fill_values(nc, pool, K, p)
            (norm_pool(nc, pool, K, p) if p == A2 else l3_pool(nc, pool, K))
        else:
            fill_selectors(nc, pool, K, p, count)
            (l3_experts_pool(nc, pool, K) if p == F3 else norm_pool(nc, pool, K, p))
        count += FILLS[p]


def started(eng, K):
    eng.wait_ge(K.const_steps, 5)
    eng.wait_ge(K.par_loaded, PAR)
    eng.wait_ge(K.x_loaded, 16 * UNITS)


def scalar_program(nc, act, K):
    started(act, K)
    act.activation(K.gates[:, :], K.gates[:, :], ACT.Tanh).then_inc(K.gates_ready, 1)
    for p in K.phases:
        if p != K.phases[0]:
            act.wait_ge(K.x_done.sem, K.x_done.start[p])
        act.wait_ge(K.fill, fills(K, p))
        if p in (A0, A1):
            small_scalar(nc, act, K, p)
        elif p == A2:
            l2_scalar(nc, act, K)
        elif p == A3:
            l3_scalar(nc, act, K)
        elif p == F3:
            l3_experts_scalar(nc, act, K)
        else:
            experts_scalar(nc, act, K, p)


def vector_program(nc, dve, K):
    started(dve, K)
    dve.wait_ge(K.gates_ready, 1)
    dve.wait_ge(K.router_psum, 1)
    dve.tensor_copy(K.router[:, :], K.bank[7][:, 0:52]).then_inc(K.router_ready, 1)
    dve.wait_ge(K.router_ready, 1)
    for p in K.phases:
        if p != K.phases[0]:
            dve.wait_ge(K.x_done.sem, K.x_done.start[p])
        dve.wait_ge(K.fill, fills(K, p))
        if p in (A0, A1):
            small_vector(nc, dve, K, p)
        elif p == A2:
            l2_vector(nc, dve, K)
        elif p == A3:
            l3_vector(nc, dve, K)
        else:
            if p != F3:
                dve.tensor_copy(K.sel[:, :, :], K.v[p].selraw).then_inc(K.sel_ready, 1)
            (l3_experts_vector(nc, dve, K) if p == F3 else experts_vector(nc, dve, K, p))


def tensor_program(nc, pe, K):
    started(pe, K)
    nc.tensor.transpose(K.bank[7][:, 0:52], K.router_raw[:, :], K.ident[0:52, 0:52]).then_inc(K.router_psum, 1)
    pe.wait_ge(K.router_ready, 1)
    sels = 0
    for p in K.phases:
        if p != K.phases[0]:
            pe.wait_ge(K.x_done.sem, K.x_done.start[p])
        pe.wait_ge(K.fill, fills(K, p))
        if p in CHUNKS:
            sels += 1
            pe.wait_ge(K.sel_ready, sels)
        if p in (A0, A1):
            small_tensor(nc, pe, K, p)
        elif p == A2:
            l2_tensor(nc, pe, K)
        elif p == A3:
            l3_tensor(nc, pe, K)
        elif p == F3:
            l3_experts_tensor(nc, pe, K)
        else:
            experts_tensor(nc, pe, K, p)


def kernel(**inputs):
    import numpy as np
    import concourse.bacc as bacc
    from concourse.bass_utils import run_bass_kernel_spmd

    nc = bacc.Bacc("TRN2", target_bir_lowering=False, num_devices=1)
    arrays, args = {}, {}
    for name, value in inputs.items():
        a = np.ascontiguousarray(value)
        key = name
        if a.dtype == np.bool_:
            a, key = a.view(np.int32), "mask"
        arrays[f"in_{name}"] = a
        args[key] = nc.dram_tensor(f"in_{name}", a.shape, mybir.dt.from_np(a.dtype), kind="ExternalInput").ap()
    out = nc.dram_tensor("out", (SEQS, SEQ, D), F32, kind="ExternalOutput").ap()
    build(nc, args, out)
    r = run_bass_kernel_spmd(nc, [arrays], core_ids=[0])
    return r.results[0]["out"]
```

```python
import concourse.bass as bass
from concourse import mybir
from contextlib import ExitStack

F32 = mybir.dt.float32
F32R = mybir.dt.float32r
U8 = mybir.dt.uint8
I32 = mybir.dt.int32
ALU = mybir.AluOpType
ACT = mybir.ActivationFunctionType
AX = mybir.AxisListType

P = 128
SEQS, SEQ, D, DC = 64, 64, 128, 96
TILES = SEQS * SEQ // P
UNIT = 4
UNITS = TILES // UNIT
COLS = UNIT * P
EPS = 1e-5
A0, F0, A1, F1, A2, F2, A3, F3 = range(8)
ATTENTION = (A0, A1, A2, A3)
HEADS, DH = 16, 8
GROUP = HEADS // 2
CLAMP = 10000.0
HEADS2, DH2 = 8, 64
PAIRS2 = HEADS2 // 2
HEADS3 = 2
KEYS3 = 2 * SEQ
MASKED = 1e30
EXPERTS = {F0: 32, F1: 8, F2: 8, F3: 4}
TOP = {F0: 6, F1: 2, F2: 2, F3: 2}
SHARED = {F0: 1, F1: 2, F2: 1}
CHUNKS = {F0: 17, F1: 18, F2: 9}
HID3 = 256
FRONT2, FRONT3 = 14, 11
PAD = 16


class Signal:

    def __init__(self, sem, counts, phases):
        self.sem, self.counts, self.start = sem, counts, {}
        total = 0
        for p in phases:
            self.start[p] = total
            total += UNITS * counts.get(p, 0)

    def value(self, p, s, n):
        return self.start[p] + s * self.counts[p] + n

    def due(self, p, s, n):
        value = self.value(p, s, n)
        return not isinstance(value, int) or value > self.start[p]


class Steps:

    def __init__(self, signal, p, s, n=0):
        self.sem, self.counted, self.p, self.s, self.n = signal.sem, signal, p, s, n

    def one(self):
        self.n += 1
        return 1

    def value(self):
        return self.counted.value(self.p, self.s, self.n)

    def ended(self):
        assert self.n == self.counted.counts[self.p], (self.p, self.n)


def over_units(eng, body):
    body(0, 0, False)
    with eng.Fori(0, (UNITS - 2) // 2) as i:
        body(i * 2 + 1, 1, False)
        body(i * 2 + 2, 0, False)
    body(UNITS - 1, 1, True)


def over_units_ahead(eng, body):
    body(0, 0, 2)
    body(1, 1, 2)
    with eng.Fori(0, (UNITS - 4) // 2) as i:
        body(i * 2 + 2, 0, 2)
        body(i * 2 + 3, 1, 2)
    body(UNITS - 2, 0, 1)
    body(UNITS - 1, 1, 0)


def build(nc, A, out, phases=tuple(range(8))):
    ctx = ExitStack()
    with ctx:
        K = allocate(nc, ctx, A, out, phases)
        block = ctx.enter_context(nc.Block())

        @block.sync
        def _(sp):
            sync_program(nc, sp, K)

        @block.gpsimd
        def _(pool):
            pool_program(nc, pool, K)

        @block.scalar
        def _(act):
            scalar_program(nc, act, K)

        @block.vector
        def _(dve):
            vector_program(nc, dve, K)

        @block.tensor
        def _(pe):
            tensor_program(nc, pe, K)


class Kernel:
    pass


def allocate(nc, ctx, A, out, phases):
    K = Kernel()
    K.A, K.out, K.phases = A, out, phases

    def sb(name, shape, dt=F32):
        return ctx.enter_context(nc.sbuf_tensor(name, shape, dt))

    def signal(name, counts):
        return Signal(ctx.enter_context(nc.semaphore(name)), counts, phases)

    def once(name):
        return ctx.enter_context(nc.semaphore(name))

    every = {p: 1 for p in range(8)}
    attn = {p: 1 for p in ATTENTION}
    four = {p: UNIT for p in ATTENTION}
    K.ln_steps = signal("ln_steps", {p: 11 for p in range(8)})
    K.rstd_ready = signal("rstd_ready", every)
    K.y_ready = signal("y_ready", every)
    own = {p: 1 for p in range(8) if p not in (A2, A3)}
    K.yT_psum = signal("yT_psum", own)
    K.yT_ready = signal("yT_ready", own)
    K.ctx_loaded = signal("ctx_loaded", {p: 16 for p in ATTENTION})
    K.cln_steps = signal("cln_steps", {A0: 11, A3: 11})
    K.crstd_ready = signal("crstd_ready", {A0: 1, A3: 1})
    K.c_ready = signal("c_ready", {A0: 1, A3: 1})
    K.cT_psum = signal("cT_psum", {A0: 1, A1: 1})
    K.cT_ready = signal("cT_ready", {A0: 1, A1: 1})
    K.q_psum = signal("q_psum", {A0: 1, A1: 1})
    K.q_ready = signal("q_ready", {A0: 1, A1: 1})
    K.k_psum = signal("k_psum", {A0: 1, A1: 1})
    K.k_ready = signal("k_ready", {A0: 1, A1: 1})
    K.v_psum = signal("v_psum", {A0: 1, A1: 1})
    K.v_ready = signal("v_ready", {A0: 1, A1: 1, A3: 1})
    K.front_psum = signal("front_psum", {A2: FRONT2, A3: FRONT3})
    K.front_read = signal("front_read", {A2: FRONT2, A3: FRONT3})
    K.kbd_ready = signal("kbd_ready", {A0: UNIT, A1: UNIT})
    K.s_psum = signal("s_psum", four)
    K.max_steps = signal("max_steps", {A0: UNIT, A1: 2 * UNIT, A2: UNIT, A3: 2 * UNIT})
    K.shift_ready = signal("shift_ready", four)
    K.probs_ready = signal("probs_ready", four)
    K.pT_psum = signal("pT_psum", four)
    K.pT_ready = signal("pT_ready", four)
    K.av_psum = signal("av_psum", four)
    K.sum_steps = signal("sum_steps", four)
    K.out_ready = signal("out_ready", four)
    K.oT_psum = signal("oT_psum", {A1: 1, A2: PAIRS2, A3: 1})
    K.oT_ready = signal("oT_ready", {A1: 1, A2: PAIRS2, A3: 1})
    K.proj_psum = signal("proj_psum", {A1: 1, A2: 1, A3: 1})
    K.res_steps = signal("res_steps", {A0: 1, A1: 1, A2: 1, A3: 1, F3: 11})
    K.x_done = signal("x_done", every)
    K.squares = signal("squares", {A3: UNIT})
    K.rms_steps = signal("rms_steps", {A3: 2 * UNIT})
    K.rms_ready = signal("rms_ready", {A3: UNIT})
    K.qk_normed = signal("qk_normed", {A3: UNIT})
    K.maskbias = signal("maskbias", {A3: 1})
    ch = dict(CHUNKS)
    routed = {p: CHUNKS[p] - SHARED[p] for p in CHUNKS}
    K.g_psum = signal("g_psum", ch | {F3: H3})
    K.u_psum = signal("u_psum", ch)
    K.c_psum = signal("c_psum", routed)
    K.y_high = signal("y_high", {F0: 1, F1: 1})
    K.y_low = signal("y_low", {F0: 1, F1: 1})
    K.scaled_made = signal("scaled_made", {F2: 8})
    K.hid_made = signal("hid_made", ch)
    K.hid_high = signal("hid_high", ch)
    K.silu_ready = signal("silu_ready", ch)
    K.prod_steps = signal("prod_steps", {F0: routed[F0], F1: routed[F1]})
    K.hid_ready = signal("hid_ready", ch | {F3: Q3})
    K.down_done = signal("down_done", ch | {F3: E3})
    K.dt_ready = signal("dt_ready", {p: 1 for p in CHUNKS})
    K.outT_psum = signal("outT_psum", {p: 1 for p in CHUNKS})
    K.logits_psum = signal("logits_psum", {p: 1 for p in EXPERTS})
    K.logits_ready = signal("logits_ready", {F0: 1})
    K.exp_ready = signal("exp_ready", {F1: 1, F2: 1, F3: 1})
    K.route_steps = signal("route_steps", {F0: 39, F1: 21, F2: 22, F3: 27})
    K.cw_psum = signal("cw_psum", {p: 1 for p in CHUNKS})
    K.cw_steps = signal("cw_steps", {p: 1 for p in CHUNKS})
    K.cwT_ready = signal("cwT_ready", {p: 1 for p in CHUNKS})
    K.sq_ready = signal("sq_ready", {F3: UNIT})
    K.var_steps = signal("var_steps", {F3: UNIT})
    K.rinv_ready = signal("rinv_ready", {F3: UNIT})
    K.z_ready = signal("z_ready", {F3: UNIT})
    K.zT_psum = signal("zT_psum", {F3: Q3})
    K.mix_steps = signal("mix_steps", {F3: E3})
    K.ostat_ready = signal("ostat_ready", {F3: 1})
    K.onorm_ready = signal("onorm_ready", {F3: 1})
    K.r2_steps = signal("r2_steps", {F3: 3})
    K.r2_ready = signal("r2_ready", {F3: 1})
    K.scale_steps = signal("scale_steps", {F3: 2})
    K.x_first = once("x_first")
    K.x_rest = once("x_rest")
    K.par_first = once("par_first")
    K.par_loaded = once("par_loaded")
    K.loaded = {p: once(f"weights_{p}") for p in range(8)}
    K.stored = once("stored")
    K.prep = once("prep")
    K.ident_ready = once("ident_ready")
    K.const_steps = once("const_steps")
    K.gates_ready = once("gates_ready")
    K.par_steps = once("par_steps")
    K.prep_psum = once("prep_psum")
    K.high = {p: once(f"high_{p}") for p in CHUNKS}
    K.low = {p: once(f"low_{p}") for p in CHUNKS}
    K.fill = once("fill")
    K.sel_ready = once("sel_ready")
    K.l3w_psum = once("l3w_psum")
    K.l3w_ready = once("l3w_ready")
    K.w3_steps = once("w3_steps")
    K.bias3_psum = once("bias3_psum")
    K.router_psum = once("router_psum")
    K.router_ready = once("router_ready")

    K.X = sb("X", [P, TILES, D])
    K.mask_words = sb("mask_words", [P, TILES, SEQ // 4], I32)
    K.mask = K.mask_words[:, :, :].bitcast(U8)
    K.ident = sb("ident", [P, P])
    K.ones = sb("ones", [P, P])
    K.gates = sb("gates", [P, 8])
    K.cols = sb("cols", [P, 48])
    K.rows = sb("rows", [P, 7 * D + 40])
    K.wp = {
        A0: {n: sb(f"L0_{n}", [r, D]) for n, r in (("q", D), ("k", DC), ("v", DC))},
        A1: {n: sb(f"L1_{n}", [r, D]) for n, r in (("q", D), ("k", DC), ("v", DC), ("o", D))},
        A2: {"q": sb("L2_q", [D, 4 * D]), "k": sb("L2_k", [DC, 4 * D]), "v": sb("L2_v", [DC, 4 * D]),
             "o": sb("L2_o", [D, 4, D])},
        A3: {"qkv": sb("L3_qkv", [D, 3 * D]), "kv": sb("L3_kv", [DC, 2 * D]),
             "o": sb("L3_o", [D, D])},
    }
    landing = sb("landing", [P, 3 * CHUNKS[F1] * P])
    K.raw = {p: landing[:, 0:3 * CHUNKS[p] * P].rearrange("p (w j n) -> p w j n", w=3, j=CHUNKS[p]) for p in CHUNKS}
    at = 3 * CHUNKS[F2] * P
    K.w1 = landing[:, at:at + 4 * HID3].rearrange("p (e h) -> p e h", e=4)
    at += 4 * HID3
    K.w2 = landing[:, at:at + 4 * HID3].rearrange("p (c d) -> p c d", c=8)
    at += 4 * HID3
    K.wp[A3]["raw"] = landing[:, at:at + 6 * D].rearrange("p (c d) -> p c d", c=6)
    K.router_raw = sb("router_raw", [52, D])
    K.router = sb("router", [P, 52])
    K.sel = sb("sel", [64, 16, P], F32R)
    K.cwT = sb("cwT", [64, 2, COLS], F32R)
    K.yT = [sb(f"yT{b}", [P, COLS]) for b in range(2)]
    K.yt = sb("yt", [P, UNIT, D])
    K.stats = sb("stats", [P, UNIT, 6])
    K.lnw = sb("lnw", [P, 6, UNIT])
    K.cstats = sb("cstats", [P, UNIT, 6])
    K.clnw = sb("clnw", [P, 6, UNIT])
    K.minus_half = sb("minus_half", [P, 32])
    K.route = sb("route", [P, 2048])
    K.touch = sb("touch", [P, 1])
    K.arena_cols = 21504
    with nc.sbuf_tensor("arena", [P, K.arena_cols], F32) as arena:
        K.arena = arena
    K.arena_r = sb("arena_r", [P, K.arena_cols], F32R)
    K.ctx = [sb(f"ctx{b}", [P, UNIT, DC])[:, :, :] for b in range(2)]
    K.ps = ctx.enter_context(nc.psum_tensor("ps", [P, 8, 512], F32))
    K.bank = [K.ps[:, i, :] for i in range(8)]

    K.col = {n: K.cols[:, i:i + 1] for i, n in enumerate(
        ["q_b", "k_b", "ln_g", "ln_b", "tln_g", "tln_b", "bq", "bk", "bv",
         "ln_l_g", "ln_l_b", "ln_x_g", "ln_x_b", "rn_g", "rn_b", "qn_g", "kn_g"])}
    K.ln3_g = K.cols[:, 20:28]
    K.ln3_b = K.cols[:, 28:36]
    K.logit_bias3 = K.cols[:, 36:40]
    K.row = {n: K.rows[:, i * D:(i + 1) * D] for i, n in enumerate(["v_b", "bo1", "bo2", "bo3", "on_g", "on_b"])}
    K.ebias0 = K.rows[:, 6 * D:6 * D + 32]
    K.ebias1 = K.rows[:, 6 * D + 32:6 * D + 40]
    K.eps_col = K.cols[:, 40:41]
    K.rcol = {F0: K.router[:, 0:32], F1: K.router[:, 32:40], F2: K.router[:, 40:48], F3: K.router[:, 48:52]}
    K.v = {p: carve(K, p) for p in range(8)}
    return K


class Views:

    def __init__(self, K):
        self.K, self.at = K, 0

    def take(self, *shape, rows=P, split=False):
        n = 1
        for x in shape:
            n *= x
        v = (self.K.arena_r if split else self.K.arena)[0:rows, self.at:self.at + n]
        self.at += n
        assert self.at <= self.K.arena_cols, self.at
        names = " ".join("abcde"[:len(shape)])
        if len(shape) > 1:
            v = v.rearrange(f"p ({names}) -> p {names}", **{n: x for n, x in zip("abcde", shape)})
        return v


def carve(K, p):
    V = Views(K)
    if p in ATTENTION:
        V.ctx = K.ctx
        V.ctxn = V.take(UNIT, DC)
        V.cT = [V.take(COLS, rows=DC) for _ in range(2)]
    if p in (A0, A1):
        zeroed = V.at
        V.qz = [V.take(2, UNIT, P) for _ in range(2)]
        V.vd = [V.take(UNIT, GROUP, 2, 2, DH + 1) for _ in range(2)]
        V.zeroed = (zeroed, V.at)
        V.ksel = [V.take(2, UNIT, SEQ) for _ in range(2)]
        V.kbd = [V.take(2, GROUP, SEQ) for _ in range(2)]
        V.probs = [V.take(HEADS, SEQ) for _ in range(2)]
        V.pT = [V.take(GROUP, P) for _ in range(2)]
        V.out = [V.take(UNIT, D) for _ in range(2)]
        V.outT = V.take(COLS)
        V.res = V.take(UNIT, D)
        V.max = V.take(2, HEADS)
        V.rsum = V.take(HEADS)
        V.diag = V.take(GROUP)
    if p == A2:
        V.q = [V.take(PAIRS2, COLS) for _ in range(2)]
        V.k = [V.take(PAIRS2, COLS) for _ in range(2)]
        V.vd = [V.take(UNIT, 2, PAIRS2, DH2 + 1) for _ in range(2)]
        V.probs = [V.take(PAIRS2, 2, SEQ) for _ in range(2)]
        V.pT = [V.take(PAIRS2, P) for _ in range(2)]
        V.out = V.take(UNIT, PAIRS2, 2, DH2)
        V.outT = V.take(PAIRS2, COLS)
        V.res = V.take(UNIT, D)
        V.max = V.take(2, 2, PAIRS2)
        V.rsum = V.take(2, PAIRS2)
    if p == A3:
        V.raw = V.take(UNIT, 5, D)
        V.sq = V.take(UNIT, 3, D)
        V.ss = V.take(UNIT, 3, 2)
        V.rms = V.take(UNIT, 3, 2)
        V.normed = V.take(3, UNIT, D)
        V.q = [V.take(COLS) for _ in range(2)]
        V.k = [V.take(UNIT, 2, 2, SEQ) for _ in range(2)]
        V.vd = [V.take(UNIT, 2, 2, DH2 + 1) for _ in range(2)]
        V.mb = [V.take(UNIT, KEYS3) for _ in range(2)]
        V.probs = [V.take(2, KEYS3) for _ in range(2)]
        V.pT = [V.take(2, P) for _ in range(2)]
        V.out = V.take(UNIT, 2, DH2)
        V.outT = V.take(COLS)
        V.res = V.take(UNIT, D)
        V.max = V.take(2, 2)
        V.rsum = V.take(2)
    if p in CHUNKS:
        V.silu = [V.take(COLS) for _ in range(2)]
        V.prod = [V.take(COLS) for _ in range(2)]
        V.selraw = K.arena[0:64, 0:16 * P].rearrange("p (a n) -> p a n", a=16)
        V.hid = [V.take(COLS) for _ in range(2)]
        V.dt = V.take(COLS)
        V.hid_hi = [V.take(COLS, split=True) for _ in range(2)]
        V.hid_lo = [V.take(COLS, split=True) for _ in range(2)]
        V.y_hi = [V.take(COLS, split=True) for _ in range(2)]
        V.y_lo = [V.take(COLS, split=True) for _ in range(2)]
        V.w_hi = V.take(3, CHUNKS[p], P, split=True)
        V.w_lo = V.take(3, CHUNKS[p], P, split=True)
    if p == F2:
        V.scaled = [V.take(COLS) for _ in range(2)]
    if p == F3:
        V.z = [V.take(UNIT, E3 * HID3) for _ in range(2)]
        V.hid = [V.take(COLS) for _ in range(4)]
        V.sq = V.take(2 * E3, HID3)
        V.ss, V.var, V.rinv = V.take(2, E3), V.take(2, E3), V.take(2, E3)
        V.cw = [V.take(UNIT, 8) for _ in range(2)]
        V.mixed = V.take(UNIT, D)
        V.onorm = V.take(UNIT, D)
        V.gated = V.take(UNIT, D)
        V.rn_b = V.take(P)
        V.wmean = V.take(E3)
    return V


def xs(K, s, t):
    return K.X[:, bass.ds(s * UNIT + t, 1), :].rearrange("p a d -> p (a d)")


def xu(K, s):
    return K.X[:, bass.ds(s * UNIT, UNIT), :]


def half(x):
    return slice(SEQ * x, SEQ * (x + 1))


def sync_program(nc, sp, K):
    A = K.A
    x_v = A["x"].rearrange("(t b) s d -> (b s) t d", b=2)
    c_v = A["ctx_768"].rearrange("(t b) s d -> (b s) t d", b=2)

    def load_ctx(p, s, b):
        if p in (A0, A3):
            if K.c_ready.due(p, s, 0):
                sp.wait_ge(K.c_ready.sem, K.c_ready.value(p, s, 0))
        elif p == A1:
            if K.cT_psum.due(p, s, 0):
                sp.wait_ge(K.cT_psum.sem, K.cT_psum.value(p, s, 0))
        else:
            if K.front_psum.due(p, s, 1 - FRONT2):
                sp.wait_ge(K.front_psum.sem, K.front_psum.value(p, s, 1 - FRONT2))
        sp.dma_start(K.v[p].ctx[b], c_v[:, bass.ds(s * UNIT, UNIT), :]).then_inc(K.ctx_loaded.sem, 16)

    def column(name, vec, rows=slice(0, P)):
        n = rows.stop - rows.start
        sp.dma_start(K.col[name][rows], vec.rearrange("(p o) -> p o", p=n)).then_inc(K.par_loaded, 16)

    def row(dst, vec, arrived=K.par_loaded):
        n = vec.shape[0]
        sp.dma_start(dst, vec.rearrange("(o n) -> o n", o=1).to_broadcast([P, n])).then_inc(arrived, 16)

    issued = set()

    def load(p, dst, src):
        issued.add(p)
        sp.dma_start(dst, src).then_inc(K.loaded[p], 16)

    first = 2 * UNIT
    sp.dma_start(K.X[:, 0:first, :], x_v[:, 0:first, :]).then_inc(K.x_first, 16)
    if K.phases[0] == A0:
        load_ctx(A0, 0, 0)
    for n in ("q", "k", "v"):
        load(A0, K.wp[A0][n][:, :], A[f"L0_xattn_{n}_w"])
    row(K.gates[:, 0:4], A["g_xattn"], K.par_first)
    row(K.gates[:, 4:8], A["g_ffn"], K.par_first)
    row(K.row["v_b"], A["L0_xattn_v_b"], K.par_first)
    sp.dma_start(K.X[:, first:, :], x_v[:, first:, :]).then_inc(K.x_rest, 16)
    if K.phases[0] == A0:
        load_ctx(A0, 1, 1)
    for n in ("bq", "bk", "bv"):
        column(n, A[f"L1_xattn_{n}"])
    for n in ("ln_l_g", "ln_l_b"):
        column(n, A[f"L3_xattn_{n}"])
    for n in ("ln_x_g", "ln_x_b"):
        column(n, A[f"L3_xattn_{n}"], slice(0, DC))
    for n in ("rn_g", "rn_b"):
        column(n, A[f"L3_ffn_{n}"])
    for n in ("qn_g", "kn_g"):
        for h in range(2):
            column(n, A[f"L3_xattn_{n}"], half(h))
    with nc.allow_non_contiguous_dma("sixteen short vectors"):
        for dst, n in ((K.ln3_g, "ln_g"), (K.ln3_b, "ln_b")):
            sp.dma_start(dst, A[f"L3_ffn_{n}"].rearrange("e (c p) -> p (e c)", p=P)).then_inc(K.par_loaded, 16)
    row(K.row["bo1"], A["L1_xattn_bo"])
    row(K.row["bo2"], A["L2_xattn_bo"])
    row(K.row["bo3"], A["L3_xattn_bo"])
    row(K.row["on_g"], A["L3_ffn_on_g"])
    row(K.row["on_b"], A["L3_ffn_on_b"])
    row(K.ebias0, A["L0_ffn_e_score_correction_bias"])
    row(K.ebias1, A["L1_ffn_experts_bias"])
    for at, name in ((0, "L0_ffn_gate_weight"), (32, "L1_ffn_router_w"), (40, "L2_ffn_gate_w"), (48, "L3_ffn_router_w")):
        n = A[name].shape[0]
        sp.dma_start(K.router_raw[at:at + n, :], A[name]).then_inc(K.par_loaded, 16)
    if F0 in K.phases:
        raw = K.raw[F0]
        load(F0, raw[:, 0, 0, :], A["L0_ffn_shared_gate_w"])
        load(F0, raw[:, 1, 0, :], A["L0_ffn_shared_up_w"])
        load(F0, raw[:, 2, 0, :], A["L0_ffn_shared_down_w"])
        gu = A["L0_ffn_experts_gate_up"].rearrange("(j m) r h -> m r j h", m=2)
        for m in range(2):
            for which in range(2):
                load(F0, raw[half(m), which, 1:17, :], gu[m, half(which), :, :])
        dn = A["L0_ffn_experts_down"].rearrange("(j m) h i -> m h j i", m=2)
        for m in range(2):
            load(F0, raw[:, 2, 1:17, half(m)], dn[m])
    for n in ("q", "k", "v", "o"):
        load(A1, K.wp[A1][n][:, :], A[f"L1_xattn_W{n}"])
    for n in ("q", "k", "v"):
        load(A2, K.wp[A2][n][:, :], A[f"L2_xattn_W{n}"])
    load(A2, K.wp[A2]["o"][:, :, :], A["L2_xattn_Wo"].rearrange("(c p) n -> p c n", p=P))
    mask = A["mask"].rearrange("(t b) k -> b t k", b=2)
    for x in range(2):
        load(A3, K.mask_words[half(x), :, :], mask[x:x + 1].to_broadcast([SEQ, TILES, SEQ // 4]))

    def load_late():
        for which, n in ((0, "w1"), (1, "w3"), (2, "w2")):
            load(F2, K.raw[F2][:, which, 0, :], A[f"L2_ffn_{n}s"][0])
            load(F2, K.raw[F2][:, which, 1:9, :], A[f"L2_ffn_{n}"].rearrange("e d h -> d e h"))
        L3 = K.wp[A3]["raw"]
        load(A3, L3[:, 0, :], A["L3_xattn_Wq"])
        load(A3, L3[:, 1:3, :], A["L3_xattn_Wlkv"].rearrange("(c p) n -> p c n", p=P))
        load(A3, L3[:, 3, :], A["L3_xattn_Wo"])
        load(A3, L3[:, 4:6, 0:DC], A["L3_xattn_Wkv"].rearrange("(c p) n -> p c n", p=P))
        load(F3, K.w1, A["L3_ffn_w1"].rearrange("e d h -> d e h"))
        load(F3, K.w2, A["L3_ffn_w2"].rearrange("e (c p) d -> p (e c) d", p=P))

    def load_f1():
        for which, n in ((0, "w1"), (1, "w3")):
            for at, src in ((0, A[f"L1_ffn_s{n}"]), (2, A[f"L1_ffn_{n}"])):
                e = src.shape[0]
                load(F1, K.raw[F1][:, which, at:at + 2 * e, :].rearrange("p (e c) h -> p e (c h)", e=e),
                     src.rearrange("e d h -> d e h"))
        for at, src in ((0, A["L1_ffn_sw2"]), (2, A["L1_ffn_w2"])):
            e = src.shape[0]
            load(F1, K.raw[F1][:, 2, at:at + 2 * e, :], src.rearrange("e (c p) d -> p (e c) d", p=P))

    if F1 in K.phases and F0 not in K.phases:
        load_f1()
    if F0 not in K.phases and F1 not in K.phases:
        load_late()
    for p in K.phases:
        if p == F0:
            sp.wait_ge(K.low[F0], len(PREP_GROUPS))
            load_f1()
        if p == F1:
            sp.wait_ge(K.low[F1], 3)
            load_late()
        if p in ATTENTION:
            early = p == A0
            if p != K.phases[0]:
                q = K.phases[K.phases.index(p) - 1]
                assert q not in ATTENTION
                if q != K.phases[0]:
                    sp.wait_ge(K.x_done.sem, K.x_done.start[q])
            if not early:
                load_ctx(p, 0, 0)
            def body(s, b, last):
                if not last and not (early and isinstance(s, int) and s == 0):
                    load_ctx(p, s + 1, 1 - b)
            over_units(sp, body)
    for p in sorted(issued):
        if p == A3 and F3 not in issued:
            sp.wait_ge(K.loaded[p], 16 * 2)
        else:
            sp.wait_ge(K.loaded[p], 16 * LOADS[p])
    last = K.phases[-1]
    out_v = K.out.rearrange("(t b) s d -> (b s) t d", b=2)
    for s in range(UNITS):
        sp.wait_ge(K.x_done.sem, K.x_done.value(last, s, 1))
        sp.dma_start(out_v[:, s * UNIT:(s + 1) * UNIT, :], K.X[:, s * UNIT:(s + 1) * UNIT, :]).then_inc(K.stored, 16)
    sp.wait_ge(K.stored, 16 * UNITS)


PAR_FIRST = 16 * (3 + 6)
PAR = 16 * (3 + 2 + 2 + 2 + 4 + 2 + 7 + 4)
YT_PIECE = {A2: 5, A3: 1}
LOADS = {A0: 3, F0: 3 + 4 + 2, A1: 4, F1: 6, A2: 4, F2: 6, A3: 6, F3: 2}
PREP_GROUPS = [(i, min(4, 51 - i)) for i in range(0, 51, 4)]


def whole_first(first, y, t):
    if first:
        return slice(0, P), slice(t * P, (t + 1) * P)
    return half(y), slice(t * P + y * SEQ, t * P + (y + 1) * SEQ)


def ln_statistics(nc, dve, K, p, s, steps, stats, w, source, n, twice):
    for t in range(UNIT):
        dve.bn_stats(stats[:, t, :], source(t)).then_inc(steps.sem, steps.one())
    mean2, dif, m2, sq, mean, var = (w[:, i, :] for i in range(6))
    dve.wait_ge(steps.sem, steps.value())
    dve.tensor_tensor(mean2, stats[:, :, 1], stats[:, :, 4], ALU.add).then_inc(steps.sem, steps.one())
    dve.tensor_tensor(dif, stats[:, :, 1], stats[:, :, 4], ALU.subtract).then_inc(steps.sem, steps.one())
    dve.tensor_tensor(m2, stats[:, :, 2], stats[:, :, 5], ALU.add).then_inc(steps.sem, steps.one())
    dve.wait_ge(steps.sem, steps.value())
    dve.tensor_scalar(mean, mean2, 0.5, None, ALU.mult).then_inc(steps.sem, steps.one())
    dve.scalar_tensor_tensor(out=sq, in0=dif, scalar=0.25, in1=dif, op0=ALU.mult, op1=ALU.mult).then_inc(steps.sem, steps.one())
    dve.wait_ge(steps.sem, steps.value())
    dve.scalar_tensor_tensor(out=var, in0=m2, scalar=1.0 / n, in1=sq, op0=ALU.mult, op1=ALU.add).then_inc(steps.sem, steps.one())
    dve.wait_ge(steps.sem, steps.value())
    a, b = (1.0 + EPS, EPS * EPS) if twice else (1.0, EPS)
    dve.tensor_scalar(dif, var, a, b, ALU.mult, ALU.add).then_inc(steps.sem, steps.one())


def ln_apply(nc, dve, out, source, w, ready):
    for t in range(UNIT):
        last = dve.tensor_scalar(out[:, t, :], source(t), w[:, 4, t:t + 1], w[:, 0, t:t + 1],
                                 ALU.subtract, ALU.mult)
    last.then_inc(ready.sem, 1)


def x_statistics(nc, dve, K, p, s):
    steps = Steps(K.ln_steps, p, s)
    ln_statistics(nc, dve, K, p, s, steps, K.stats, K.lnw, lambda t: xs(K, s, t), D, p in (A0, A3))
    steps.ended()


def x_normed(nc, dve, K, p, s):
    dve.wait_ge(K.rstd_ready.sem, K.rstd_ready.value(p, s, 1))
    if p in (A2, A3):
        if K.front_psum.due(p, s, YT_PIECE[p] + 1 - K.front_psum.counts[p]):
            dve.wait_ge(K.front_psum.sem, K.front_psum.value(p, s, YT_PIECE[p] + 1 - K.front_psum.counts[p]))
    else:
        if K.yT_psum.due(p, s, 0):
            dve.wait_ge(K.yT_psum.sem, K.yT_psum.value(p, s, 0))
    ln_apply(nc, dve, K.yt, lambda t: xs(K, s, t), K.lnw, K.y_ready)


def ctx_statistics(nc, dve, K, p, s, b):
    dve.wait_ge(K.ctx_loaded.sem, K.ctx_loaded.value(p, s, 16))
    steps = Steps(K.cln_steps, p, s)
    ln_statistics(nc, dve, K, p, s, steps, K.cstats, K.clnw, lambda t: K.v[p].ctx[b][:, t, :], DC, False)
    steps.ended()


def ctx_normed(nc, dve, K, p, s, b):
    dve.wait_ge(K.crstd_ready.sem, K.crstd_ready.value(p, s, 1))
    if p == A3:
        if K.front_psum.due(p, s, 1 - FRONT3):
            dve.wait_ge(K.front_psum.sem, K.front_psum.value(p, s, 1 - FRONT3))
    else:
        if K.cT_psum.due(p, s, 0):
            dve.wait_ge(K.cT_psum.sem, K.cT_psum.value(p, s, 0))
    ln_apply(nc, dve, K.v[p].ctxn, lambda t: K.v[p].ctx[b][:, t, :], K.clnw, K.c_ready)


def rstd_pool(nc, pool, K, p, s, ctx):
    steps, ready, w = (K.cln_steps, K.crstd_ready, K.clnw) if ctx else (K.ln_steps, K.rstd_ready, K.lnw)
    pool.wait_ge(steps.sem, steps.value(p, s, steps.counts[p]))
    pool.tensor_tensor(w[:, 0, :], w[:, 1, :], K.minus_half[:, 0:UNIT], ALU.pow).then_inc(ready.sem, 1)


def following(K, p):
    i = K.phases.index(p) + 1
    return K.phases[i] if i < len(K.phases) else None


def router_norm(nc, dve, K, s):
    w = K.lnw
    steps = Steps(K.r2_steps, F3, s)
    dve.wait_ge(K.rstd_ready.sem, K.rstd_ready.value(F3, s, 1))
    dve.tensor_tensor(w[:, 3, :], w[:, 0, :], w[:, 0, :], ALU.mult).then_inc(steps.sem, steps.one())
    dve.wait_ge(steps.sem, steps.value())
    dve.tensor_tensor(w[:, 3, :], w[:, 3, :], w[:, 5, :], ALU.mult).then_inc(steps.sem, steps.one())
    dve.wait_ge(steps.sem, steps.value())
    dve.tensor_scalar(w[:, 3, :], w[:, 3, :], EPS, None, ALU.add).then_inc(steps.sem, steps.one())


def router_norm_pool(nc, pool, K, s):
    pool.wait_ge(K.r2_steps.sem, K.r2_steps.value(F3, s, 3))
    pool.tensor_tensor(K.lnw[:, 2, :], K.lnw[:, 3, :], K.minus_half[:, 0:UNIT], ALU.pow).then_inc(K.r2_ready.sem, 1)


def norm_first(nc, dve, K, q):
    if q is not None:
        if q == A3:
            ctx_statistics(nc, dve, K, q, 0, 0)
        x_statistics(nc, dve, K, q, 0)
        if q == F3:
            router_norm(nc, dve, K, 0)
        x_normed(nc, dve, K, q, 0)


def norm_first_pool(nc, pool, K, q):
    if q is not None:
        if q == A3:
            rstd_pool(nc, pool, K, q, 0, True)
        rstd_pool(nc, pool, K, q, 0, False)
        if q == F3:
            router_norm_pool(nc, pool, K, 0)


def transpose4(nc, K, bank, source, rows, cols=P):
    for t in range(UNIT):
        last = nc.tensor.transpose(bank[0:rows, t * P:(t + 1) * P], source(t), K.ident[:, :])
    return last


def yT_evacuate(nc, act, K, p, s, b, bank):
    ready = K.front_read if p in (A2, A3) else K.yT_ready
    if p not in (A2, A3):
        act.wait_ge(K.yT_psum.sem, K.yT_psum.value(p, s, 1))
    g, o = {A0: ("ln_g", "ln_b"), A3: ("ln_l_g", "ln_l_b")}.get(p, (None, None))
    if g:
        act.activation(K.yT[b][:, :], bank, ACT.Identity, scale=K.col[g], bias=K.col[o]).then_inc(ready.sem, 1)
    else:
        act.activation(K.yT[b][:, :], bank, ACT.Copy).then_inc(ready.sem, 1)


def cT_evacuate(nc, act, K, p, s, b, bank):
    ready = K.front_read if p in (A2, A3) else K.cT_ready
    if p not in (A2, A3):
        act.wait_ge(K.cT_psum.sem, K.cT_psum.value(p, s, 1))
    g, o = {A0: ("tln_g", "tln_b"), A3: ("ln_x_g", "ln_x_b")}.get(p, (None, None))
    dst = K.v[p].cT[b]
    if g:
        act.activation(dst, bank[0:DC, :], ACT.Identity, scale=K.col[g][0:DC], bias=K.col[o][0:DC]).then_inc(ready.sem, 1)
    else:
        act.activation(dst, bank[0:DC, :], ACT.Copy).then_inc(ready.sem, 1)


S_BANKS = ((0, 1), (2, 3))
PT_BANKS = (4, 5)
O_BANK, X_BANK = 6, 7


def small_tensor(nc, pe, K, p):
    V, W = K.v[p], K.wp[p]
    bank, mm = K.bank, nc.tensor.matmul

    def context(s, b):
        if p == A0:
            pe.wait_ge(K.c_ready.sem, K.c_ready.value(p, s, 1))
        else:
            pe.wait_ge(K.ctx_loaded.sem, K.ctx_loaded.value(p, s, 16))
        if K.v_ready.due(p, s, 0):
            pe.wait_ge(K.v_ready.sem, K.v_ready.value(p, s, 0))
        src = V.ctxn if p == A0 else V.ctx[b]
        transpose4(nc, K, bank[X_BANK], lambda t: src[:, t, :], DC).then_inc(K.cT_psum.sem, 1)

    def keys(s, b):
        pe.wait_ge(K.cT_ready.sem, K.cT_ready.value(p, s, 1))
        mm(bank[X_BANK], W["k"][:, :], V.cT[b], start=True, stop=True).then_inc(K.k_psum.sem, 1)

    def stream(s):
        pe.wait_ge(K.y_ready.sem, K.y_ready.value(p, s, 1))
        pe.wait_ge(K.k_ready.sem, K.k_ready.value(p, s, 1))
        transpose4(nc, K, bank[X_BANK], lambda t: K.yt[:, t, :], P).then_inc(K.yT_psum.sem, 1)

    def queries(s, b):
        pe.wait_ge(K.yT_ready.sem, K.yT_ready.value(p, s, 1))
        mm(bank[X_BANK], W["q"][:, :], K.yT[b][:, :], start=True, stop=True).then_inc(K.q_psum.sem, 1)

    def values(s, b):
        pe.wait_ge(K.q_ready.sem, K.q_ready.value(p, s, 1))
        if p == A1 and K.res_steps.due(p, s, -1):
            pe.wait_ge(K.res_steps.sem, K.res_steps.value(p, s, -1))
        for t in range(UNIT):
            last = mm(bank[X_BANK][:, t * P:(t + 1) * P], V.cT[b][:, t * P:(t + 1) * P], W["v"][:, :],
                      start=True, stop=True)
        last.then_inc(K.v_psum.sem, 1)

    def scores(s, b, t):
        pe.wait_ge(K.kbd_ready.sem, K.kbd_ready.value(p, s, t + 1))
        if K.shift_ready.due(p, s, t - 1):
            pe.wait_ge(K.shift_ready.sem, K.shift_ready.value(p, s, t - 1))
        if t == 0:
            pe.wait_ge(K.q_ready.sem, K.q_ready.value(p, s, 1))
        for g in range(2):
            last = mm(bank[S_BANKS[t % 2][g]], V.qz[b][:, g, t, :], V.kbd[t % 2][:, g, :, :].rearrange("p h k -> p (h k)"),
                      start=True, stop=True)
        last.then_inc(K.s_psum.sem, 1)

    def turned(s, t):
        pe.wait_ge(K.probs_ready.sem, K.probs_ready.value(p, s, t + 1))
        if K.pT_ready.due(p, s, t):
            pe.wait_ge(K.pT_ready.sem, K.pT_ready.value(p, s, t))
        pr = V.probs[t % 2].rearrange("p h k -> p (h k)")
        for j in range(GROUP):
            last = nc.tensor.transpose(bank[PT_BANKS[j // 4]][:, (j % 4) * P:(j % 4 + 1) * P],
                                       pr[:, j * P:(j + 1) * P], K.ident[:, :])
        last.then_inc(K.pT_psum.sem, 1)

    def weighted(s, b, t):
        pe.wait_ge(K.pT_ready.sem, K.pT_ready.value(p, s, t + 1))
        if K.out_ready.due(p, s, t):
            pe.wait_ge(K.out_ready.sem, K.out_ready.value(p, s, t))
        if t == 0:
            pe.wait_ge(K.v_ready.sem, K.v_ready.value(p, s, 1))
        n = 2 * 2 * (DH + 1)
        for j in range(GROUP):
            last = mm(bank[O_BANK][:, j * n:(j + 1) * n], V.pT[t % 2][:, j, :],
                      V.vd[b][:, t, j, :, :, :].rearrange("p x h d -> p (x h d)"), start=True, stop=True)
        last.then_inc(K.av_psum.sem, 1)

    def outputs_turned(s, b, following):
        pe.wait_ge(K.out_ready.sem, K.out_ready.value(p, s, UNIT))
        if following is not None:
            pe.wait_ge(K.q_ready.sem, K.q_ready.value(p, following, 1))
        elif K.x_done.due(p, s, 0):
            pe.wait_ge(K.x_done.sem, K.x_done.value(p, s, 0))
        transpose4(nc, K, bank[X_BANK], lambda t: V.out[b][:, t, :], P).then_inc(K.oT_psum.sem, 1)

    def project(s):
        pe.wait_ge(K.oT_ready.sem, K.oT_ready.value(p, s, 1))
        for t in range(UNIT):
            last = mm(bank[X_BANK][:, t * P:(t + 1) * P], V.outT[:, t * P:(t + 1) * P], W["o"][:, :],
                      start=True, stop=True)
        last.then_inc(K.proj_psum.sem, 1)

    pe.wait_ge(K.loaded[p], 16 * LOADS[p])
    context(0, 0)
    keys(0, 0)
    stream(0)
    queries(0, 0)
    values(0, 0)
    scores(0, 0, 0)
    scores(0, 0, 1)

    def body(s, b, later):
        n, nb = s + 1, 1 - b
        back = p == A1 and not (isinstance(s, int) and s == 0)
        turned(s, 0)
        if later:
            context(n, nb)
        scores(s, b, 2)
        if later:
            keys(n, nb)
        weighted(s, b, 0)
        if later:
            stream(n)
        turned(s, 1)
        if later:
            queries(n, nb)
        scores(s, b, 3)
        if back:
            outputs_turned(s - 1, nb, n if later else None)
        weighted(s, b, 1)
        if back:
            project(s - 1)
        turned(s, 2)
        if later:
            scores(n, nb, 0)
            values(n, nb)
        weighted(s, b, 2)
        turned(s, 3)
        if later:
            scores(n, nb, 1)
        weighted(s, b, 3)
    over_units_ahead(pe, body)
    if p == A1:
        outputs_turned(UNITS - 1, 1, None)
        project(UNITS - 1)


def small_scalar(nc, act, K, p):
    V = K.v[p]
    bank = K.bank
    x = bank[X_BANK]

    def queries(s, b):
        act.wait_ge(K.q_psum.sem, K.q_psum.value(p, s, 1))
        name = "q_b" if p == A0 else "bq"
        xv = x.rearrange("p (t y q) -> p t y q", t=UNIT, y=2)
        for g in range(2):
            for y in range(2):
                last = act.activation(V.qz[b][half(y), g, :, half(y)], xv[half(g), :, y, :], ACT.Identity,
                                      bias=K.col[name][half(g)])
        last.then_inc(K.q_ready.sem, 1)

    def values(s, b):
        act.wait_ge(K.v_psum.sem, K.v_psum.value(p, s, 1))
        xv = x.rearrange("p (t j h d) -> p t j h d", t=UNIT, j=GROUP, h=2)
        for y in range(2):
            for hh in range(2):
                last = act.activation(V.vd[b][half(hh), :, :, y, hh, 0:DH], xv[half(y), :, :, hh, :], ACT.Copy)
        last.then_inc(K.v_ready.sem, 1)

    def probs(s, t):
        act.wait_ge(K.shift_ready.sem, K.shift_ready.value(p, s, t + 1))
        pr = V.probs[t % 2]
        act.activation(pr, pr, ACT.Exp, scale=DH ** -0.5).then_inc(K.probs_ready.sem, 1)

    def turned(s, t):
        if p == A0:
            act.wait_ge(K.pT_psum.sem, K.pT_psum.value(p, s, t + 1))
            if K.av_psum.due(p, s, t - 1):
                act.wait_ge(K.av_psum.sem, K.av_psum.value(p, s, t - 1))
            act.activation(V.pT[t % 2], K.ps[:, PT_BANKS[0]:PT_BANKS[1] + 1, :].rearrange("p b (j q) -> p (b j) q", q=P),
                           ACT.Copy).then_inc(K.pT_ready.sem, 1)

    def outputs_turned(s):
        act.wait_ge(K.oT_psum.sem, K.oT_psum.value(p, s, 1))
        if K.proj_psum.due(p, s, 0):
            act.wait_ge(K.proj_psum.sem, K.proj_psum.value(p, s, 0))
        act.activation(V.outT, x, ACT.Identity, bias=K.col["bv"]).then_inc(K.oT_ready.sem, 1)

    cT_evacuate(nc, act, K, p, 0, 0, x)
    yT_evacuate(nc, act, K, p, 0, 0, x)
    act.wait_ge(K.fill, fills(K, p))
    queries(0, 0)
    values(0, 0)
    probs(0, 0)

    def body(s, b, later):
        n, nb = s + 1, 1 - b
        turned(s, 0)
        probs(s, 1)
        if later:
            cT_evacuate(nc, act, K, p, n, nb, x)
            yT_evacuate(nc, act, K, p, n, nb, x)
        turned(s, 1)
        probs(s, 2)
        if later:
            queries(n, nb)
        if p == A1 and not (isinstance(s, int) and s == 0):
            outputs_turned(s - 1)
        turned(s, 2)
        probs(s, 3)
        if later:
            values(n, nb)
        turned(s, 3)
        if later:
            probs(n, 0)
    over_units_ahead(act, body)
    if p == A1:
        outputs_turned(UNITS - 1)


def small_vector(nc, dve, K, p):
    V = K.v[p]
    x = K.bank[X_BANK]

    def keys(s, b):
        dve.wait_ge(K.k_psum.sem, K.k_psum.value(p, s, 1))
        if K.kbd_ready.due(p, s, -UNIT):
            dve.wait_ge(K.kbd_ready.sem, K.kbd_ready.value(p, s, -UNIT))
        name = "k_b" if p == A0 else "bk"
        xv = x.rearrange("p (t y k) -> p t y k", t=UNIT, y=2)
        for g in range(2):
            for y in range(2):
                last = dve.tensor_scalar(V.ksel[b][half(y), g, :, :], xv[half(g), :, y, :], K.col[name][half(g)], None,
                                         ALU.add)
        last.then_inc(K.k_ready.sem, 1)

    def shift(s, t):
        steps = Steps(K.max_steps, p, s, t * (K.max_steps.counts[p] // UNIT))
        dve.wait_ge(K.s_psum.sem, K.s_psum.value(p, s, t + 1))
        lo, hi = S_BANKS[t % 2]
        sc = K.ps[:, lo:hi + 1, :].rearrange("p b (h k) -> p (b h) k", k=SEQ)
        mx = V.max[:, t % 2, :]
        dve.tensor_reduce(mx, sc, axis=AX.X, op=ALU.max).then_inc(steps.sem, steps.one())
        c = CLAMP * DH ** 0.5
        if p == A1:
            dve.wait_ge(steps.sem, steps.value())
            dve.tensor_scalar(mx, mx, c, -c, ALU.min, ALU.max).then_inc(steps.sem, steps.one())
        dve.wait_ge(steps.sem, steps.value())
        if K.pT_psum.due(p, s, t - 1):
            dve.wait_ge(K.pT_psum.sem, K.pT_psum.value(p, s, t - 1))
        mxb = mx.unsqueeze(2).to_broadcast([P, HEADS, SEQ])
        if p == A1:
            dve.scalar_tensor_tensor(out=V.probs[t % 2], in0=sc, scalar=-c, in1=mxb, op0=ALU.max,
                                     op1=ALU.subtract).then_inc(K.shift_ready.sem, 1)
        else:
            dve.tensor_tensor(V.probs[t % 2], sc, mxb, ALU.subtract).then_inc(K.shift_ready.sem, 1)

    def turned(s, t):
        if p == A1:
            dve.wait_ge(K.pT_psum.sem, K.pT_psum.value(p, s, t + 1))
            if K.av_psum.due(p, s, t - 1):
                dve.wait_ge(K.av_psum.sem, K.av_psum.value(p, s, t - 1))
            dve.tensor_scalar(V.pT[t % 2], K.ps[:, PT_BANKS[0]:PT_BANKS[1] + 1, :].rearrange("p b (j q) -> p (b j) q", q=P),
                              1.0, None, ALU.min).then_inc(K.pT_ready.sem, 1)

    def outputs(s, b, t):
        dve.wait_ge(K.av_psum.sem, K.av_psum.value(p, s, t + 1))
        if t == 0 and p == A1:
            if K.oT_psum.due(p, s, -1):
                dve.wait_ge(K.oT_psum.sem, K.oT_psum.value(p, s, -1))
        steps = Steps(K.sum_steps, p, s, t)
        o = K.bank[O_BANK][:, 0:GROUP * 4 * (DH + 1)].rearrange("p (j y h d) -> p j y h d", j=GROUP, y=2, h=2)
        rs = V.rsum.rearrange("p (j h) -> p j h", h=2)
        for y in range(2):
            last = dve.reciprocal(rs[half(y)], o[half(y), :, y, :, DH])
        last.then_inc(steps.sem, steps.one())
        dve.wait_ge(steps.sem, steps.value())
        for y in range(2):
            last = dve.tensor_tensor(V.out[b][half(y), t, :].rearrange("p (j h d) -> p j h d", j=GROUP, h=2),
                                     o[half(y), :, y, :, 0:DH],
                                     rs[half(y)].unsqueeze(3).to_broadcast([SEQ, GROUP, 2, DH]), ALU.mult)
        last.then_inc(K.out_ready.sem, 1)

    def residual(s, b):
        if p == A0:
            dve.wait_ge(K.out_ready.sem, K.out_ready.value(p, s, UNIT))
            src, add = V.out[b], K.row["v_b"]
        else:
            dve.wait_ge(K.proj_psum.sem, K.proj_psum.value(p, s, 1))
            src, add = x.rearrange("p (t d) -> p t d", t=UNIT), K.row["bo1"]
        add_residual(nc, dve, K, p, s, V.res, src, add)

    def statistics(s, b):
        x_statistics(nc, dve, K, p, s)
        if p == A0:
            ctx_statistics(nc, dve, K, p, s, b)

    def normed(s, b):
        if p == A0:
            ctx_normed(nc, dve, K, p, s, b)
        x_normed(nc, dve, K, p, s)

    if p == A0:
        ctx_statistics(nc, dve, K, p, 0, 0)
        ctx_normed(nc, dve, K, p, 0, 0)
    if p == K.phases[0]:
        norm_first(nc, dve, K, p)
    keys(0, 0)
    statistics(1, 1)
    shift(0, 0)
    normed(1, 1)
    shift(0, 1)

    def body(s, b, later):
        n, nb = s + 1, 1 - b
        turned(s, 0)
        shift(s, 2)
        if later:
            keys(n, nb)
        outputs(s, b, 0)
        turned(s, 1)
        shift(s, 3)
        if later == 2:
            statistics(s + 2, b)
        outputs(s, b, 1)
        if not (isinstance(s, int) and s == 0):
            residual(s - 1, nb)
        turned(s, 2)
        if later:
            shift(n, 0)
        outputs(s, b, 2)
        turned(s, 3)
        if later == 2:
            normed(s + 2, b)
        if later:
            shift(n, 1)
        outputs(s, b, 3)
    if p == A0:
        dve.wait_ge(K.x_rest, 16)
    over_units_ahead(dve, body)
    norm_first(nc, dve, K, following(K, p))
    residual(UNITS - 1, 1)


def add_residual(nc, dve, K, p, s, tmp, src, add):
    gate = K.gates[:, p // 2:p // 2 + 1]
    if K.x_done.due(p, s, 0):
        dve.wait_ge(K.x_done.sem, K.x_done.value(p, s, 0))
    dve.tensor_tensor(tmp, src, add.unsqueeze(1).to_broadcast([P, UNIT, D]), ALU.add).then_inc(K.res_steps.sem, 1)
    dve.wait_ge(K.res_steps.sem, K.res_steps.value(p, s, 1))
    dve.scalar_tensor_tensor(out=xu(K, s), in0=tmp, scalar=gate, in1=xu(K, s), op0=ALU.mult,
                             op1=ALU.add).then_inc(K.x_done.sem, 1)


def small_pool(nc, pool, K, p):
    V = K.v[p]

    def spread(s, b, t):
        if t == 0:
            pool.wait_ge(K.k_ready.sem, K.k_ready.value(p, s, 1))
        if K.s_psum.due(p, s, t - 1):
            pool.wait_ge(K.s_psum.sem, K.s_psum.value(p, s, t - 1))
        for g in range(2):
            last = pool.tensor_tensor(V.kbd[t % 2][:, g, :, :],
                                      V.ksel[b][:, g, t, :].unsqueeze(1).to_broadcast([P, GROUP, SEQ]),
                                      V.diag.unsqueeze(2).to_broadcast([P, GROUP, SEQ]), ALU.mult)
        last.then_inc(K.kbd_ready.sem, 1)

    def factors(s):
        rstd_pool(nc, pool, K, p, s, False)
        if p == A0:
            rstd_pool(nc, pool, K, p, s, True)

    if p == A0:
        rstd_pool(nc, pool, K, p, 0, True)
    if p == K.phases[0]:
        norm_first_pool(nc, pool, K, p)
    spread(0, 0, 0)
    spread(0, 0, 1)
    factors(1)

    def body(s, b, later):
        n, nb = s + 1, 1 - b
        spread(s, b, 2)
        spread(s, b, 3)
        if later:
            spread(n, nb, 0)
        if later == 2:
            factors(s + 2)
        if later:
            spread(n, nb, 1)
    over_units_ahead(pool, body)


def small_fill(nc, pool, K, p, count):
    V = K.v[p]
    lo, hi = V.zeroed
    pool.memset(K.arena[:, lo:hi], 0.0).then_inc(K.fill, 1)
    pool.memset(V.diag, 1.0).then_inc(K.fill, 1)
    pool.wait_ge(K.fill, count + 2)
    for b in range(2):
        for hh in range(2):
            pool.memset(V.vd[b][half(hh), :, :, :, hh, DH].rearrange("p t j y -> p (t j) y"), 1.0)
    for y in range(2):
        dg = V.diag[half(y)]
        pool.affine_select(out=dg, in_=dg, compare_op=ALU.is_ge, fill=0.0, base=0,
                           pattern=[[-DH, GROUP]], channel_multiplier=1).then_inc(K.fill, 1)
    pool.wait_ge(K.fill, count + 4)
    for y in range(2):
        dg = V.diag[half(y)]
        pool.affine_select(out=dg, in_=dg, compare_op=ALU.is_ge, fill=0.0, base=DH - 1,
                           pattern=[[DH, GROUP]], channel_multiplier=-1).then_inc(K.fill, 1)
    pool.wait_ge(K.fill, count + 6)
    return count + 6


PT2_BANK = 2
O2_BANKS = (3, 4)


def piece_bank(K, i):
    return K.bank[5 + i % 3]


def l2_tensor(nc, pe, K):
    p = A2
    V, W = K.v[p], K.wp[p]
    mm = nc.tensor.matmul

    def piece(s, b, i):
        if K.front_read.due(p, s, max(0, i - 2)):
            pe.wait_ge(K.front_read.sem, K.front_read.value(p, s, max(0, i - 2)))
        if i == 0:
            pe.wait_ge(K.ctx_loaded.sem, K.ctx_loaded.value(p, s, 16))
            if K.res_steps.due(p, s, -1):
                pe.wait_ge(K.res_steps.sem, K.res_steps.value(p, s, -1))
        bank = piece_bank(K, i)
        if i == 0:
            last = transpose4(nc, K, bank, lambda t: V.ctx[b][:, t, :], DC)
        elif i < 5:
            pe.wait_ge(K.front_read.sem, K.front_read.value(p, s, 1))
            last = mm(bank, W["k"][:, (i - 1) * P:i * P], V.cT[b], start=True, stop=True)
        elif i == 5:
            pe.wait_ge(K.y_ready.sem, K.y_ready.value(p, s, 1))
            last = transpose4(nc, K, bank, lambda t: K.yt[:, t, :], P)
        elif i < 10:
            pe.wait_ge(K.front_read.sem, K.front_read.value(p, s, 6))
            last = mm(bank, W["q"][:, (i - 6) * P:(i - 5) * P], K.yT[b][:, :], start=True, stop=True)
        else:
            t = i - 10
            last = mm(bank, V.cT[b][:, t * P:(t + 1) * P], W["v"][:, :], start=True, stop=True)
        last.then_inc(K.front_psum.sem, 1)

    def scores(s, b, t):
        if K.shift_ready.due(p, s, t):
            pe.wait_ge(K.shift_ready.sem, K.shift_ready.value(p, s, t))
        pe.wait_ge(K.front_read.sem, K.front_read.value(p, s, 10))
        for j in range(PAIRS2):
            for h in range(2):
                for y in range(2):
                    tok = slice(t * P + y * SEQ, t * P + (y + 1) * SEQ)
                    rows, qs = whole_first(j + h + y == 0, y, t)
                    last = mm(K.bank[h][rows, j * SEQ:(j + 1) * SEQ], V.q[b][half(h), j, qs],
                              V.k[b][half(h), j, tok], start=True, stop=True)
        last.then_inc(K.s_psum.sem, 1)

    def turned(s, t):
        pe.wait_ge(K.probs_ready.sem, K.probs_ready.value(p, s, t + 1))
        if K.pT_ready.due(p, s, t):
            pe.wait_ge(K.pT_ready.sem, K.pT_ready.value(p, s, t))
        for j in range(PAIRS2):
            last = nc.tensor.transpose(K.bank[PT2_BANK][:, j * P:(j + 1) * P],
                                       V.probs[t % 2][:, j, :, :].rearrange("p h k -> p (h k)"), K.ident[:, :])
        last.then_inc(K.pT_psum.sem, 1)

    def weighted(s, b, t):
        pe.wait_ge(K.pT_ready.sem, K.pT_ready.value(p, s, t + 1))
        if K.out_ready.due(p, s, t):
            pe.wait_ge(K.out_ready.sem, K.out_ready.value(p, s, t))
        if t == 0:
            pe.wait_ge(K.front_read.sem, K.front_read.value(p, s, FRONT2))
        n = DH2 + 1
        for j in range(PAIRS2):
            for h in range(2):
                for y in range(2):
                    rows, qs = whole_first(j + h + y == 0, y, 0)
                    last = mm(K.bank[O2_BANKS[h]][rows, j * n:(j + 1) * n], V.pT[t % 2][half(h), j, qs],
                              V.vd[b][half(h), t, y, j, :], start=True, stop=True)
        last.then_inc(K.av_psum.sem, 1)

    def project(s, nxt):
        pe.wait_ge(K.out_ready.sem, K.out_ready.value(p, s, UNIT))
        if nxt is not None:
            pe.wait_ge(K.front_read.sem, K.front_read.value(p, nxt, FRONT2))
        for j in range(PAIRS2):
            if K.oT_ready.due(p, s, j - 2):
                pe.wait_ge(K.oT_ready.sem, K.oT_ready.value(p, s, j - 2))
            transpose4(nc, K, piece_bank(K, FRONT2 + j),
                       lambda t: V.out[:, t, j, :, :].rearrange("p h d -> p (h d)"), P).then_inc(K.oT_psum.sem, 1)
        pe.wait_ge(K.oT_ready.sem, K.oT_ready.value(p, s, PAIRS2))
        bank = piece_bank(K, FRONT2 + PAIRS2)
        for t in range(UNIT):
            for j in range(PAIRS2):
                last = mm(bank[:, t * P:(t + 1) * P], V.outT[:, j, t * P:(t + 1) * P], W["o"][:, j, :],
                          start=j == 0, stop=j == PAIRS2 - 1)
        last.then_inc(K.proj_psum.sem, 1)

    pe.wait_ge(K.loaded[p], 16 * LOADS[p])
    for i in range(FRONT2):
        piece(0, 0, i)
    scores(0, 0, 0)

    def body(s, b, last):
        def pieces(lo, hi):
            if not last:
                for i in range(lo, hi):
                    piece(s + 1, 1 - b, i)
        pieces(0, 2)
        turned(s, 0)
        scores(s, b, 1)
        pieces(2, 5)
        weighted(s, b, 0)
        turned(s, 1)
        pieces(5, 6)
        scores(s, b, 2)
        pieces(6, 9)
        weighted(s, b, 1)
        turned(s, 2)
        scores(s, b, 3)
        pieces(9, 12)
        weighted(s, b, 2)
        turned(s, 3)
        if not last:
            scores(s + 1, 1 - b, 0)
        pieces(12, 14)
        weighted(s, b, 3)
        project(s, None if last else s + 1)
    over_units(pe, body)


def l2_scalar(nc, act, K):
    p = A2
    V = K.v[p]

    def piece(s, b, i):
        act.wait_ge(K.front_psum.sem, K.front_psum.value(p, s, i + 1))
        bank = piece_bank(K, i)
        if i == 0:
            cT_evacuate(nc, act, K, p, s, b, bank)
        elif i < 5:
            act.activation(V.k[b][:, i - 1, :], bank, ACT.Copy).then_inc(K.front_read.sem, 1)
        elif i == 5:
            yT_evacuate(nc, act, K, p, s, b, bank)
        elif i < 10:
            act.activation(V.q[b][:, i - 6, :], bank, ACT.Copy).then_inc(K.front_read.sem, 1)
        else:
            t = i - 10
            v = bank.rearrange("p (j h d) -> p j h d", j=PAIRS2, h=2)
            for y in range(2):
                for h in range(2):
                    last = act.activation(V.vd[b][half(h), t, y, :, 0:DH2], v[half(y), :, h, :], ACT.Copy)
            last.then_inc(K.front_read.sem, 1)

    def probs(s, t):
        act.wait_ge(K.shift_ready.sem, K.shift_ready.value(p, s, t + 1))
        pr = V.probs[t % 2]
        act.activation(pr, pr, ACT.Exp, scale=DH2 ** -0.5).then_inc(K.probs_ready.sem, 1)

    def turned(s, t):
        act.wait_ge(K.pT_psum.sem, K.pT_psum.value(p, s, t + 1))
        if K.av_psum.due(p, s, t - 1):
            act.wait_ge(K.av_psum.sem, K.av_psum.value(p, s, t - 1))
        act.activation(V.pT[t % 2], K.bank[PT2_BANK].rearrange("p (j q) -> p j q", q=P),
                       ACT.Copy).then_inc(K.pT_ready.sem, 1)

    for i in range(FRONT2):
        piece(0, 0, i)
    probs(0, 0)

    def body(s, b, last):
        def pieces(lo, hi):
            if not last:
                for i in range(lo, hi):
                    piece(s + 1, 1 - b, i)
        pieces(0, 2)
        turned(s, 0)
        probs(s, 1)
        pieces(2, 5)
        turned(s, 1)
        pieces(5, 6)
        probs(s, 2)
        pieces(6, 9)
        turned(s, 2)
        probs(s, 3)
        pieces(9, 12)
        turned(s, 3)
        if not last:
            probs(s + 1, 0)
        pieces(12, 14)
        for j in range(PAIRS2):
            act.wait_ge(K.oT_psum.sem, K.oT_psum.value(p, s, j + 1))
            if K.proj_psum.due(p, s, 0):
                act.wait_ge(K.proj_psum.sem, K.proj_psum.value(p, s, 0))
            act.activation(V.outT[:, j, :], piece_bank(K, FRONT2 + j), ACT.Copy).then_inc(K.oT_ready.sem, 1)
    over_units(act, body)


def l2_vector(nc, dve, K):
    p = A2
    V = K.v[p]

    def shift(s, t):
        steps = Steps(K.max_steps, p, s, t)
        dve.wait_ge(K.s_psum.sem, K.s_psum.value(p, s, t + 1))
        sc = K.ps[:, 0:2, 0:PAIRS2 * SEQ].rearrange("p h (j k) -> p h j k", k=SEQ)
        mx = V.max[:, t % 2, :, :]
        dve.tensor_reduce(mx, sc, axis=AX.X, op=ALU.max).then_inc(steps.sem, steps.one())
        dve.wait_ge(steps.sem, steps.value())
        if K.pT_psum.due(p, s, t - 1):
            dve.wait_ge(K.pT_psum.sem, K.pT_psum.value(p, s, t - 1))
        dve.tensor_tensor(V.probs[t % 2].rearrange("p j h k -> p h j k"), sc,
                          mx.unsqueeze(3).to_broadcast([P, 2, PAIRS2, SEQ]), ALU.subtract).then_inc(K.shift_ready.sem, 1)

    def outputs(s, t):
        dve.wait_ge(K.av_psum.sem, K.av_psum.value(p, s, t + 1))
        if t == 0:
            if K.oT_psum.due(p, s, 0):
                dve.wait_ge(K.oT_psum.sem, K.oT_psum.value(p, s, 0))
        steps = Steps(K.sum_steps, p, s, t)
        o = K.ps[:, O2_BANKS[0]:O2_BANKS[1] + 1, 0:PAIRS2 * (DH2 + 1)].rearrange("p h (j d) -> p h j d", j=PAIRS2)
        dve.reciprocal(V.rsum, o[:, :, :, DH2]).then_inc(steps.sem, steps.one())
        dve.wait_ge(steps.sem, steps.value())
        dve.tensor_tensor(V.out[:, t].rearrange("p j h d -> p h j d"), o[:, :, :, 0:DH2],
                          V.rsum.unsqueeze(3).to_broadcast([P, 2, PAIRS2, DH2]), ALU.mult).then_inc(K.out_ready.sem, 1)

    if p == K.phases[0]:
        norm_first(nc, dve, K, p)
    shift(0, 0)

    def body(s, b, last):
        if not last:
            x_statistics(nc, dve, K, p, s + 1)
        shift(s, 1)
        if not last:
            x_normed(nc, dve, K, p, s + 1)
        outputs(s, 0)
        shift(s, 2)
        outputs(s, 1)
        shift(s, 3)
        outputs(s, 2)
        if not last:
            shift(s + 1, 0)
        outputs(s, 3)
        if last:
            norm_first(nc, dve, K, following(K, p))
        dve.wait_ge(K.proj_psum.sem, K.proj_psum.value(p, s, 1))
        add_residual(nc, dve, K, p, s, V.res,
                     piece_bank(K, FRONT2 + PAIRS2).rearrange("p (t d) -> p t d", t=UNIT), K.row["bo2"])
    over_units(dve, body)


def norm_pool(nc, pool, K, p):
    if p == K.phases[0]:
        norm_first_pool(nc, pool, K, p)

    def body(s, b, last):
        if not last:
            rstd_pool(nc, pool, K, p, s + 1, False)
    over_units(pool, body)


S3_BANKS = ((0, 1), (2, 3))
PT3_BANK, O3_BANK = 4, 5
PIECE3 = (6, 7, 6, 7, 6, 7, 6, 7, 6, 7, 6)
OT3_BANK, Y3_BANK = 6, 7


def l3_tensor(nc, pe, K):
    p = A3
    V, W = K.v[p], K.wp[p]
    mm = nc.tensor.matmul

    def piece(s, b, i):
        bank = K.bank[PIECE3[i]]
        if i == 0:
            pe.wait_ge(K.c_ready.sem, K.c_ready.value(p, s, 1))
            if K.front_read.due(p, s, 0):
                pe.wait_ge(K.front_read.sem, K.front_read.value(p, s, 0))
            last = transpose4(nc, K, bank, lambda t: V.ctxn[:, t, :], DC)
        elif i == 1:
            pe.wait_ge(K.y_ready.sem, K.y_ready.value(p, s, 1))
            if K.res_steps.due(p, s, -1):
                pe.wait_ge(K.res_steps.sem, K.res_steps.value(p, s, -1))
            last = transpose4(nc, K, bank, lambda t: K.yt[:, t, :], P)
        elif i < 4:
            pe.wait_ge(K.front_read.sem, K.front_read.value(p, s, i - 1))
            for t in range(2):
                tt = 2 * (i - 2) + t
                last = mm(bank[:, t * 2 * D:(t + 1) * 2 * D], V.cT[b][:, tt * P:(tt + 1) * P], W["kv"][:, :],
                          start=True, stop=True)
        elif i < 8:
            t = i - 4
            pe.wait_ge(K.front_read.sem, K.front_read.value(p, s, i - 1))
            last = mm(bank[:, 0:3 * D], K.yT[b][:, t * P:(t + 1) * P], W["qkv"][:, :], start=True, stop=True)
        else:
            if i == 8:
                pe.wait_ge(K.qk_normed.sem, K.qk_normed.value(p, s, UNIT))
                pe.wait_ge(K.front_read.sem, K.front_read.value(p, s, 8))
            elif i == 10:
                pe.wait_ge(K.front_read.sem, K.front_read.value(p, s, 9))
            last = transpose4(nc, K, bank, lambda t: V.normed[:, i - 8, t, :], P)
        last.then_inc(K.front_psum.sem, 1)

    def scores(s, b, t):
        if t == 0:
            pe.wait_ge(K.front_read.sem, K.front_read.value(p, s, FRONT3))
        if K.shift_ready.due(p, s, t - 1):
            pe.wait_ge(K.shift_ready.sem, K.shift_ready.value(p, s, t - 1))
        for h in range(2):
            for y in range(2):
                rows, qs = whole_first(h + y == 0, y, t)
                last = mm(K.bank[S3_BANKS[t % 2][h]][rows, 0:KEYS3], V.q[b][half(h), qs],
                          V.k[b][half(h), t, y, :, :].rearrange("p c k -> p (c k)"), start=True, stop=True)
        last.then_inc(K.s_psum.sem, 1)

    def turned(s, t):
        pe.wait_ge(K.probs_ready.sem, K.probs_ready.value(p, s, t + 1))
        if K.pT_ready.due(p, s, t):
            pe.wait_ge(K.pT_ready.sem, K.pT_ready.value(p, s, t))
        for h in range(2):
            last = nc.tensor.transpose(K.bank[PT3_BANK][:, h * P:(h + 1) * P], V.probs[t % 2][:, h, :], K.ident[:, :])
        last.then_inc(K.pT_psum.sem, 1)

    def weighted(s, b, t):
        pe.wait_ge(K.pT_ready.sem, K.pT_ready.value(p, s, t + 1))
        if K.out_ready.due(p, s, t):
            pe.wait_ge(K.out_ready.sem, K.out_ready.value(p, s, t))
        if t == 0:
            pe.wait_ge(K.v_ready.sem, K.v_ready.value(p, s, 1))
        n = DH2 + 1
        for h in range(2):
            for y in range(2):
                last = mm(K.bank[O3_BANK][half(y), h * n:(h + 1) * n], V.pT[t % 2][:, h, half(y)],
                          V.vd[b][:, t, y, h, :], start=True, stop=True)
        last.then_inc(K.av_psum.sem, 1)

    def outputs_turned(s):
        pe.wait_ge(K.out_ready.sem, K.out_ready.value(p, s, UNIT))
        transpose4(nc, K, K.bank[OT3_BANK], lambda t: V.out[:, t].rearrange("p h d -> p (h d)"), P).then_inc(K.oT_psum.sem, 1)

    def project(s):
        pe.wait_ge(K.oT_ready.sem, K.oT_ready.value(p, s, 1))
        if K.x_done.due(p, s, 0):
            pe.wait_ge(K.x_done.sem, K.x_done.value(p, s, 0))
        for t in range(UNIT):
            last = mm(K.bank[Y3_BANK][:, t * P:(t + 1) * P], V.outT[:, t * P:(t + 1) * P], W["o"][:, :],
                      start=True, stop=True)
        last.then_inc(K.proj_psum.sem, 1)

    def pieces(s, b, lo, hi):
        for i in range(lo, hi):
            piece(s, b, i)

    pe.wait_ge(K.loaded[p], 16 * LOADS[p])
    raw = W["raw"]
    for n, i in enumerate((2, 0, 1, 3)):
        nc.tensor.transpose(K.bank[0][:, n * P:(n + 1) * P], raw[:, i, :], K.ident[:, :])
    for c in range(2):
        last = nc.tensor.transpose(K.bank[1][0:DC, c * P:(c + 1) * P], raw[:, 4 + c, 0:DC], K.ident[:, :])
    last.then_inc(K.l3w_psum, 1)
    pe.wait_ge(K.l3w_ready, 3)
    pieces(0, 0, 0, FRONT3)
    scores(0, 0, 0)
    scores(0, 0, 1)

    def body(s, b, later):
        n, nb = s + 1, 1 - b

        def ahead(lo, hi):
            if later:
                pieces(n, nb, lo, hi)
        back = not (isinstance(s, int) and s == 0)
        turned(s, 0)
        if back:
            outputs_turned(s - 1)
        scores(s, b, 2)
        if back:
            project(s - 1)
        weighted(s, b, 0)
        ahead(0, 4)
        turned(s, 1)
        scores(s, b, 3)
        ahead(4, 8)
        weighted(s, b, 1)
        turned(s, 2)
        weighted(s, b, 2)
        turned(s, 3)
        weighted(s, b, 3)
        ahead(8, 11)
        if later:
            scores(n, nb, 0)
            scores(n, nb, 1)
    over_units_ahead(pe, body)
    outputs_turned(UNITS - 1)
    project(UNITS - 1)


def l3_scalar(nc, act, K):
    p = A3
    V, W = K.v[p], K.wp[p]

    def piece(s, b, i):
        act.wait_ge(K.front_psum.sem, K.front_psum.value(p, s, i + 1))
        bank = K.bank[PIECE3[i]]
        if i == 0:
            cT_evacuate(nc, act, K, p, s, b, bank)
            return
        if i == 1:
            yT_evacuate(nc, act, K, p, s, b, bank)
            return
        if i < 8:
            if K.qk_normed.due(p, s, 0):
                act.wait_ge(K.qk_normed.sem, K.qk_normed.value(p, s, 0))
            if K.v_ready.due(p, s, 0):
                act.wait_ge(K.v_ready.sem, K.v_ready.value(p, s, 0))
        if i < 4:
            last = act.activation(V.raw[:, 2 * (i - 2):2 * (i - 1), 3:5, :].rearrange("p t c d -> p t (c d)"),
                                  bank.rearrange("p (t n) -> p t n", t=2), ACT.Copy)
        elif i < 8:
            last = act.activation(V.raw[:, i - 4, 0:3, :].rearrange("p c d -> p (c d)"), bank[:, 0:3 * D], ACT.Copy)
        elif i == 8:
            last = act.activation(V.q[b], bank, ACT.Copy, scale=K.col["qn_g"])
        else:
            last = act.activation(V.k[b][:, :, :, 10 - i, :] if i == 10 else V.k[b][:, :, :, 1, :],
                                  bank.rearrange("p (t y k) -> p t y k", t=UNIT, y=2), ACT.Copy, scale=K.col["kn_g"])
        last.then_inc(K.front_read.sem, 1)
        if 4 <= i < 8:
            t = i - 4
            act.wait_ge(K.front_read.sem, K.front_read.value(p, s, i + 1))
            if K.rms_steps.due(p, s, 0):
                act.wait_ge(K.rms_steps.sem, K.rms_steps.value(p, s, 0))
            act.activation(V.sq[:, t, :, :], V.raw[:, t, 1:4, :], ACT.Square).then_inc(K.squares.sem, 1)

    def probs(s, t):
        act.wait_ge(K.shift_ready.sem, K.shift_ready.value(p, s, t + 1))
        pr = V.probs[t % 2]
        act.activation(pr, pr, ACT.Exp, scale=DH2 ** -0.5).then_inc(K.probs_ready.sem, 1)

    def turned(s, t):
        act.wait_ge(K.pT_psum.sem, K.pT_psum.value(p, s, t + 1))
        if K.av_psum.due(p, s, t - 1):
            act.wait_ge(K.av_psum.sem, K.av_psum.value(p, s, t - 1))
        act.activation(V.pT[t % 2], K.bank[PT3_BANK][:, 0:2 * P].rearrange("p (h q) -> p h q", q=P),
                       ACT.Copy).then_inc(K.pT_ready.sem, 1)

    def outputs_turned(s):
        act.wait_ge(K.oT_psum.sem, K.oT_psum.value(p, s, 1))
        if K.proj_psum.due(p, s, 0):
            act.wait_ge(K.proj_psum.sem, K.proj_psum.value(p, s, 0))
        act.activation(V.outT, K.bank[OT3_BANK], ACT.Copy).then_inc(K.oT_ready.sem, 1)

    act.wait_ge(K.l3w_psum, 1)
    act.activation(W["qkv"][:, :], K.bank[0][:, 0:3 * P], ACT.Copy).then_inc(K.l3w_ready, 1)
    act.activation(W["o"][:, :], K.bank[0][:, 3 * P:4 * P], ACT.Copy).then_inc(K.l3w_ready, 1)
    act.activation(W["kv"][:, :], K.bank[1][0:DC, 0:2 * P], ACT.Copy).then_inc(K.l3w_ready, 1)
    for i in range(FRONT3):
        piece(0, 0, i)
    probs(0, 0)

    def body(s, b, later):
        n, nb = s + 1, 1 - b

        def ahead(lo, hi):
            if later:
                for i in range(lo, hi):
                    piece(n, nb, i)
        turned(s, 0)
        probs(s, 1)
        if not (isinstance(s, int) and s == 0):
            outputs_turned(s - 1)
        ahead(0, 4)
        turned(s, 1)
        probs(s, 2)
        ahead(4, 8)
        turned(s, 2)
        probs(s, 3)
        turned(s, 3)
        ahead(8, 11)
        if later:
            probs(n, 0)
    over_units_ahead(act, body)
    outputs_turned(UNITS - 1)


def l3_vector(nc, dve, K):
    p = A3
    V = K.v[p]

    def shift(s, b, t):
        steps = Steps(K.max_steps, p, s, 2 * t)
        dve.wait_ge(K.s_psum.sem, K.s_psum.value(p, s, t + 1))
        if K.pT_psum.due(p, s, t - 1):
            dve.wait_ge(K.pT_psum.sem, K.pT_psum.value(p, s, t - 1))
        if t == 0:
            dve.wait_ge(K.maskbias.sem, K.maskbias.value(p, s, 1))
        lo, hi = S3_BANKS[t % 2]
        pr, mx = V.probs[t % 2], V.max[:, t % 2, :]
        dve.tensor_tensor(pr, K.ps[:, lo:hi + 1, 0:KEYS3],
                          V.mb[b][:, t, :].unsqueeze(1).to_broadcast([P, 2, KEYS3]), ALU.add).then_inc(steps.sem, steps.one())
        dve.wait_ge(steps.sem, steps.value())
        dve.tensor_reduce(mx, pr, axis=AX.X, op=ALU.max).then_inc(steps.sem, steps.one())
        dve.wait_ge(steps.sem, steps.value())
        dve.tensor_tensor(pr, pr, mx.unsqueeze(2).to_broadcast([P, 2, KEYS3]), ALU.subtract).then_inc(K.shift_ready.sem, 1)

    def outputs(s, t):
        dve.wait_ge(K.av_psum.sem, K.av_psum.value(p, s, t + 1))
        if t == 0:
            if K.oT_psum.due(p, s, 0):
                dve.wait_ge(K.oT_psum.sem, K.oT_psum.value(p, s, 0))
        steps = Steps(K.sum_steps, p, s, t)
        o = K.bank[O3_BANK][:, 0:2 * (DH2 + 1)].rearrange("p (h d) -> p h d", h=2)
        dve.reciprocal(V.rsum, o[:, :, DH2]).then_inc(steps.sem, steps.one())
        dve.wait_ge(steps.sem, steps.value())
        dve.tensor_tensor(V.out[:, t], o[:, :, 0:DH2], V.rsum.unsqueeze(2).to_broadcast([P, 2, DH2]),
                          ALU.mult).then_inc(K.out_ready.sem, 1)

    def mask_bias(s, b):
        if K.shift_ready.due(p, s, -UNIT):
            dve.wait_ge(K.shift_ready.sem, K.shift_ready.value(p, s, -UNIT))
        dve.tensor_scalar(V.mb[b][:, :, 0:SEQ], K.mask[:, bass.ds(s * UNIT, UNIT), :], 1.0, MASKED,
                          ALU.subtract, ALU.mult).then_inc(K.maskbias.sem, 1)

    def values(s, b):
        dve.wait_ge(K.front_read.sem, K.front_read.value(p, s, 8))
        for src, slot in ((0, 4), (1, 0)):
            for y in range(2):
                last = dve.tensor_copy(V.vd[b][half(src), :, y, :, 0:DH2],
                                       V.raw[half(y), :, slot, :].rearrange("p t (h d) -> p t h d", h=2))
        last.then_inc(K.v_ready.sem, 1)

    def square_sums(s, t):
        dve.wait_ge(K.squares.sem, K.squares.value(p, s, t + 1))
        steps = Steps(K.rms_steps, p, s, 2 * t)
        dve.tensor_reduce(V.ss[:, t, :, :], V.sq[:, t, :, :].rearrange("p c (h d) -> p c h d", h=2), axis=AX.X,
                          op=ALU.add).then_inc(steps.sem, steps.one())
        dve.wait_ge(steps.sem, steps.value())
        dve.tensor_scalar(V.ss[:, t, :, :], V.ss[:, t, :, :], 1.0 / DH2, 1e-16, ALU.mult,
                          ALU.max).then_inc(steps.sem, steps.one())

    def rms_normed(s, t):
        dve.wait_ge(K.rms_ready.sem, K.rms_ready.value(p, s, t + 1))
        if K.front_psum.due(p, s, 0):
            dve.wait_ge(K.front_psum.sem, K.front_psum.value(p, s, 0))
        dve.tensor_tensor(V.normed[:, :, t, :].rearrange("p c (h d) -> p c h d", h=2),
                          V.raw[:, t, 1:4, :].rearrange("p c (h d) -> p c h d", h=2),
                          V.rms[:, t, :, :].unsqueeze(3).to_broadcast([P, 3, 2, DH2]), ALU.mult)\
            .then_inc(K.qk_normed.sem, 1)

    def residual(s):
        dve.wait_ge(K.proj_psum.sem, K.proj_psum.value(p, s, 1))
        add_residual(nc, dve, K, p, s, V.res, K.bank[Y3_BANK].rearrange("p (t d) -> p t d", t=UNIT), K.row["bo3"])

    def statistics(s, b):
        ctx_statistics(nc, dve, K, p, s, b)
        x_statistics(nc, dve, K, p, s)

    def normed(s, b):
        ctx_normed(nc, dve, K, p, s, b)
        x_normed(nc, dve, K, p, s)

    if p == K.phases[0]:
        norm_first(nc, dve, K, p)
    ctx_normed(nc, dve, K, p, 0, 0)
    mask_bias(0, 0)
    for t in range(UNIT):
        square_sums(0, t)
    values(0, 0)
    statistics(1, 1)
    for t in range(UNIT):
        rms_normed(0, t)
    normed(1, 1)
    shift(0, 0, 0)
    shift(0, 0, 1)

    def body(s, b, later):
        n, nb = s + 1, 1 - b
        shift(s, b, 2)
        if not (isinstance(s, int) and s == 0):
            residual(s - 1)
        outputs(s, 0)
        shift(s, b, 3)
        if later == 2:
            statistics(s + 2, b)
        outputs(s, 1)
        if later:
            for t in range(UNIT):
                square_sums(n, t)
            values(n, nb)
            rms_normed(n, 0)
            rms_normed(n, 1)
        outputs(s, 2)
        if later:
            rms_normed(n, 2)
            rms_normed(n, 3)
        outputs(s, 3)
        if later:
            mask_bias(n, nb)
        if later == 2:
            normed(s + 2, b)
        if later:
            shift(n, nb, 0)
            shift(n, nb, 1)
    over_units_ahead(dve, body)
    norm_first(nc, dve, K, following(K, p))
    residual(UNITS - 1)


def l3_pool(nc, pool, K):
    p = A3
    V = K.v[p]

    def front(s):
        rstd_pool(nc, pool, K, p, s, True)
        rstd_pool(nc, pool, K, p, s, False)

    def factors(s):
        for t in range(UNIT):
            pool.wait_ge(K.rms_steps.sem, K.rms_steps.value(p, s, 2 * t + 2))
            pool.tensor_tensor(V.rms[:, t, :, :].rearrange("p c h -> p (c h)"), V.ss[:, t, :, :].rearrange("p c h -> p (c h)"),
                               K.minus_half[:, 0:6], ALU.pow).then_inc(K.rms_ready.sem, 1)

    if p == K.phases[0]:
        norm_first_pool(nc, pool, K, p)
    factors(0)
    front(1)

    def body(s, b, later):
        if later == 2:
            front(s + 2)
        if later:
            factors(s + 1)
    over_units_ahead(pool, body)


G_BANKS, U_BANKS, C_BANKS, D_BANK, R_BANK = (0, 1), (2, 3), (4, 7), 5, 6
NORM_AT = {F0: 2, F1: 2, F2: 1}
BACK_AT = {F0: 3, F1: 3, F2: 2}
AT = {F0: (4, 6, 15), F1: (4, 6, 11), F2: (3, 4, 7)}
ROUTE_PARTS = {F0: 8, F1: 3, F2: 1, F3: 1}


def side(p, b, j):
    return (b * CHUNKS[p] + j) % 2


def chunk(p, s, b, j):
    J = CHUNKS[p]
    return (s, b, j) if j < J else (s + 1, 1 - b, j - J)


def expert_of(p, r):
    return r // 2 if p == F1 else r


def front_tensor(nc, pe, K, p, s, b, part, bank):
    if part == 0:
        pe.wait_ge(K.y_ready.sem, K.y_ready.value(p, s, 1))
        if K.x_done.due(p, s, -1):
            pe.wait_ge(K.x_done.sem, K.x_done.value(p, s, -1))
        transpose4(nc, K, bank, lambda t: K.yt[:, t, :], P).then_inc(K.yT_psum.sem, 1)
    elif part == 1:
        pe.wait_ge(K.yT_ready.sem, K.yT_ready.value(p, s, 1))
        E = EXPERTS[p]
        for t in range(UNIT):
            last = nc.tensor.matmul(bank[:, t * E:(t + 1) * E], K.yT[b][:, t * P:(t + 1) * P], K.rcol[p], start=True, stop=True)
        last.then_inc(K.logits_psum.sem, 1)
    else:
        E = 32 if p == F0 else 8
        pe.wait_ge(K.route_steps.sem, K.route_steps.value(p, s, K.route_steps.counts[p]))
        cw = route_views(K, p).cw
        transpose4(nc, K, bank, lambda t: cw[:, t, :], E).then_inc(K.cw_psum.sem, 1)


def back_tensor(nc, pe, K, p, s, nxt, bank):
    pe.wait_ge(K.dt_ready.sem, K.dt_ready.value(p, s, 1))
    if nxt is not None:
        pe.wait_ge(K.cwT_ready.sem, K.cwT_ready.value(p, nxt, 1))
    else:
        pe.wait_ge(K.x_done.sem, K.x_done.value(p, s, 0))
    transpose4(nc, K, bank, lambda t: K.v[p].dt[:, t * P:(t + 1) * P], P).then_inc(K.outT_psum.sem, 1)


def experts_tensor(nc, pe, K, p):
    V = K.v[p]
    J, SH = CHUNKS[p], SHARED[p]
    mm, bank = nc.tensor.matmul, K.bank

    def product(out, which, j, high, low, start=True, stop=True):
        mm(out, V.w_hi[:, which, j, :], high, start=start, stop=False)
        mm(out, V.w_hi[:, which, j, :], low, start=False, stop=False)
        return mm(out, V.w_lo[:, which, j, :], high, start=False, stop=stop)

    def rows_product(out, which, b, j):
        if p == F2:
            rows = V.scaled[(j - SH) % 2] if j >= SH else K.yT[b][:, :]
            return mm(out, K.raw[F2][:, which, j, :], rows, start=True, stop=True)
        return product(out, which, j, V.y_hi[b], V.y_lo[b])

    def combine(s, b, r):
        if r == 0:
            pe.wait_ge(K.cwT_ready.sem, K.cwT_ready.value(p, s, 1))
        if p == F2:
            if K.scaled_made.due(p, s, r - 1):
                pe.wait_ge(K.scaled_made.sem, K.scaled_made.value(p, s, r - 1))
        else:
            if K.hid_made.due(p, s, r + SH - 1):
                pe.wait_ge(K.hid_made.sem, K.hid_made.value(p, s, r + SH - 1))
        mm(bank[C_BANKS[r % 2]], K.sel[:, expert_of(p, r), :], K.cwT[:, b, :], start=True, stop=True).then_inc(K.c_psum.sem, 1)

    def up(s, b, j):
        if p == F2 and j >= SH:
            pe.wait_ge(K.scaled_made.sem, K.scaled_made.value(p, s, j - SH + 1))
        if K.silu_ready.due(p, s, j - 1):
            pe.wait_ge(K.silu_ready.sem, K.silu_ready.value(p, s, j - 1))
        rows_product(bank[G_BANKS[side(p, b, j)]], 0, b, j).then_inc(K.g_psum.sem, 1)
        if K.hid_made.due(p, s, j - 1):
            pe.wait_ge(K.hid_made.sem, K.hid_made.value(p, s, j - 1))
        rows_product(bank[U_BANKS[side(p, b, j)]], 1, b, j).then_inc(K.u_psum.sem, 1)

    def down(s, b, j):
        if j == 0 and K.dt_ready.due(p, s, 0):
            pe.wait_ge(K.dt_ready.sem, K.dt_ready.value(p, s, 0))
        pe.wait_ge(K.hid_ready.sem, K.hid_ready.value(p, s, j + 1))
        product(bank[D_BANK], 2, j, V.hid_hi[side(p, b, j)], V.hid_lo[side(p, b, j)], start=j == 0,
                stop=j == J - 1).then_inc(K.down_done.sem, 1)

    def step(s, b, j, last):
        cs, cb, cj = chunk(p, s, b, j + 2)
        if p == F2 and cj >= SH and not (last and j + 2 >= J):
            combine(cs, cb, cj - SH)
        cs, cb, cj = chunk(p, s, b, j)
        if not (last and j >= J):
            if cj == 0 and p == F2:
                pe.wait_ge(K.yT_ready.sem, K.yT_ready.value(p, cs, 1))
            elif cj == 0:
                pe.wait_ge(K.y_low.sem, K.y_low.value(p, cs, 1))
            up(cs, cb, cj)
            if p != F2 and cj >= SH:
                combine(cs, cb, cj - SH)

    def body(s, b, last):
        for j in range(2, J + 2):
            step(s, b, j, last)
            down(s, b, j - 2)
            if j == BACK_AT[p] and not (isinstance(s, int) and s == 0):
                back_tensor(nc, pe, K, p, s - 1, s, bank[R_BANK])
            if not last and j in AT[p]:
                front_tensor(nc, pe, K, p, s + 1, 1 - b, AT[p].index(j), bank[R_BANK])

    pe.wait_ge(K.loaded[p], 16 * LOADS[p])
    if p == F0:
        raw = K.raw[F0].rearrange("p w j n -> p (w j) n")
        for n, (i0, m) in enumerate(PREP_GROUPS):
            if n >= 2:
                pe.wait_ge(K.low[F0], n - 1)
            for i in range(m):
                last = nc.tensor.transpose(bank[n % 2][:, i * P:(i + 1) * P], raw[:, i0 + i, :], K.ident[:, :])
            last.then_inc(K.prep_psum, 1)
    front_tensor(nc, pe, K, p, 0, 0, 0, bank[R_BANK])
    front_tensor(nc, pe, K, p, 0, 0, 1, bank[R_BANK])
    pe.wait_ge(K.low[p], len(groups(p)))
    pe.wait_ge(K.sel_ready, sum(q in CHUNKS for q in K.phases[:K.phases.index(p) + 1]))
    if p == F2:
        front_tensor(nc, pe, K, p, 0, 0, 2, bank[R_BANK])
        combine(0, 0, 0)
    step(0, 0, 0, False)
    if p == F0:
        front_tensor(nc, pe, K, p, 0, 0, 2, bank[R_BANK])
    step(0, 0, 1, False)
    if p == F1:
        front_tensor(nc, pe, K, p, 0, 0, 2, bank[R_BANK])
    over_units(pe, body)
    back_tensor(nc, pe, K, p, UNITS - 1, None, bank[R_BANK])


def groups(p):
    return {F0: range(len(PREP_GROUPS)), F1: range(3), F2: range(2, 3)}[p]


def weight_group(K, p, n):
    V = K.v[p]
    if p == F0:
        i0, m = PREP_GROUPS[n]
        hi, lo = (w.rearrange("p w j n -> p (w j) n")[:, i0:i0 + m, :] for w in (V.w_hi, V.w_lo))
        return K.bank[n % 2][:, 0:m * P].rearrange("p (w n) -> p w n", n=P), hi, lo
    return K.raw[p][:, n], V.w_hi[:, n], V.w_lo[:, n]


def experts_scalar(nc, act, K, p):
    V = K.v[p]
    J, SH = CHUNKS[p], SHARED[p]

    def high(s, b, j):
        act.wait_ge(K.hid_made.sem, K.hid_made.value(p, s, j + 1))
        if K.down_done.due(p, s, j - 1):
            act.wait_ge(K.down_done.sem, K.down_done.value(p, s, j - 1))
        act.activation(V.hid_hi[side(p, b, j)], V.hid[side(p, b, j)], ACT.Copy).then_inc(K.hid_high.sem, 1)

    def step(s, b, j, last):
        cs, cb, cj = chunk(p, s, b, j)
        if not (last and j >= J):
            act.wait_ge(K.g_psum.sem, K.g_psum.value(p, cs, cj + 1))
            if K.hid_made.due(p, cs, cj - 1):
                act.wait_ge(K.hid_made.sem, K.hid_made.value(p, cs, cj - 1))
            act.activation(V.silu[side(p, cb, cj)], K.bank[G_BANKS[side(p, cb, cj)]],
                           ACT.Silu).then_inc(K.silu_ready.sem, 1)

    def body(s, b, last):
        for j in range(1, J + 1):
            step(s, b, j, last)
            high(s, b, j - 1)
            if j == 1 and not (isinstance(s, int) and s == 0):
                scale_outputs(nc, act, K, p, s - 1, K.bank[D_BANK])
            if not last and j in AT[p]:
                front(s + 1, 1 - b, AT[p].index(j))

    def front(s, b, part):
        front_scalar(nc, act, K, p, s, b, part, K.bank[R_BANK])
        if part == 0 and p != F2:
            act.wait_ge(K.yT_ready.sem, K.yT_ready.value(p, s, 1))
            act.activation(V.y_hi[b], K.yT[b][:, :], ACT.Copy).then_inc(K.y_high.sem, 1)

    def weights_high(n):
        src, hi, _ = weight_group(K, p, n)
        if p == F0:
            act.wait_ge(K.prep_psum, n + 1)
        act.activation(hi, src, ACT.Copy).then_inc(K.high[p], 1)

    if p == F0:
        for n in groups(p):
            weights_high(n)
        front(0, 0, 0)
    else:
        act.wait_ge(K.loaded[p], 16 * LOADS[p])
        front(0, 0, 0)
        for n in groups(p):
            weights_high(n)
    act.wait_ge(K.fill, fills(K, p))
    front(0, 0, 1)
    front(0, 0, 2)
    step(0, 0, 0, False)
    over_units(act, body)
    scale_outputs(nc, act, K, p, UNITS - 1, K.bank[D_BANK])


def experts_pool(nc, pool, K, p):
    V = K.v[p]

    def rows_low(s, b):
        pool.wait_ge(K.y_high.sem, K.y_high.value(p, s, 1))
        pool.tensor_tensor(V.y_lo[b], K.yT[b][:, :], V.y_hi[b].bitcast(F32), ALU.subtract).then_inc(K.y_low.sem, 1)

    def body(s, b, last):
        for j in range(CHUNKS[p]):
            pool.wait_ge(K.hid_high.sem, K.hid_high.value(p, s, j + 1))
            if K.down_done.due(p, s, j - 1):
                pool.wait_ge(K.down_done.sem, K.down_done.value(p, s, j - 1))
            i = side(p, b, j)
            pool.tensor_tensor(V.hid_lo[i], V.hid[i], V.hid_hi[i].bitcast(F32),
                               ALU.subtract).then_inc(K.hid_ready.sem, 1)
            if not last and j == 0:
                rstd_pool(nc, pool, K, p, s + 1, False)
            if not last and j == AT[p][0] and p != F2:
                rows_low(s + 1, 1 - b)

    if p == K.phases[0]:
        norm_first_pool(nc, pool, K, p)
    if p != F2:
        rows_low(0, 0)
    over_units(pool, body)


def scale_outputs(nc, act, K, p, s, bank):
    act.wait_ge(K.down_done.sem, K.down_done.value(p, s, K.down_done.counts[p]))
    if K.x_done.due(p, s, 0):
        act.wait_ge(K.x_done.sem, K.x_done.value(p, s, 0))
    scale = K.gates[:, 4 + p // 2:5 + p // 2]
    act.activation(K.v[p].dt, bank, ACT.Copy, scale=scale).then_inc(K.dt_ready.sem, 1)


def front_scalar(nc, act, K, p, s, b, part, bank):
    R = route_views(K, p)
    if part == 0:
        yT_evacuate(nc, act, K, p, s, b, bank)
    elif part == 1 and p == F0:
        act.wait_ge(K.logits_psum.sem, K.logits_psum.value(p, s, 1))
        if K.route_steps.due(p, s, 0):
            act.wait_ge(K.route_steps.sem, K.route_steps.value(p, s, 0))
        act.activation(R.score, bank[:, 0:UNIT * 32].rearrange("p (t e) -> p t e", t=UNIT), ACT.Tanh,
                       scale=0.5).then_inc(K.logits_ready.sem, 1)
    elif part == 1:
        act.wait_ge(K.route_steps.sem, K.route_steps.value(p, s, R1_STEPS[p]))
        act.activation(R.e, R.d, ACT.Exp).then_inc(K.exp_ready.sem, 1)


R1_STEPS = {F1: 7, F2: 3, F3: 4}


def route_views(K, p):
    R = Kernel()
    E = 32 if p == F0 else 8
    R.E, at = E, 0
    tile = K.route

    def take(*shape):
        nonlocal at
        n = 1
        for x in shape:
            n *= x
        v = tile[:, at:at + n]
        at += n
        assert at <= 2048
        if len(shape) > 1:
            v = v.rearrange("p (a b) -> p a b", a=shape[0])
        return v

    R.count = [take(UNIT, PAD + 32) for _ in range(3)]
    R.score, R.biased, R.masked = take(UNIT, E), take(UNIT, E), take(UNIT, E)
    R.best, R.tmp, R.d, R.e, R.sel, R.cw = (take(UNIT, n) for n in (8, E, E, E, E, E))
    R.group, R.gsel = take(UNIT, 8), take(UNIT, 8)
    R.n, R.sum, R.inv = take(UNIT, 1), take(UNIT, 1), take(UNIT, 1)
    R.touch = take(UNIT, 1)
    return R


def top_marks(nc, dve, R, steps, out, values, threshold, E):
    eq = R.count[0]
    thr = threshold.to_broadcast([P, UNIT, E])
    dve.tensor_tensor(out, values, thr, ALU.is_gt).then_inc(steps.sem, steps.one())
    dve.tensor_tensor(eq[:, :, PAD:PAD + E], values, thr, ALU.is_equal).then_inc(steps.sem, steps.one())
    dve.wait_ge(steps.sem, steps.value())
    dve.tensor_reduce(R.n, out, axis=AX.X, op=ALU.add).then_inc(steps.sem, steps.one())


def top_ranks(nc, dve, R, steps, E):
    src, at, sh = R.count[0], 1, 1
    while sh < E:
        dst = R.count[at]
        dve.tensor_tensor(dst[:, :, PAD:PAD + E], src[:, :, PAD:PAD + E], src[:, :, PAD - sh:PAD - sh + E],
                          ALU.add).then_inc(steps.sem, steps.one())
        dve.wait_ge(steps.sem, steps.value())
        src, at, sh = dst, 3 - at, 2 * sh


def top_pick(nc, dve, R, steps, out, E, k):
    doublings = E.bit_length() - 1
    ranks = R.count[2 - doublings % 2]
    tmp = R.tmp[:, :, 0:E]
    dve.tensor_tensor(tmp, ranks[:, :, PAD:PAD + E], R.n.to_broadcast([P, UNIT, E]), ALU.add).then_inc(steps.sem, steps.one())
    dve.wait_ge(steps.sem, steps.value())
    dve.scalar_tensor_tensor(out=tmp, in0=tmp, scalar=float(k), in1=R.count[0][:, :, PAD:PAD + E], op0=ALU.is_le,
                             op1=ALU.mult).then_inc(steps.sem, steps.one())
    dve.wait_ge(steps.sem, steps.value())
    dve.tensor_tensor(out, out, tmp, ALU.add).then_inc(steps.sem, steps.one())
    dve.wait_ge(steps.sem, steps.value())


def best8(nc, dve, R, steps, values):
    dve.wait_ge(steps.sem, steps.value())
    dve.tensor_copy(R.touch, values[:, :, 0:1]).then_inc(steps.sem, steps.one())
    for t in range(UNIT):
        dve.max(R.best[:, t, :], values[:, t, :]).then_inc(steps.sem, steps.one())
    dve.wait_ge(steps.sem, steps.value())


def route_first(nc, dve, K, p, s, bank):
    R = route_views(K, p)
    steps = Steps(K.route_steps, p, s)
    if p == F0:
        return steps
    dve.wait_ge(K.logits_psum.sem, K.logits_psum.value(p, s, 1))
    n = EXPERTS[p]
    lg = bank[:, 0:UNIT * n].rearrange("p (t e) -> p t e", t=UNIT)
    if p == F1:
        dve.tensor_tensor(R.score, lg, K.ebias1.unsqueeze(1).to_broadcast([P, UNIT, 8]), ALU.add).then_inc(steps.sem, steps.one())
        best8(nc, dve, R, steps, R.score)
        dve.tensor_tensor(R.d, R.score, R.best[:, :, 0:1].to_broadcast([P, UNIT, 8]), ALU.subtract).then_inc(steps.sem, steps.one())
    elif p == F2:
        dve.tensor_copy(R.score, lg).then_inc(steps.sem, steps.one())
        dve.wait_ge(steps.sem, steps.value())
        dve.tensor_reduce(R.sum, R.score, axis=AX.X, op=ALU.max).then_inc(steps.sem, steps.one())
        dve.wait_ge(steps.sem, steps.value())
        dve.tensor_tensor(R.d, R.score, R.sum.to_broadcast([P, UNIT, 8]), ALU.subtract).then_inc(steps.sem, steps.one())
    else:
        dve.wait_ge(K.r2_ready.sem, K.r2_ready.value(p, s, 1))
        r2 = K.lnw[:, 2, :].unsqueeze(2)
        dve.tensor_tensor(R.tmp[:, :, 0:4], lg, r2.to_broadcast([P, UNIT, 4]), ALU.mult).then_inc(steps.sem, steps.one())
        dve.wait_ge(steps.sem, steps.value())
        dve.tensor_tensor(R.score[:, :, 0:4], R.tmp[:, :, 0:4], K.logit_bias3.unsqueeze(1).to_broadcast([P, UNIT, 4]),
                          ALU.add).then_inc(steps.sem, steps.one())
        dve.wait_ge(steps.sem, steps.value())
        dve.tensor_reduce(R.sum, R.score, axis=AX.X, op=ALU.max).then_inc(steps.sem, steps.one())
        dve.wait_ge(steps.sem, steps.value())
        dve.tensor_tensor(R.d, R.score, R.sum.to_broadcast([P, UNIT, 8]), ALU.subtract).then_inc(steps.sem, steps.one())
    assert steps.n == R1_STEPS[p]
    return steps


def route_second(nc, dve, K, p, s, steps, part, b=0):
    R = route_views(K, p)
    E, k = R.E, TOP[p]

    def over_sum(out, values, extra, scale):
        dve.tensor_reduce(R.sum, values, axis=AX.X, op=ALU.add).then_inc(steps.sem, steps.one())
        dve.wait_ge(steps.sem, steps.value())
        dve.tensor_scalar(R.sum, R.sum, extra, None, ALU.add).then_inc(steps.sem, steps.one())
        dve.wait_ge(steps.sem, steps.value())
        dve.reciprocal(R.inv, R.sum).then_inc(steps.sem, steps.one())
        dve.wait_ge(steps.sem, steps.value())
        dve.scalar_tensor_tensor(out=out, in0=values, scalar=scale, in1=R.inv.to_broadcast([P, UNIT, E]),
                                 op0=ALU.mult, op1=ALU.mult).then_inc(steps.sem, steps.one())

    if p == F0 and part == 0:
        dve.wait_ge(K.logits_ready.sem, K.logits_ready.value(p, s, 1))
        dve.tensor_scalar(R.score, R.score, 0.5, 0.5, ALU.mult, ALU.add).then_inc(steps.sem, steps.one())
        dve.wait_ge(steps.sem, steps.value())
        dve.tensor_tensor(R.biased, R.score, K.ebias0.unsqueeze(1).to_broadcast([P, UNIT, 32]), ALU.add).then_inc(steps.sem, steps.one())
        dve.wait_ge(steps.sem, steps.value())
        dve.tensor_reduce(R.group.rearrange("p t g -> p (t g)"), R.biased.rearrange("p t (g e) -> p (t g) e", e=4),
                          axis=AX.X, op=ALU.max).then_inc(steps.sem, steps.one())
    elif p == F0 and part == 1:
        best8(nc, dve, R, steps, R.group)
        top_marks(nc, dve, R, steps, R.gsel, R.group, R.best[:, :, 3:4], 8)
    elif p == F0 and part == 2:
        top_ranks(nc, dve, R, steps, 8)
        top_pick(nc, dve, R, steps, R.gsel, 8, 4)
    elif p == F0 and part == 3:
        dve.tensor_tensor(R.masked.rearrange("p t (g e) -> p (t g) e", e=4), R.biased.rearrange("p t (g e) -> p (t g) e", e=4),
                          R.gsel.rearrange("p t g -> p (t g)").unsqueeze(2).to_broadcast([P, UNIT * 8, 4]),
                          ALU.mult).then_inc(steps.sem, steps.one())
        best8(nc, dve, R, steps, R.masked)
    elif p == F0 and part == 4:
        top_marks(nc, dve, R, steps, R.sel, R.masked, R.best[:, :, k - 1:k], 32)
    elif p == F0 and part == 5:
        top_ranks(nc, dve, R, steps, 32)
    elif p == F0 and part == 6:
        top_pick(nc, dve, R, steps, R.sel, 32, k)
        dve.tensor_tensor(R.d, R.score, R.sel, ALU.mult).then_inc(steps.sem, steps.one())
    elif p == F0:
        dve.wait_ge(steps.sem, steps.value())
        if K.cw_psum.due(p, s, 0):
            dve.wait_ge(K.cw_psum.sem, K.cw_psum.value(p, s, 0))
        over_sum(R.cw, R.d, 1e-20, 2.5)
    elif p == F1 and part == 0:
        top_marks(nc, dve, R, steps, R.sel, R.score, R.best[:, :, k - 1:k], 8)
    elif p == F1 and part == 1:
        top_ranks(nc, dve, R, steps, 8)
        top_pick(nc, dve, R, steps, R.sel, 8, k)
    elif p == F1:
        dve.wait_ge(K.exp_ready.sem, K.exp_ready.value(p, s, 1))
        dve.tensor_tensor(R.tmp, R.e, R.sel, ALU.mult).then_inc(steps.sem, steps.one())
        dve.wait_ge(steps.sem, steps.value())
        if K.cw_psum.due(p, s, 0):
            dve.wait_ge(K.cw_psum.sem, K.cw_psum.value(p, s, 0))
        over_sum(R.cw, R.tmp, 0.0, 1.0)
    else:
        dve.wait_ge(K.exp_ready.sem, K.exp_ready.value(p, s, 1))
        over_sum(R.masked, R.e, 0.0, 1.0)
        best8(nc, dve, R, steps, R.masked)
        top_marks(nc, dve, R, steps, R.sel, R.masked, R.best[:, :, k - 1:k], 8)
        top_ranks(nc, dve, R, steps, 8)
        top_pick(nc, dve, R, steps, R.sel, 8, k)
        if p == F2:
            if K.cw_psum.due(p, s, 0):
                dve.wait_ge(K.cw_psum.sem, K.cw_psum.value(p, s, 0))
            dve.tensor_tensor(R.cw, R.masked, R.sel, ALU.mult).then_inc(steps.sem, steps.one())
        else:
            dve.tensor_tensor(R.biased, R.masked, R.sel, ALU.mult).then_inc(steps.sem, steps.one())
            dve.wait_ge(steps.sem, steps.value())
            if K.mix_steps.due(p, s, -E3):
                dve.wait_ge(K.mix_steps.sem, K.mix_steps.value(p, s, -E3))
            over_sum(K.v[p].cw[b], R.biased, 1e-8, 1.0)
    if part == ROUTE_PARTS[p] - 1:
        steps.ended()


def split_combine(nc, dve, K, p, s, b, bank):
    E = 32 if p == F0 else 8
    dve.wait_ge(K.cw_psum.sem, K.cw_psum.value(p, s, 1))
    if K.c_psum.due(p, s, -K.c_psum.counts[p]):
        dve.wait_ge(K.c_psum.sem, K.c_psum.value(p, s, -K.c_psum.counts[p]))
    dve.tensor_copy(K.cwT[0:E, b, :], bank[0:E, :]).then_inc(K.cw_steps.sem, 1)
    dve.wait_ge(K.cw_steps.sem, K.cw_steps.value(p, s, 1))
    dve.tensor_tensor(K.cwT[32:32 + E, b, :], bank[0:E, :], K.cwT[0:E, b, :].bitcast(F32),
                      ALU.subtract).then_inc(K.cwT_ready.sem, 1)


def experts_vector(nc, dve, K, p):
    V = K.v[p]
    J, SH = CHUNKS[p], SHARED[p]
    r_bank = K.bank[R_BANK]

    def scaled(s, b, r):
        dve.wait_ge(K.c_psum.sem, K.c_psum.value(p, s, r + 1))
        if r == 0:
            dve.wait_ge(K.yT_ready.sem, K.yT_ready.value(p, s, 1))
        if K.u_psum.due(p, s, r + SH - 1):
            dve.wait_ge(K.u_psum.sem, K.u_psum.value(p, s, r + SH - 1))
        dve.tensor_tensor(V.scaled[r % 2], K.yT[b][:, :], K.bank[C_BANKS[r % 2]], ALU.mult).then_inc(K.scaled_made.sem, 1)

    def hidden(s, b, j):
        dve.wait_ge(K.silu_ready.sem, K.silu_ready.value(p, s, j + 1))
        dve.wait_ge(K.u_psum.sem, K.u_psum.value(p, s, j + 1))
        if K.hid_ready.due(p, s, j - 1):
            dve.wait_ge(K.hid_ready.sem, K.hid_ready.value(p, s, j - 1))
        i = side(p, b, j)
        u = K.bank[U_BANKS[i]]
        if p == F2 or j < SH:
            dve.tensor_tensor(V.hid[i], V.silu[i], u, ALU.mult).then_inc(K.hid_made.sem, 1)
            return
        r = j - SH
        dve.tensor_tensor(V.prod[i], V.silu[i], u, ALU.mult).then_inc(K.prod_steps.sem, 1)
        dve.wait_ge(K.c_psum.sem, K.c_psum.value(p, s, r + 1))
        dve.wait_ge(K.prod_steps.sem, K.prod_steps.value(p, s, r + 1))
        dve.tensor_tensor(V.hid[i], V.prod[i], K.bank[C_BANKS[r % 2]], ALU.mult).then_inc(K.hid_made.sem, 1)

    def added(s):
        dve.wait_ge(K.outT_psum.sem, K.outT_psum.value(p, s, 1))
        dve.tensor_tensor(xu(K, s), r_bank.rearrange("p (t d) -> p t d", t=UNIT), xu(K, s), ALU.add).then_inc(K.x_done.sem, 1)

    def body(s, b, last):
        for j in range(J):
            cs, cb, cj = chunk(p, s, b, j + 2)
            if p == F2 and cj >= SH and not (last and j + 2 >= J):
                scaled(cs, cb, cj - SH)
            hidden(s, b, j)
            if j == BACK_AT[p] and not (isinstance(s, int) and s == 0):
                added(s - 1)
            if last:
                continue
            if j == 0:
                x_statistics(nc, dve, K, p, s + 1)
            if j == NORM_AT[p]:
                x_normed(nc, dve, K, p, s + 1)
            if j == AT[p][1]:
                steps = route_first(nc, dve, K, p, s + 1, r_bank)
            if 0 <= j - AT[p][1] - 1 < ROUTE_PARTS[p]:
                route_second(nc, dve, K, p, s + 1, steps, j - AT[p][1] - 1)
            if j == AT[p][2]:
                split_combine(nc, dve, K, p, s + 1, 1 - b, r_bank)

    if p == K.phases[0]:
        norm_first(nc, dve, K, p)
    if p != F0:
        dve.wait_ge(K.loaded[p], 16 * LOADS[p])
    for i, n in enumerate(groups(p)):
        src, hi, lo = weight_group(K, p, n)
        dve.wait_ge(K.high[p], i + 1)
        dve.tensor_tensor(lo, src, hi.bitcast(F32), ALU.subtract).then_inc(K.low[p], 1)
    dve.wait_ge(K.fill, fills(K, p))
    dve.tensor_copy(K.sel[:, :, :], V.selraw).then_inc(K.sel_ready, 1)
    steps = route_first(nc, dve, K, p, 0, r_bank)
    for part in range(ROUTE_PARTS[p]):
        route_second(nc, dve, K, p, 0, steps, part)
    split_combine(nc, dve, K, p, 0, 0, r_bank)
    if p == F2:
        scaled(0, 0, 0)
    over_units(dve, body)
    norm_first(nc, dve, K, following(K, p))
    added(UNITS - 1)


H3_BANKS, T3_BANKS, D3_BANK, R3_BANK = (0, 1, 2, 3), (4, 5), 6, 7
E3 = EXPERTS[F3]
Q3 = E3 * HID3 // P
H3 = 2 * UNIT


def l3_experts_tensor(nc, pe, K):
    p = F3
    V = K.v[p]
    mm, bank = nc.tensor.matmul, K.bank

    def rows(s):
        pe.wait_ge(K.y_ready.sem, K.y_ready.value(p, s, 1))
        n = R1_STEPS[p] - K.route_steps.counts[p]
        if K.route_steps.due(p, s, n):
            pe.wait_ge(K.route_steps.sem, K.route_steps.value(p, s, n))
        transpose4(nc, K, bank[R3_BANK], lambda t: K.yt[:, t, :], P).then_inc(K.yT_psum.sem, 1)

    def logits(s, b):
        pe.wait_ge(K.yT_ready.sem, K.yT_ready.value(p, s, 1))
        for t in range(UNIT):
            last = mm(bank[R3_BANK][:, t * E3:(t + 1) * E3], K.yT[b][:, t * P:(t + 1) * P], K.rcol[p],
                      start=True, stop=True)
        last.then_inc(K.logits_psum.sem, 1)

    def hidden(s, b, i):
        t, g = i // 2, i % 2
        if i == 0:
            pe.wait_ge(K.yT_ready.sem, K.yT_ready.value(p, s, 1))
        if K.z_ready.due(p, s, t - 1):
            pe.wait_ge(K.z_ready.sem, K.z_ready.value(p, s, t - 1))
        mm(bank[H3_BANKS[i % 4]], K.yT[b][:, t * P:(t + 1) * P],
           K.w1[:, 2 * g:2 * g + 2, :].rearrange("p e h -> p (e h)"), start=True, stop=True).then_inc(K.g_psum.sem, 1)

    def turned(s, b, q):
        if q == 0:
            pe.wait_ge(K.z_ready.sem, K.z_ready.value(p, s, UNIT))
        if K.hid_ready.due(p, s, q - 1):
            pe.wait_ge(K.hid_ready.sem, K.hid_ready.value(p, s, q - 1))
        transpose4(nc, K, bank[T3_BANKS[q % 2]], lambda t: V.z[b][:, t, q * P:(q + 1) * P], P).then_inc(K.zT_psum.sem, 1)

    def down(s, e):
        pe.wait_ge(K.hid_ready.sem, K.hid_ready.value(p, s, 2 * e + 2))
        if K.mix_steps.due(p, s, e):
            pe.wait_ge(K.mix_steps.sem, K.mix_steps.value(p, s, e))
        for t in range(UNIT):
            for c in range(2):
                last = mm(bank[D3_BANK][:, t * D:(t + 1) * D], V.hid[(2 * e + c) % 4][:, t * P:(t + 1) * P],
                          K.w2[:, 2 * e + c, :], start=c == 0, stop=c == 1)
        last.then_inc(K.down_done.sem, 1)

    def body(s, b, later):
        n, nb = s + 1, 1 - b

        def first_stage(*products):
            if later:
                for i in products:
                    hidden(n, nb, i)
        turned(s, b, 0)
        first_stage(0, 1)
        turned(s, b, 1)
        turned(s, b, 2)
        first_stage(2, 3)
        turned(s, b, 3)
        down(s, 0)
        if later:
            logits(n, nb)
        turned(s, b, 4)
        first_stage(4)
        turned(s, b, 5)
        down(s, 1)
        first_stage(5)
        turned(s, b, 6)
        first_stage(6)
        turned(s, b, 7)
        down(s, 2)
        first_stage(7)
        if later == 2:
            rows(s + 2)
        down(s, 3)

    pe.wait_ge(K.w3_steps, 4 + 1)
    mm(bank[R3_BANK][:, 0:E3], V.rn_b, K.rcol[F3], start=True, stop=True).then_inc(K.bias3_psum, 1)
    pe.wait_ge(K.w3_steps, 4 + 1 + 2)
    rows(0)
    logits(0, 0)
    for i in range(H3):
        hidden(0, 0, i)
    rows(1)
    over_units_ahead(pe, body)


def l3_experts_scalar(nc, act, K):
    p = F3
    V = K.v[p]

    def squares(s, t):
        act.wait_ge(K.g_psum.sem, K.g_psum.value(p, s, 2 * t + 2))
        if K.var_steps.due(p, s, t - 1):
            act.wait_ge(K.var_steps.sem, K.var_steps.value(p, s, t - 1))
        for e in range(E3):
            last = act.activation(V.sq[:, (t % 2) * E3 + e, :], K.bank[H3_BANKS[(2 * t + e // 2) % 4]][:, (e % 2) * HID3:(e % 2 + 1) * HID3],
                                  ACT.Square, accum_out=V.ss[:, t % 2, e:e + 1])
        last.then_inc(K.sq_ready.sem, 1)

    def relu(s, q):
        act.wait_ge(K.zT_psum.sem, K.zT_psum.value(p, s, q + 1))
        if K.down_done.due(p, s, (q - 4) // 2 + 1):
            act.wait_ge(K.down_done.sem, K.down_done.value(p, s, (q - 4) // 2 + 1))
        act.activation(V.hid[q % 4], K.bank[T3_BANKS[q % 2]], ACT.Relu, scale=K.ln3_g[:, q:q + 1],
                       bias=K.ln3_b[:, q:q + 1]).then_inc(K.hid_ready.sem, 1)

    def exponentials(s):
        R = route_views(K, p)
        act.wait_ge(K.route_steps.sem, K.route_steps.value(p, s, R1_STEPS[p]))
        act.activation(R.e, R.d, ACT.Exp).then_inc(K.exp_ready.sem, 1)

    def body(s, b, later):
        n = s + 1
        relu(s, 0)
        if later:
            squares(n, 0)
        relu(s, 1)
        relu(s, 2)
        if later:
            squares(n, 1)
        relu(s, 3)
        relu(s, 4)
        relu(s, 5)
        if later:
            exponentials(n)
            squares(n, 2)
        relu(s, 6)
        relu(s, 7)
        if later:
            squares(n, 3)
        if later == 2:
            yT_evacuate(nc, act, K, p, s + 2, b, K.bank[R3_BANK])

    yT_evacuate(nc, act, K, p, 0, 0, K.bank[R3_BANK])
    exponentials(0)
    for t in range(UNIT):
        squares(0, t)
    yT_evacuate(nc, act, K, p, 1, 1, K.bank[R3_BANK])
    over_units_ahead(act, body)


def l3_experts_vector(nc, dve, K):
    p = F3
    V = K.v[p]
    r_bank = K.bank[R3_BANK]

    def variance(s, t):
        dve.wait_ge(K.sq_ready.sem, K.sq_ready.value(p, s, t + 1))
        if K.rinv_ready.due(p, s, t - 1):
            dve.wait_ge(K.rinv_ready.sem, K.rinv_ready.value(p, s, t - 1))
        dve.tensor_scalar(V.var[:, t % 2, :], V.ss[:, t % 2, :], 1.0 / HID3, EPS, ALU.mult,
                          ALU.add).then_inc(K.var_steps.sem, 1)

    def normed(s, b, t):
        dve.wait_ge(K.rinv_ready.sem, K.rinv_ready.value(p, s, t + 1))
        if t == 0 and K.zT_psum.due(p, s, -Q3):
            dve.wait_ge(K.zT_psum.sem, K.zT_psum.value(p, s, -Q3))
        for e in range(E3):
            last = dve.tensor_scalar(V.z[b][:, t, e * HID3:(e + 1) * HID3],
                                     K.bank[H3_BANKS[(2 * t + e // 2) % 4]][:, (e % 2) * HID3:(e % 2 + 1) * HID3],
                                     V.rinv[:, t % 2, e:e + 1], None, ALU.mult)
        last.then_inc(K.z_ready.sem, 1)

    def mix(s, b, e):
        dve.wait_ge(K.down_done.sem, K.down_done.value(p, s, e + 1))
        if e == 0:
            if K.onorm_ready.due(p, s, 0):
                dve.wait_ge(K.onorm_ready.sem, K.onorm_ready.value(p, s, 0))
        else:
            dve.wait_ge(K.mix_steps.sem, K.mix_steps.value(p, s, e))
        for t in range(UNIT):
            out, c = K.bank[D3_BANK][:, t * D:(t + 1) * D], V.cw[b][:, t, e:e + 1]
            if e == 0:
                last = dve.tensor_scalar(V.mixed[:, t, :], out, c, None, ALU.mult)
            else:
                last = dve.scalar_tensor_tensor(out=V.mixed[:, t, :], in0=out, scalar=c, in1=V.mixed[:, t, :],
                                                op0=ALU.mult, op1=ALU.add)
        last.then_inc(K.mix_steps.sem, 1)

    def back_statistics(s):
        dve.wait_ge(K.mix_steps.sem, K.mix_steps.value(p, s, E3))
        steps = Steps(K.res_steps, p, s)
        ln_statistics(nc, dve, K, p, s, steps, K.cstats, K.clnw, lambda t: V.mixed[:, t, :], D, False)
        steps.ended()

    def back_normed(s):
        dve.wait_ge(K.ostat_ready.sem, K.ostat_ready.value(p, s, 1))
        if K.scale_steps.due(p, s, 0):
            dve.wait_ge(K.scale_steps.sem, K.scale_steps.value(p, s, 0))
        ln_apply(nc, dve, V.onorm, lambda t: V.mixed[:, t, :], K.clnw, K.onorm_ready)

    def added(s):
        dve.wait_ge(K.scale_steps.sem, K.scale_steps.value(p, s, 2))
        dve.tensor_tensor(xu(K, s), V.gated, xu(K, s), ALU.add).then_inc(K.x_done.sem, 1)

    def body(s, b, later):
        n, nb = s + 1, 1 - b
        first = isinstance(s, int) and s == 0
        if later:
            variance(n, 0)
        if not first:
            back_normed(s - 1)
        if later:
            normed(n, nb, 0)
            variance(n, 1)
        mix(s, b, 0)
        if later:
            normed(n, nb, 1)
        if not first:
            added(s - 1)
        if later:
            steps = route_first(nc, dve, K, p, n, r_bank)
        mix(s, b, 1)
        if later:
            variance(n, 2)
        if later == 2:
            x_statistics(nc, dve, K, p, s + 2)
        if later:
            normed(n, nb, 2)
        if later == 2:
            router_norm(nc, dve, K, s + 2)
        mix(s, b, 2)
        if later:
            variance(n, 3)
        if later == 2:
            x_normed(nc, dve, K, p, s + 2)
        if later:
            normed(n, nb, 3)
            for part in range(ROUTE_PARTS[p]):
                route_second(nc, dve, K, p, n, steps, part, nb)
        mix(s, b, 3)
        back_statistics(s)

    dve.wait_ge(K.fill, fills(K, p))
    dve.wait_ge(K.loaded[p], 16 * LOADS[p])
    w1 = K.w1
    dve.tensor_reduce(V.wmean, w1, axis=AX.X, op=ALU.add).then_inc(K.w3_steps, 1)
    dve.wait_ge(K.w3_steps, 1)
    dve.tensor_scalar(V.wmean, V.wmean, 1.0 / HID3, None, ALU.mult).then_inc(K.w3_steps, 1)
    dve.wait_ge(K.w3_steps, 2)
    dve.tensor_tensor(w1, w1, V.wmean.unsqueeze(2).to_broadcast([P, E3, HID3]), ALU.subtract).then_inc(K.w3_steps, 1)
    dve.tensor_copy(V.rn_b, K.col["rn_b"].to_broadcast([P, P])).then_inc(K.w3_steps, 1)
    dve.tensor_scalar(K.rows[:, 4 * D:6 * D], K.rows[:, 4 * D:6 * D], K.gates[:, 7:8], None, ALU.mult).then_inc(K.w3_steps, 1)
    dve.wait_ge(K.bias3_psum, 1)
    dve.tensor_copy(K.logit_bias3, r_bank[:, 0:4]).then_inc(K.w3_steps, 1)
    dve.tensor_scalar(K.rcol[F3], K.rcol[F3], K.col["rn_g"], None, ALU.mult).then_inc(K.w3_steps, 1)
    dve.wait_ge(K.w3_steps, 7)
    if p == K.phases[0]:
        norm_first(nc, dve, K, p)
    steps = route_first(nc, dve, K, p, 0, r_bank)
    for part in range(ROUTE_PARTS[p]):
        route_second(nc, dve, K, p, 0, steps, part, 0)
    x_statistics(nc, dve, K, p, 1)
    for t in range(UNIT):
        variance(0, t)
        normed(0, 0, t)
    router_norm(nc, dve, K, 1)
    x_normed(nc, dve, K, p, 1)
    over_units_ahead(dve, body)
    back_normed(UNITS - 1)
    added(UNITS - 1)


def l3_experts_pool(nc, pool, K):
    p = F3
    V = K.v[p]

    def front(s):
        rstd_pool(nc, pool, K, p, s, False)
        router_norm_pool(nc, pool, K, s)

    def factors(s, t):
        pool.wait_ge(K.var_steps.sem, K.var_steps.value(p, s, t + 1))
        if K.z_ready.due(p, s, t - 1):
            pool.wait_ge(K.z_ready.sem, K.z_ready.value(p, s, t - 1))
        pool.tensor_tensor(V.rinv[:, t % 2, :], V.var[:, t % 2, :], K.minus_half[:, 0:E3],
                           ALU.pow).then_inc(K.rinv_ready.sem, 1)

    def back_factor(s):
        pool.wait_ge(K.res_steps.sem, K.res_steps.value(p, s, K.res_steps.counts[p]))
        pool.tensor_tensor(K.clnw[:, 0, :], K.clnw[:, 1, :], K.minus_half[:, 0:UNIT], ALU.pow).then_inc(K.ostat_ready.sem, 1)

    def back_gated(s):
        pool.wait_ge(K.onorm_ready.sem, K.onorm_ready.value(p, s, 1))
        if K.x_done.due(p, s, 0):
            pool.wait_ge(K.x_done.sem, K.x_done.value(p, s, 0))
        pool.tensor_tensor(V.gated, V.onorm, K.row["on_g"].unsqueeze(1).to_broadcast([P, UNIT, D]), ALU.mult)\
            .then_inc(K.scale_steps.sem, 1)
        pool.wait_ge(K.scale_steps.sem, K.scale_steps.value(p, s, 1))
        pool.tensor_tensor(V.gated, V.gated, K.row["on_b"].unsqueeze(1).to_broadcast([P, UNIT, D]), ALU.add)\
            .then_inc(K.scale_steps.sem, 1)

    if p == K.phases[0]:
        norm_first_pool(nc, pool, K, p)
    for t in range(UNIT):
        factors(0, t)
    front(1)

    def body(s, b, later):
        n = s + 1
        first = isinstance(s, int) and s == 0
        if later:
            factors(n, 0)
            factors(n, 1)
        if not first:
            back_gated(s - 1)
        if later:
            factors(n, 2)
        if later == 2:
            front(s + 2)
        if later:
            factors(n, 3)
        back_factor(s)
    over_units_ahead(pool, body)
    back_gated(UNITS - 1)


def fill_values(nc, pool, K, p):
    V = K.v[p]
    if p == A2:
        for b in range(2):
            pool.memset(V.vd[b][:, :, :, :, DH2].rearrange("p t y j -> p (t y) j"), 1.0)
    if p == A3:
        for b in range(2):
            pool.memset(V.vd[b][:, :, :, :, DH2].rearrange("p t y h -> p (t y) h"), 1.0)
            pool.memset(V.mb[b][:, :, SEQ:KEYS3], 0.0)
    pool.memset(K.touch[:, :], 0.0).then_inc(K.fill, 1)


def fill_selectors(nc, pool, K, p, count):
    V = K.v[p]
    if p != F3:
        pool.memset(V.selraw, 0.0)
        pool.memset(K.cwT[:, :, :].bitcast(F32), 0.0)
    R = route_views(K, p)
    for c in R.count:
        pool.memset(c[:, :, 0:PAD], 0.0)
    pool.memset(R.score, -MASKED)
    pool.memset(K.touch[:, :], 0.0).then_inc(K.fill, 1)
    if p == F3:
        return
    pool.wait_ge(K.fill, count + 1)
    for lo in (0, 32):
        v = V.selraw[lo:lo + 32]
        if p == F0:
            v = v.rearrange("p a (m i) -> p a m i", m=2)
            pattern = [[-2, 16], [-1, 2], [0, SEQ]]
        else:
            pattern = [[-1, 16], [0, P]]
        pool.affine_select(out=v, in_=v, compare_op=ALU.not_equal, fill=1.0, base=0, pattern=pattern,
                           channel_multiplier=1).then_inc(K.fill, 1)


FILLS = {A0: 6, A1: 6, A2: 1, A3: 1, F0: 3, F1: 3, F2: 3, F3: 1}


def fills(K, p):
    return sum(FILLS[q] for q in K.phases[:K.phases.index(p) + 1])


def pool_program(nc, pool, K):
    pool.memset(K.ident[:, :], 0.0).then_inc(K.const_steps, 1)
    pool.memset(K.ones[:, :], 1.0).then_inc(K.const_steps, 1)
    pool.memset(K.minus_half[:, :], -0.5).then_inc(K.const_steps, 1)
    pool.memset(K.eps_col, EPS).then_inc(K.const_steps, 1)
    pool.wait_ge(K.const_steps, 4)
    pool.affine_select(out=K.ident[:, :], in_=K.ident[:, :], compare_op=ALU.not_equal, fill=1.0, base=0,
                       pattern=[[-1, P]], channel_multiplier=1).then_inc(K.const_steps, 1)
    count = 0
    for p in K.phases:
        if p != K.phases[0]:
            norm_first_pool(nc, pool, K, p)
            pool.wait_ge(K.x_done.sem, K.x_done.start[p])
        if p in (A0, A1):
            assert small_fill(nc, pool, K, p, count) == count + FILLS[p]
            small_pool(nc, pool, K, p)
        elif p in ATTENTION:
            fill_values(nc, pool, K, p)
            (norm_pool(nc, pool, K, p) if p == A2 else l3_pool(nc, pool, K))
        else:
            fill_selectors(nc, pool, K, p, count)
            pool.wait_ge(K.fill, fills(K, p))
            pool.wait_ge(K.par_loaded, PAR)
            (l3_experts_pool(nc, pool, K) if p == F3 else experts_pool(nc, pool, K, p))
        count += FILLS[p]


def started(eng, K):
    eng.wait_ge(K.const_steps, 5)
    eng.wait_ge(K.par_first, PAR_FIRST)


def scalar_program(nc, act, K):
    for n, rows in (("q_b", P), ("k_b", P), ("ln_g", P), ("ln_b", P), ("tln_g", DC), ("tln_b", DC)):
        act.dma_start(K.col[n][0:rows], K.A[f"L0_xattn_{n}"].rearrange("(p o) -> p o", p=rows)).then_inc(K.par_first, 16)
    started(act, K)
    act.activation(K.gates[:, :], K.gates[:, :], ACT.Tanh).then_inc(K.gates_ready, 1)
    for p in K.phases:
        if p != K.phases[0]:
            act.wait_ge(K.x_done.sem, K.x_done.start[p])
        if p != A0:
            act.wait_ge(K.par_loaded, PAR)
        if p in (A2, A3):
            act.wait_ge(K.fill, fills(K, p))
        if p in (A0, A1):
            small_scalar(nc, act, K, p)
        elif p == A2:
            l2_scalar(nc, act, K)
        elif p == A3:
            l3_scalar(nc, act, K)
        elif p == F3:
            l3_experts_scalar(nc, act, K)
        else:
            experts_scalar(nc, act, K, p)


def vector_program(nc, dve, K):
    started(dve, K)
    dve.wait_ge(K.gates_ready, 1)
    dve.wait_ge(K.x_first, 16)
    if K.phases[0] != A0:
        dve.wait_ge(K.x_rest, 16)
    for p in K.phases:
        if p != K.phases[0]:
            dve.wait_ge(K.x_done.sem, K.x_done.start[p])
        if p != A0:
            dve.wait_ge(K.par_loaded, PAR)
        if p in (A2, A3):
            dve.wait_ge(K.fill, fills(K, p))
        if p in (A0, A1):
            small_vector(nc, dve, K, p)
        elif p == A2:
            l2_vector(nc, dve, K)
        elif p == A3:
            l3_vector(nc, dve, K)
        else:
            if p == first_experts(K):
                dve.wait_ge(K.router_psum, 1)
                dve.tensor_copy(K.router[:, :], K.bank[7][:, 0:52]).then_inc(K.router_ready, 1)
                dve.wait_ge(K.router_ready, 1)
            (l3_experts_vector(nc, dve, K) if p == F3 else experts_vector(nc, dve, K, p))


def first_experts(K):
    return next((p for p in K.phases if p in EXPERTS), None)


def tensor_program(nc, pe, K):
    started(pe, K)
    for p in K.phases:
        if p != K.phases[0]:
            pe.wait_ge(K.x_done.sem, K.x_done.start[p])
        if p != A0:
            pe.wait_ge(K.par_loaded, PAR)
        if p in (A2, A3):
            pe.wait_ge(K.fill, fills(K, p))
        if p == first_experts(K):
            nc.tensor.transpose(K.bank[7][:, 0:52], K.router_raw[:, :], K.ident[0:52, 0:52]).then_inc(K.router_psum, 1)
            pe.wait_ge(K.router_ready, 1)
        if p in (A0, A1):
            small_tensor(nc, pe, K, p)
        elif p == A2:
            l2_tensor(nc, pe, K)
        elif p == A3:
            l3_tensor(nc, pe, K)
        elif p == F3:
            l3_experts_tensor(nc, pe, K)
        else:
            experts_tensor(nc, pe, K, p)


def kernel(**inputs):
    import numpy as np
    import concourse.bacc as bacc
    from concourse.bass_utils import run_bass_kernel_spmd

    nc = bacc.Bacc("TRN2", target_bir_lowering=False, num_devices=1)
    arrays, args = {}, {}
    for name, value in inputs.items():
        a = np.ascontiguousarray(value)
        key = name
        if a.dtype == np.bool_:
            a, key = a.view(np.int32), "mask"
        arrays[f"in_{name}"] = a
        args[key] = nc.dram_tensor(f"in_{name}", a.shape, mybir.dt.from_np(a.dtype), kind="ExternalInput").ap()
    out = nc.dram_tensor("out", (SEQS, SEQ, D), F32, kind="ExternalOutput").ap()
    build(nc, args, out)
    r = run_bass_kernel_spmd(nc, [arrays], core_ids=[0])
    return r.results[0]["out"]
```
